# Optimizing a Trainium2 kernel written in Bass

```python
import numpy as np
import jax
import jax.numpy as jnp

def _softmax(x, axis=-1):
    return jax.nn.softmax(x, axis=axis)

def _gelu(x):
    return jax.nn.gelu(x, approximate=True)

def _silu(x):
    return jax.nn.silu(x)

def _sigmoid(x):
    return jax.nn.sigmoid(x)

def _layernorm(x, axis=-1, eps=1e-05):
    m = jnp.mean(x, axis=axis, keepdims=True)
    v = jnp.var(x, axis=axis, keepdims=True)
    return (x - m) / jnp.sqrt(v + eps)

def _scatter_add(tgt, idx, src, axis=0):
    return tgt.at[idx].add(src)

def _segment_sum(src, seg, n):
    return jax.ops.segment_sum(src, seg, n)
kernel_name = 'mk_audio_tower_d4_tok_aud1d1024_r4_08eda1'

def setup_inputs(seed: int=0):
    np.random.seed(seed)
    _w = jnp.asarray

    def _rec_inputs():
        import jax
        import jax.numpy as jnp
        _rk = jax.random.key(seed)
        x = -9.80646e-05 + 1.00041 * jax.random.normal(jax.random.fold_in(_rk, 1), (16, 4000), jnp.float32)
        return x
    x = _rec_inputs()

    def _L0_tok_setup():
        import jax, jax.numpy as jnp
        import numpy as np
        P = 16
        key = jax.random.key(seed)
        ks = jax.random.split(key, 7)
        B, L = (128, 1024)
        I, H = (512, 256)
        F = 2 * P
        s_in = 1.0 / np.sqrt(F)
        s_mid = 1.0 / np.sqrt(I)
        return {'x': jax.random.normal(ks[0], (B, L), jnp.float32), 'W_h': jax.random.normal(ks[1], (I, F), jnp.float32) * s_in, 'b_h': jax.random.normal(ks[2], (I,), jnp.float32) * s_in, 'W_o': jax.random.normal(ks[3], (H, I), jnp.float32) * s_mid, 'b_o': jax.random.normal(ks[4], (H,), jnp.float32) * s_mid, 'W_r': jax.random.normal(ks[5], (H, F), jnp.float32) * s_in, 'b_r': jax.random.normal(ks[6], (H,), jnp.float32) * s_in}
    _L0_tok_all = _L0_tok_setup()
    _L0_tok_in = {k: v for k, v in _L0_tok_all.items() if k in ('W_h', 'b_h', 'W_o', 'b_o', 'W_r', 'b_r')}
    del _L0_tok_all

    def _L0_attn_setup():
        import jax, jax.numpy as jnp
        import numpy as np
        DIM = 256
        DIM_HEAD = 16
        HEADS = 8
        EPS = 1e-05

        def rms_norm(x, gamma):
            n = jnp.sqrt(jnp.sum(x * x, axis=-1, keepdims=True))
            return gamma * (x / jnp.maximum(n, 1e-12)) * x.shape[-1] ** 0.5

        def second_taylor_expansion(x):
            d = x.shape[-1]
            x0 = jnp.ones(x.shape[:-1] + (1,), dtype=x.dtype)
            x2 = jnp.einsum('...i,...j->...ij', x, x) * 0.5 ** 0.5
            x2 = x2.reshape(x.shape[:-1] + (d * d,))
            return jnp.concatenate([x0, x, x2], axis=-1)
        key = jax.random.key(seed)
        ks = jax.random.split(key, 4)
        b, n = (4, 2048)
        dim_inner = DIM_HEAD * HEADS
        x = jax.random.normal(ks[0], (b, n, DIM), dtype=jnp.float32)
        gamma = jnp.ones((DIM,), dtype=jnp.float32)
        w_q = jax.random.normal(ks[1], (DIM, dim_inner), dtype=jnp.float32) * DIM ** (-0.5)
        w_kv = jax.random.normal(ks[2], (DIM, dim_inner * 2), dtype=jnp.float32) * DIM ** (-0.5)
        w_out = jax.random.normal(ks[3], (dim_inner, DIM), dtype=jnp.float32) * dim_inner ** (-0.5)
        return {'x': x, 'gamma': gamma, 'w_q': w_q, 'w_kv': w_kv, 'w_out': w_out}
    _L0_attn_all = _L0_attn_setup()
    _L0_attn_in = {k: v for k, v in _L0_attn_all.items() if k in ('gamma', 'w_q', 'w_kv', 'w_out')}
    del _L0_attn_all

    def _L0_ffn_setup():
        import jax, jax.numpy as jnp
        import numpy as np
        H = 256
        I = 256
        E = 8
        key = jax.random.key(seed)
        ks = jax.random.split(key, 8)
        s = 0.02
        x = jax.random.normal(ks[0], (4, 512, H), dtype=jnp.float32)
        Wg = jax.random.normal(ks[1], (H, E), dtype=jnp.float32) * s
        bg = jnp.zeros((E,), dtype=jnp.float32)
        W1 = jax.random.normal(ks[2], (E, H, I), dtype=jnp.float32) * s
        b1 = jnp.zeros((E, I), dtype=jnp.float32)
        W2 = jax.random.normal(ks[3], (E, I, H), dtype=jnp.float32) * s
        b2 = jnp.zeros((E, H), dtype=jnp.float32)
        return {'x': x, 'Wg': Wg, 'bg': bg, 'W1': W1, 'b1': b1, 'W2': W2, 'b2': b2}
    _L0_ffn_all = _L0_ffn_setup()
    _L0_ffn_in = {k: v for k, v in _L0_ffn_all.items() if k in ('Wg', 'bg', 'W1', 'b1', 'W2', 'b2')}
    del _L0_ffn_all

    def _L1_attn_setup():
        import jax, jax.numpy as jnp
        import numpy as np
        B, T, C, H = (2, 512, 256, 16)
        N = C // H
        TM_DIM, TD_DIM = (32, 64)
        EPS = 1e-05 * 8 ** 2

        def _forward(x, tmx, tmw, tmk, tmv, tmr, tmg, maa_w1, maa_w2, tdecay, td_w1, td_w2, u, Wr, Wk, Wv, Wg, Wo, ln_w, ln_b):
            Bq, Tq, Cq = x.shape
            xx = jnp.concatenate([jnp.zeros_like(x[:, :1]), x[:, :-1]], axis=1) - x
            xxx = x + xx * tmx
            t5 = jnp.tanh(xxx @ maa_w1).reshape(Bq, Tq, 5, TM_DIM)
            m = jnp.einsum('btfe,fec->fbtc', t5, maa_w2)
            xw = x + xx * (tmw + m[0])
            xk = x + xx * (tmk + m[1])
            xv = x + xx * (tmv + m[2])
            xr = x + xx * (tmr + m[3])
            xg = x + xx * (tmg + m[4])
            r = xr @ Wr
            k = xk @ Wk
            v = xv @ Wv
            g = jax.nn.silu(xg @ Wg)
            w = tdecay + jnp.tanh(xw @ td_w1) @ td_w2
            decay = jnp.exp(-jnp.exp(w))
            to_tbhn = lambda a: a.reshape(Bq, Tq, H, N).transpose(1, 0, 2, 3)
            rT, kT, vT, dT = (to_tbhn(a) for a in (r, k, v, decay))

            def step(S, inp):
                r_t, k_t, v_t, d_t = inp
                kv = k_t[..., :, None] * v_t[..., None, :]
                y = jnp.einsum('bhi,bhij->bhj', r_t, S + u[None, :, :, None] * kv)
                return (d_t[..., None] * S + kv, y)
            S0 = jnp.zeros((Bq, H, N, N), x.dtype)
            _, ys = jax.lax.scan(step, S0, (rT, kT, vT, dT))
            y = ys.transpose(1, 0, 2, 3).reshape(Bq, Tq, Cq)
            yh = y.reshape(Bq, Tq, H, N)
            mu = yh.mean(-1, keepdims=True)
            var = yh.var(-1, keepdims=True)
            yn = (yh - mu) / jnp.sqrt(var + EPS)
            yn = (yn * ln_w.reshape(H, N) + ln_b.reshape(H, N)).reshape(Bq, Tq, Cq)
            return yn * g @ Wo
        key = jax.random.key(seed)
        ks = jax.random.split(key, 16)
        nrm = lambda k, shp, s: jax.random.normal(k, shp, dtype=jnp.float32) * s
        uni = lambda k, shp, a: jax.random.uniform(k, shp, jnp.float32, -a, a)
        ddd = (jnp.arange(C, dtype=jnp.float32) / C).reshape(1, 1, C)
        return {'x': nrm(ks[0], (B, T, C), 1.0), 'time_maa_x': 1.0 - ddd ** 0.5, 'time_maa_w': 1.0 - ddd ** 0.5, 'time_maa_k': 1.0 - ddd ** 0.5, 'time_maa_v': 1.0 - (ddd ** 0.5 + 0.15), 'time_maa_r': 1.0 - ddd ** 0.25, 'time_maa_g': 1.0 - ddd ** 0.25, 'time_maa_w1': uni(ks[1], (C, 5 * TM_DIM), 0.0001), 'time_maa_w2': uni(ks[2], (5, TM_DIM, C), 0.0001), 'time_decay': jnp.linspace(-6.0, -1.0, C).astype(jnp.float32).reshape(1, 1, C), 'time_decay_w1': uni(ks[3], (C, TD_DIM), 0.0001), 'time_decay_w2': uni(ks[4], (TD_DIM, C), 0.0001), 'time_faaaa': nrm(ks[5], (H, N), 0.1), 'W_r': nrm(ks[6], (C, C), C ** (-0.5)), 'W_k': nrm(ks[7], (C, C), C ** (-0.5)), 'W_v': nrm(ks[8], (C, C), C ** (-0.5)), 'W_g': nrm(ks[9], (C, C), C ** (-0.5)), 'W_o': nrm(ks[10], (C, C), C ** (-0.5)), 'ln_w': jnp.ones((C,), jnp.float32), 'ln_b': jnp.zeros((C,), jnp.float32)}
    _L1_attn_all = _L1_attn_setup()
    _L1_attn_in = {k: v for k, v in _L1_attn_all.items() if k in ('time_maa_x', 'time_maa_w', 'time_maa_k', 'time_maa_v', 'time_maa_r', 'time_maa_g', 'time_maa_w1', 'time_maa_w2', 'time_decay', 'time_decay_w1', 'time_decay_w2', 'time_faaaa', 'W_r', 'W_k', 'W_v', 'W_g', 'W_o', 'ln_w', 'ln_b')}
    del _L1_attn_all

    def _L1_ffn_setup():
        import jax, jax.numpy as jnp
        import numpy as np
        BLOCK = 32
        W_BITS = 4
        ACT_BITS = 16

        def act_qdq(x):
            qmax = 2.0 ** (ACT_BITS - 1) - 1.0
            scale = jnp.maximum(jnp.max(jnp.abs(x)) / qmax, 1e-12)
            return jnp.clip(jnp.round(x / scale), -qmax - 1.0, qmax) * scale

        def fixed_qdq_u16(x):
            scale = 1.0 / 65536.0
            return jnp.clip(jnp.round(x / scale), 0.0, 65535.0) * scale

        def lpbq_dequant(w):
            O, I = w.shape
            qmax = 2.0 ** (W_BITS - 1) - 1.0
            wb = w.reshape(O, I // BLOCK, BLOCK)
            s = jnp.maximum(jnp.max(jnp.abs(wb), axis=-1, keepdims=True) / qmax, 1e-12)
            wq = jnp.clip(jnp.round(wb / s), -qmax - 1.0, qmax) * s
            return wq.reshape(O, I)
        key = jax.random.key(seed)
        k1, k2, k3, k4 = jax.random.split(key, 4)
        B, S, H, I = (2, 1024, 256, 768)
        x = jax.random.normal(k1, (B, S, H), jnp.float32)
        w_gate = jax.random.normal(k2, (I, H), jnp.float32) * 0.02
        w_up = jax.random.normal(k3, (I, H), jnp.float32) * 0.02
        w_down = jax.random.normal(k4, (H, I), jnp.float32) * 0.02
        return {'x': x, 'w_gate': w_gate, 'w_up': w_up, 'w_down': w_down}
    _L1_ffn_all = _L1_ffn_setup()
    _L1_ffn_in = {k: v for k, v in _L1_ffn_all.items() if k in ('w_gate', 'w_up', 'w_down')}
    del _L1_ffn_all

    def _L2_attn_setup():
        import jax, jax.numpy as jnp
        import numpy as np
        B, N, F, H = (2, 512, 256, 16)
        HD = F // H
        SQRT_D = float(np.sqrt(F))
        key = jax.random.key(seed)
        ks = jax.random.split(key, 9)
        s = 1.0 / np.sqrt(F)
        mk = lambda k: jax.random.uniform(k, (F, F), jnp.float32, -s, s)
        mb = lambda k: jax.random.uniform(k, (F,), jnp.float32, -s, s)
        return {'x': jax.random.normal(ks[0], (B, N, F), jnp.float32), 'Wq': mk(ks[1]), 'bq': mb(ks[2]), 'Wk': mk(ks[3]), 'bk': mb(ks[4]), 'Wv': mk(ks[5]), 'bv': mb(ks[6]), 'Wo': mk(ks[7]), 'bo': mb(ks[8])}
    _L2_attn_all = _L2_attn_setup()
    _L2_attn_in = {k: v for k, v in _L2_attn_all.items() if k in ('Wq', 'bq', 'Wk', 'bk', 'Wv', 'bv', 'Wo', 'bo')}
    del _L2_attn_all

    def _L2_ffn_setup():
        import jax, jax.numpy as jnp
        import numpy as np
        DIM = 256
        N_EXPERTS = 16
        TOP_K = 4
        N_GROUP = 4
        TOPK_GROUP = 2
        MOE_INTER = 128
        SHARED_INTER = 512
        ROUTED_SCALE = 2.5

        def relu2(x):
            return jnp.square(jax.nn.relu(x))

        def _router(x2, gate_w, bias_e):
            T = x2.shape[0]
            logits = x2 @ gate_w.T
            scores = jax.nn.sigmoid(logits)
            sc = jax.lax.stop_gradient(scores + bias_e[None, :])
            grp = sc.reshape(T, N_GROUP, N_EXPERTS // N_GROUP)
            top2, _ = jax.lax.top_k(grp, 2)
            group_scores = top2.sum(-1)
            _, gidx = jax.lax.top_k(group_scores, TOPK_GROUP)
            rows = jnp.arange(T)[:, None]
            gmask = jnp.zeros((T, N_GROUP), dtype=sc.dtype).at[rows, gidx].set(1.0)
            smask = jnp.repeat(gmask, N_EXPERTS // N_GROUP, axis=1)
            masked = jnp.where(smask > 0, sc, 0.0)
            _, topk_idx = jax.lax.top_k(masked, TOP_K)
            topk_w = jnp.take_along_axis(scores, topk_idx, axis=1)
            topk_w = topk_w / (topk_w.sum(-1, keepdims=True) + 1e-20)
            topk_w = topk_w * ROUTED_SCALE
            return (topk_idx, topk_w)
        key = jax.random.key(seed)
        ks = jax.random.split(key, 6)
        hidden_states = jax.random.normal(ks[0], (2, 512, DIM), dtype=jnp.float32)
        gate_w = jax.random.normal(ks[1], (N_EXPERTS, DIM), dtype=jnp.float32) * 0.02
        bias_e = jnp.zeros((N_EXPERTS,), dtype=jnp.float32)
        up_w = jax.random.normal(ks[2], (N_EXPERTS, MOE_INTER, DIM), dtype=jnp.float32) * 0.02
        down_w = jax.random.normal(ks[3], (N_EXPERTS, DIM, MOE_INTER), dtype=jnp.float32) * 0.02
        shared_up = jax.random.normal(ks[4], (SHARED_INTER, DIM), dtype=jnp.float32) * 0.02
        shared_down = jax.random.normal(ks[5], (DIM, SHARED_INTER), dtype=jnp.float32) * 0.02
        return {'hidden_states': hidden_states, 'gate_w': gate_w, 'bias_e': bias_e, 'up_w': up_w, 'down_w': down_w, 'shared_up': shared_up, 'shared_down': shared_down}
    _L2_ffn_all = _L2_ffn_setup()
    _L2_ffn_in = {k: v for k, v in _L2_ffn_all.items() if k in ('gate_w', 'bias_e', 'up_w', 'down_w', 'shared_up', 'shared_down')}
    del _L2_ffn_all

    def _L3_attn_setup():
        import jax, jax.numpy as jnp
        import numpy as np
        DIM = 256
        KERNEL_N = 128
        LN_EPS = 1e-05

        def _layernorm(x, g, b):
            mu = jnp.mean(x, axis=-1, keepdims=True)
            var = jnp.var(x, axis=-1, keepdims=True)
            return (x - mu) * jax.lax.rsqrt(var + LN_EPS) * g + b
        key = jax.random.key(seed)
        ks = jax.random.split(key, 6)
        x = jax.random.normal(ks[0], (4, 1024, DIM), dtype=jnp.float32)
        return {'x': x, 'Lambda_real': jax.random.normal(ks[1], (KERNEL_N,), dtype=jnp.float32), 'Lambda_imag': jax.random.normal(ks[2], (KERNEL_N,), dtype=jnp.float32), 'C_real': jax.random.normal(ks[3], (DIM, KERNEL_N), dtype=jnp.float32), 'C_imag': jax.random.normal(ks[4], (DIM, KERNEL_N), dtype=jnp.float32), 'param_D': jax.random.normal(ks[5], (DIM,), dtype=jnp.float32), 'ln_gamma': jnp.ones((DIM,), dtype=jnp.float32), 'ln_beta': jnp.zeros((DIM,), dtype=jnp.float32)}
    _L3_attn_all = _L3_attn_setup()
    _L3_attn_in = {k: v for k, v in _L3_attn_all.items() if k in ('Lambda_real', 'Lambda_imag', 'C_real', 'C_imag', 'param_D', 'ln_gamma', 'ln_beta')}
    del _L3_attn_all

    def _L3_ffn_setup():
        import jax, jax.numpy as jnp
        import numpy as np
        TOP_K = 2
        key = jax.random.key(seed)
        ks = jax.random.split(key, 6)
        B, T, H, E, F = (2, 512, 256, 8, 1024)
        s = 0.02
        return {'hidden_states': jax.random.normal(ks[0], (B, T, H), dtype=jnp.float32), 'router_w': jax.random.normal(ks[1], (E, H), dtype=jnp.float32) * s, 'w1': jax.random.normal(ks[2], (E, F, H), dtype=jnp.float32) * s, 'b1': jax.random.normal(ks[3], (E, F), dtype=jnp.float32) * s, 'w2': jax.random.normal(ks[4], (E, H, F), dtype=jnp.float32) * s, 'b2': jax.random.normal(ks[5], (E, H), dtype=jnp.float32) * s}
    _L3_ffn_all = _L3_ffn_setup()
    _L3_ffn_in = {k: v for k, v in _L3_ffn_all.items() if k in ('router_w', 'w1', 'b1', 'w2', 'b2')}
    del _L3_ffn_all
    return {'x': x, 'L0_tok_W_h': _L0_tok_in['W_h'], 'L0_tok_b_h': _L0_tok_in['b_h'], 'L0_tok_W_o': _L0_tok_in['W_o'], 'L0_tok_b_o': _L0_tok_in['b_o'], 'L0_tok_W_r': _L0_tok_in['W_r'], 'L0_tok_b_r': _L0_tok_in['b_r'], 'L0_attn_gamma': _L0_attn_in['gamma'], 'L0_attn_w_q': _L0_attn_in['w_q'], 'L0_attn_w_kv': _L0_attn_in['w_kv'], 'L0_attn_w_out': _L0_attn_in['w_out'], 'L0_ffn_Wg': _L0_ffn_in['Wg'], 'L0_ffn_bg': _L0_ffn_in['bg'], 'L0_ffn_W1': _L0_ffn_in['W1'], 'L0_ffn_b1': _L0_ffn_in['b1'], 'L0_ffn_W2': _L0_ffn_in['W2'], 'L0_ffn_b2': _L0_ffn_in['b2'], 'L1_attn_time_maa_x': _L1_attn_in['time_maa_x'], 'L1_attn_time_maa_w': _L1_attn_in['time_maa_w'], 'L1_attn_time_maa_k': _L1_attn_in['time_maa_k'], 'L1_attn_time_maa_v': _L1_attn_in['time_maa_v'], 'L1_attn_time_maa_r': _L1_attn_in['time_maa_r'], 'L1_attn_time_maa_g': _L1_attn_in['time_maa_g'], 'L1_attn_time_maa_w1': _L1_attn_in['time_maa_w1'], 'L1_attn_time_maa_w2': _L1_attn_in['time_maa_w2'], 'L1_attn_time_decay': _L1_attn_in['time_decay'], 'L1_attn_time_decay_w1': _L1_attn_in['time_decay_w1'], 'L1_attn_time_decay_w2': _L1_attn_in['time_decay_w2'], 'L1_attn_time_faaaa': _L1_attn_in['time_faaaa'], 'L1_attn_W_r': _L1_attn_in['W_r'], 'L1_attn_W_k': _L1_attn_in['W_k'], 'L1_attn_W_v': _L1_attn_in['W_v'], 'L1_attn_W_g': _L1_attn_in['W_g'], 'L1_attn_W_o': _L1_attn_in['W_o'], 'L1_attn_ln_w': _L1_attn_in['ln_w'], 'L1_attn_ln_b': _L1_attn_in['ln_b'], 'L1_ffn_w_gate': _L1_ffn_in['w_gate'], 'L1_ffn_w_up': _L1_ffn_in['w_up'], 'L1_ffn_w_down': _L1_ffn_in['w_down'], 'L2_attn_Wq': _L2_attn_in['Wq'], 'L2_attn_bq': _L2_attn_in['bq'], 'L2_attn_Wk': _L2_attn_in['Wk'], 'L2_attn_bk': _L2_attn_in['bk'], 'L2_attn_Wv': _L2_attn_in['Wv'], 'L2_attn_bv': _L2_attn_in['bv'], 'L2_attn_Wo': _L2_attn_in['Wo'], 'L2_attn_bo': _L2_attn_in['bo'], 'L2_ffn_gate_w': _L2_ffn_in['gate_w'], 'L2_ffn_bias_e': _L2_ffn_in['bias_e'], 'L2_ffn_up_w': _L2_ffn_in['up_w'], 'L2_ffn_down_w': _L2_ffn_in['down_w'], 'L2_ffn_shared_up': _L2_ffn_in['shared_up'], 'L2_ffn_shared_down': _L2_ffn_in['shared_down'], 'L3_attn_Lambda_real': _L3_attn_in['Lambda_real'], 'L3_attn_Lambda_imag': _L3_attn_in['Lambda_imag'], 'L3_attn_C_real': _L3_attn_in['C_real'], 'L3_attn_C_imag': _L3_attn_in['C_imag'], 'L3_attn_param_D': _L3_attn_in['param_D'], 'L3_attn_ln_gamma': _L3_attn_in['ln_gamma'], 'L3_attn_ln_beta': _L3_attn_in['ln_beta'], 'L3_ffn_router_w': _L3_ffn_in['router_w'], 'L3_ffn_w1': _L3_ffn_in['w1'], 'L3_ffn_b1': _L3_ffn_in['b1'], 'L3_ffn_w2': _L3_ffn_in['w2'], 'L3_ffn_b2': _L3_ffn_in['b2']}

def reference(x, L0_tok_W_h, L0_tok_b_h, L0_tok_W_o, L0_tok_b_o, L0_tok_W_r, L0_tok_b_r, L0_attn_gamma, L0_attn_w_q, L0_attn_w_kv, L0_attn_w_out, L0_ffn_Wg, L0_ffn_bg, L0_ffn_W1, L0_ffn_b1, L0_ffn_W2, L0_ffn_b2, L1_attn_time_maa_x, L1_attn_time_maa_w, L1_attn_time_maa_k, L1_attn_time_maa_v, L1_attn_time_maa_r, L1_attn_time_maa_g, L1_attn_time_maa_w1, L1_attn_time_maa_w2, L1_attn_time_decay, L1_attn_time_decay_w1, L1_attn_time_decay_w2, L1_attn_time_faaaa, L1_attn_W_r, L1_attn_W_k, L1_attn_W_v, L1_attn_W_g, L1_attn_W_o, L1_attn_ln_w, L1_attn_ln_b, L1_ffn_w_gate, L1_ffn_w_up, L1_ffn_w_down, L2_attn_Wq, L2_attn_bq, L2_attn_Wk, L2_attn_bk, L2_attn_Wv, L2_attn_bv, L2_attn_Wo, L2_attn_bo, L2_ffn_gate_w, L2_ffn_bias_e, L2_ffn_up_w, L2_ffn_down_w, L2_ffn_shared_up, L2_ffn_shared_down, L3_attn_Lambda_real, L3_attn_Lambda_imag, L3_attn_C_real, L3_attn_C_imag, L3_attn_param_D, L3_attn_ln_gamma, L3_attn_ln_beta, L3_ffn_router_w, L3_ffn_w1, L3_ffn_b1, L3_ffn_w2, L3_ffn_b2):
    import jax
    import jax.numpy as jnp

    def _L0_tok_ref(x, W_h, b_h, W_o, b_o, W_r, b_r):
        import jax, jax.numpy as jnp
        import numpy as np
        P = 16
        B, L = x.shape
        pad = -L % P
        mask = jnp.ones_like(x)
        if pad > 0:
            x = jnp.pad(x, ((0, 0), (pad, 0)))
            mask = jnp.pad(mask, ((0, 0), (pad, 0)))
        xp = x.reshape(B, -1, P)
        mp = mask.reshape(B, -1, P)
        x_cat = jnp.concatenate([xp, mp], axis=-1)
        hid = jax.nn.silu(jnp.einsum('bnf,if->bni', x_cat, W_h) + b_h)
        out = jnp.einsum('bni,hi->bnh', hid, W_o) + b_o
        res = jnp.einsum('bnf,hf->bnh', x_cat, W_r) + b_r
        return out + res

    def _L0_attn_ref(x, gamma, w_q, w_kv, w_out):
        import jax, jax.numpy as jnp
        import numpy as np
        DIM = 256
        DIM_HEAD = 16
        HEADS = 8
        EPS = 1e-05

        def rms_norm(x, gamma):
            n = jnp.sqrt(jnp.sum(x * x, axis=-1, keepdims=True))
            return gamma * (x / jnp.maximum(n, 1e-12)) * x.shape[-1] ** 0.5

        def second_taylor_expansion(x):
            d = x.shape[-1]
            x0 = jnp.ones(x.shape[:-1] + (1,), dtype=x.dtype)
            x2 = jnp.einsum('...i,...j->...ij', x, x) * 0.5 ** 0.5
            x2 = x2.reshape(x.shape[:-1] + (d * d,))
            return jnp.concatenate([x0, x, x2], axis=-1)
        b, n, _ = x.shape
        h, dh = (HEADS, DIM_HEAD)
        normed = rms_norm(x, gamma)
        q = (normed @ w_q).reshape(b, n, h, dh).transpose(0, 2, 1, 3)
        kv = (normed @ w_kv).reshape(b, n, 2, h, dh).transpose(2, 0, 3, 1, 4)
        k, v = (kv[0], kv[1])
        q = q * dh ** (-0.5)
        q = second_taylor_expansion(q)
        k = second_taylor_expansion(k)
        kv_state = jnp.einsum('bhnd,bhne->bhde', k, v)
        k_sum = jnp.sum(k, axis=2)
        den = jnp.einsum('bhnd,bhd->bhn', q, k_sum)
        qk_inv = 1.0 / jnp.maximum(den, EPS)
        out = jnp.einsum('bhnd,bhde->bhne', q, kv_state) * qk_inv[..., None]
        out = out.transpose(0, 2, 1, 3).reshape(b, n, h * dh)
        return out @ w_out

    def _L0_ffn_ref(x, Wg, bg, W1, b1, W2, b2):
        import jax, jax.numpy as jnp
        import numpy as np
        H = 256
        I = 256
        E = 8
        B, S, Hd = x.shape
        xf = x.reshape(-1, Hd)
        logits = xf @ Wg + bg
        gates = jax.nn.softmax(logits, axis=-1)
        idx = jnp.argmax(gates, axis=-1)
        h = jax.nn.gelu(jnp.einsum('th,ehi->tei', xf, W1) + b1, approximate=False)
        y = jnp.einsum('tei,eih->teh', h, W2) + b2
        out = jnp.take_along_axis(y, idx[:, None, None], axis=1)[:, 0, :]
        return out.reshape(B, S, Hd)

    def _L1_attn_ref(x, time_maa_x, time_maa_w, time_maa_k, time_maa_v, time_maa_r, time_maa_g, time_maa_w1, time_maa_w2, time_decay, time_decay_w1, time_decay_w2, time_faaaa, W_r, W_k, W_v, W_g, W_o, ln_w, ln_b):
        import jax, jax.numpy as jnp
        import numpy as np
        B, T, C, H = (2, 512, 256, 16)
        N = C // H
        TM_DIM, TD_DIM = (32, 64)
        EPS = 1e-05 * 8 ** 2

        def _forward(x, tmx, tmw, tmk, tmv, tmr, tmg, maa_w1, maa_w2, tdecay, td_w1, td_w2, u, Wr, Wk, Wv, Wg, Wo, ln_w, ln_b):
            Bq, Tq, Cq = x.shape
            xx = jnp.concatenate([jnp.zeros_like(x[:, :1]), x[:, :-1]], axis=1) - x
            xxx = x + xx * tmx
            t5 = jnp.tanh(xxx @ maa_w1).reshape(Bq, Tq, 5, TM_DIM)
            m = jnp.einsum('btfe,fec->fbtc', t5, maa_w2)
            xw = x + xx * (tmw + m[0])
            xk = x + xx * (tmk + m[1])
            xv = x + xx * (tmv + m[2])
            xr = x + xx * (tmr + m[3])
            xg = x + xx * (tmg + m[4])
            r = xr @ Wr
            k = xk @ Wk
            v = xv @ Wv
            g = jax.nn.silu(xg @ Wg)
            w = tdecay + jnp.tanh(xw @ td_w1) @ td_w2
            decay = jnp.exp(-jnp.exp(w))
            to_tbhn = lambda a: a.reshape(Bq, Tq, H, N).transpose(1, 0, 2, 3)
            rT, kT, vT, dT = (to_tbhn(a) for a in (r, k, v, decay))

            def step(S, inp):
                r_t, k_t, v_t, d_t = inp
                kv = k_t[..., :, None] * v_t[..., None, :]
                y = jnp.einsum('bhi,bhij->bhj', r_t, S + u[None, :, :, None] * kv)
                return (d_t[..., None] * S + kv, y)
            S0 = jnp.zeros((Bq, H, N, N), x.dtype)
            _, ys = jax.lax.scan(step, S0, (rT, kT, vT, dT))
            y = ys.transpose(1, 0, 2, 3).reshape(Bq, Tq, Cq)
            yh = y.reshape(Bq, Tq, H, N)
            mu = yh.mean(-1, keepdims=True)
            var = yh.var(-1, keepdims=True)
            yn = (yh - mu) / jnp.sqrt(var + EPS)
            yn = (yn * ln_w.reshape(H, N) + ln_b.reshape(H, N)).reshape(Bq, Tq, Cq)
            return yn * g @ Wo
        return _forward(x, time_maa_x, time_maa_w, time_maa_k, time_maa_v, time_maa_r, time_maa_g, time_maa_w1, time_maa_w2, time_decay, time_decay_w1, time_decay_w2, time_faaaa, W_r, W_k, W_v, W_g, W_o, ln_w, ln_b)

    def _L1_ffn_ref(x, w_gate, w_up, w_down):
        import jax, jax.numpy as jnp
        import numpy as np
        BLOCK = 32
        W_BITS = 4
        ACT_BITS = 16

        def act_qdq(x):
            qmax = 2.0 ** (ACT_BITS - 1) - 1.0
            scale = jnp.maximum(jnp.max(jnp.abs(x)) / qmax, 1e-12)
            return jnp.clip(jnp.round(x / scale), -qmax - 1.0, qmax) * scale

        def fixed_qdq_u16(x):
            scale = 1.0 / 65536.0
            return jnp.clip(jnp.round(x / scale), 0.0, 65535.0) * scale

        def lpbq_dequant(w):
            O, I = w.shape
            qmax = 2.0 ** (W_BITS - 1) - 1.0
            wb = w.reshape(O, I // BLOCK, BLOCK)
            s = jnp.maximum(jnp.max(jnp.abs(wb), axis=-1, keepdims=True) / qmax, 1e-12)
            wq = jnp.clip(jnp.round(wb / s), -qmax - 1.0, qmax) * s
            return wq.reshape(O, I)
        x = act_qdq(x)
        up = act_qdq(x @ lpbq_dequant(w_up).T)
        gate = act_qdq(x @ lpbq_dequant(w_gate).T)
        sig = fixed_qdq_u16(jax.nn.sigmoid(gate))
        gate = act_qdq(gate * sig)
        o = act_qdq(gate * up)
        return o @ lpbq_dequant(w_down).T

    def _L2_attn_ref(x, Wq, bq, Wk, bk, Wv, bv, Wo, bo):
        import jax, jax.numpy as jnp
        import numpy as np
        B, N, F, H = (2, 512, 256, 16)
        HD = F // H
        SQRT_D = float(np.sqrt(F))
        b, n, f = x.shape
        q = (x @ Wq.T + bq).reshape(b, n, H, HD)
        k = (x @ Wk.T + bk).reshape(b, n, H, HD)
        v = (x @ Wv.T + bv).reshape(b, n, H, HD)
        score = jnp.einsum('bihd,bjhd->bhij', q, k)
        attn = jax.nn.softmax(score / SQRT_D, axis=-1)
        o = jnp.einsum('bhij,bjhd->bihd', attn, v).reshape(b, n, f)
        return o @ Wo.T + bo

    def _L2_ffn_ref(hidden_states, gate_w, bias_e, up_w, down_w, shared_up, shared_down):
        import jax, jax.numpy as jnp
        import numpy as np
        DIM = 256
        N_EXPERTS = 16
        TOP_K = 4
        N_GROUP = 4
        TOPK_GROUP = 2
        MOE_INTER = 128
        SHARED_INTER = 512
        ROUTED_SCALE = 2.5

        def relu2(x):
            return jnp.square(jax.nn.relu(x))

        def _router(x2, gate_w, bias_e):
            T = x2.shape[0]
            logits = x2 @ gate_w.T
            scores = jax.nn.sigmoid(logits)
            sc = jax.lax.stop_gradient(scores + bias_e[None, :])
            grp = sc.reshape(T, N_GROUP, N_EXPERTS // N_GROUP)
            top2, _ = jax.lax.top_k(grp, 2)
            group_scores = top2.sum(-1)
            _, gidx = jax.lax.top_k(group_scores, TOPK_GROUP)
            rows = jnp.arange(T)[:, None]
            gmask = jnp.zeros((T, N_GROUP), dtype=sc.dtype).at[rows, gidx].set(1.0)
            smask = jnp.repeat(gmask, N_EXPERTS // N_GROUP, axis=1)
            masked = jnp.where(smask > 0, sc, 0.0)
            _, topk_idx = jax.lax.top_k(masked, TOP_K)
            topk_w = jnp.take_along_axis(scores, topk_idx, axis=1)
            topk_w = topk_w / (topk_w.sum(-1, keepdims=True) + 1e-20)
            topk_w = topk_w * ROUTED_SCALE
            return (topk_idx, topk_w)
        B, S, D = hidden_states.shape
        x2 = hidden_states.reshape(-1, D)
        T = x2.shape[0]
        topk_idx, topk_w = _router(x2, gate_w, bias_e)
        rows = jnp.arange(T)[:, None]
        combine = jnp.zeros((T, N_EXPERTS), dtype=topk_w.dtype).at[rows, topk_idx].add(topk_w)

        def body(acc, inp):
            wu, wd, cw = inp
            y = relu2(x2 @ wu.T) @ wd.T
            return (acc + cw[:, None] * y, None)
        routed, _ = jax.lax.scan(body, jnp.zeros_like(x2), (up_w, down_w, combine.T))
        shared = relu2(x2 @ shared_up.T) @ shared_down.T
        out = routed + shared
        return out.reshape(B, S, D)

    def _L3_attn_ref(x, Lambda_real, Lambda_imag, C_real, C_imag, param_D, ln_gamma, ln_beta):
        import jax, jax.numpy as jnp
        import numpy as np
        DIM = 256
        KERNEL_N = 128
        LN_EPS = 1e-05

        def _layernorm(x, g, b):
            mu = jnp.mean(x, axis=-1, keepdims=True)
            var = jnp.var(x, axis=-1, keepdims=True)
            return (x - mu) * jax.lax.rsqrt(var + LN_EPS) * g + b
        seq_len = x.shape[1]
        u = _layernorm(x, ln_gamma, ln_beta)
        residual = u * param_D
        Lambda = -jnp.exp(Lambda_real) + 1j * jnp.exp(Lambda_imag)
        C = (C_real + 1j * C_imag) * (jnp.exp(Lambda) - 1.0) / Lambda
        arange = jnp.arange(seq_len, dtype=jnp.float32)
        S = jnp.exp(Lambda[:, None] * arange[None, :])
        K = jnp.einsum('dn,nl->dl', C, S).real
        u_t = jnp.swapaxes(u, 1, 2)
        n_fft = seq_len * 2
        u_f = jnp.fft.rfft(u_t, n=n_fft, axis=-1)
        K_f = jnp.fft.rfft(K, n=n_fft, axis=-1)
        y = jnp.fft.irfft(u_f * K_f, n=n_fft, axis=-1)[..., :seq_len]
        y = jnp.swapaxes(y, 1, 2)
        return y + residual

    def _L3_ffn_ref(hidden_states, router_w, w1, b1, w2, b2):
        import jax, jax.numpy as jnp
        import numpy as np
        TOP_K = 2
        x = hidden_states
        router_logits = jnp.einsum('bth,eh->bte', x, router_w)
        topk_values, topk_indices = jax.lax.top_k(router_logits, TOP_K)
        topk_weights = jax.nn.softmax(topk_values.astype(jnp.float32), axis=-1).astype(x.dtype)
        h1 = jnp.einsum('bth,efh->btef', x, w1) + b1
        h1 = jax.nn.gelu(h1, approximate=False)
        expert_outputs = jnp.einsum('btef,ehf->bteh', h1, w2) + b2
        gather_idx = topk_indices[..., None]
        topk_expert_outputs = jnp.take_along_axis(expert_outputs, gather_idx, axis=2)
        mixed_output = jnp.sum(topk_expert_outputs * topk_weights[..., None], axis=2)
        return mixed_output
    h = _L0_tok_ref(x, L0_tok_W_h, L0_tok_b_h, L0_tok_W_o, L0_tok_b_o, L0_tok_W_r, L0_tok_b_r)
    h = h + _L0_attn_ref(_layernorm(h, axis=-1), L0_attn_gamma, L0_attn_w_q, L0_attn_w_kv, L0_attn_w_out)
    h = h + _L0_ffn_ref(_layernorm(h, axis=-1), L0_ffn_Wg, L0_ffn_bg, L0_ffn_W1, L0_ffn_b1, L0_ffn_W2, L0_ffn_b2)
    h = h + _L1_attn_ref(_layernorm(h, axis=-1), L1_attn_time_maa_x, L1_attn_time_maa_w, L1_attn_time_maa_k, L1_attn_time_maa_v, L1_attn_time_maa_r, L1_attn_time_maa_g, L1_attn_time_maa_w1, L1_attn_time_maa_w2, L1_attn_time_decay, L1_attn_time_decay_w1, L1_attn_time_decay_w2, L1_attn_time_faaaa, L1_attn_W_r, L1_attn_W_k, L1_attn_W_v, L1_attn_W_g, L1_attn_W_o, L1_attn_ln_w, L1_attn_ln_b)
    h = h + _L1_ffn_ref(_layernorm(h, axis=-1), L1_ffn_w_gate, L1_ffn_w_up, L1_ffn_w_down)
    h = h + _L2_attn_ref(_layernorm(h, axis=-1), L2_attn_Wq, L2_attn_bq, L2_attn_Wk, L2_attn_bk, L2_attn_Wv, L2_attn_bv, L2_attn_Wo, L2_attn_bo)
    h = h + _L2_ffn_ref(_layernorm(h, axis=-1), L2_ffn_gate_w, L2_ffn_bias_e, L2_ffn_up_w, L2_ffn_down_w, L2_ffn_shared_up, L2_ffn_shared_down)
    h = h + _L3_attn_ref(_layernorm(h, axis=-1), L3_attn_Lambda_real, L3_attn_Lambda_imag, L3_attn_C_real, L3_attn_C_imag, L3_attn_param_D, L3_attn_ln_gamma, L3_attn_ln_beta)
    h = h + _L3_ffn_ref(_layernorm(h, axis=-1), L3_ffn_router_w, L3_ffn_w1, L3_ffn_b1, L3_ffn_w2, L3_ffn_b2)
    return h

_drawn_inputs = setup_inputs


def setup_inputs(seed=0):
    import zlib

    import numpy as np

    out = dict(_drawn_inputs(seed))
    spreads = {'L0_attn_gamma': (1.0, 0.2),
     'L0_ffn_bg': (0.0, 0.1),
     'L0_ffn_b1': (0.0, 0.376),
     'L0_ffn_b2': (0.0, 0.1),
     'L1_attn_ln_w': (1.0, 0.2),
     'L1_attn_ln_b': (0.0, 0.1),
     'L2_ffn_bias_e': (0.0, 0.373),
     'L3_attn_ln_gamma': (1.0, 0.2),
     'L3_attn_ln_beta': (0.0, 0.1)}
    factors = {'L1_attn_time_maa_x': 64.0,
     'L1_attn_time_maa_w': 200.0,
     'L1_attn_time_maa_w1': 64.0,
     'L1_attn_time_maa_w2': 64.0,
     'L1_attn_time_decay_w1': 200.0,
     'L1_attn_time_decay_w2': 200.0,
     'L1_ffn_w_up': 2.67,
     'L1_ffn_w_down': 2.675,
     'L2_attn_Wq': 8.0,
     'L2_attn_bq': 8.0,
     'L2_attn_Wk': 8.0,
     'L2_attn_bk': 200.0,
     'L2_attn_bv': 3.644,
     'L2_ffn_gate_w': 3.73,
     'L3_ffn_router_w': 7.555,
     'L3_ffn_w1': 7.426,
     'L3_ffn_b1': 8.0,
     'L3_ffn_w2': 7.393,
     'L3_ffn_b2': 39.267}
    for name, (base, spread) in spreads.items():
        noise = np.random.default_rng([zlib.crc32(name.encode()), seed]).standard_normal(out[name].shape)
        drawn = base * np.exp(spread * noise) if base else spread * noise
        out[name] = jnp.asarray(drawn.astype(out[name].dtype))
    for name, factor in factors.items():
        out[name] = (out[name] * factor).astype(out[name].dtype)
    return out
```

```python
from contextlib import ExitStack

import concourse.bass as bass
from concourse import mybir

F32 = mybir.dt.float32
I32 = mybir.dt.int32
BF16 = mybir.dt.bfloat16
ACT = mybir.ActivationFunctionType
ALU = mybir.AluOpType
AX = mybir.AxisListType
ds = bass.ds

SEQS = 16
SEQ = 250
C = 256
P = 128
KC = C // P
TT = 125
NT = SEQS * SEQ // TT
UT = 4
UNIT = UT * TT
NU = NT // UT
TOK = SEQS * SEQ
BANK = 512
LN_EPS = 1e-5


class Steps:

    def __init__(self, eng, sem):
        self.eng, self.sem, self.base, self.k, self.turn, self.per = eng, sem, 0, 0, None, 0

    def then(self, ins):
        ins.then_inc(self.sem, 1)
        self.k += 1
        value = self.base + self.k
        self.eng.wait_ge(self.sem, value if self.turn is None else self.turn * self.per + value)

    def enter(self, turn, per):
        self.base += self.k
        self.k, self.turn, self.per = 0, turn, per

    def leave(self, turns):
        assert self.k == self.per, (self.k, self.per)
        self.base += self.per * turns
        self.k, self.turn = 0, None


class Core:

    def __init__(self, nc, ctx, dram):
        self.nc, self.ctx, self.dram = nc, ctx, dram
        self.h = ctx.enter_context(nc.sbuf_tensor("h", [TT, NT, C], F32))
        self.ident = ctx.enter_context(nc.sbuf_tensor("ident", [P, P], F32))


class Layer:

    def __init__(self, core, name):
        self.core, self.nc, self.name, self.stack = core, core.nc, name, ExitStack()
        self.sems = []

    def __enter__(self):
        self.stack.__enter__()
        return self

    def __exit__(self, *a):
        if self.sems and a[0] is None:
            with self.nc.Block() as block:

                @block.gpsimd
                def _(pool):
                    for sem in self.sems:
                        pool.sem_clear(sem)
        return self.stack.__exit__(*a)

    def sb(self, name, shape, dt=F32):
        return self.stack.enter_context(self.nc.sbuf_tensor(f"{self.name}_{name}", shape, dt))

    def ps(self, name, shape, dt=F32):
        return self.stack.enter_context(self.nc.psum_tensor(f"{self.name}_{name}", shape, dt))

    def sem(self, name):
        self.sems.append(self.stack.enter_context(self.nc.semaphore(f"{self.name}_{name}")))
        return self.sems[-1]


def constants(core):
    nc, ident = core.nc, core.ident
    with Layer(core, "const") as L:
        filled = L.sem("filled")
        with nc.Block() as block:

            @block.gpsimd
            def _(pool):
                nc.gpsimd.memset(ident[:], 0.0).then_inc(filled, 1)
                pool.wait_ge(filled, 1)
                nc.gpsimd.affine_select(out=ident[:], in_=ident[:], compare_op=ALU.not_equal, fill=1.0,
                                        base=0, pattern=[[-1, P]], channel_multiplier=1)


def store_stream(core, dst):
    nc = core.nc
    with Layer(core, "out") as L:
        stored = L.sem("stored")
        with nc.Block() as block:

            @block.sync
            def _(sp):
                sp.dma_start(dst.rearrange("b (s p) c -> p (b s) c", p=TT), core.h[:]).then_inc(stored, 16)
                sp.wait_ge(stored, 16)


def layer_norm(core, name, xT, rms_gain=None):
    nc, h, ident = core.nc, core.h, core.ident
    with Layer(core, name) as L:
        stats = L.sb("stats", [TT, 2, UT, 6])
        moments = L.sb("moments", [TT, 2, UT, 2])
        eps_var = L.sb("eps_var", [TT, 2, UT])
        power = L.sb("power", [TT, UT])
        rstd = L.sb("rstd", [TT, 2, UT])
        xn = L.sb("xn", [TT, 2, UT, C])
        square = L.sb("square", [TT, UT, C])
        norm2 = L.sb("norm2", [TT, 2, UT])
        rnorm = L.sb("rnorm", [TT, 2, UT])
        turned = [L.ps(f"turned{s}", [P, KC, BANK]) for s in range(2)]
        steps = L.sem("steps")
        power_set = L.sem("power_set")
        var_ready = L.sem("var_ready")
        rstd_ready = L.sem("rstd_ready")
        norm_ready = L.sem("norm_ready")
        rnorm_ready = L.sem("rnorm_ready")
        xn_ready = L.sem("xn_ready")
        xn_free = L.sem("xn_free")
        out_ready = L.sem("out_ready")
        rms = rms_gain is not None

        with nc.Block() as block:

            @block.vector
            def _(dve):
                st = Steps(dve, steps)
                nc.vector.memset(power[:], -0.5).then_inc(power_set, 1)
                with dve.Fori(0, NU // 2) as i:
                    st.enter(i, 2 * (2 + (3 if rms else 0)))
                    for s in range(2):
                        u = i * 2 + s
                        for t in range(UT):
                            ins = nc.vector.bn_stats(stats[:, s, t, :], h[:, ds(u * UT + t, 1), :])
                        st.then(ins)
                        dve.nop(nofuse=True)
                        for t in range(UT):
                            ins = nc.vector.bn_aggr(moments[:, s, t, :], stats[:, s, t, :])
                        st.then(ins)
                        nc.vector.tensor_scalar(eps_var[:, s, :], moments[:, s, :, 1], LN_EPS, None,
                                                ALU.add).then_inc(var_ready, 1)
                        dve.wait_ge(rstd_ready, u + 1)
                        dve.wait_ge(xn_free, u + 1)
                        for t in range(UT):
                            ins = nc.vector.tensor_scalar(xn[:, s, t, :], h[:, ds(u * UT + t, 1), :].rearrange("p a c -> p (a c)"),
                                                          moments[:, s, t, 0:1], rstd[:, s, t:t + 1],
                                                          ALU.subtract, ALU.mult)
                        if rms:
                            st.then(ins)
                            st.then(nc.vector.tensor_tensor(square[:], xn[:, s, :, :], xn[:, s, :, :], ALU.mult))
                            st.then(nc.vector.reduce_sum(norm2[:, s, :], square[:], AX.X))
                            nc.vector.tensor_scalar(norm2[:, s, :], norm2[:, s, :], 1e-24, None,
                                                    ALU.max).then_inc(norm_ready, 1)
                            dve.wait_ge(rnorm_ready, u + 1)
                            for t in range(UT):
                                ins = nc.vector.tensor_scalar(xn[:, s, t, :], xn[:, s, t, :], rnorm[:, s, t:t + 1],
                                                              float(C) ** 0.5, ALU.mult, ALU.mult)
                        ins.then_inc(xn_ready, 1)
                    st.leave(NU // 2)

            @block.gpsimd
            def _(pool):
                pool.wait_ge(power_set, 1)
                with pool.Fori(0, NU // 2) as i:
                    for s in range(2):
                        u = i * 2 + s
                        pool.wait_ge(var_ready, u + 1)
                        nc.gpsimd.tensor_tensor(rstd[:, s, :], eps_var[:, s, :], power[:], ALU.pow).then_inc(rstd_ready, 1)
                        if rms:
                            pool.wait_ge(norm_ready, u + 1)
                            nc.gpsimd.tensor_tensor(rnorm[:, s, :], norm2[:, s, :], power[:], ALU.pow).then_inc(rnorm_ready, 1)

            @block.tensor
            def _(pe):
                pe.sem_inc(xn_free, 2)
                with pe.Fori(0, NU // 2) as i:
                    for s in range(2):
                        u = i * 2 + s
                        pe.wait_ge(xn_ready, u + 1)
                        pe.wait_ge(out_ready, u + 1)
                        for t in range(UT):
                            for k in range(KC):
                                ins = nc.tensor.transpose(turned[s][:, k, t * TT:(t + 1) * TT],
                                                          xn[:, s, t, k * P:(k + 1) * P], ident[0:TT, 0:TT])
                        ins.then_inc(xn_free, 1)

            @block.scalar
            def _(act):
                act.sem_inc(out_ready, 2)
                with act.Fori(0, NU // 2) as i:
                    for s in range(2):
                        u = i * 2 + s
                        act.wait_ge(xn_free, u + 3)
                        for k in range(KC):
                            if rms:
                                ins = nc.scalar.activation(xT[:, k, ds(u * UNIT, UNIT)], turned[s][:, k, 0:UNIT],
                                                           ACT.Copy, scale=rms_gain[:, k:k + 1])
                            else:
                                ins = nc.scalar.activation(xT[:, k, ds(u * UNIT, UNIT)], turned[s][:, k, 0:UNIT], ACT.Copy)
                        ins.then_inc(out_ready, 1)


def token_patches(core):
    nc, h, dram = core.nc, core.h, core.dram
    hid_w, hid_tiles = dram["tok_wh"].shape[1], dram["tok_wh"].shape[1] // P
    pa, rows, mrows = dram["tok_x"].shape[0], dram["tok_wr"].shape[0], dram["tok_wh"].shape[0]
    with Layer(core, "tok") as L:
        patch = L.sb("patch", [rows, TOK])
        unit = L.sb("unit", [rows, 2, UNIT])
        wh = L.sb("wh", [mrows, hid_w])
        bh = L.sb("bh", [P, hid_tiles])
        wo = L.sb("wo", [P, hid_tiles, C])
        wr = L.sb("wr", [rows, C])
        hid = L.sb("hid", [P, 2, hid_tiles, UNIT])
        hid_ps = [L.ps(f"hid_ps{s}", [P, BANK]) for s in range(4)]
        y_ps = [L.ps(f"y_ps{s}", [TT, UT // 2, BANK]) for s in range(2)]
        ones_set = L.sem("ones_set")
        loaded = L.sem("loaded")
        unit_ready = L.sem("unit_ready")
        hid_ready = L.sem("hid_ready")
        hid_done = L.sem("hid_done")
        y_ready = L.sem("y_ready")
        y_free = L.sem("y_free")
        with nc.Block() as block:

            @block.sync
            def _(sp):
                sp.wait_ge(ones_set, 1)
                for dst, src in ((patch[0:pa, :], dram["tok_x"]), (wh[:], dram["tok_wh"]), (bh[:], dram["tok_bh"]),
                                 (wo[:], dram["tok_wo"]), (wr[:], dram["tok_wr"])):
                    sp.dma_start(dst, src).then_inc(loaded, 16)

            @block.gpsimd
            def _(pool):
                nc.gpsimd.memset(patch[:], 1.0).then_inc(ones_set, 1)
                pool.wait_ge(loaded, 16 * 5)
                with pool.Fori(0, NU // 2) as i:
                    for s in range(2):
                        u = i * 2 + s
                        pool.wait_ge(y_free, u + 1)
                        nc.gpsimd.tensor_copy(unit[:, s, :], patch[:, ds(u * UNIT, UNIT)]).then_inc(unit_ready, 1)

            @block.tensor
            def _(pe):
                with pe.Fori(0, NU // 2) as i:
                    for s in range(2):
                        u = i * 2 + s
                        pe.wait_ge(unit_ready, u + 1)
                        for m in range(hid_tiles):
                            pe.wait_ge(hid_done, u * hid_tiles + m + 1)
                            nc.tensor.matmul(hid_ps[m % 4][:, 0:UNIT], wh[:, m * P:(m + 1) * P], unit[0:mrows, s, :],
                                             start=True, stop=True).then_inc(hid_ready, 1)
                        pe.wait_ge(hid_done, u * hid_tiles + hid_tiles + 4)
                        pe.wait_ge(y_free, u + 1)
                        for t in range(UT):
                            y = y_ps[s][:, t // 2, (t % 2) * C:(t % 2 + 1) * C]
                            nc.tensor.matmul(y, unit[:, s, t * TT:(t + 1) * TT], wr[:], start=(t % 2 == 0), stop=False,
                                             skip_group_check=True)
                            for m in range(hid_tiles):
                                ins = nc.tensor.matmul(y, hid[:, s, m, t * TT:(t + 1) * TT], wo[:, m, :], start=False,
                                                       stop=(m == hid_tiles - 1), skip_group_check=True)
                        ins.then_inc(y_ready, 1)

            @block.scalar
            def _(act):
                act.sem_inc(hid_done, 4)
                act.wait_ge(loaded, 16 * 5)
                with act.Fori(0, NU // 2) as i:
                    for s in range(2):
                        u = i * 2 + s
                        act.wait_ge(y_free, u + 1)
                        for m in range(hid_tiles):
                            act.wait_ge(hid_ready, u * hid_tiles + m + 1)
                            nc.scalar.activation(hid[:, s, m, :], hid_ps[m % 4][:, 0:UNIT], ACT.Silu,
                                                 bias=bh[:, m:m + 1]).then_inc(hid_done, 1)

            @block.vector
            def _(dve):
                dve.sem_inc(y_free, 2)
                with dve.Fori(0, NU // 2) as i:
                    for s in range(2):
                        u = i * 2 + s
                        dve.wait_ge(y_ready, u + 1)
                        nc.vector.tensor_copy(h[:, ds(u * UT, UT), :],
                                              y_ps[s][:, :, :].rearrange("p a (b c) -> p (a b) c", c=C)).then_inc(y_free, 1)


def route(core, name, xT, sel, wg, bg, pick, b2=None):
    nc, h, ident = core.nc, core.h, core.ident
    E = sel.shape[2]
    with Layer(core, name) as L:
        wg_sb = L.sb("wg", [P, KC, E])
        bg_sb = L.sb("bg", [E, 1])
        b2_sb = L.sb("b2", [E, C])
        logitT = L.sb("logitT", [E, UNIT])
        v = L.sb("v", [TT, UT, E])
        before = L.sb("before", [TT, E, E])
        work = pick.buffers(L, E)
        selT = L.sb("selT", [E, UT, TT])
        logit_ps = L.ps("logit_ps", [E, BANK])
        v_ps = L.ps("v_ps", [TT, UT, E])
        selT_ps = L.ps("selT_ps", [E, UT, P])
        b_ps = L.ps("b_ps", [TT, 2, BANK])
        loaded = L.sem("loaded")
        table = L.sem("table")
        logit_ready = L.sem("logit_ready")
        logitT_ready = L.sem("logitT_ready")
        v_ready = L.sem("v_ready")
        v_taken = L.sem("v_taken")
        sel_ready = L.sem("sel_ready")
        selT_ready = L.sem("selT_ready")
        selT_taken = L.sem("selT_taken")
        b_ready = L.sem("b_ready")
        unit_done = L.sem("unit_done")
        steps = L.sem("steps")
        act_ready = L.sem("act_ready")
        act_asked = L.sem("act_asked")
        n_loads = 1 + (bg is not None) + (b2 is not None) + pick.loads

        with nc.Block() as block:

            @block.sync
            def _(sp):
                sp.dma_start(wg_sb[:], wg).then_inc(loaded, 16)
                if bg is not None:
                    sp.dma_start(bg_sb[:], bg).then_inc(loaded, 16)
                if b2 is not None:
                    sp.dma_start(b2_sb[:], b2).then_inc(loaded, 16)
                pick.load(sp, work, loaded)

            @block.gpsimd
            def _(pool):
                nc.gpsimd.memset(before[:], 1.0).then_inc(table, 1)
                pool.wait_ge(table, 1)
                nc.gpsimd.affine_select(out=before[:], in_=before[:], compare_op=ALU.is_gt, fill=0.0, base=0,
                                        pattern=[[1, E], [-1, E]], channel_multiplier=0).then_inc(table, 1)

            @block.tensor
            def _(pe):
                pe.wait_ge(loaded, 16 * n_loads)
                with pe.Fori(0, NU) as u:
                    pe.wait_ge(unit_done, u + 1)
                    for k in range(KC):
                        ins = nc.tensor.matmul(logit_ps[:, 0:UNIT], wg_sb[:, k, :], xT[:, k, ds(u * UNIT, UNIT)],
                                               start=(k == 0), stop=(k == KC - 1))
                    ins.then_inc(logit_ready, 1)
                    pe.wait_ge(logitT_ready, u + 1)
                    pe.nop(nofuse=True)
                    for t in range(UT):
                        ins = nc.tensor.transpose(v_ps[:, t, :], logitT[:, t * TT:(t + 1) * TT], ident[0:E, 0:E])
                    ins.then_inc(v_ready, 1)
                    if b2 is not None:
                        pe.wait_ge(sel_ready, u + 1)
                        for t in range(UT):
                            ins = nc.tensor.transpose(selT_ps[:, t, 0:TT], v[:, t, :], ident[0:TT, 0:TT])
                        ins.then_inc(selT_ready, 1)
                        pe.wait_ge(selT_taken, u + 1)
                        for t in range(UT):
                            ins = nc.tensor.matmul(b_ps[:, t // 2, (t % 2) * C:(t % 2 + 1) * C], selT[:, t, :], b2_sb[:],
                                                   start=(t % 2 == 0), stop=True, skip_group_check=True)
                        ins.then_inc(b_ready, 1)

            @block.scalar
            def _(act):
                act.wait_ge(loaded, 16 * n_loads)
                with act.Fori(0, NU) as u:
                    act.wait_ge(logit_ready, u + 1)
                    if bg is not None:
                        nc.scalar.activation(logitT[:], logit_ps[:, 0:UNIT], ACT.Identity, bias=bg_sb[:, 0:1]).then_inc(logitT_ready, 1)
                    else:
                        nc.scalar.activation(logitT[:], logit_ps[:, 0:UNIT], pick.on_logits).then_inc(logitT_ready, 1)
                    if pick.asks_act:
                        act.wait_ge(act_asked, u + 1)
                        pick.on_act(nc, work).then_inc(act_ready, 1)
                    if b2 is not None:
                        act.wait_ge(selT_ready, u + 1)
                        nc.scalar.copy(selT[:], selT_ps[:, :, 0:TT]).then_inc(selT_taken, 1)

            @block.vector
            def _(dve):
                st = Steps(dve, steps)
                dve.sem_inc(unit_done, 1)
                dve.wait_ge(table, 2)
                dve.wait_ge(loaded, 16 * n_loads)
                with dve.Fori(0, NU) as u:
                    st.enter(u, 1 + pick.steps)
                    dve.wait_ge(v_ready, u + 1)
                    st.then(nc.vector.tensor_copy(v[:], v_ps[:]))
                    pick.run(nc, dve, st, v, before, work, act_asked, act_ready, u)
                    ins = nc.vector.tensor_copy(sel[:, ds(u * UT, UT), :], v[:])
                    if b2 is not None:
                        ins.then_inc(sel_ready, 1)
                        dve.wait_ge(b_ready, u + 1)
                        ins = nc.vector.tensor_tensor(h[:, ds(u * UT, UT), :], b_ps[:, :, :].rearrange("p a (b c) -> p (a b) c", c=C),
                                                      h[:, ds(u * UT, UT), :], ALU.add)
                    ins.then_inc(unit_done, 1)
                    st.leave(NU)


def rank_of(nc, st, v, before, gt, ge, rank):
    E = v.shape[2]
    mine = v.rearrange("p t e -> p (t e)").unsqueeze(2).broadcast_to([TT, UT * E, E])
    other = v.unsqueeze(2).broadcast_to([TT, UT, E, E])
    g4 = gt.rearrange("p (t e) j -> p t e j", t=UT)
    q4 = ge.rearrange("p (t e) j -> p t e j", t=UT)
    mine4 = v.unsqueeze(3).broadcast_to([TT, UT, E, E])
    nc.vector.tensor_tensor(g4, other, mine4, ALU.is_gt)
    st.then(nc.vector.tensor_tensor(q4, other, mine4, ALU.is_equal))
    st.then(nc.vector.tensor_tensor(q4, q4, before.unsqueeze(1).broadcast_to([TT, UT, E, E]), ALU.mult))
    st.then(nc.vector.tensor_tensor(gt, gt, ge, ALU.add))
    st.then(nc.vector.reduce_sum(rank.rearrange("p t e -> p (t e)"), gt, AX.X))


class PickTop1:
    loads, steps, asks_act, on_logits = 0, 5, False, None

    def buffers(self, L, E):
        return dict(gt=L.sb("gt", [TT, UT * E, E]), ge=L.sb("ge", [TT, UT * E, E]), rank=L.sb("rank", [TT, UT, E]))

    def load(self, sp, w, loaded):
        pass

    def run(self, nc, dve, st, v, before, w, asked, answered, u):
        rank_of(nc, st, v[:], before[:], w["gt"][:], w["ge"][:], w["rank"][:])
        st.then(nc.vector.tensor_scalar(v[:], w["rank"][:], 0.5, None, ALU.is_lt))


def experts(core, name, xT, sel, n_experts, tiles, w1, b1, w2, squared_relu=False):
    nc, h = core.nc, core.h
    slots = min(2, n_experts)
    with Layer(core, name) as L:
        w1_sb = [L.sb(f"w1_{s}", [P, KC, tiles * P]) for s in range(slots)]
        w2_sb = [L.sb(f"w2_{s}", [P, tiles, C]) for s in range(slots)]
        b1_sb = [L.sb(f"b1_{s}", [P, tiles]) for s in range(slots)]
        hid = L.sb("hid", [P, 2, UNIT])
        relu = L.sb("relu", [P, 2, UNIT])
        hid_ps = [L.ps(f"hid_ps{s}", [P, BANK]) for s in range(2)]
        y_ps = [L.ps(f"y_ps{s}", [TT, UT // 2, BANK]) for s in range(2)]
        w_ready = [L.sem(f"w_ready{s}") for s in range(slots)]
        hid_ready = L.sem("hid_ready")
        hid_done = L.sem("hid_done")
        hid_used = L.sem("hid_used")
        y_ready = L.sem("y_ready")
        y_free = L.sem("y_free")
        relued = L.sem("relued")
        loads = 2 + (b1 is not None)
        body = 2 * tiles

        def over_experts(eng, run):
            if n_experts == 1:
                run(0, 0, 0)
            else:
                with eng.Fori(0, n_experts // 2) as pair:
                    for s in range(2):
                        run(pair * 2 + s, s, pair)

        with nc.Block() as block:

            @block.sync
            def _(sp):
                def load(e, s, turn):
                    pairs = [(w1_sb[s], w1), (w2_sb[s], w2)] + ([(b1_sb[s], b1)] if b1 is not None else [])
                    for dst, src in pairs:
                        flat = dst[:] if len(dst.shape) == 2 else dst[:].rearrange("p a b -> p (a b)")
                        sp.dma_start(flat, src[ds(e, 1)].rearrange("a p n -> p (a n)")).then_inc(w_ready[s], 16)
                for s in range(slots):
                    load(s, s, 0)
                if n_experts > 2:
                    with sp.Fori(1, n_experts // 2) as pair:
                        for s in range(2):
                            sp.wait_ge(hid_used, (pair * 2 + s - 1) * (NU * tiles) + 2)
                            load(pair * 2 + s, s, pair)

            @block.tensor
            def _(pe):
                pe.sem_inc(hid_used, 2)

                def expert(e, s, turn):
                    pe.wait_ge(w_ready[s], (turn + 1) * (16 * loads))
                    pe.nop(nofuse=True)
                    with pe.Fori(0, NU // 2) as i:
                        first = e * (NU * tiles) + i * body
                        units = e * NU + i * 2

                        def up(q):
                            u, m = q // tiles, q % tiles
                            pe.wait_ge(hid_done, first + q + 1)
                            for k in range(KC):
                                ins = nc.tensor.matmul(hid_ps[q % 2][:, 0:UNIT], w1_sb[s][:, k, m * P:(m + 1) * P],
                                                       xT[:, k, ds((i * 2 + u) * UNIT, UNIT)],
                                                       start=(k == 0), stop=(k == KC - 1))
                            ins.then_inc(hid_ready, 1)

                        def down(q):
                            u, m = q // tiles, q % tiles
                            pe.wait_ge(hid_done, first + q + 3)
                            if m == 0:
                                pe.wait_ge(y_free, units + u + 1)
                            for t in range(UT):
                                y = y_ps[u][:, t // 2, (t % 2) * C:(t % 2 + 1) * C]
                                ins = nc.tensor.matmul(y, hid[:, q % 2, t * TT:(t + 1) * TT], w2_sb[s][:, m, :],
                                                       start=(m == 0 and t % 2 == 0), stop=(m == tiles - 1),
                                                       skip_group_check=True)
                            ins.then_inc(hid_used, 1)

                        for q in range(body):
                            up(q)
                            if q:
                                down(q - 1)
                        down(body - 1)
                over_experts(pe, expert)

            @block.scalar
            def _(act):
                act.sem_inc(hid_done, 2)

                def expert(e, s, turn):
                    act.wait_ge(w_ready[s], (turn + 1) * (16 * loads))
                    with act.Fori(0, NU // 2) as i:
                        first = e * (NU * tiles) + i * body
                        for q in range(body):
                            m = q % tiles
                            act.wait_ge(hid_ready, first + q + 1)
                            act.wait_ge(hid_used, first + q + 1)
                            if squared_relu:
                                nc.scalar.activation(relu[:, q % 2, :], hid_ps[q % 2][:, 0:UNIT], ACT.Relu).then_inc(relued, 1)
                                act.wait_ge(relued, first + q + 1)
                                ins = nc.scalar.activation(hid[:, q % 2, :], relu[:, q % 2, :], ACT.Square)
                            else:
                                ins = nc.scalar.activation(hid[:, q % 2, :], hid_ps[q % 2][:, 0:UNIT], ACT.Gelu,
                                                           bias=b1_sb[s][:, m:m + 1])
                            ins.then_inc(hid_done, 1)
                over_experts(act, expert)

            @block.vector
            def _(dve):
                dve.sem_inc(y_free, 2)

                def expert(e, s, turn):
                    with dve.Fori(0, NU // 2) as i:
                        for u in range(2):
                            dve.wait_ge(hid_used, e * (NU * tiles) + i * body + (u + 1) * tiles + 2)
                            for t in range(UT):
                                tile = ds((i * 2 + u) * UT + t, 1)
                                y = y_ps[u][:, t // 2, (t % 2) * C:(t % 2 + 1) * C]
                                mine = h[:, tile, :].rearrange("p a c -> p (a c)")
                                if sel is None:
                                    ins = nc.vector.tensor_tensor(mine, y, mine, ALU.add)
                                else:
                                    weight = sel[:, tile, ds(e, 1)].rearrange("p a e -> p (a e)")
                                    ins = nc.vector.scalar_tensor_tensor(out=mine, in0=y, scalar=weight, in1=mine,
                                                                         op0=ALU.mult, op1=ALU.add)
                            ins.then_inc(y_free, 1)
                over_experts(dve, expert)


def top1_experts(core):
    d = core.dram
    E, tiles = d["f0_w1"].shape[0], d["f0_w2"].shape[2] // C
    with Layer(core, "f0") as L:
        xT = L.sb("xT", [P, KC, TOK])
        sel = L.sb("sel", [TT, NT, E])
        layer_norm(core, "f0ln", xT)
        route(core, "f0rt", xT, sel, d["f0_wg"], d["f0_bg"], PickTop1(), d["f0_b2"])
        experts(core, "f0ex", xT, sel, E, tiles, d["f0_w1"], d["f0_b1"], d["f0_w2"])


class PickTop2:
    loads, steps, asks_act, on_logits = 0, 10, True, ACT.Copy

    def buffers(self, L, E):
        return dict(gt=L.sb("gt", [TT, UT * E, E]), ge=L.sb("ge", [TT, UT * E, E]), rank=L.sb("rank", [TT, UT, E]),
                    top=L.sb("top", [TT, UT]), fall=L.sb("fall", [TT, UT, E]), grown=L.sb("grown", [TT, UT, E]),
                    keep=L.sb("keep", [TT, UT, E]), total=L.sb("total", [TT, UT]))

    def load(self, sp, w, loaded):
        pass

    def on_act(self, nc, w):
        return nc.scalar.activation(w["grown"][:], w["fall"][:], ACT.Exp)

    def run(self, nc, dve, st, v, before, w, asked, answered, u):
        E = v.shape[2]
        st.then(nc.vector.reduce_max(w["top"][:], v[:], AX.X))
        nc.vector.tensor_tensor(w["fall"][:], v[:], w["top"][:].unsqueeze(2).broadcast_to([TT, UT, E]),
                                ALU.subtract).then_inc(asked, 1)
        rank_of(nc, st, v[:], before[:], w["gt"][:], w["ge"][:], w["rank"][:])
        st.then(nc.vector.tensor_scalar(w["keep"][:], w["rank"][:], 1.5, None, ALU.is_lt))
        dve.wait_ge(answered, u + 1)
        st.then(nc.vector.tensor_tensor(v[:], w["grown"][:], w["keep"][:], ALU.mult))
        st.then(nc.vector.reduce_sum(w["total"][:], v[:], AX.X))
        st.then(nc.vector.reciprocal(w["total"][:], w["total"][:]))
        st.then(nc.vector.tensor_tensor(v[:], v[:], w["total"][:].unsqueeze(2).broadcast_to([TT, UT, E]), ALU.mult))


class PickGrouped:
    steps, asks_act, on_logits, loads = 21, False, ACT.Sigmoid, 1
    GROUPS, SCALE = 4, 2.5

    def __init__(self, bias):
        self.bias = bias

    def buffers(self, L, E):
        G = self.GROUPS
        return dict(gt=L.sb("gt", [TT, UT * E, E]), ge=L.sb("ge", [TT, UT * E, E]), rank=L.sb("rank", [TT, UT, E]),
                    ggt=L.sb("ggt", [TT, UT * G, G]), gge=L.sb("gge", [TT, UT * G, G]), grank=L.sb("grank", [TT, UT, G]),
                    biased=L.sb("biased", [TT, UT, E]), bias=L.sb("bias", [TT, E]), hi=L.sb("hi", [TT, UT * G, 2]),
                    lo=L.sb("lo", [TT, UT * G, 2]), first=L.sb("first", [TT, UT, G]), second=L.sb("second", [TT, UT, G]),
                    runner=L.sb("runner", [TT, UT, G]), total=L.sb("total", [TT, UT]), gbefore=L.sb("gbefore", [TT, G, G]))

    def load(self, sp, w, loaded):
        sp.dma_start(w["bias"][:], self.bias.broadcast_to([TT, self.bias.shape[1]])).then_inc(loaded, 16)

    def run(self, nc, dve, st, v, before, w, asked, answered, u):
        E, G = v.shape[2], self.GROUPS
        n = E // G
        biased, hi, lo = w["biased"][:], w["hi"][:], w["lo"][:]
        wide = [TT, UT, E]
        nc.vector.tensor_copy(w["gbefore"][:], before[:, 0:G, 0:G])
        st.then(nc.vector.tensor_tensor(biased, v[:], w["bias"][:].unsqueeze(1).broadcast_to(wide), ALU.add))
        b4 = biased.rearrange("p t (g a b) -> p (t g) a b", g=G, a=2)
        nc.vector.tensor_tensor(hi, b4[:, :, 0, :], b4[:, :, 1, :], ALU.max)
        st.then(nc.vector.tensor_tensor(lo, b4[:, :, 0, :], b4[:, :, 1, :], ALU.min))
        flat = [w[x][:].rearrange("p t g -> p (t g)") for x in ("first", "second", "runner")]
        nc.vector.tensor_tensor(flat[0], hi[:, :, 0], hi[:, :, 1], ALU.max)
        nc.vector.tensor_tensor(flat[1], hi[:, :, 0], hi[:, :, 1], ALU.min)
        st.then(nc.vector.tensor_tensor(flat[2], lo[:, :, 0], lo[:, :, 1], ALU.max))
        st.then(nc.vector.tensor_tensor(flat[1], flat[1], flat[2], ALU.max))
        st.then(nc.vector.tensor_tensor(flat[0], flat[0], flat[1], ALU.add))
        rank_of(nc, st, w["first"][:], w["gbefore"][:], w["ggt"][:], w["gge"][:], w["grank"][:])
        st.then(nc.vector.tensor_scalar(w["grank"][:], w["grank"][:], 1.5, None, ALU.is_lt))
        in_group = w["grank"][:].rearrange("p t g -> p (t g)").unsqueeze(2).broadcast_to([TT, UT * G, n])
        b3 = biased.rearrange("p t (g n) -> p (t g) n", g=G)
        st.then(nc.vector.tensor_tensor(b3, b3, in_group, ALU.mult))
        rank_of(nc, st, biased, before[:], w["gt"][:], w["ge"][:], w["rank"][:])
        st.then(nc.vector.scalar_tensor_tensor(out=v[:], in0=w["rank"][:], scalar=3.5, in1=v[:], op0=ALU.is_lt, op1=ALU.mult))
        st.then(nc.vector.reduce_sum(w["total"][:], v[:], AX.X))
        st.then(nc.vector.tensor_scalar(w["total"][:], w["total"][:], 1e-20, None, ALU.add))
        st.then(nc.vector.reciprocal(w["total"][:], w["total"][:]))
        st.then(nc.vector.tensor_scalar(w["total"][:], w["total"][:], self.SCALE, None, ALU.mult))
        st.then(nc.vector.tensor_tensor(v[:], v[:], w["total"][:].unsqueeze(2).broadcast_to(wide), ALU.mult))


def grouped_experts(core):
    d = core.dram
    E, tiles = d["f2_w1"].shape[0], d["f2_w2"].shape[2] // C
    with Layer(core, "f2") as L:
        xT = L.sb("xT", [P, KC, TOK])
        sel = L.sb("sel", [TT, NT, E])
        layer_norm(core, "f2ln", xT)
        route(core, "f2rt", xT, sel, d["f2_wg"], None, PickGrouped(d["f2_bias"]))
        experts(core, "f2ex", xT, sel, E, tiles, d["f2_w1"], None, d["f2_w2"], squared_relu=True)
        experts(core, "f2sh", xT, None, 1, d["f2_s2"].shape[2] // C, d["f2_s1"], None, d["f2_s2"], squared_relu=True)


def top2_experts(core):
    d = core.dram
    E, tiles = d["f3_w1"].shape[0], d["f3_w2"].shape[2] // C
    with Layer(core, "f3") as L:
        xT = L.sb("xT", [P, KC, TOK])
        sel = L.sb("sel", [TT, NT, E])
        layer_norm(core, "f3ln", xT)
        route(core, "f3rt", xT, sel, d["f3_wg"], None, PickTop2(), d["f3_b2"])
        experts(core, "f3ex", xT, sel, E, tiles, d["f3_w1"], d["f3_b1"], d["f3_w2"])


def head_rows(h):
    return slice(32 * (h % 4), 32 * (h % 4) + 16), h // 4


def softmax_attention(core):
    nc, h, ident, d = core.nc, core.h, core.ident, core.dram
    HEADS, HD, HALF = 16, 16, SEQ // 2
    G = HEADS // 4
    SCORE = float(C) ** -0.5
    with Layer(core, "a2") as L:
        xT = L.sb("xT", [P, KC, TOK])
        layer_norm(core, "a2ln", xT)
        wq = L.sb("wq", [P, KC, G * P])
        wk = L.sb("wk", [P, KC, G * P])
        bq = L.sb("bq", [P, G])
        bk = L.sb("bk", [P, G])
        wv = L.sb("wv", [P, KC, C])
        bv = L.sb("bv", [TT, C])
        wo = L.sb("wo", [P, KC, C])
        bo = L.sb("bo", [1, C])
        ones = L.sb("ones", [1, TT])
        x = L.sb("x", [P, KC, SEQ])
        q = L.sb("q", [P, G, SEQ])
        k = L.sb("k", [P, G, SEQ])
        v = L.sb("v", [HALF, 2, C])
        top = L.sb("top", [HALF, HEADS, 2])
        total = L.sb("total", [HALF, HEADS, 2])
        probs = L.sb("probs", [HALF, 2, 2, SEQ])
        probsT = L.sb("probsT", [HALF, 2, 2, SEQ])
        o = L.sb("o", [HALF, 2, C])
        oT = L.sb("oT", [P, KC, SEQ])
        score_ps = [L.ps(f"score_ps{s}", [HALF, 2, BANK // 2]) for s in range(2)]
        probsT_ps = [L.ps(f"probsT_ps{s}", [HALF, 2, BANK // 2]) for s in range(2)]
        o_ps = L.ps("o_ps", [HALF, 2, C])
        proj_ps = [L.ps(f"proj_ps{s}", [P, 2, BANK // 2]) for s in range(3)]
        loaded = L.sem("loaded")
        ones_set = L.sem("ones_set")
        x_ready = L.sem("x_ready")
        proj_ready = L.sem("proj_ready")
        act_out = L.sem("act_out")
        dve_out = L.sem("dve_out")
        score_ready = L.sem("score_ready")
        top_ready = L.sem("top_ready")
        probs_ready = L.sem("probs_ready")
        turned = L.sem("turned")
        probsT_ready = L.sem("probsT_ready")
        av_done = L.sem("av_done")
        o_ready = L.sem("o_ready")
        steps = L.sem("steps")
        loads = [(wq, "a2_wq"), (wk, "a2_wk"), (bq, "a2_bq"), (bk, "a2_bk"), (wv, "a2_wv"), (wo, "a2_wo"), (bo, "a2_bo")]
        all_loaded = 16 * (len(loads) + 1)

        with nc.Block() as block:

            @block.sync
            def _(sp):
                for dst, name in loads:
                    sp.dma_start(dst[:], d[name]).then_inc(loaded, 16)
                sp.dma_start(bv[:], d["a2_bv"].broadcast_to([TT, C])).then_inc(loaded, 16)

            @block.gpsimd
            def _(pool):
                nc.gpsimd.memset(ones[:], 1.0).then_inc(ones_set, 1)
                nc.gpsimd.tensor_copy(x[:], xT[:, :, 0:SEQ]).then_inc(x_ready, 1)
                with pool.Fori(1, SEQS) as b:
                    pool.wait_ge(proj_ready, b * 7 - 2)
                    nc.gpsimd.tensor_copy(x[:], xT[:, :, ds(b * SEQ, SEQ)]).then_inc(x_ready, 1)

            @block.tensor
            def _(pe):
                pe.wait_ge(loaded, all_loaded)
                pe.wait_ge(ones_set, 1)
                with pe.Fori(0, SEQS) as b:
                    pe.wait_ge(x_ready, b + 1)
                    pe.nop(nofuse=True)
                    pe.wait_ge(dve_out, b * 2 + 1)
                    for n, (w, g0) in enumerate(((wq, 0), (wq, 2), (wk, 0), (wk, 2))):
                        if n == 3:
                            pe.wait_ge(act_out, b * 5 + 1)
                        for g in range(2):
                            for c in range(KC):
                                ins = nc.tensor.matmul(proj_ps[n % 3][:, g, 0:SEQ], w[:, c, (g0 + g) * P:(g0 + g + 1) * P],
                                                       x[:, c, :], start=(c == 0), stop=(c == KC - 1))
                        ins.then_inc(proj_ready, 1)
                    pe.wait_ge(act_out, b * 5 + 2)
                    for a in range(2):
                        for c in range(KC):
                            ins = nc.tensor.matmul(proj_ps[1][0:HALF, a, :], x[:, c, a * HALF:(a + 1) * HALF], wv[:, c, :],
                                                   start=(c == 0), stop=(c == KC - 1))
                    ins.then_inc(proj_ready, 1)
                    pe.wait_ge(act_out, b * 5 + 4)
                    pe.nop(nofuse=True)

                    def score(n):
                        rows, g = head_rows(n)
                        if n >= 2:
                            pe.wait_ge(probs_ready, b * HEADS + n - 1)
                        for a in range(2):
                            ins = nc.tensor.matmul(score_ps[n % 2][:, a, 0:SEQ], q[rows, g, a * HALF:(a + 1) * HALF],
                                                   k[rows, g, :], start=True, stop=True)
                        ins.then_inc(score_ready, 1)

                    def turn(n):
                        pe.wait_ge(probs_ready, b * HEADS + n + 1)
                        if n >= 2:
                            pe.nop(nofuse=True)
                            pe.wait_ge(probsT_ready, b * HEADS + n - 1)
                        for a in range(2):
                            for kh in range(2):
                                ins = nc.tensor.transpose(probsT_ps[n % 2][:, kh, a * HALF:(a + 1) * HALF],
                                                          probs[:, n % 2, a, kh * HALF:(kh + 1) * HALF], ident[0:HALF, 0:HALF])
                        ins.then_inc(turned, 1)

                    def mix(n):
                        pe.wait_ge(probsT_ready, b * HEADS + n + 1)
                        if n == 0:
                            pe.nop(nofuse=True)
                            pe.wait_ge(dve_out, b * 2 + 2)
                        for a in range(2):
                            for kh in range(2):
                                ins = nc.tensor.matmul(o_ps[:, a, n * HD:(n + 1) * HD],
                                                       probsT[:, n % 2, kh, a * HALF:(a + 1) * HALF],
                                                       v[:, kh, n * HD:(n + 1) * HD], start=(kh == 0), stop=(kh == 1))
                        ins.then_inc(av_done, 1)

                    for n in range(HEADS + 2):
                        if n < HEADS:
                            score(n)
                        if 1 <= n <= HEADS:
                            turn(n - 1)
                        if n >= 2:
                            mix(n - 2)
                    pe.wait_ge(o_ready, b + 1)
                    for a in range(2):
                        for c in range(KC):
                            ins = nc.tensor.transpose(proj_ps[2][:, c, a * HALF:(a + 1) * HALF], o[:, a, c * P:(c + 1) * P],
                                                      ident[0:HALF, 0:HALF])
                    ins.then_inc(proj_ready, 1)
                    pe.wait_ge(act_out, b * 5 + 5)
                    for a in range(2):
                        nc.tensor.matmul(proj_ps[0][0:HALF, a, :], ones[:], bo[:], start=True, stop=False)
                        for c in range(KC):
                            ins = nc.tensor.matmul(proj_ps[0][0:HALF, a, :], oT[:, c, a * HALF:(a + 1) * HALF], wo[:, c, :],
                                                   start=False, stop=(c == KC - 1))
                    ins.then_inc(proj_ready, 1)

            @block.scalar
            def _(act):
                act.wait_ge(loaded, all_loaded)
                with act.Fori(0, SEQS) as b:
                    for n, (dst, bias, g0) in enumerate(((q, bq, 0), (q, bq, 2), (k, bk, 0), (k, bk, 2))):
                        act.wait_ge(proj_ready, b * 7 + n + 1)
                        for g in range(2):
                            ins = nc.scalar.activation(dst[:, g0 + g, :], proj_ps[n % 3][:, g, 0:SEQ], ACT.Identity,
                                                       bias=bias[:, g0 + g:g0 + g + 1])
                        ins.then_inc(act_out, 1)
                    for n in range(HEADS):
                        act.wait_ge(top_ready, b * HEADS + n + 1)
                        if n >= 2:
                            act.wait_ge(turned, b * HEADS + n - 1)
                        for a in range(2):
                            ins = nc.scalar.activation(probs[:, n % 2, a, :], score_ps[n % 2][:, a, 0:SEQ], ACT.Exp,
                                                       bias=top[:, n, a:a + 1], scale=SCORE, accum_out=total[:, n, a:a + 1])
                        ins.then_inc(probs_ready, 1)
                    act.wait_ge(proj_ready, b * 7 + 6)
                    nc.scalar.copy(oT[:], proj_ps[2][:, :, 0:SEQ]).then_inc(act_out, 1)

            @block.vector
            def _(dve):
                st = Steps(dve, steps)
                dve.sem_inc(dve_out, 1)
                dve.wait_ge(loaded, all_loaded)
                with dve.Fori(0, SEQS) as b:
                    st.enter(b, HEADS + 1)
                    dve.wait_ge(proj_ready, b * 7 + 5)
                    nc.vector.tensor_tensor(v[:], proj_ps[1][0:HALF, :, :], bv[:].unsqueeze(1).broadcast_to([TT, 2, C]),
                                            ALU.add).then_inc(dve_out, 1)
                    for n in range(HEADS + 1):
                        if n < HEADS:
                            dve.wait_ge(score_ready, b * HEADS + n + 1)
                            st.then(nc.vector.reduce_max(top[:, n, :], score_ps[n % 2][:, :, 0:SEQ], AX.X))
                            nc.vector.tensor_scalar(top[:, n, :], top[:, n, :], -SCORE, None, ALU.mult).then_inc(top_ready, 1)
                        if n >= 1:
                            m = n - 1
                            dve.wait_ge(turned, b * HEADS + m + 1)
                            if m >= 2:
                                dve.wait_ge(av_done, b * HEADS + m - 1)
                            nc.vector.tensor_copy(probsT[:, m % 2, :, :], probsT_ps[m % 2][:, :, 0:SEQ]).then_inc(probsT_ready, 1)
                    dve.wait_ge(probs_ready, (b + 1) * HEADS)
                    st.then(nc.vector.reciprocal(total[:], total[:]))
                    dve.wait_ge(av_done, (b + 1) * HEADS)
                    for a in range(2):
                        ins = nc.vector.tensor_tensor(o[:, a, :].rearrange("p (n e) -> p n e", n=HEADS),
                                                      o_ps[:, a, :].rearrange("p (n e) -> p n e", n=HEADS),
                                                      total[:, :, a:a + 1].broadcast_to([HALF, HEADS, HD]), ALU.mult)
                    ins.then_inc(o_ready, 1)
                    dve.wait_ge(proj_ready, b * 7 + 7)
                    nc.vector.tensor_tensor(h[:, ds(b * 2, 2), :], proj_ps[0][0:HALF, :, :], h[:, ds(b * 2, 2), :],
                                            ALU.add).then_inc(dve_out, 1)
                    st.leave(SEQS)


def taylor_attention(core):
    nc, h, ident, d = core.nc, core.h, core.ident, core.dram
    HEADS, HD, HALF = 8, 16, SEQ // 2
    G, HC, VW = HEADS // 4, HEADS * HD, HEADS * (HD + 1)
    SCALE, DEN_EPS = float(HD) ** -0.5, 1e-5
    with Layer(core, "a0") as L:
        xT = L.sb("xT", [P, KC, TOK])
        gamma = L.sb("gamma", [P, KC])
        wq = L.sb("wq", [P, KC, G * P])
        wk = L.sb("wk", [P, KC, G * P])
        wv = L.sb("wv", [P, KC, HC])
        wo = L.sb("wo", [P, C])
        loaded = L.sem("loaded")
        with nc.Block() as block:

            @block.sync
            def _(sp):
                for dst, name in ((gamma, "a0_gamma"), (wq, "a0_wq"), (wk, "a0_wk"), (wv, "a0_wv"), (wo, "a0_wo")):
                    sp.dma_start(dst[:], d[name]).then_inc(loaded, 16)
                sp.wait_ge(loaded, 16 * 5)
        layer_norm(core, "a0ln", xT, rms_gain=gamma)
        ones = L.sb("ones", [HALF, HALF])
        one = L.sb("one", [P, 1])
        x = L.sb("x", [P, KC, SEQ])
        q = L.sb("q", [P, G, SEQ])
        k = L.sb("k", [P, G, SEQ])
        v = L.sb("v", [HALF, 2, VW])
        square = L.sb("square", [HALF, 2, 2, SEQ])
        den = L.sb("den", [HALF, 2, HEADS])
        o = L.sb("o", [HALF, 2, HC])
        oT = L.sb("oT", [P, SEQ])
        s_ps = [L.ps(f"s_ps{s}", [HALF, 2, BANK // 2]) for s in range(2)]
        o_ps = L.ps("o_ps", [HALF, 2, BANK // 2])
        proj_ps = [L.ps(f"proj_ps{s}", [P, 2, BANK // 2]) for s in range(3)]
        ones_set = L.sem("ones_set")
        x_ready = L.sem("x_ready")
        proj_ready = L.sem("proj_ready")
        act_out = L.sem("act_out")
        dve_out = L.sem("dve_out")
        s_ready = L.sem("s_ready")
        square_ready = L.sem("square_ready")
        av_done = L.sem("av_done")
        o_ready = L.sem("o_ready")
        steps = L.sem("steps")

        with nc.Block() as block:

            @block.gpsimd
            def _(pool):
                nc.gpsimd.memset(ones[:], 1.0)
                nc.gpsimd.memset(one[:], 1.0)
                nc.gpsimd.memset(v[:], 1.0).then_inc(ones_set, 1)
                nc.gpsimd.tensor_copy(x[:], xT[:, :, 0:SEQ]).then_inc(x_ready, 1)
                with pool.Fori(1, SEQS) as b:
                    pool.wait_ge(proj_ready, b * 5 - 2)
                    nc.gpsimd.tensor_copy(x[:], xT[:, :, ds(b * SEQ, SEQ)]).then_inc(x_ready, 1)

            @block.tensor
            def _(pe):
                pe.wait_ge(ones_set, 1)
                with pe.Fori(0, SEQS) as b:
                    pe.wait_ge(x_ready, b + 1)
                    pe.nop(nofuse=True)
                    pe.wait_ge(dve_out, b * 2 + 1)
                    for n, w in enumerate((wq, wk)):
                        for g in range(G):
                            for c in range(KC):
                                ins = nc.tensor.matmul(proj_ps[n][:, g, 0:SEQ], w[:, c, g * P:(g + 1) * P],
                                                       x[:, c, :], start=(c == 0), stop=(c == KC - 1))
                        ins.then_inc(proj_ready, 1)
                    for a in range(2):
                        for c in range(KC):
                            ins = nc.tensor.matmul(proj_ps[2][0:HALF, a, 0:HC], x[:, c, a * HALF:(a + 1) * HALF], wv[:, c, :],
                                                   start=(c == 0), stop=(c == KC - 1))
                    ins.then_inc(proj_ready, 1)
                    pe.wait_ge(act_out, b * 3 + 2)
                    pe.nop(nofuse=True)

                    def score(n):
                        rows, g = head_rows(n)
                        if n >= 2:
                            pe.wait_ge(square_ready, b * HEADS + n - 1)
                        for kh in range(2):
                            ins = nc.tensor.matmul(s_ps[n % 2][:, kh, 0:SEQ], k[rows, g, kh * HALF:(kh + 1) * HALF],
                                                   q[rows, g, :], start=True, stop=True)
                        ins.then_inc(s_ready, 1)

                    def mix(n):
                        pe.wait_ge(square_ready, b * HEADS + n + 1)
                        for a in range(2):
                            for kh in range(2):
                                ins = nc.tensor.matmul(o_ps[:, a, n * (HD + 1):(n + 1) * (HD + 1)],
                                                       square[:, n % 2, kh, a * HALF:(a + 1) * HALF],
                                                       v[:, kh, n * (HD + 1):(n + 1) * (HD + 1)], start=False, stop=(kh == 1),
                                                       skip_group_check=True)
                        ins.then_inc(av_done, 1)

                    score(0)
                    score(1)
                    pe.wait_ge(dve_out, b * 2 + 2)
                    for a in range(2):
                        for kh in range(2):
                            nc.tensor.matmul(o_ps[:, a, 0:VW], ones[:], v[:, kh, :], start=(a == 0 and kh == 0), stop=False,
                                             skip_group_check=True)
                    for n in range(2, HEADS + 2):
                        mix(n - 2)
                        if n < HEADS:
                            score(n)
                    pe.wait_ge(o_ready, b + 1)
                    for a in range(2):
                        ins = nc.tensor.transpose(proj_ps[0][:, 0, a * HALF:(a + 1) * HALF], o[:, a, :], ident[0:HALF, 0:HALF])
                    ins.then_inc(proj_ready, 1)
                    pe.wait_ge(act_out, b * 3 + 3)
                    for a in range(2):
                        ins = nc.tensor.matmul(proj_ps[1][0:HALF, a, :], oT[:, a * HALF:(a + 1) * HALF], wo[:],
                                               start=True, stop=True)
                    ins.then_inc(proj_ready, 1)

            @block.scalar
            def _(act):
                act.wait_ge(ones_set, 1)
                with act.Fori(0, SEQS) as b:
                    for n, dst in enumerate((q, k)):
                        act.wait_ge(proj_ready, b * 5 + n + 1)
                        nc.scalar.copy(dst[:], proj_ps[n][:, :, 0:SEQ]).then_inc(act_out, 1)
                    for n in range(HEADS):
                        act.wait_ge(s_ready, b * HEADS + n + 1)
                        if n >= 2:
                            act.wait_ge(av_done, b * HEADS + n - 1)
                        nc.scalar.activation(square[:, n % 2, :, :], s_ps[n % 2][:, :, 0:SEQ], ACT.Square,
                                             bias=one[0:HALF, :], scale=SCALE).then_inc(square_ready, 1)
                    act.wait_ge(proj_ready, b * 5 + 4)
                    nc.scalar.copy(oT[:], proj_ps[0][:, 0, 0:SEQ]).then_inc(act_out, 1)

            @block.vector
            def _(dve):
                st = Steps(dve, steps)
                dve.wait_ge(ones_set, 1)
                dve.sem_inc(dve_out, 1)
                with dve.Fori(0, SEQS) as b:
                    st.enter(b, 2)
                    dve.wait_ge(proj_ready, b * 5 + 3)
                    for a in range(2):
                        ins = nc.vector.tensor_copy(v[:, a, :].rearrange("p (n e) -> p n e", n=HEADS)[:, :, 0:HD],
                                                    proj_ps[2][0:HALF, a, 0:HC].rearrange("p (n e) -> p n e", n=HEADS))
                    ins.then_inc(dve_out, 1)
                    dve.wait_ge(av_done, (b + 1) * HEADS)
                    both = o_ps[:, :, 0:VW].rearrange("p a (n e) -> p a n e", n=HEADS)
                    st.then(nc.vector.tensor_scalar(den[:].unsqueeze(3), both[:, :, :, HD:HD + 1], 0.5, DEN_EPS, ALU.mult, ALU.max))
                    st.then(nc.vector.reciprocal(den[:], den[:]))
                    for a in range(2):
                        ins = nc.vector.scalar_tensor_tensor(out=o[:, a, :].rearrange("p (n e) -> p n e", n=HEADS),
                                                             in0=both[:, a, :, 0:HD], scalar=0.5,
                                                             in1=den[:, a, :].unsqueeze(2).broadcast_to([HALF, HEADS, HD]),
                                                             op0=ALU.mult, op1=ALU.mult)
                    ins.then_inc(o_ready, 1)
                    dve.wait_ge(proj_ready, b * 5 + 5)
                    nc.vector.tensor_tensor(h[:, ds(b * 2, 2), :], proj_ps[1][0:HALF, :, :], h[:, ds(b * 2, 2), :],
                                            ALU.add).then_inc(dve_out, 1)
                    st.leave(SEQS)


def token_norm(core, name, u, gain, shift):
    nc, h = core.nc, core.h
    with Layer(core, name) as L:
        stats = L.sb("stats", [TT, UT, 6])
        moments = L.sb("moments", [TT, 2, UT, 2])
        eps_var = L.sb("eps_var", [TT, 2, UT])
        rstd = L.sb("rstd", [TT, 2, UT])
        power = L.sb("power", [TT, UT])
        steps = L.sem("steps")
        power_set = L.sem("power_set")
        var_ready = L.sem("var_ready")
        rstd_ready = L.sem("rstd_ready")
        y_ready = L.sem("y_ready")
        with nc.Block() as block:

            @block.vector
            def _(dve):
                st = Steps(dve, steps)
                nc.vector.memset(power[:], -0.5).then_inc(power_set, 1)
                with dve.Fori(0, NU) as i:
                    st.enter(i, 5)
                    for r, src in enumerate((h, u)):
                        for t in range(UT):
                            ins = nc.vector.bn_stats(stats[:, t, :], src[:, ds(i * UT + t, 1), :])
                        st.then(ins)
                        dve.nop(nofuse=True)
                        for t in range(UT):
                            ins = nc.vector.bn_aggr(moments[:, r, t, :], stats[:, t, :])
                        st.then(ins)
                        nc.vector.tensor_scalar(eps_var[:, r, :], moments[:, r, :, 1], LN_EPS, None,
                                                ALU.add).then_inc(var_ready, 1)
                        dve.wait_ge(rstd_ready, i * 2 + r + 1)
                        for t in range(UT):
                            tile = ds(i * UT + t, 1)
                            ins = nc.vector.tensor_scalar(u[:, tile, :], src[:, tile, :], moments[:, r, t, 0:1],
                                                          rstd[:, r, t:t + 1], ALU.subtract, ALU.mult)
                        if r == 0:
                            st.then(ins)
                            dve.nop(nofuse=True)
                        else:
                            ins.then_inc(y_ready, 1)
                    st.leave(NU)

            @block.gpsimd
            def _(pool):
                pool.wait_ge(power_set, 1)
                with pool.Fori(0, NU) as i:
                    for r in range(2):
                        pool.wait_ge(var_ready, i * 2 + r + 1)
                        nc.gpsimd.tensor_tensor(rstd[:, r, :], eps_var[:, r, :], power[:], ALU.pow).then_inc(rstd_ready, 1)
        gained = L.sem("gained")
        wide = [TT, NT // 2, C]
        with nc.Block() as block:

            @block.vector
            def _(dve):
                mine = u[:, 0:NT // 2, :]
                nc.vector.tensor_tensor(mine, mine, gain.unsqueeze(1).broadcast_to(wide), ALU.mult).then_inc(gained, 1)
                dve.wait_ge(gained, 1)
                nc.vector.tensor_tensor(mine, mine, shift.unsqueeze(1).broadcast_to(wide), ALU.add)

            @block.gpsimd
            def _(pool):
                mine = u[:, NT // 2:NT, :]
                nc.gpsimd.tensor_tensor(mine, mine, gain.unsqueeze(1).broadcast_to(wide), ALU.mult).then_inc(y_ready, 1)
                pool.wait_ge(y_ready, NU + 1)
                nc.gpsimd.tensor_tensor(mine, mine, shift.unsqueeze(1).broadcast_to(wide), ALU.add)


def kernel_spectrum(core, F, KR, KR2, KI):
    nc, d = core.nc, core.dram
    PI = 3.1415925
    ROUND = 12582912.0
    TURN = (6.28125, 0.0019350051879882812, 3.0199159819120313e-07)
    with Layer(core, "ks") as L:
        lre = L.sb("lre", [P, 1])
        lim = L.sb("lim", [P, 1])
        cre = L.sb("cre", [P, C])
        cim = L.sb("cim", [P, C])
        step_i = L.sb("step_i", [P, SEQ], I32)
        step = L.sb("step", [P, SEQ])
        decay = L.sb("decay", [P, SEQ])
        angle = L.sb("angle", [P, SEQ])
        turns = L.sb("turns", [P, SEQ])
        sine = L.sb("sine", [P, SEQ])
        half = L.sb("half", [P, SEQ])
        small = L.sb("small", [P, 10])
        term = L.sb("term", [P, 2, C])
        K = L.sb("K", [TT, 2, C])
        K_ps = L.ps("K_ps", [TT, 2, C])
        spec_ps = L.ps("spec_ps", [TT, 4, C])
        loaded, stepped, rates, args, waves = (L.sem(n) for n in ("loaded", "stepped", "rates", "args", "waves"))
        modes, k_ready, k_out, spectrum = (L.sem(n) for n in ("modes", "k_ready", "k_out", "spectrum"))
        steps = L.sem("steps")
        a, b, m, nr, t1, t2, wr, wi = (small[:, i:i + 1] for i in range(8))
        with nc.Block() as block:

            @block.sync
            def _(sp):
                for dst, name in ((lre, "a3_lre"), (lim, "a3_lim"), (cre, "a3_cre"), (cim, "a3_cim")):
                    sp.dma_start(dst[:], d[name]).then_inc(loaded, 16)

            @block.gpsimd
            def _(pool):
                nc.gpsimd.iota(step_i[:], [[1, SEQ]], base=0, channel_multiplier=0).then_inc(stepped, 1)

            @block.scalar
            def _(act):
                act.wait_ge(loaded, 64)
                nc.scalar.activation(a, lre[:], ACT.Exp)
                nc.scalar.activation(b, lim[:], ACT.Exp).then_inc(rates, 1)
                act.wait_ge(args, 1)
                nc.scalar.activation(decay[:], decay[:], ACT.Exp)
                nc.scalar.activation(sine[:], angle[:], ACT.Sin)
                nc.scalar.activation(half[:], angle[:], ACT.Sin, scale=0.5).then_inc(waves, 1)

            @block.vector
            def _(dve):
                st = Steps(dve, steps)
                V = nc.vector
                dve.wait_ge(stepped, 1)
                st.then(V.tensor_copy(step[:], step_i[:]))
                dve.wait_ge(rates, 1)
                V.tensor_scalar(decay[:], step[:], a, -1.0, ALU.mult, ALU.mult)
                st.then(V.tensor_scalar(angle[:], step[:], b, None, ALU.mult))
                st.then(V.tensor_scalar(turns[:], angle[:], 0.15915494309189535, ROUND, ALU.mult, ALU.add))
                st.then(V.tensor_scalar(turns[:], turns[:], ROUND, None, ALU.subtract))
                for part in TURN:
                    st.then(V.scalar_tensor_tensor(out=angle[:], in0=turns[:], scalar=-part, in1=angle[:],
                                                   op0=ALU.mult, op1=ALU.add))
                V.tensor_scalar(angle[:], angle[:], PI, -PI, ALU.min, ALU.max).then_inc(args, 1)
                dve.wait_ge(waves, 1)
                st.then(V.tensor_tensor(half[:], half[:], half[:], ALU.mult))
                st.then(V.tensor_scalar(half[:], half[:], -2.0, 1.0, ALU.mult, ALU.add))
                V.tensor_tensor(half[:], half[:], decay[:], ALU.mult)
                st.then(V.tensor_tensor(sine[:], sine[:], decay[:], ALU.mult))
                st.then(V.tensor_tensor(m, a, a, ALU.mult))
                V.tensor_scalar(nr, half[:, 1:2], 1.0, None, ALU.subtract)
                st.then(V.scalar_tensor_tensor(out=m, in0=b, scalar=b, in1=m, op0=ALU.mult, op1=ALU.add))
                V.tensor_tensor(t1, nr, a, ALU.mult)
                V.tensor_tensor(t2, sine[:, 1:2], a, ALU.mult)
                st.then(V.reciprocal(m, m))
                V.scalar_tensor_tensor(out=wr, in0=sine[:, 1:2], scalar=b, in1=t1, op0=ALU.mult, op1=ALU.subtract)
                st.then(V.scalar_tensor_tensor(out=wi, in0=nr, scalar=b, in1=t2, op0=ALU.mult, op1=ALU.add))
                V.tensor_scalar(wr, wr, m, None, ALU.mult)
                st.then(V.tensor_scalar(wi, wi, m, -1.0, ALU.mult, ALU.mult))
                V.tensor_scalar(term[:, 0, :], cim[:], wi, None, ALU.mult)
                st.then(V.tensor_scalar(term[:, 1, :], cre[:], wi, None, ALU.mult))
                st.then(V.scalar_tensor_tensor(out=term[:, 0, :], in0=cre[:], scalar=wr, in1=term[:, 0, :],
                                               op0=ALU.mult, op1=ALU.subtract))
                st.then(V.scalar_tensor_tensor(out=term[:, 1, :], in0=cim[:], scalar=wr, in1=term[:, 1, :],
                                               op0=ALU.mult, op1=ALU.add))
                V.tensor_scalar(term[:, 1, :], term[:, 1, :], -1.0, None, ALU.mult).then_inc(modes, 1)
                dve.wait_ge(k_ready, 1)
                V.tensor_copy(K[:], K_ps[:]).then_inc(k_out, 1)
                dve.wait_ge(spectrum, 1)
                V.tensor_copy(KR[:], spec_ps[:, 0:2, :])
                V.tensor_copy(KR2[:], spec_ps[:, 0:2, :])
                st.then(V.tensor_copy(KI[:], spec_ps[:, 2:4, :]))
                V.tensor_copy(KR2[0:1, 0, :], spec_ps[0:1, 2, :])
                V.memset(KI[0:1, 0, :], 0.0)

            @block.tensor
            def _(pe):
                pe.wait_ge(modes, 1)
                for s in range(2):
                    nc.tensor.matmul(K_ps[:, s, :], half[:, s * TT:(s + 1) * TT], term[:, 0, :], start=True, stop=False)
                    ins = nc.tensor.matmul(K_ps[:, s, :], sine[:, s * TT:(s + 1) * TT], term[:, 1, :], start=False, stop=True)
                ins.then_inc(k_ready, 1)
                pe.wait_ge(k_out, 1)
                for j in range(4):
                    for s in range(2):
                        ins = nc.tensor.matmul(spec_ps[:, j, :], F[:, s, j * TT:(j + 1) * TT], K[:, s, :],
                                               start=(s == 0), stop=(s == 1))
                ins.then_inc(spectrum, 1)


def long_convolution(core):
    nc, h, d = core.nc, core.h, core.dram
    with Layer(core, "a3") as L:
        u = L.sb("u", [TT, NT, C])
        gain = L.sb("gain", [TT, C])
        shift = L.sb("shift", [TT, C])
        skip = L.sb("skip", [TT, C])
        F = L.sb("F", [TT, 2, 2 * SEQ])
        G = L.sb("G", [TT, 4, SEQ])
        KR = L.sb("KR", [TT, 2, C])
        KR2 = L.sb("KR2", [TT, 2, C])
        KI = L.sb("KI", [TT, 2, C])
        loaded = L.sem("loaded")
        with nc.Block() as block:

            @block.sync
            def _(sp):
                for dst, name in ((gain, "a3_gain"), (shift, "a3_shift"), (skip, "a3_skip")):
                    sp.dma_start(dst[:], d[name].broadcast_to([TT, C])).then_inc(loaded, 16)
                for dst, name in ((F, "a3_F"), (G, "a3_G")):
                    sp.dma_start(dst[:], d[name]).then_inc(loaded, 16)
                sp.wait_ge(loaded, 16 * 5)
        kernel_spectrum(core, F, KR, KR2, KI)
        token_norm(core, "a3ln", u, gain[:], shift[:])
        prod = L.sb("prod", [TT, 4, 2, C])
        Y = L.sb("Y", [TT, 4, 2, C])
        ud = L.sb("ud", [TT, 4, C])
        f_ps = [L.ps(f"f_ps{j}", [TT, 2, 2, C]) for j in range(2)]
        y_ps = L.ps("y_ps", [TT, 2, 2, C])
        f_ready = L.sem("f_ready")
        prod_ready = L.sem("prod_ready")
        Y_ready = L.sem("Y_ready")
        y_ready = L.sem("y_ready")
        ud_ready = L.sem("ud_ready")
        done = L.sem("done")
        steps = L.sem("steps")
        with nc.Block() as block:

            @block.tensor
            def _(pe):
                with pe.Fori(0, SEQS // 2) as i:
                    pe.wait_ge(done, i + 1)
                    for j in range(2):
                        for part in range(2):
                            for s in range(2):
                                x = u[:, ds(i * 4, 4), :].rearrange("p (b s) c -> p b s c", s=2)[:, :, s, :]
                                ins = nc.tensor.matmul(f_ps[j][:, part, :, :], F[:, s, (2 * part + j) * TT:(2 * part + j + 1) * TT],
                                                       x, start=(s == 0), stop=(s == 1))
                        ins.then_inc(f_ready, 1)
                    pe.wait_ge(Y_ready, i * 2 + 2)
                    for s in range(2):
                        for slot in range(4):
                            ins = nc.tensor.matmul(y_ps[:, s, :, :], G[:, slot, s * TT:(s + 1) * TT], Y[:, slot, :, :],
                                                   start=(slot == 0), stop=(slot == 3))
                    ins.then_inc(y_ready, 1)

            @block.vector
            def _(dve):
                st = Steps(dve, steps)
                dve.sem_inc(done, 1)
                wide = [TT, 2, C]
                with dve.Fori(0, SEQS // 2) as i:
                    st.enter(i, 1)
                    for j in range(2):
                        dve.wait_ge(f_ready, i * 2 + j + 1)
                        if j == 1:
                            dve.nop(nofuse=True)
                            dve.wait_ge(Y_ready, i * 2 + 1)
                        cu, su = f_ps[j][:, 0, :, :], f_ps[j][:, 1, :, :]
                        kr, kr2, ki = (k[:, j:j + 1, :].broadcast_to(wide) for k in (KR, KR2, KI))
                        nc.vector.tensor_tensor(prod[:, 0, :, :], cu, kr, ALU.mult)
                        nc.vector.tensor_tensor(prod[:, 1, :, :], su, ki, ALU.mult)
                        nc.vector.tensor_tensor(prod[:, 2, :, :], su, kr2, ALU.mult)
                        nc.vector.tensor_tensor(prod[:, 3, :, :], cu, ki, ALU.mult).then_inc(prod_ready, 1)
                    dve.wait_ge(y_ready, i + 1)
                    mine = h[:, ds(i * 4, 4), :].rearrange("p (b s) c -> p s b c", s=2)
                    st.then(nc.vector.tensor_tensor(mine, y_ps[:], mine, ALU.add))
                    dve.wait_ge(ud_ready, i + 1)
                    nc.vector.tensor_tensor(h[:, ds(i * 4, 4), :], ud[:], h[:, ds(i * 4, 4), :], ALU.add).then_inc(done, 1)
                    st.leave(SEQS // 2)

            @block.gpsimd
            def _(pool):
                with pool.Fori(0, SEQS // 2) as i:
                    pool.wait_ge(done, i + 1)
                    nc.gpsimd.tensor_tensor(ud[:], u[:, ds(i * 4, 4), :], skip[:].unsqueeze(1).broadcast_to([TT, 4, C]),
                                            ALU.mult).then_inc(ud_ready, 1)
                    for j in range(2):
                        pool.wait_ge(prod_ready, i * 2 + j + 1)
                        nc.gpsimd.tensor_tensor(Y[:, j, :, :], prod[:, 0, :, :], prod[:, 1, :, :], ALU.subtract)
                        nc.gpsimd.tensor_tensor(Y[:, 2 + j, :, :], prod[:, 2, :, :], prod[:, 3, :, :],
                                                ALU.add).then_inc(Y_ready, 1)


ROUND = 12582912.0
QMAX = 32767.0
U16 = 65536.0


class Scale:

    def __init__(self, L, name):
        self.most = L.sb(f"{name}_most", [P, 1])
        self.all = L.sb(f"{name}_all", [P, 1])
        self.step = L.sb(f"{name}_step", [P, 1])
        self.inverse = L.sb(f"{name}_inverse", [P, 1])


def make_scales(core, name, pairs):
    nc = core.nc
    with Layer(core, name) as L:
        steps, most_ready, all_ready = L.sem("steps"), L.sem("most_ready"), L.sem("all_ready")
        with nc.Block() as block:

            @block.vector
            def _(dve):
                st = Steps(dve, steps)
                for s, maxima in pairs:
                    nc.vector.reduce_max(s.most[:], maxima, AX.X).then_inc(most_ready, 1)
                for n, (s, _) in enumerate(pairs):
                    dve.wait_ge(all_ready, n + 1)
                    st.then(nc.vector.tensor_scalar(s.step[:], s.all[:], 1.0 / QMAX, 1e-12, ALU.mult, ALU.max))
                    nc.vector.reciprocal(s.inverse[:], s.step[:])

            @block.gpsimd
            def _(pool):
                for n, (s, _) in enumerate(pairs):
                    pool.wait_ge(most_ready, n + 1)
                    nc.gpsimd.partition_all_reduce(s.all[:], s.most[:], P, bass.bass_isa.ReduceOp.max).then_inc(all_ready, 1)


def block_weights(core, name, w_dram, wT, tiles, width):
    nc, ident = core.nc, core.ident
    BLOCK, W_QMAX = 32, 7.0
    NB = tiles * width // BLOCK
    NC = width // P
    with Layer(core, name) as L:
        w = L.sb("w", [P, tiles, width])
        inverse = L.sb("inverse", [P, NB])
        step = L.sb("step", [P, NB])
        turned = [L.ps(f"turned{s}", [P, BANK]) for s in range(2)]
        loaded, steps, w_ready, t_ready, t_out = (L.sem(n) for n in ("loaded", "steps", "w_ready", "t_ready", "t_out"))
        blocks = w[:].rearrange("p t (n b) -> p (t n) b", b=BLOCK)
        wide = [P, NB, BLOCK]
        banks = tiles * NC // 4
        with nc.Block() as block:

            @block.sync
            def _(sp):
                sp.dma_start(w[:], w_dram).then_inc(loaded, 16)

            @block.vector
            def _(dve):
                st = Steps(dve, steps)
                dve.wait_ge(loaded, 16)
                st.then(nc.vector.reduce_max(step[:], blocks, AX.X, apply_absolute_value=True))
                st.then(nc.vector.tensor_scalar(step[:], step[:], 1.0 / W_QMAX, 1e-12, ALU.mult, ALU.max))
                st.then(nc.vector.reciprocal(inverse[:], step[:]))
                st.then(nc.vector.tensor_tensor(blocks, blocks, inverse[:].unsqueeze(2).broadcast_to(wide), ALU.mult))
                st.then(nc.vector.tensor_scalar(w[:], w[:], ROUND, ROUND, ALU.add, ALU.subtract))
                st.then(nc.vector.tensor_scalar(w[:], w[:], W_QMAX, -W_QMAX - 1.0, ALU.min, ALU.max))
                nc.vector.tensor_tensor(blocks, blocks, step[:].unsqueeze(2).broadcast_to(wide), ALU.mult).then_inc(w_ready, 1)

            @block.tensor
            def _(pe):
                pe.wait_ge(w_ready, 1)
                for g in range(banks):
                    if g >= 2:
                        pe.wait_ge(t_out, g - 1)
                    for n in range(4 * g, 4 * g + 4):
                        c, t = n // tiles, n % tiles
                        ins = nc.tensor.transpose(turned[g % 2][:, (n % 4) * P:(n % 4 + 1) * P], w[:, t, c * P:(c + 1) * P], ident[:])
                    ins.then_inc(t_ready, 1)

            @block.scalar
            def _(act):
                out = wT.rearrange("p c o -> p (c o)")
                for g in range(banks):
                    act.wait_ge(t_ready, g + 1)
                    nc.scalar.copy(out[:, g * BANK:(g + 1) * BANK], turned[g % 2][:]).then_inc(t_out, 1)


def quantised_mlp(core):
    nc, h, d = core.nc, core.h, core.dram
    I = d["f1_gate"].shape[1] * P
    M = I // P
    with Layer(core, "f1") as L:
        gateT = L.sb("gateT", [P, KC, I])
        upT = L.sb("upT", [P, KC, I])
        downT = L.sb("downT", [P, M, C])
        block_weights(core, "f1wg", d["f1_gate"], gateT[:], M, C)
        block_weights(core, "f1wu", d["f1_up"], upT[:], M, C)
        block_weights(core, "f1wd", d["f1_down"], downT[:], C // P, I)
        rounder = L.sb("rounder", [P, 1])
        x_max = L.sb("x_max", [P, KC * NU])
        gate_max = L.sb("gate_max", [P, NU * M])
        up_max = L.sb("up_max", [P, NU * M])
        act_max = L.sb("act_max", [P, NU * M])
        out_max = L.sb("out_max", [P, NU * M])
        sx, sg, su, sa, so = (Scale(L, n) for n in ("sx", "sg", "su", "sa", "so"))
        act_step = L.sb("act_step", [P, 1])
        gate = L.sb("gate", [P, M, TOK])
        with Layer(core, "f1x") as LX:
            xT = LX.sb("xT", [P, KC, TOK])
            layer_norm(core, "f1ln", xT)
            tmp = LX.sb("tmp", [P, 2, UNIT])
            x_done = LX.sem("x_done")
            set_ = LX.sem("set")
            with nc.Block() as block:

                @block.vector
                def _(dve):
                    nc.vector.memset(rounder[:], ROUND)
                    nc.vector.reduce_max(x_max[:].rearrange("p (k u) -> p k u", k=KC),
                                         xT[:].rearrange("p k (u n) -> p k u n", u=NU), AX.X, apply_absolute_value=True)
            make_scales(core, "f1sx", [(sx, x_max[:])])

            rounded, clipped = LX.sem("rounded"), LX.sem("clipped")
            with nc.Block() as block:

                @block.scalar
                def _(act):
                    with act.Fori(0, NU) as u:
                        part = xT[:, :, ds(u * UNIT, UNIT)]
                        nc.scalar.activation(part, part, ACT.Identity, bias=rounder[:], scale=sx.inverse[:]).then_inc(rounded, 1)

                @block.vector
                def _(dve):
                    with dve.Fori(0, NU) as u:
                        part = xT[:, :, ds(u * UNIT, UNIT)]
                        dve.wait_ge(rounded, u + 1)
                        nc.vector.tensor_scalar(part, part, ROUND + QMAX, ROUND - QMAX - 1.0, ALU.min, ALU.max).then_inc(clipped, 1)
                        dve.wait_ge(clipped, u + 1)
                        nc.vector.tensor_scalar(part, part, ROUND, sx.step[:], ALU.subtract, ALU.mult)

            with Layer(core, "f1p") as LP:
                g_ps = [LP.ps(f"g_ps{s}", [P, BANK]) for s in range(2)]
                u_ps = [LP.ps(f"u_ps{s}", [P, BANK]) for s in range(2)]
                g_ready, u_ready, g_out, u_seen = (LP.sem(n) for n in ("g_ready", "u_ready", "g_out", "u_seen"))
                with nc.Block() as block:

                    @block.tensor
                    def _(pe):
                        with pe.Fori(0, NU) as u:
                            for m in range(M):
                                n = u * M + m
                                pe.wait_ge(g_out, n + 1)
                                for k in range(KC):
                                    ins = nc.tensor.matmul(g_ps[m % 2][:, 0:UNIT], gateT[:, k, m * P:(m + 1) * P],
                                                           xT[:, k, ds(u * UNIT, UNIT)], start=(k == 0), stop=(k == KC - 1))
                                ins.then_inc(g_ready, 1)
                                pe.wait_ge(u_seen, n + 1)
                                for k in range(KC):
                                    ins = nc.tensor.matmul(u_ps[m % 2][:, 0:UNIT], upT[:, k, m * P:(m + 1) * P],
                                                           xT[:, k, ds(u * UNIT, UNIT)], start=(k == 0), stop=(k == KC - 1))
                                ins.then_inc(u_ready, 1)

                    @block.scalar
                    def _(act):
                        act.sem_inc(g_out, 2)
                        with act.Fori(0, NU) as u:
                            for m in range(M):
                                act.wait_ge(g_ready, u * M + m + 1)
                                nc.scalar.copy(gate[:, m, ds(u * UNIT, UNIT)], g_ps[m % 2][:, 0:UNIT]).then_inc(g_out, 1)

                    @block.vector
                    def _(dve):
                        dve.sem_inc(u_seen, 2)
                        with dve.Fori(0, NU) as u:
                            for m in range(M):
                                n = u * M + m
                                dve.wait_ge(g_out, n + 3)
                                nc.vector.reduce_max(gate_max[:, ds(n, 1)], gate[:, m, ds(u * UNIT, UNIT)], AX.X,
                                                     apply_absolute_value=True)
                                dve.wait_ge(u_ready, n + 1)
                                nc.vector.reduce_max(up_max[:, ds(n, 1)], u_ps[m % 2][:, 0:UNIT], AX.X,
                                                     apply_absolute_value=True).then_inc(u_seen, 1)
            make_scales(core, "f1sg", [(sg, gate_max[:]), (su, up_max[:])])

            with Layer(core, "f1s") as LS:
                sig = LS.sb("sig", [P, 2, UNIT])
                rounded, g_ready, sig_ready, tile_done, steps = (LS.sem(n) for n in ("rounded", "g_ready", "sig_ready", "tile_done", "steps"))
                stepped = LS.sem("stepped")
                with nc.Block() as block:

                    @block.scalar
                    def _(act):
                        with act.Fori(0, NU) as u:
                            for m in range(M):
                                part = gate[:, m, ds(u * UNIT, UNIT)]
                                nc.scalar.activation(part, part, ACT.Identity, bias=rounder[:], scale=sg.inverse[:]).then_inc(rounded, 1)
                            for m in range(M):
                                n = u * M + m
                                act.wait_ge(g_ready, n + 1)
                                act.nop(nofuse=True)
                                act.wait_ge(tile_done, n + 1)
                                act.nop(nofuse=True)
                                nc.scalar.activation(sig[:, m % 2, :], gate[:, m, ds(u * UNIT, UNIT)], ACT.Sigmoid,
                                                     scale=U16).then_inc(sig_ready, 1)

                    @block.vector
                    def _(dve):
                        st = Steps(dve, steps)
                        nc.vector.tensor_scalar(act_step[:], sg.step[:], 1.0 / U16, None, ALU.mult).then_inc(stepped, 1)
                        dve.wait_ge(stepped, 1)
                        dve.sem_inc(tile_done, 2)
                        with dve.Fori(0, NU) as u:
                            st.enter(u, 4 * M)
                            for m in range(M):
                                part = gate[:, m, ds(u * UNIT, UNIT)]
                                dve.wait_ge(rounded, u * M + m + 1)
                                st.then(nc.vector.tensor_scalar(part, part, ROUND + QMAX, ROUND - QMAX - 1.0, ALU.min, ALU.max))
                                nc.vector.tensor_scalar(part, part, ROUND, act_step[:], ALU.subtract, ALU.mult).then_inc(g_ready, 1)
                            for m in range(M):
                                n = u * M + m
                                part, s = gate[:, m, ds(u * UNIT, UNIT)], sig[:, m % 2, :]
                                dve.wait_ge(sig_ready, n + 1)
                                st.then(nc.vector.tensor_scalar(s, s, U16, ROUND, ALU.mult, ALU.add))
                                st.then(nc.vector.tensor_scalar(s, s, ROUND, ROUND + U16 - 1.0, ALU.max, ALU.min))
                                st.then(nc.vector.scalar_tensor_tensor(out=part, in0=s, scalar=-ROUND, in1=part, op0=ALU.add, op1=ALU.mult))
                                nc.vector.reduce_max(act_max[:, ds(n, 1)], part, AX.X, apply_absolute_value=True).then_inc(tile_done, 1)
                            st.leave(NU)
            make_scales(core, "f1sa", [(sa, act_max[:])])

            with Layer(core, "f1u") as LU:
                up = LU.sb("up", [P, 2, UNIT])
                u_ps = [LU.ps(f"u_ps{s}", [P, BANK]) for s in range(2)]
                u_ready, u_out, g_out, up_free, steps = (LU.sem(n) for n in ("u_ready", "u_out", "g_out", "up_free", "steps"))
                with nc.Block() as block:

                    @block.tensor
                    def _(pe):
                        with pe.Fori(0, NU) as u:
                            for m in range(M):
                                pe.wait_ge(u_out, u * M + m + 1)
                                for k in range(KC):
                                    ins = nc.tensor.matmul(u_ps[m % 2][:, 0:UNIT], upT[:, k, m * P:(m + 1) * P],
                                                           xT[:, k, ds(u * UNIT, UNIT)], start=(k == 0), stop=(k == KC - 1))
                                ins.then_inc(u_ready, 1)

                    @block.scalar
                    def _(act):
                        act.sem_inc(u_out, 2)
                        with act.Fori(0, NU) as u:
                            for m in range(M):
                                n = u * M + m
                                part = gate[:, m, ds(u * UNIT, UNIT)]
                                nc.scalar.activation(part, part, ACT.Identity, bias=rounder[:], scale=sa.inverse[:]).then_inc(g_out, 1)
                                act.wait_ge(u_ready, n + 1)
                                act.nop(nofuse=True)
                                act.wait_ge(up_free, n + 1)
                                nc.scalar.activation(up[:, m % 2, :], u_ps[m % 2][:, 0:UNIT], ACT.Identity, bias=rounder[:],
                                                     scale=su.inverse[:]).then_inc(u_out, 1)

                    @block.vector
                    def _(dve):
                        st = Steps(dve, steps)
                        dve.sem_inc(up_free, 2)
                        with dve.Fori(0, NU) as u:
                            st.enter(u, 3 * M)
                            for m in range(M):
                                n = u * M + m
                                part, mine = gate[:, m, ds(u * UNIT, UNIT)], up[:, m % 2, :]
                                dve.wait_ge(g_out, n + 1)
                                nc.vector.tensor_scalar(part, part, ROUND + QMAX, ROUND - QMAX - 1.0, ALU.min, ALU.max)
                                dve.wait_ge(u_out, n + 3)
                                st.then(nc.vector.tensor_scalar(mine, mine, ROUND + QMAX, ROUND - QMAX - 1.0, ALU.min, ALU.max))
                                nc.vector.tensor_scalar(part, part, ROUND, sa.step[:], ALU.subtract, ALU.mult)
                                st.then(nc.vector.tensor_scalar(mine, mine, ROUND, su.step[:], ALU.subtract, ALU.mult))
                                st.then(nc.vector.tensor_tensor(part, part, mine, ALU.mult))
                                nc.vector.reduce_max(out_max[:, ds(n, 1)], part, AX.X, apply_absolute_value=True).then_inc(up_free, 1)
                            st.leave(NU)
        make_scales(core, "f1so", [(so, out_max[:])])

        with Layer(core, "f1d") as LD:
            q = LD.sb("q", [P, 2, M, UNIT])
            y_ps = [LD.ps(f"y_ps{s}", [TT, 2, BANK]) for s in range(2)]
            rounded, q_ready, y_ready, y_free, steps = (LD.sem(n) for n in ("rounded", "q_ready", "y_ready", "y_free", "steps"))
            with nc.Block() as block:

                @block.scalar
                def _(act):
                    with act.Fori(0, NU // 2) as i:
                        for s in range(2):
                            u = i * 2 + s
                            act.wait_ge(y_free, u + 1)
                            act.nop(nofuse=True)
                            nc.scalar.activation(q[:, s, :, :], gate[:, :, ds(u * UNIT, UNIT)], ACT.Identity, bias=rounder[:],
                                                 scale=so.inverse[:]).then_inc(rounded, 1)

                @block.tensor
                def _(pe):
                    with pe.Fori(0, NU // 2) as i:
                        for s in range(2):
                            u = i * 2 + s
                            pe.wait_ge(q_ready, u + 1)
                            for t in range(UT):
                                for m in range(M):
                                    ins = nc.tensor.matmul(y_ps[s][:, t // 2, (t % 2) * C:(t % 2 + 1) * C],
                                                           q[:, s, m, t * TT:(t + 1) * TT], downT[:, m, :],
                                                           start=(m == 0), stop=(m == M - 1))
                            ins.then_inc(y_ready, 1)

                @block.vector
                def _(dve):
                    st = Steps(dve, steps)
                    dve.sem_inc(y_free, 2)

                    def quantise(u, s):
                        dve.wait_ge(rounded, u + 1)
                        st.then(nc.vector.tensor_scalar(q[:, s, :, :], q[:, s, :, :], ROUND + QMAX, ROUND - QMAX - 1.0, ALU.min, ALU.max))
                        nc.vector.tensor_scalar(q[:, s, :, :], q[:, s, :, :], ROUND, so.step[:], ALU.subtract, ALU.mult).then_inc(q_ready, 1)

                    def add(u, s):
                        dve.wait_ge(y_ready, u + 1)
                        nc.vector.tensor_tensor(h[:, ds(u * UT, UT), :], y_ps[s][:, :, :].rearrange("p a (b c) -> p (a b) c", c=C),
                                                h[:, ds(u * UT, UT), :], ALU.add).then_inc(y_free, 1)

                    quantise(0, 0)
                    with dve.Fori(0, NU // 2 - 1) as i:
                        st.enter(i, 2)
                        for s in range(2):
                            quantise(i * 2 + s + 1, (s + 1) % 2)
                            add(i * 2 + s, s)
                        st.leave(NU // 2 - 1)
                    quantise(NU - 1, 1)
                    add(NU - 2, 0)
                    add(NU - 1, 1)


def recurrent_mix(core):
    nc, h, d = core.nc, core.h, core.dram
    HN, MIX, TM, TD = 16, 5, 32, 64
    G = C // P * HN // 2
    GN_EPS = 1e-5 * 64
    with Layer(core, "m1") as L:
        xT = L.sb("xT", [P, KC, TOK])
        layer_norm(core, "m1ln", xT)
        w1 = L.sb("w1", [P, KC, MIX * TM])
        w2a = L.sb("w2a", [P, C])
        w2b = L.sb("w2b", [TM, C])
        mx = L.sb("mx", [P, KC])
        mf = L.sb("mf", [P, MIX, KC])
        tdecay = L.sb("tdecay", [P, KC])
        td1 = L.sb("td1", [P, KC, TD])
        td2 = L.sb("td2", [TD, C])
        bonus = L.sb("bonus", [P, KC])
        wr, wk, wv, wg, wo = (L.sb(n, [P, KC, C]) for n in ("wr", "wk", "wv", "wg", "wo"))
        ln_w = L.sb("ln_w", [P, KC])
        ln_b = L.sb("ln_b", [P, KC])
        spread = L.sb("spread", [P, HN, P])
        gather = L.sb("gather", [P, HN, P])
        same = L.sb("same", [P, P])
        mean16 = L.sb("mean16", [P, P])
        xs = L.sb("xs", [P, KC, SEQ + 1])
        xx = L.sb("xx", [P, KC, SEQ])
        xxx = L.sb("xxx", [P, KC, SEQ])
        t5 = L.sb("t5", [P, 2, SEQ])
        mixed = L.sb("mixed", [P, 2, KC, SEQ])
        xf = L.sb("xf", [P, MIX, KC, SEQ])
        tw = L.sb("tw", [TD, SEQ])
        decay = L.sb("decay", [P, KC, SEQ])
        r, k, v, g = (L.sb(n, [P, KC, SEQ]) for n in ("r", "k", "v", "g"))
        ruk = L.sb("ruk", [P, KC, SEQ])
        yu = L.sb("yu", [P, KC, SEQ])
        kv = L.sb("kv", [P, 2, 2, SEQ])
        S = L.sb("S", [P, 2, 2, SEQ + 1])
        rS = L.sb("rS", [P, 2, 2, SEQ])
        y = L.sb("y", [P, KC, SEQ])
        square = L.sb("square", [P, KC, SEQ])
        gn_eps = L.sb("gn_eps", [P, 1])
        pr = [L.ps(f"pr{s}", [P, KC, BANK // 2]) for s in range(3)]
        vrep = [L.ps(f"vrep{s}", [P, 2, BANK // 2]) for s in range(2)]
        y_ps = L.ps("y_ps", [P, KC, BANK // 2])
        aux = L.ps("aux", [P, KC, BANK // 2])
        out_ps = L.ps("out_ps", [TT, 2, C])
        names = ("loaded const xs_ready xxx_ready pr_ready act_ev dve_ev xf_ready d_ready ruk_ready yu_ready vrep_ready "
                 "S_ready rS_ready y_part y_ready mean_ready yc_ready sq_ready var_ready std_ready z_ready "
                 "out_ready turn_done steps").split()
        (loaded, const, xs_ready, xxx_ready, pr_ready, act_ev, dve_ev, xf_ready, d_ready, ruk_ready, yu_ready, vrep_ready,
         S_ready, rS_ready, y_part, y_ready, mean_ready, yc_ready, sq_ready, var_ready, std_ready, z_ready,
         out_ready, turn_done, steps) = (L.sem(n) for n in names)
        loads = [(w1, "m1_w1"), (w2a, "m1_w2a"), (w2b, "m1_w2b"), (mx, "m1_mx"), (mf, "m1_mf"), (tdecay, "m1_tdecay"),
                 (td1, "m1_td1"), (td2, "m1_td2"), (bonus, "m1_bonus"), (wr, "m1_wr"), (wk, "m1_wk"), (wv, "m1_wv"),
                 (wg, "m1_wg"), (wo, "m1_wo"), (ln_w, "m1_lnw"), (ln_b, "m1_lnb"), (spread, "m1_spread"),
                 (gather, "m1_gather"), (same, "m1_same")]
        all_loaded = 16 * len(loads)

        with nc.Block() as block:

            @block.sync
            def _(sp):
                for dst, name in loads:
                    sp.dma_start(dst[:], d[name]).then_inc(loaded, 16)

            @block.gpsimd
            def _(pool):
                pool.wait_ge(loaded, all_loaded)
                nc.gpsimd.memset(xs[:], 0.0)
                nc.gpsimd.memset(S[:], 0.0)
                nc.gpsimd.memset(gn_eps[:], GN_EPS)
                nc.gpsimd.tensor_scalar(mean16[:], same[:], 1.0 / HN, None, ALU.mult).then_inc(const, 1)
                pool.wait_ge(const, 1)
                with pool.Fori(0, SEQS) as b:
                    pool.wait_ge(turn_done, b + 1)
                    nc.gpsimd.tensor_copy(xs[:, :, 1:SEQ + 1], xT[:, :, ds(b * SEQ, SEQ)]).then_inc(xs_ready, 1)
                    pool.wait_ge(xs_ready, b + 1)
                    for f in range(MIX):
                        pool.wait_ge(dve_ev, b * MIX + f + 1)
                        nc.gpsimd.tensor_tensor(xf[:, f, :, :], mixed[:, f % 2, :, :], xs[:, :, 1:SEQ + 1],
                                                ALU.add).then_inc(xf_ready, 1)
                    pool.wait_ge(act_ev, b * 7 + 6)
                    for n in range(G):
                        c = n // (HN // 2)
                        pool.wait_ge(S_ready, b * G + n + 1)
                        if n >= 2:
                            pool.nop(nofuse=True)
                            pool.wait_ge(y_part, b * G + n - 1)
                        nc.gpsimd.tensor_tensor(rS[:, n % 2, :, :], S[:, n % 2, :, 0:SEQ],
                                                r[:, c:c + 1, :].broadcast_to([P, 2, SEQ]), ALU.mult).then_inc(rS_ready, 1)

            @block.tensor
            def _(pe):
                pe.wait_ge(const, 1)
                with pe.Fori(0, SEQS) as b:

                    def project(n, lhs, rhs, rows=P):
                        for c in range(len(lhs)):
                            for i in range(len(rhs)):
                                ins = nc.tensor.matmul(pr[n % 3][0:rows, c, 0:SEQ], lhs[c][i], rhs[i],
                                                       start=(i == 0), stop=(i == len(rhs) - 1))
                        ins.then_inc(pr_ready, 1)

                    def weights(w):
                        return [[w[:, i, c * P:(c + 1) * P] for i in range(KC)] for c in range(KC)]

                    def stream(f):
                        return [xf[:, f, i, :] for i in range(KC)]

                    pe.wait_ge(xxx_ready, b + 1)
                    for i in range(KC):
                        nc.tensor.matmul(pr[0][:, 0, 0:SEQ], w1[:, i, 0:4 * TM], xxx[:, i, :], start=(i == 0), stop=(i == KC - 1))
                    for i in range(KC):
                        ins = nc.tensor.matmul(pr[0][0:TM, 1, 0:SEQ], w1[:, i, 4 * TM:], xxx[:, i, :], start=(i == 0), stop=(i == KC - 1))
                    ins.then_inc(pr_ready, 1)
                    pe.wait_ge(act_ev, b * 7 + 1)
                    for f in range(MIX):
                        if f >= 3:
                            pe.wait_ge(dve_ev, b * MIX + f - 2)
                        rows = slice(TM * f, TM * f + TM)
                        lhs = [[(w2a[rows, c * P:(c + 1) * P] if f < 4 else w2b[:, c * P:(c + 1) * P])] for c in range(KC)]
                        project(f + 1, lhs, [t5[rows, 0, :] if f < 4 else t5[0:TM, 1, :]])
                    pe.wait_ge(xf_ready, b * MIX + 1)
                    pe.nop(nofuse=True)
                    pe.wait_ge(dve_ev, b * MIX + 3)
                    project(6, [[td1[:, i, :] for i in range(KC)]], stream(0), rows=TD)
                    pe.wait_ge(dve_ev, b * MIX + 4)
                    pe.nop(nofuse=True)
                    pe.wait_ge(xf_ready, b * MIX + 2)
                    project(7, weights(wk), stream(1))
                    pe.wait_ge(dve_ev, b * MIX + 5)
                    pe.nop(nofuse=True)
                    pe.wait_ge(act_ev, b * 7 + 2)
                    project(8, [[td2[:, c * P:(c + 1) * P]] for c in range(KC)], [tw[:]])
                    pe.wait_ge(xf_ready, b * MIX + 3)
                    project(9, weights(wv), stream(2))
                    pe.wait_ge(xf_ready, b * MIX + 4)
                    pe.nop(nofuse=True)
                    pe.wait_ge(act_ev, b * 7 + 3)
                    project(10, weights(wr), stream(3))
                    pe.wait_ge(xf_ready, b * MIX + 5)
                    pe.nop(nofuse=True)
                    pe.wait_ge(act_ev, b * 7 + 4)
                    project(11, weights(wg), stream(4))
                    pe.wait_ge(act_ev, b * 7 + 5)

                    def spread_v(n):
                        c, j = n // (HN // 2), 2 * (n % (HN // 2))
                        if n >= 2:
                            pe.wait_ge(S_ready, b * G + n - 1)
                        for s in range(2):
                            ins = nc.tensor.matmul(vrep[n % 2][:, s, 0:SEQ], spread[:, j + s, :], v[:, c, :], start=True, stop=True)
                        ins.then_inc(vrep_ready, 1)

                    def sum_i(n):
                        c, j = n // (HN // 2), 2 * (n % (HN // 2))
                        pe.wait_ge(rS_ready, b * G + n + 1)
                        for s in range(2):
                            ins = nc.tensor.matmul(y_ps[:, c, 0:SEQ], gather[:, j + s, :], rS[:, n % 2, s, :],
                                                   start=(j + s == 0), stop=(j + s == HN - 1))
                        ins.then_inc(y_part, 1)

                    for n in range(G + 2):
                        if n < G:
                            spread_v(n)
                        if n == 1:
                            pe.wait_ge(ruk_ready, b + 1)
                            for c in range(KC):
                                ins = nc.tensor.matmul(aux[:, c, 0:SEQ], same[:], ruk[:, c, :], start=True, stop=True)
                            ins.then_inc(yu_ready, 1)
                        if n >= 2:
                            sum_i(n - 2)
                    pe.wait_ge(y_ready, b + 1)
                    for c in range(KC):
                        ins = nc.tensor.matmul(aux[:, c, 0:SEQ], mean16[:], y[:, c, :], start=True, stop=True)
                    ins.then_inc(mean_ready, 1)
                    pe.wait_ge(sq_ready, b + 1)
                    for c in range(KC):
                        ins = nc.tensor.matmul(aux[:, c, 0:SEQ], mean16[:], square[:, c, :], start=True, stop=True)
                    ins.then_inc(var_ready, 1)
                    pe.wait_ge(z_ready, b + 1)
                    for a in range(2):
                        for i in range(KC):
                            ins = nc.tensor.matmul(out_ps[:, a, :], y[:, i, a * TT:(a + 1) * TT], wo[:, i, :],
                                                   start=(i == 0), stop=(i == KC - 1))
                    ins.then_inc(out_ready, 1)

            @block.scalar
            def _(act):
                act.wait_ge(const, 1)
                with act.Fori(0, SEQS) as b:
                    act.wait_ge(pr_ready, b * 12 + 1)
                    nc.scalar.activation(t5[:, 0, :], pr[0][:, 0, 0:SEQ], ACT.Tanh)
                    nc.scalar.activation(t5[0:TM, 1, :], pr[0][0:TM, 1, 0:SEQ], ACT.Tanh).then_inc(act_ev, 1)
                    act.wait_ge(pr_ready, b * 12 + 7)
                    nc.scalar.activation(tw[:], pr[0][0:TD, 0, 0:SEQ], ACT.Tanh).then_inc(act_ev, 1)
                    act.wait_ge(pr_ready, b * 12 + 8)
                    nc.scalar.copy(k[:], pr[1][:, :, 0:SEQ]).then_inc(act_ev, 1)
                    act.wait_ge(pr_ready, b * 12 + 9)
                    for c in range(KC):
                        ins = nc.scalar.activation(decay[:, c, :], pr[2][:, c, 0:SEQ], ACT.Exp, bias=tdecay[:, c:c + 1])
                    ins.then_inc(act_ev, 1)
                    act.wait_ge(act_ev, b * 7 + 4)
                    nc.scalar.activation(decay[:], decay[:], ACT.Exp, scale=-1.0).then_inc(d_ready, 1)
                    act.wait_ge(pr_ready, b * 12 + 10)
                    nc.scalar.copy(v[:], pr[0][:, :, 0:SEQ]).then_inc(act_ev, 1)
                    act.wait_ge(pr_ready, b * 12 + 11)
                    nc.scalar.copy(r[:], pr[1][:, :, 0:SEQ]).then_inc(act_ev, 1)
                    act.wait_ge(pr_ready, b * 12 + 12)
                    nc.scalar.activation(g[:], pr[2][:, :, 0:SEQ], ACT.Silu).then_inc(act_ev, 1)
                    act.wait_ge(yc_ready, b + 1)
                    nc.scalar.activation(square[:], y[:], ACT.Square).then_inc(sq_ready, 1)
                    act.wait_ge(var_ready, b + 1)
                    nc.scalar.activation(square[:], aux[:, :, 0:SEQ], ACT.Sqrt, bias=gn_eps[:]).then_inc(std_ready, 1)

            @block.vector
            def _(dve):
                st = Steps(dve, steps)
                V = nc.vector
                dve.wait_ge(const, 1)
                dve.sem_inc(turn_done, 1)
                with dve.Fori(0, SEQS) as b:
                    st.enter(b, 1 + G + 3)
                    dve.wait_ge(xs_ready, b + 1)
                    st.then(V.tensor_tensor(xx[:], xs[:, :, 0:SEQ], xs[:, :, 1:SEQ + 1], ALU.subtract))
                    for c in range(KC):
                        ins = V.scalar_tensor_tensor(out=xxx[:, c, :], in0=xx[:, c, :], scalar=mx[:, c:c + 1],
                                                     in1=xs[:, c, 1:SEQ + 1], op0=ALU.mult, op1=ALU.add)
                    ins.then_inc(xxx_ready, 1)
                    for f in range(MIX):
                        dve.wait_ge(pr_ready, b * 12 + f + 2)
                        if f >= 2:
                            dve.nop(nofuse=True)
                            dve.wait_ge(xf_ready, b * MIX + f - 1)
                        for c in range(KC):
                            ins = V.scalar_tensor_tensor(out=mixed[:, f % 2, c, :], in0=pr[(f + 1) % 3][:, c, 0:SEQ],
                                                         scalar=mf[:, f, c:c + 1], in1=xx[:, c, :], op0=ALU.add, op1=ALU.mult)
                        ins.then_inc(dve_ev, 1)
                    dve.wait_ge(act_ev, b * 7 + 6)
                    for c in range(KC):
                        ins = V.scalar_tensor_tensor(out=ruk[:, c, :], in0=r[:, c, :], scalar=bonus[:, c:c + 1],
                                                     in1=k[:, c, :], op0=ALU.mult, op1=ALU.mult)
                    ins.then_inc(ruk_ready, 1)
                    dve.wait_ge(d_ready, b + 1)
                    for n in range(G):
                        c = n // (HN // 2)
                        dve.wait_ge(vrep_ready, b * G + n + 1)
                        st.then(V.tensor_tensor(kv[:, n % 2, :, :], vrep[n % 2][:, :, 0:SEQ],
                                                k[:, c:c + 1, :].broadcast_to([P, 2, SEQ]), ALU.mult))
                        if n >= 2:
                            dve.nop(nofuse=True)
                            dve.wait_ge(rS_ready, b * G + n - 1)
                            dve.nop(nofuse=True)
                        for s in range(2):
                            ins = V.tensor_tensor_scan(S[:, n % 2, s, 1:SEQ], decay[:, c, 0:SEQ - 1], kv[:, n % 2, s, 0:SEQ - 1],
                                                       0.0, ALU.mult, ALU.add)
                        ins.then_inc(S_ready, 1)
                        if n == 3:
                            dve.wait_ge(yu_ready, b + 1)
                            V.tensor_tensor(yu[:], aux[:, :, 0:SEQ], v[:], ALU.mult)
                    dve.wait_ge(y_part, (b + 1) * G)
                    V.tensor_tensor(y[:], y_ps[:, :, 0:SEQ], yu[:], ALU.add).then_inc(y_ready, 1)
                    dve.wait_ge(mean_ready, b + 1)
                    V.tensor_tensor(y[:], y[:], aux[:, :, 0:SEQ], ALU.subtract).then_inc(yc_ready, 1)
                    dve.wait_ge(std_ready, b + 1)
                    st.then(V.reciprocal(square[:], square[:]))
                    st.then(V.tensor_tensor(y[:], y[:], square[:], ALU.mult))
                    for c in range(KC):
                        ins = V.tensor_scalar(y[:, c, :], y[:, c, :], ln_w[:, c:c + 1], ln_b[:, c:c + 1], ALU.mult, ALU.add)
                    st.then(ins)
                    dve.nop(nofuse=True)
                    dve.wait_ge(act_ev, (b + 1) * 7)
                    V.tensor_tensor(y[:], y[:], g[:], ALU.mult).then_inc(z_ready, 1)
                    dve.wait_ge(out_ready, b + 1)
                    V.tensor_tensor(h[:, ds(b * 2, 2), :], out_ps[:], h[:, ds(b * 2, 2), :], ALU.add).then_inc(turn_done, 1)
                    st.leave(SEQS)


LAYERS = [token_patches, taylor_attention, top1_experts, recurrent_mix, quantised_mlp, softmax_attention, grouped_experts, long_convolution, top2_experts]


def tower(nc, dram, out):
    with ExitStack() as ctx:
        core = Core(nc, ctx, dram)
        constants(core)
        for layer in LAYERS:
            layer(core)
        store_stream(core, out)


def layouts(a):
    import numpy as np

    def cm(w):
        return w.reshape(-1, P, w.shape[-1]).transpose(1, 0, 2)

    def flat(w):
        return w.reshape(w.shape[0], -1)

    def columns(b):
        return b.reshape(-1, P).T

    def up(w):
        return w.reshape(w.shape[0], KC, P, -1).transpose(0, 2, 1, 3).reshape(w.shape[0], P, -1)

    def down(w):
        return w.reshape(w.shape[0], -1, P, w.shape[2]).transpose(0, 2, 1, 3).reshape(w.shape[0], P, -1)

    def bias(b):
        return b.reshape(b.shape[0], -1, P).transpose(0, 2, 1)

    d = {}
    patch = 16
    d["tok_x"] = a["x"].reshape(-1, patch).T
    d["tok_wh"] = a["L0_tok_W_h"].T
    d["tok_bh"] = columns(a["L0_tok_b_h"])
    d["tok_wo"] = cm(a["L0_tok_W_o"].T)
    d["tok_wr"] = np.concatenate([a["L0_tok_W_r"].T, a["L0_tok_b_r"][None], a["L0_tok_b_o"][None]])
    d["f0_wg"] = cm(a["L0_ffn_Wg"])
    d["f0_bg"] = a["L0_ffn_bg"][:, None]
    d["f0_w1"] = up(a["L0_ffn_W1"])
    d["f0_b1"] = bias(a["L0_ffn_b1"])
    d["f0_w2"] = down(a["L0_ffn_W2"])
    d["f0_b2"] = a["L0_ffn_b2"]
    d["f2_wg"] = cm(a["L2_ffn_gate_w"].T)
    d["f2_bias"] = a["L2_ffn_bias_e"][None]
    d["f2_w1"] = up(a["L2_ffn_up_w"].transpose(0, 2, 1))
    d["f2_w2"] = down(a["L2_ffn_down_w"].transpose(0, 2, 1))
    d["f2_s1"] = up(a["L2_ffn_shared_up"].T[None])
    d["f2_s2"] = down(a["L2_ffn_shared_down"].T[None])
    d["f3_wg"] = cm(a["L3_ffn_router_w"].T)
    d["f3_w1"] = up(a["L3_ffn_w1"].transpose(0, 2, 1))
    d["f3_b1"] = bias(a["L3_ffn_b1"])
    d["f3_w2"] = down(a["L3_ffn_w2"].transpose(0, 2, 1))
    d["f3_b2"] = a["L3_ffn_b2"]
    def spread(w):
        heads = w.reshape(w.shape[:-1] + (-1, 16))
        return np.concatenate([heads, np.zeros_like(heads)], -1).reshape(w.shape[:-1] + (-1,))

    for n in ("q", "k"):
        d["a2_w" + n] = cm(spread(a["L2_attn_W" + n].T))
        d["a2_b" + n] = columns(spread(a["L2_attn_b" + n]))
    for n in ("v", "o"):
        d["a2_w" + n] = cm(a["L2_attn_W" + n].T)
        d["a2_b" + n] = a["L2_attn_b" + n][None]
    def spread(w):
        heads = w.reshape(w.shape[:-1] + (-1, 16))
        return np.concatenate([heads, np.zeros_like(heads)], -1).reshape(w.shape[:-1] + (-1,))

    d["a0_gamma"] = columns(a["L0_attn_gamma"])
    d["a0_wq"] = cm(spread(a["L0_attn_w_q"]))
    kv = a["L0_attn_w_kv"]
    d["a0_wk"], d["a0_wv"] = cm(spread(kv[:, :kv.shape[1] // 2])), cm(kv[:, kv.shape[1] // 2:])
    d["a0_wo"] = a["L0_attn_w_out"]
    d["a3_lre"], d["a3_lim"] = a["L3_attn_Lambda_real"][:, None], a["L3_attn_Lambda_imag"][:, None]
    d["a3_cre"], d["a3_cim"] = a["L3_attn_C_real"].T, a["L3_attn_C_imag"].T
    d["a3_gain"], d["a3_shift"], d["a3_skip"] = (a["L3_attn_" + n][None] for n in ("ln_gamma", "ln_beta", "param_D"))
    f, t = np.arange(SEQ)[:, None], np.arange(SEQ)[None, :]
    turn = np.pi * ((f * t) % (2 * SEQ)) / SEQ
    sines = np.sin(turn)
    sines[0] = np.cos(np.pi * t[0])
    waves = np.concatenate([np.cos(turn), sines])
    weight = np.full((2, SEQ, 1), 2.0)
    weight[:, 0] = 1.0
    d["a3_F"] = waves.T.reshape(2, TT, 2 * SEQ).transpose(1, 0, 2).astype(np.float32)
    d["a3_G"] = (waves * weight.reshape(-1, 1) / (2 * SEQ)).reshape(4, TT, SEQ).transpose(1, 0, 2).astype(np.float32)
    d["f1_gate"], d["f1_up"], d["f1_down"] = (cm(a["L1_ffn_w_" + n]) for n in ("gate", "up", "down"))
    m = {n[len("L1_attn_"):]: v for n, v in a.items() if n.startswith("L1_attn_")}
    d["m1_w1"] = cm(m["time_maa_w1"])
    w2 = m["time_maa_w2"]
    d["m1_w2a"], d["m1_w2b"] = w2[:4].reshape(P, C), w2[4]
    d["m1_mx"] = columns(m["time_maa_x"].reshape(-1))
    d["m1_mf"] = np.stack([columns(m["time_maa_" + f].reshape(-1)) for f in "wkvrg"], 1)
    d["m1_tdecay"], d["m1_bonus"] = columns(m["time_decay"].reshape(-1)), columns(m["time_faaaa"].reshape(-1))
    d["m1_td1"], d["m1_td2"] = cm(m["time_decay_w1"]), m["time_decay_w2"]
    for n in "rkvgo":
        d["m1_w" + n] = cm(m["W_" + n])
    d["m1_lnw"], d["m1_lnb"] = columns(m["ln_w"]), columns(m["ln_b"])
    ch = np.arange(P)
    same = (ch[:, None] // 16 == ch[None, :] // 16)
    spread01 = (same[:, None, :] & (ch[:, None, None] % 16 == np.arange(16)[None, :, None])).astype(np.float32)
    d["m1_spread"], d["m1_gather"] = spread01, spread01.transpose(2, 1, 0)
    d["m1_same"] = same.astype(np.float32)
    return {n: np.ascontiguousarray(v) for n, v in d.items()}


def kernel(**inputs):
    import numpy as _np
    import concourse.bacc as _bacc
    from concourse import mybir as _mybir
    from concourse.bass_utils import run_bass_kernel_spmd as _run

    nc = _bacc.Bacc("TRN2", target_bir_lowering=False, num_devices=1)
    arrays, dram = {}, {}
    for name, a in layouts(inputs).items():
        arrays[f"in_{name}_dram"] = a
        dram[name] = nc.dram_tensor(f"in_{name}_dram", a.shape, _mybir.dt.from_np(a.dtype), kind="ExternalInput").ap()
    out = nc.dram_tensor("out_0_dram", (SEQS, SEQ, C), _mybir.dt.float32, kind="ExternalOutput").ap()
    tower(nc, dram, out)
    r = _run(nc, [arrays], core_ids=[0])
    return r.results[0]["out_0_dram"]
```

```python
from contextlib import ExitStack

import concourse.bass as bass
from concourse import mybir

F32 = mybir.dt.float32
I32 = mybir.dt.int32
BF16 = mybir.dt.bfloat16
ACT = mybir.ActivationFunctionType
ALU = mybir.AluOpType
AX = mybir.AxisListType
ds = bass.ds

SEQS = 16
SEQ = 250
C = 256
P = 128
KC = C // P
TT = 125
NT = SEQS * SEQ // TT
UT = 4
UNIT = UT * TT
NU = NT // UT
TOK = SEQS * SEQ
BANK = 512
LN_EPS = 1e-5


class Steps:

    def __init__(self, eng, sem):
        self.eng, self.sem, self.base, self.k, self.turn, self.per = eng, sem, 0, 0, None, 0

    def then(self, ins):
        ins.then_inc(self.sem, 1)
        self.k += 1
        value = self.base + self.k
        self.eng.wait_ge(self.sem, value if self.turn is None else self.turn * self.per + value)

    def enter(self, turn, per):
        self.base += self.k
        self.k, self.turn, self.per = 0, turn, per

    def leave(self, turns):
        assert self.k == self.per, (self.k, self.per)
        self.base += self.per * turns
        self.k, self.turn = 0, None


class Core:

    def __init__(self, nc, ctx, dram):
        self.nc, self.ctx, self.dram = nc, ctx, dram
        self.h = ctx.enter_context(nc.sbuf_tensor("h", [TT, NT, C], F32))
        self.ident = ctx.enter_context(nc.sbuf_tensor("ident", [P, P], F32))


class Layer:

    def __init__(self, core, name):
        self.core, self.nc, self.name, self.stack = core, core.nc, name, ExitStack()
        self.sems = []

    def __enter__(self):
        self.stack.__enter__()
        return self

    def __exit__(self, *a):
        if self.sems and a[0] is None:
            with self.nc.Block() as block:

                @block.gpsimd
                def _(pool):
                    for sem in self.sems:
                        pool.sem_clear(sem)
        return self.stack.__exit__(*a)

    def sb(self, name, shape, dt=F32):
        return self.stack.enter_context(self.nc.sbuf_tensor(f"{self.name}_{name}", shape, dt))

    def ps(self, name, shape, dt=F32):
        return self.stack.enter_context(self.nc.psum_tensor(f"{self.name}_{name}", shape, dt))

    def sem(self, name):
        self.sems.append(self.stack.enter_context(self.nc.semaphore(f"{self.name}_{name}")))
        return self.sems[-1]

    def pool_dma_sem(self, name):
        return self.core.ctx.enter_context(self.nc.semaphore(f"{self.name}_{name}"))


def constants(core):
    nc, ident = core.nc, core.ident
    with Layer(core, "const") as L:
        filled = L.sem("filled")
        with nc.Block() as block:

            @block.gpsimd
            def _(pool):
                nc.gpsimd.memset(ident[:], 0.0).then_inc(filled, 1)
                pool.wait_ge(filled, 1)
                nc.gpsimd.affine_select(out=ident[:], in_=ident[:], compare_op=ALU.not_equal, fill=1.0,
                                        base=0, pattern=[[-1, P]], channel_multiplier=1)


def store_stream(core, dst):
    nc = core.nc
    with Layer(core, "out") as L:
        stored = L.sem("stored")
        with nc.Block() as block:

            @block.sync
            def _(sp):
                sp.dma_start(dst.rearrange("b (s p) c -> p (b s) c", p=TT), core.h[:]).then_inc(stored, 16)
                sp.wait_ge(stored, 16)


def layer_norm(core, name, xT, rms_gain=None, keep=None):
    nc, h, ident = core.nc, core.h, core.ident
    with Layer(core, name) as L:
        stats = L.sb("stats", [TT, 2, UT, 6])
        moments = L.sb("moments", [TT, 2, UT, 2])
        eps_var = L.sb("eps_var", [TT, 2, UT])
        power = L.sb("power", [TT, UT])
        rstd = L.sb("rstd", [TT, 2, UT])
        xn = L.sb("xn", [TT, 2, UT, C])
        square = L.sb("square", [TT, UT, C])
        norm2 = L.sb("norm2", [TT, 2, UT])
        rnorm = L.sb("rnorm", [TT, 2, UT])
        turned = [L.ps(f"turned{s}", [P, KC, BANK]) for s in range(2)]
        steps = L.sem("steps")
        power_set = L.sem("power_set")
        var_ready = L.sem("var_ready")
        rstd_ready = L.sem("rstd_ready")
        norm_ready = L.sem("norm_ready")
        rnorm_ready = L.sem("rnorm_ready")
        xn_ready = L.sem("xn_ready")
        xn_free = L.sem("xn_free")
        out_ready = L.sem("out_ready")
        kept = L.sem("kept")
        rms = rms_gain is not None

        with nc.Block() as block:

            @block.vector
            def _(dve):
                st = Steps(dve, steps)
                nc.vector.memset(power[:], -0.5).then_inc(power_set, 1)

                def measure(u, s):
                    for t in range(UT):
                        ins = nc.vector.bn_stats(stats[:, s, t, :], h[:, ds(u * UT + t, 1), :])
                    st.then(ins)
                    dve.nop(nofuse=True)
                    for t in range(UT):
                        ins = nc.vector.bn_aggr(moments[:, s, t, :], stats[:, s, t, :])
                    st.then(ins)
                    nc.vector.tensor_scalar(eps_var[:, s, :], moments[:, s, :, 1], LN_EPS, None,
                                            ALU.add).then_inc(var_ready, 1)

                def normalise(u, s):
                    dve.wait_ge(rstd_ready, u + 1)
                    dve.nop(nofuse=True)
                    dve.wait_ge(xn_free, u + 1)
                    if keep is not None:
                        dve.nop(nofuse=True)
                        dve.wait_ge(kept, u + 1)
                    for t in range(UT):
                        ins = nc.vector.tensor_scalar(xn[:, s, t, :], h[:, ds(u * UT + t, 1), :].rearrange("p a c -> p (a c)"),
                                                      moments[:, s, t, 0:1], rstd[:, s, t:t + 1],
                                                      ALU.subtract, ALU.mult)
                    if rms:
                        st.then(ins)
                        st.then(nc.vector.tensor_tensor(square[:], xn[:, s, :, :], xn[:, s, :, :], ALU.mult))
                        st.then(nc.vector.reduce_sum(norm2[:, s, :], square[:], AX.X))
                        nc.vector.tensor_scalar(norm2[:, s, :], norm2[:, s, :], 1e-24, None,
                                                ALU.max).then_inc(norm_ready, 1)
                        dve.wait_ge(rnorm_ready, u + 1)
                        for t in range(UT):
                            ins = nc.vector.tensor_scalar(xn[:, s, t, :], xn[:, s, t, :], rnorm[:, s, t:t + 1],
                                                          float(C) ** 0.5, ALU.mult, ALU.mult)
                    ins.then_inc(xn_ready, 1)

                measure(0, 0)
                with dve.Fori(0, NU // 2 - 1) as i:
                    st.enter(i, 2 * (2 + (3 if rms else 0)))
                    for s in range(2):
                        measure(i * 2 + s + 1, 1 - s)
                        normalise(i * 2 + s, s)
                    st.leave(NU // 2 - 1)
                measure(NU - 1, 1)
                normalise(NU - 2, 0)
                normalise(NU - 1, 1)

            @block.gpsimd
            def _(pool):
                pool.wait_ge(power_set, 1)
                if keep is not None:
                    pool.sem_inc(kept, 2)
                with pool.Fori(0, NU // 2) as i:
                    for s in range(2):
                        u = i * 2 + s
                        pool.wait_ge(var_ready, u + 1)
                        nc.gpsimd.tensor_tensor(rstd[:, s, :], eps_var[:, s, :], power[:], ALU.pow).then_inc(rstd_ready, 1)
                        if rms:
                            pool.wait_ge(norm_ready, u + 1)
                            nc.gpsimd.tensor_tensor(rnorm[:, s, :], norm2[:, s, :], power[:], ALU.pow).then_inc(rnorm_ready, 1)
                        if keep is not None:
                            pool.wait_ge(xn_ready, u + 1)
                            nc.gpsimd.tensor_copy(keep[:, ds(u * UT, UT), :], xn[:, s, :, :]).then_inc(kept, 1)

            @block.tensor
            def _(pe):
                pe.sem_inc(xn_free, 2)
                with pe.Fori(0, NU // 2) as i:
                    for s in range(2):
                        u = i * 2 + s
                        pe.wait_ge(xn_ready, u + 1)
                        pe.wait_ge(out_ready, u + 1)
                        for t in range(UT):
                            for k in range(KC):
                                ins = nc.tensor.transpose(turned[s][:, k, t * TT:(t + 1) * TT],
                                                          xn[:, s, t, k * P:(k + 1) * P], ident[0:TT, 0:TT])
                        ins.then_inc(xn_free, 1)

            @block.scalar
            def _(act):
                act.sem_inc(out_ready, 2)
                with act.Fori(0, NU // 2) as i:
                    for s in range(2):
                        u = i * 2 + s
                        act.wait_ge(xn_free, u + 3)
                        for k in range(KC):
                            if rms:
                                ins = nc.scalar.activation(xT[:, k, ds(u * UNIT, UNIT)], turned[s][:, k, 0:UNIT],
                                                           ACT.Copy, scale=rms_gain[:, k:k + 1])
                            else:
                                ins = nc.scalar.activation(xT[:, k, ds(u * UNIT, UNIT)], turned[s][:, k, 0:UNIT], ACT.Copy)
                        ins.then_inc(out_ready, 1)


def token_patches(core):
    nc, h, dram = core.nc, core.h, core.dram
    hid_w, hid_tiles = dram["tok_wh"].shape[1], dram["tok_wh"].shape[1] // P
    pa, rows, mrows = dram["tok_x"].shape[0], dram["tok_wr"].shape[0], dram["tok_wh"].shape[0]
    with Layer(core, "tok") as L:
        patch = L.sb("patch", [rows, TOK])
        unit = L.sb("unit", [rows, 2, UNIT])
        wh = L.sb("wh", [mrows, hid_w])
        bh = L.sb("bh", [P, hid_tiles])
        wo = L.sb("wo", [P, hid_tiles, C])
        wr = L.sb("wr", [rows, C])
        hid = L.sb("hid", [P, 2, hid_tiles, UNIT])
        hid_ps = [L.ps(f"hid_ps{s}", [P, BANK]) for s in range(4)]
        y_ps = [L.ps(f"y_ps{s}", [TT, UT // 2, BANK]) for s in range(2)]
        ones_set = L.sem("ones_set")
        loaded = L.sem("loaded")
        unit_ready = L.sem("unit_ready")
        hid_ready = L.sem("hid_ready")
        hid_done = L.sem("hid_done")
        y_ready = L.sem("y_ready")
        y_free = L.sem("y_free")
        with nc.Block() as block:

            @block.sync
            def _(sp):
                sp.wait_ge(ones_set, 1)
                for dst, src in ((patch[0:pa, :], dram["tok_x"]), (wh[:], dram["tok_wh"]), (bh[:], dram["tok_bh"]),
                                 (wo[:], dram["tok_wo"]), (wr[:], dram["tok_wr"])):
                    sp.dma_start(dst, src).then_inc(loaded, 16)

            @block.gpsimd
            def _(pool):
                nc.gpsimd.memset(patch[:], 1.0).then_inc(ones_set, 1)
                pool.wait_ge(loaded, 16 * 5)
                with pool.Fori(0, NU // 2) as i:
                    for s in range(2):
                        u = i * 2 + s
                        pool.wait_ge(y_free, u + 1)
                        nc.gpsimd.tensor_copy(unit[:, s, :], patch[:, ds(u * UNIT, UNIT)]).then_inc(unit_ready, 1)

            @block.tensor
            def _(pe):
                with pe.Fori(0, NU // 2) as i:
                    for s in range(2):
                        u = i * 2 + s
                        pe.wait_ge(unit_ready, u + 1)
                        for m in range(hid_tiles):
                            pe.wait_ge(hid_done, u * hid_tiles + m + 1)
                            nc.tensor.matmul(hid_ps[m % 4][:, 0:UNIT], wh[:, m * P:(m + 1) * P], unit[0:mrows, s, :],
                                             start=True, stop=True).then_inc(hid_ready, 1)
                        pe.wait_ge(hid_done, u * hid_tiles + hid_tiles + 4)
                        pe.wait_ge(y_free, u + 1)
                        for t in range(UT):
                            y = y_ps[s][:, t // 2, (t % 2) * C:(t % 2 + 1) * C]
                            nc.tensor.matmul(y, unit[:, s, t * TT:(t + 1) * TT], wr[:], start=(t % 2 == 0), stop=False,
                                             skip_group_check=True)
                            for m in range(hid_tiles):
                                ins = nc.tensor.matmul(y, hid[:, s, m, t * TT:(t + 1) * TT], wo[:, m, :], start=False,
                                                       stop=(m == hid_tiles - 1), skip_group_check=True)
                        ins.then_inc(y_ready, 1)

            @block.scalar
            def _(act):
                act.sem_inc(hid_done, 4)
                act.wait_ge(loaded, 16 * 5)
                with act.Fori(0, NU // 2) as i:
                    for s in range(2):
                        u = i * 2 + s
                        act.wait_ge(y_free, u + 1)
                        for m in range(hid_tiles):
                            act.wait_ge(hid_ready, u * hid_tiles + m + 1)
                            nc.scalar.activation(hid[:, s, m, :], hid_ps[m % 4][:, 0:UNIT], ACT.Silu,
                                                 bias=bh[:, m:m + 1]).then_inc(hid_done, 1)

            @block.vector
            def _(dve):
                dve.sem_inc(y_free, 2)
                with dve.Fori(0, NU // 2) as i:
                    for s in range(2):
                        u = i * 2 + s
                        dve.wait_ge(y_ready, u + 1)
                        nc.vector.tensor_copy(h[:, ds(u * UT, UT), :],
                                              y_ps[s][:, :, :].rearrange("p a (b c) -> p (a b) c", c=C)).then_inc(y_free, 1)


def route(core, name, xT, v, wg, bg, pick):
    nc, ident = core.nc, core.ident
    E = v.shape[2]
    with Layer(core, name) as L:
        wg_sb = L.sb("wg", [P, KC, E])
        bg_sb = L.sb("bg", [E, 1])
        logitT = L.sb("logitT", [E, 2, UNIT])
        before = L.sb("before", [TT, E, E])
        work = pick.buffers(L, E)
        logit_ps = [L.ps(f"logit_ps{s}", [E, BANK]) for s in range(2)]
        v_ps = L.ps("v_ps", [TT, NT, E])
        loaded = L.sem("loaded")
        table = L.sem("table")
        logit_ready = L.sem("logit_ready")
        logitT_ready = L.sem("logitT_ready")
        turned = L.sem("turned")
        steps = L.sem("steps")
        act_ready = L.sem("act_ready")
        act_asked = L.sem("act_asked")
        n_loads = 1 + (bg is not None) + pick.loads

        with nc.Block() as block:

            @block.sync
            def _(sp):
                sp.dma_start(wg_sb[:], wg).then_inc(loaded, 16)
                if bg is not None:
                    sp.dma_start(bg_sb[:], bg).then_inc(loaded, 16)
                pick.load(sp, work, loaded)

            @block.gpsimd
            def _(pool):
                nc.gpsimd.memset(before[:], 1.0).then_inc(table, 1)
                pool.wait_ge(table, 1)
                nc.gpsimd.affine_select(out=before[:], in_=before[:], compare_op=ALU.is_gt, fill=0.0, base=0,
                                        pattern=[[1, E], [-1, E]], channel_multiplier=0).then_inc(table, 1)

            @block.tensor
            def _(pe):
                pe.wait_ge(loaded, 16 * n_loads)
                for u in range(NU + 1):
                    if u < NU:
                        if u >= 2:
                            pe.wait_ge(logitT_ready, u - 1)
                        for k in range(KC):
                            ins = nc.tensor.matmul(logit_ps[u % 2][:, 0:UNIT], wg_sb[:, k, :], xT[:, k, u * UNIT:(u + 1) * UNIT],
                                                   start=(k == 0), stop=(k == KC - 1))
                        ins.then_inc(logit_ready, 1)
                    if u >= 1:
                        pe.wait_ge(logitT_ready, u)
                        for t in range(UT):
                            ins = nc.tensor.transpose(v_ps[:, (u - 1) * UT + t, :], logitT[:, (u - 1) % 2, t * TT:(t + 1) * TT],
                                                      ident[0:E, 0:E])
                        ins.then_inc(turned, 1)

            @block.scalar
            def _(act):
                act.wait_ge(loaded, 16 * n_loads)
                for u in range(NU):
                    act.wait_ge(logit_ready, u + 1)
                    if u >= 2:
                        act.wait_ge(turned, u - 1)
                    if bg is not None:
                        ins = nc.scalar.activation(logitT[:, u % 2, :], logit_ps[u % 2][:, 0:UNIT], ACT.Identity, bias=bg_sb[:, 0:1])
                    else:
                        ins = nc.scalar.activation(logitT[:, u % 2, :], logit_ps[u % 2][:, 0:UNIT], pick.on_logits)
                    ins.then_inc(logitT_ready, 1)
                if pick.asks_act:
                    act.wait_ge(act_asked, 1)
                    pick.on_act(nc, work).then_inc(act_ready, 1)

            @block.vector
            def _(dve):
                st = Steps(dve, steps)
                dve.wait_ge(table, 2)
                dve.wait_ge(loaded, 16 * n_loads)
                dve.wait_ge(turned, NU)
                st.then(nc.vector.tensor_copy(v[:], v_ps[:]))
                pick.run(nc, dve, st, v, before, work, act_asked, act_ready)


def rank_of(nc, st, v, before, gt, ge, rank):
    E = v.shape[2]
    other = v.unsqueeze(2).broadcast_to([TT, NT, E, E])
    g4 = gt.rearrange("p (t e) j -> p t e j", t=NT)
    q4 = ge.rearrange("p (t e) j -> p t e j", t=NT)
    mine4 = v.unsqueeze(3).broadcast_to([TT, NT, E, E])
    nc.vector.tensor_tensor(g4, other, mine4, ALU.is_gt)
    st.then(nc.vector.tensor_tensor(q4, other, mine4, ALU.is_equal))
    st.then(nc.vector.tensor_tensor(q4, q4, before.unsqueeze(1).broadcast_to([TT, NT, E, E]), ALU.mult))
    st.then(nc.vector.tensor_tensor(gt, gt, ge, ALU.add))
    st.then(nc.vector.reduce_sum(rank.rearrange("p t e -> p (t e)"), gt, AX.X))


class PickTop1:
    loads, asks_act, on_logits = 0, False, None

    def __init__(self, ranks=None):
        self.ranks = ranks

    def buffers(self, L, E):
        return dict(gt=L.sb("gt", [TT, NT * E, E]), ge=L.sb("ge", [TT, NT * E, E]), rank=self.ranks or L.sb("rank", [TT, NT, E]))

    def load(self, sp, w, loaded):
        pass

    def run(self, nc, dve, st, v, before, w, asked, answered):
        rank_of(nc, st, v[:], before[:], w["gt"][:], w["ge"][:], w["rank"][:])
        st.then(nc.vector.tensor_scalar(v[:], w["rank"][:], 0.5, None, ALU.is_lt))


def experts(core, name, xT, sel, n_experts, tiles, w1, b1, w2, squared_relu=False):
    nc, h = core.nc, core.h
    slots = min(2, n_experts)
    with Layer(core, name) as L:
        w1_sb = [L.sb(f"w1_{s}", [P, KC, tiles * P]) for s in range(slots)]
        w2_sb = [L.sb(f"w2_{s}", [P, tiles, C]) for s in range(slots)]
        b1_sb = [L.sb(f"b1_{s}", [P, tiles]) for s in range(slots)]
        hid = L.sb("hid", [P, 2, UNIT])
        relu = L.sb("relu", [P, 2, UNIT])
        hid_ps = [L.ps(f"hid_ps{s}", [P, BANK]) for s in range(2)]
        y_ps = [L.ps(f"y_ps{s}", [TT, UT // 2, BANK]) for s in range(2)]
        w_ready = [L.sem(f"w_ready{s}") for s in range(slots)]
        hid_ready = L.sem("hid_ready")
        hid_done = L.sem("hid_done")
        hid_used = L.sem("hid_used")
        y_ready = L.sem("y_ready")
        y_free = L.sem("y_free")
        relued = L.sem("relued")
        loads = 2 + (b1 is not None)
        body = 2 * tiles

        def over_experts(eng, run):
            if n_experts == 1:
                run(0, 0, 0)
            else:
                with eng.Fori(0, n_experts // 2) as pair:
                    for s in range(2):
                        run(pair * 2 + s, s, pair)

        with nc.Block() as block:

            @block.sync
            def _(sp):
                def load(e, s, turn):
                    pairs = [(w1_sb[s], w1), (w2_sb[s], w2)] + ([(b1_sb[s], b1)] if b1 is not None else [])
                    for dst, src in pairs:
                        flat = dst[:] if len(dst.shape) == 2 else dst[:].rearrange("p a b -> p (a b)")
                        sp.dma_start(flat, src[ds(e, 1)].rearrange("a p n -> p (a n)")).then_inc(w_ready[s], 16)
                for s in range(slots):
                    load(s, s, 0)
                if n_experts > 2:
                    with sp.Fori(1, n_experts // 2) as pair:
                        for s in range(2):
                            sp.wait_ge(hid_used, (pair * 2 + s - 1) * (NU * tiles) + 2)
                            load(pair * 2 + s, s, pair)

            @block.tensor
            def _(pe):
                pe.sem_inc(hid_used, 2)

                def expert(e, s, turn):
                    pe.wait_ge(w_ready[s], (turn + 1) * (16 * loads))
                    pe.nop(nofuse=True)
                    with pe.Fori(0, NU // 2) as i:
                        first = e * (NU * tiles) + i * body
                        units = e * NU + i * 2

                        def up(q):
                            u, m = q // tiles, q % tiles
                            pe.wait_ge(hid_done, first + q + 1)
                            for k in range(KC):
                                ins = nc.tensor.matmul(hid_ps[q % 2][:, 0:UNIT], w1_sb[s][:, k, m * P:(m + 1) * P],
                                                       xT[:, k, ds((i * 2 + u) * UNIT, UNIT)],
                                                       start=(k == 0), stop=(k == KC - 1))
                            ins.then_inc(hid_ready, 1)

                        def down(q):
                            u, m = q // tiles, q % tiles
                            pe.wait_ge(hid_done, first + q + 3)
                            if m == 0:
                                pe.wait_ge(y_free, units + u + 1)
                            for t in range(UT):
                                y = y_ps[u][:, t // 2, (t % 2) * C:(t % 2 + 1) * C]
                                ins = nc.tensor.matmul(y, hid[:, q % 2, t * TT:(t + 1) * TT], w2_sb[s][:, m, :],
                                                       start=(m == 0 and t % 2 == 0), stop=(m == tiles - 1),
                                                       skip_group_check=True)
                            ins.then_inc(hid_used, 1)

                        for q in range(body):
                            up(q)
                            if q:
                                down(q - 1)
                        down(body - 1)
                over_experts(pe, expert)

            @block.scalar
            def _(act):
                act.sem_inc(hid_done, 2)

                def expert(e, s, turn):
                    act.wait_ge(w_ready[s], (turn + 1) * (16 * loads))
                    with act.Fori(0, NU // 2) as i:
                        first = e * (NU * tiles) + i * body
                        for q in range(body):
                            m = q % tiles
                            act.wait_ge(hid_ready, first + q + 1)
                            act.wait_ge(hid_used, first + q + 1)
                            if squared_relu:
                                nc.scalar.activation(relu[:, q % 2, :], hid_ps[q % 2][:, 0:UNIT], ACT.Relu).then_inc(relued, 1)
                                act.wait_ge(relued, first + q + 1)
                                ins = nc.scalar.activation(hid[:, q % 2, :], relu[:, q % 2, :], ACT.Square)
                            else:
                                ins = nc.scalar.activation(hid[:, q % 2, :], hid_ps[q % 2][:, 0:UNIT], ACT.Gelu,
                                                           bias=b1_sb[s][:, m:m + 1])
                            ins.then_inc(hid_done, 1)
                over_experts(act, expert)

            @block.vector
            def _(dve):
                dve.sem_inc(y_free, 2)

                def expert(e, s, turn):
                    with dve.Fori(0, NU // 2) as i:
                        for u in range(2):
                            dve.wait_ge(hid_used, e * (NU * tiles) + i * body + (u + 1) * tiles + 2)
                            for t in range(UT):
                                tile = ds((i * 2 + u) * UT + t, 1)
                                y = y_ps[u][:, t // 2, (t % 2) * C:(t % 2 + 1) * C]
                                mine = h[:, tile, :].rearrange("p a c -> p (a c)")
                                if sel is None:
                                    ins = nc.vector.tensor_tensor(mine, y, mine, ALU.add)
                                else:
                                    weight = sel[:, tile, ds(e, 1)].rearrange("p a e -> p (a e)")
                                    ins = nc.vector.scalar_tensor_tensor(out=mine, in0=y, scalar=weight, in1=mine,
                                                                         op0=ALU.mult, op1=ALU.add)
                            ins.then_inc(y_free, 1)
                over_experts(dve, expert)


class PickTop2:
    loads, asks_act, on_logits = 0, True, ACT.Copy

    def __init__(self, ranks=None):
        self.ranks = ranks

    def buffers(self, L, E):
        return dict(gt=L.sb("gt", [TT, NT * E, E]), ge=L.sb("ge", [TT, NT * E, E]), rank=self.ranks or L.sb("rank", [TT, NT, E]),
                    top=L.sb("top", [TT, NT]), fall=L.sb("fall", [TT, NT, E]), grown=L.sb("grown", [TT, NT, E]),
                    keep=L.sb("keep", [TT, NT, E]), total=L.sb("total", [TT, NT]))

    def load(self, sp, w, loaded):
        pass

    def on_act(self, nc, w):
        return nc.scalar.activation(w["grown"][:], w["fall"][:], ACT.Exp)

    def run(self, nc, dve, st, v, before, w, asked, answered):
        E = v.shape[2]
        st.then(nc.vector.reduce_max(w["top"][:], v[:], AX.X))
        nc.vector.tensor_tensor(w["fall"][:], v[:], w["top"][:].unsqueeze(2).broadcast_to([TT, NT, E]),
                                ALU.subtract).then_inc(asked, 1)
        rank_of(nc, st, v[:], before[:], w["gt"][:], w["ge"][:], w["rank"][:])
        st.then(nc.vector.tensor_scalar(w["keep"][:], w["rank"][:], 1.5, None, ALU.is_lt))
        dve.wait_ge(answered, 1)
        st.then(nc.vector.tensor_tensor(v[:], w["grown"][:], w["keep"][:], ALU.mult))
        st.then(nc.vector.reduce_sum(w["total"][:], v[:], AX.X))
        st.then(nc.vector.reciprocal(w["total"][:], w["total"][:]))
        st.then(nc.vector.tensor_tensor(v[:], v[:], w["total"][:].unsqueeze(2).broadcast_to([TT, NT, E]), ALU.mult))


class PickGrouped:
    asks_act, on_logits, loads = False, ACT.Sigmoid, 1
    GROUPS, SCALE = 4, 2.5

    def __init__(self, bias):
        self.bias = bias

    def buffers(self, L, E):
        G = self.GROUPS
        return dict(gt=L.sb("gt", [TT, NT * E, E]), ge=L.sb("ge", [TT, NT * E, E]), rank=L.sb("rank", [TT, NT, E]),
                    ggt=L.sb("ggt", [TT, NT * G, G]), gge=L.sb("gge", [TT, NT * G, G]), grank=L.sb("grank", [TT, NT, G]),
                    biased=L.sb("biased", [TT, NT, E]), bias=L.sb("bias", [TT, E]), hi=L.sb("hi", [TT, NT * G, 2]),
                    lo=L.sb("lo", [TT, NT * G, 2]), first=L.sb("first", [TT, NT, G]), second=L.sb("second", [TT, NT, G]),
                    runner=L.sb("runner", [TT, NT, G]), total=L.sb("total", [TT, NT]), gbefore=L.sb("gbefore", [TT, G, G]))

    def load(self, sp, w, loaded):
        sp.dma_start(w["bias"][:], self.bias.broadcast_to([TT, self.bias.shape[1]])).then_inc(loaded, 16)

    def run(self, nc, dve, st, v, before, w, asked, answered):
        E, G = v.shape[2], self.GROUPS
        n = E // G
        biased, hi, lo = w["biased"][:], w["hi"][:], w["lo"][:]
        wide = [TT, NT, E]
        nc.vector.tensor_copy(w["gbefore"][:], before[:, 0:G, 0:G])
        st.then(nc.vector.tensor_tensor(biased, v[:], w["bias"][:].unsqueeze(1).broadcast_to(wide), ALU.add))
        b4 = biased.rearrange("p t (g a b) -> p (t g) a b", g=G, a=2)
        nc.vector.tensor_tensor(hi, b4[:, :, 0, :], b4[:, :, 1, :], ALU.max)
        st.then(nc.vector.tensor_tensor(lo, b4[:, :, 0, :], b4[:, :, 1, :], ALU.min))
        flat = [w[x][:].rearrange("p t g -> p (t g)") for x in ("first", "second", "runner")]
        nc.vector.tensor_tensor(flat[0], hi[:, :, 0], hi[:, :, 1], ALU.max)
        nc.vector.tensor_tensor(flat[1], hi[:, :, 0], hi[:, :, 1], ALU.min)
        st.then(nc.vector.tensor_tensor(flat[2], lo[:, :, 0], lo[:, :, 1], ALU.max))
        st.then(nc.vector.tensor_tensor(flat[1], flat[1], flat[2], ALU.max))
        st.then(nc.vector.tensor_tensor(flat[0], flat[0], flat[1], ALU.add))
        rank_of(nc, st, w["first"][:], w["gbefore"][:], w["ggt"][:], w["gge"][:], w["grank"][:])
        st.then(nc.vector.tensor_scalar(w["grank"][:], w["grank"][:], 1.5, None, ALU.is_lt))
        in_group = w["grank"][:].rearrange("p t g -> p (t g)").unsqueeze(2).broadcast_to([TT, NT * G, n])
        b3 = biased.rearrange("p t (g n) -> p (t g) n", g=G)
        st.then(nc.vector.tensor_tensor(b3, b3, in_group, ALU.mult))
        rank_of(nc, st, biased, before[:], w["gt"][:], w["ge"][:], w["rank"][:])
        st.then(nc.vector.scalar_tensor_tensor(out=v[:], in0=w["rank"][:], scalar=3.5, in1=v[:], op0=ALU.is_lt, op1=ALU.mult))
        st.then(nc.vector.reduce_sum(w["total"][:], v[:], AX.X))
        st.then(nc.vector.tensor_scalar(w["total"][:], w["total"][:], 1e-20, None, ALU.add))
        st.then(nc.vector.reciprocal(w["total"][:], w["total"][:]))
        st.then(nc.vector.tensor_scalar(w["total"][:], w["total"][:], self.SCALE, None, ALU.mult))
        st.then(nc.vector.tensor_tensor(v[:], v[:], w["total"][:].unsqueeze(2).broadcast_to(wide), ALU.mult))


def grouped_experts(core):
    d = core.dram
    E, tiles = d["f2_w1"].shape[0], d["f2_w2"].shape[2] // C
    with Layer(core, "f2") as L:
        xT = L.sb("xT", [P, KC, TOK])
        sel = L.sb("sel", [TT, NT, E])
        layer_norm(core, "f2ln", xT)
        route(core, "f2rt", xT, sel, d["f2_wg"], None, PickGrouped(d["f2_bias"]))
        experts(core, "f2ex", xT, sel, E, tiles, d["f2_w1"], None, d["f2_w2"], squared_relu=True)
        experts(core, "f2sh", xT, None, 1, d["f2_s2"].shape[2] // C, d["f2_s1"], None, d["f2_s2"], squared_relu=True)


def routed_layer(core, name, n_picked, pick, w1, b1, w2, b2, wg, bg):
    nc, h, ident = core.nc, core.h, core.ident
    E, F = w1.shape[0], w1.shape[2] // KC
    FT = F // P
    FC = min(F, BANK)
    TILES = -(-(TOK * n_picked + E * (P - 1)) // P // 2) * 2
    ROUNDER = 12582912.0
    x_slots = nc.dram_tensor(f"{name}_x_slots", (TILES * P, C), F32, kind="Internal").ap()
    y_slots = nc.dram_tensor(f"{name}_y_slots", (TILES * P, C), F32, kind="Internal").ap()
    with Layer(core, name) as L:
        w1_sb = L.sb("w1", [P, E, KC * F])
        b1_sb = L.sb("b1", [P, E, FT])
        b2_sb = L.sb("b2", [1, E, C])
        ones = L.sb("ones", [1, P])
        weight = L.sb("weight", [TT, n_picked, NT])
        slot = L.sb("slot", [TT, n_picked, NT], mybir.dt.uint32)
        owner = L.sb("owner", [1, TILES], I32)
        w1_loaded = L.sem("w1_loaded")
        cleared = L.sem("cleared")
        with Layer(core, name + "p") as LP:
            xT = LP.sb("xT", [P, KC, TOK])
            keep = LP.sb("keep", [TT, NT, C])
            sel = LP.sb("sel", [TT, NT, E])
            ranks = LP.sb("ranks", [TT, NT, E])
            zeros = LP.sb("zeros", [P, 2 * C])
            zeroed = LP.sem("zeroed")
            with nc.Block() as block:

                @block.gpsimd
                def _(pool):
                    nc.gpsimd.memset(ones[:], 1.0)
                    nc.gpsimd.memset(zeros[:], 0.0).then_inc(zeroed, 1)

                @block.sync
                def _(sp):
                    sp.wait_ge(zeroed, 1)
                    with sp.Fori(0, TILES // 2) as i:
                        sp.dma_start(x_slots[ds(i * 2 * P, 2 * P), :].rearrange("(p a) c -> p (a c)", a=2),
                                     zeros[:]).then_inc(cleared, 16)
                    for e in range(E):
                        sp.dma_start(w1_sb[:, e, :], w1[e]).then_inc(w1_loaded, 16)
                        sp.dma_start(b1_sb[:, e, :], b1[e]).then_inc(w1_loaded, 16)
                    sp.dma_start(b2_sb[0:1, :, :].rearrange("a e c -> a (e c)"), b2.rearrange("(a e) c -> a (e c)", a=1)).then_inc(w1_loaded, 16)
            layer_norm(core, name + "ln", xT, keep=keep)
            route(core, name + "rt", xT, sel, wg, bg, pick(ranks))
            assign_slots(core, name + "as", n_picked, TILES, sel, ranks, weight, slot, owner, ROUNDER)
            sent = LP.pool_dma_sem("sent")
            with nc.Block() as block:

                @block.gpsimd
                def _(pool):
                    pool.wait_ge(cleared, 16 * (TILES // 2))
                    for t in range(NT):
                        for n in range(n_picked):
                            pool.indirect_dma_start(x_slots, bass.IndirectOffsetOnAxis(ap=slot[:, n, t:t + 1], axis=0),
                                                    keep[:, t, :], None).then_inc(sent, 16)
                    pool.wait_ge(sent, 16 * NT * n_picked)
        slot_experts(core, name + "ex", TILES, E, FT, FC, w1_sb, b1_sb, w2, b2_sb, ones, owner, x_slots, y_slots, w1_loaded)
        collect(core, name + "co", n_picked, y_slots, slot, weight)


def assign_slots(core, name, n_picked, TILES, sel, ranks, weight, slot, owner, ROUNDER):
    nc = core.nc
    E = sel.shape[2]
    with Layer(core, name) as L:
        before = L.sb("before", [TT, TT])
        ones = L.sb("ones", [TT, TT])
        ones_row = L.sb("ones_row", [TT, NT])
        chosen = L.sb("chosen", [TT, NT, E])
        total = L.sb("total", [TT, NT, E])
        running = L.sb("running", [TT, NT, E])
        position = L.sb("position", [TT, NT, E])
        hot = L.sb("hot", [TT, NT, E])
        value = L.sb("value", [TT, NT])
        tiles = L.sb("tiles", [TT, E])
        ends = L.sb("ends", [TT, E])
        first = L.sb("first", [TT, E])
        number_i = L.sb("number_i", [1, TILES], I32)
        number = L.sb("number", [1, TILES])
        past = L.sb("past", [1, TILES, E])
        who = L.sb("who", [1, TILES])
        pos_ps = L.ps("pos_ps", [TT, NT * E])
        total_ps = L.ps("total_ps", [TT, NT * E])
        const, chosen_ready, counted, steps = (L.sem(n) for n in ("const", "chosen_ready", "counted", "steps"))
        with nc.Block() as block:

            @block.gpsimd
            def _(pool):
                nc.gpsimd.memset(ones[:], 1.0).then_inc(const, 1)
                nc.gpsimd.memset(ones_row[:], 1.0)
                nc.gpsimd.iota(number_i[:], [[1, TILES]], base=0, channel_multiplier=0)
                pool.wait_ge(const, 1)
                nc.gpsimd.affine_select(out=before[:], in_=ones[:], compare_op=ALU.is_gt, fill=0.0, base=0,
                                        pattern=[[1, TT]], channel_multiplier=-1).then_inc(const, 1)

            @block.tensor
            def _(pe):
                pe.wait_ge(const, 2)
                pe.wait_ge(chosen_ready, 1)
                flat = chosen[:].rearrange("p t e -> p (t e)")
                nc.tensor.matmul(pos_ps[:], before[:], flat, start=True, stop=True)
                nc.tensor.matmul(total_ps[:], ones[:], flat, start=True, stop=True).then_inc(counted, 1)

            @block.vector
            def _(dve):
                st = Steps(dve, steps)
                V = nc.vector
                V.tensor_scalar(chosen[:], ranks[:], n_picked - 0.5, None, ALU.is_lt).then_inc(chosen_ready, 1)
                dve.wait_ge(const, 2)
                dve.wait_ge(counted, 1)
                st.then(V.tensor_copy(total[:].rearrange("p t e -> p (t e)"), total_ps[:]))
                for e in range(E):
                    ins = V.tensor_tensor_scan(running[:, :, e], ones_row[:], total[:, :, e], 0.0, ALU.mult, ALU.add)
                st.then(ins)
                st.then(V.tensor_scalar(tiles[:], running[:, NT - 1, :], 1.0 / P, 0.5 - 0.5 / P, ALU.mult, ALU.add))
                st.then(V.tensor_scalar(tiles[:], tiles[:], ROUNDER, ROUNDER, ALU.add, ALU.subtract))
                st.then(V.tensor_tensor_scan(ends[:], ones_row[:, 0:E], tiles[:], 0.0, ALU.mult, ALU.add))
                st.then(V.tensor_tensor(first[:], ends[:], tiles[:], ALU.subtract))
                st.then(V.tensor_scalar(first[:], first[:], float(P), None, ALU.mult))
                V.tensor_copy(number[:], number_i[:])
                st.then(V.tensor_tensor(position[:], running[:], total[:], ALU.subtract))
                st.then(V.tensor_tensor(position[:].rearrange("p t e -> p (t e)"), position[:].rearrange("p t e -> p (t e)"),
                                        pos_ps[:], ALU.add))
                st.then(V.tensor_tensor(position[:], position[:], first[:].unsqueeze(1).broadcast_to([TT, NT, E]), ALU.add))
                for n in range(n_picked):
                    st.then(V.tensor_scalar(hot[:], ranks[:], float(n), None, ALU.is_equal))
                    st.then(V.tensor_tensor(chosen[:], hot[:], position[:], ALU.mult))
                    st.then(V.reduce_sum(value[:], chosen[:], AX.X))
                    st.then(V.tensor_copy(slot[:, n, :], value[:]))
                    st.then(V.tensor_tensor(chosen[:], hot[:], sel[:], ALU.mult))
                    st.then(V.reduce_sum(weight[:, n, :], chosen[:], AX.X))
                st.then(V.tensor_tensor(past[:], ends[0:1, :].unsqueeze(1).broadcast_to([1, TILES, E]),
                                        number[:].unsqueeze(2).broadcast_to([1, TILES, E]), ALU.is_le))
                st.then(V.reduce_sum(who[:], past[:], AX.X))
                st.then(V.tensor_scalar(who[:], who[:], float(E - 1), None, ALU.min))
                V.tensor_copy(owner[:], who[:])


def slot_experts(core, name, TILES, E, FT, FC, w1_sb, b1_sb, w2, b2_sb, ones, owner, x_slots, y_slots, w1_loaded):
    nc, ident = core.nc, core.ident
    F = FT * P
    CHUNKS = F // FC
    PER = FC // P
    with Layer(core, name) as L:
        w2_sb = L.sb("w2", [P, E, FT * C])
        x = L.sb("x", [P, 2, C])
        xT = L.sb("xT", [P, 2, KC, P])
        pre = L.sb("pre", [P, F])
        hidT = L.sb("hidT", [P, 2, FT, P])
        y = L.sb("y", [P, 2, C])
        xT_ps = L.ps("xT_ps", [P, KC, P])
        up_ps = [L.ps(f"up_ps{c}", [P, FC]) for c in range(CHUNKS)]
        turn_ps = [L.ps(f"turn_ps{c}", [P, PER, P]) for c in range(CHUNKS)]
        y_ps = [L.ps(f"y_ps{s}", [P, C]) for s in range(2)]
        w2_loaded, stored = L.sem("w2_loaded"), [L.pool_dma_sem(f"stored{s}") for s in range(2)]
        x_loaded = [L.sem(f"x_loaded{s}") for s in range(2)]
        x_turned, xT_ready, up_ready, pre_ready, turned, hid_ready, y_ready, y_out = (
            L.sem(n) for n in ("x_turned", "xT_ready", "up_ready", "pre_ready", "turned", "hid_ready", "y_ready", "y_out"))
        with nc.Block() as block:

            @block.sync
            def _(sp):
                def fetch(i, s):
                    sp.dma_start(x[:, s, :], x_slots[ds(i * P, P), :]).then_inc(x_loaded[s], 16)

                fetch(0, 0)
                fetch(1, 1)
                for e in range(E):
                    sp.dma_start(w2_sb[:, e, :], w2[e]).then_inc(w2_loaded, 16)
                with sp.Fori(0, TILES // 2 - 1) as i:
                    for s in range(2):
                        sp.wait_ge(x_turned, i * 2 + s + 1)
                        fetch(i * 2 + s + 2, s)

            @block.gpsimd
            def _(pool):
                with pool.Fori(0, TILES // 2) as i:
                    for s in range(2):
                        pool.wait_ge(y_out, i * 2 + s + 1)
                        pool.dma_start(y_slots[ds((i * 2 + s) * P, P), :], y[:, s, :]).then_inc(stored[s], 16)
                for s in range(2):
                    pool.wait_ge(stored[s], 16 * (TILES // 2))

            @block.tensor
            def _(pe):
                def turn_x(i, s, turn):
                    pe.wait_ge(x_loaded[s], (turn + 1) * 16)
                    for k in range(KC):
                        ins = nc.tensor.transpose(xT_ps[:, k, :], x[:, s, k * P:(k + 1) * P], ident[:])
                    ins.then_inc(x_turned, 1)

                pe.wait_ge(w1_loaded, 32 * E + 16)
                pe.wait_ge(w2_loaded, 16 * E)
                turn_x(0, 0, 0)

                def expert_of(i):
                    return pe.value_load(owner[0:1, ds(i, 1)], min_val=0, max_val=E - 1)

                def up(i, s):
                    e = expert_of(i)
                    pe.wait_ge(xT_ready, i + 1)
                    for c in range(CHUNKS):
                        for k in range(KC):
                            ins = nc.tensor.matmul(up_ps[c][:], xT[:, s, k, :],
                                                   w1_sb[:, ds(e, 1), k * F + c * FC:k * F + (c + 1) * FC].rearrange("p a f -> p (a f)"),
                                                   start=(k == 0), stop=(k == KC - 1))
                        ins.then_inc(up_ready, 1)

                def turn_pre(i):
                    for c in range(CHUNKS):
                        pe.wait_ge(pre_ready, i * CHUNKS + c + 1)
                        for j in range(PER):
                            m = c * PER + j
                            ins = nc.tensor.transpose(turn_ps[c][:, j, :], pre[:, m * P:(m + 1) * P], ident[:])
                        ins.then_inc(turned, 1)

                def down(i, s):
                    e = expert_of(i)
                    pe.wait_ge(hid_ready, (i + 1) * CHUNKS)
                    nc.tensor.matmul(y_ps[s][:], ones[:], b2_sb[:, ds(e, 1), :].rearrange("p a f -> p (a f)"), start=True, stop=False)
                    for m in range(FT):
                        ins = nc.tensor.matmul(y_ps[s][:], hidT[:, s, m, :],
                                               w2_sb[:, ds(e, 1), m * C:(m + 1) * C].rearrange("p a f -> p (a f)"),
                                               start=False, stop=(m == FT - 1))
                    ins.then_inc(y_ready, 1)

                up(0, 0)
                turn_x(1, 1, 0)
                turn_pre(0)
                with pe.Fori(0, TILES // 2 - 1) as i:
                    for n, s, turn in ((i * 2 + 1, 1, i + 1), (i * 2 + 2, 0, i + 1)):
                        up(n, s)
                        turn_x(n + 1, 1 - s, turn)
                        down(n - 1, 1 - s)
                        turn_pre(n)
                up(TILES - 1, 1)
                down(TILES - 2, 0)
                turn_pre(TILES - 1)
                down(TILES - 1, 1)

            @block.vector
            def _(dve):
                def take_x(i, s):
                    dve.wait_ge(x_turned, i + 1)
                    nc.vector.tensor_copy(xT[:, s, :, :], xT_ps[:]).then_inc(xT_ready, 1)

                def take_pre(i, first=False):
                    for c in range(CHUNKS):
                        dve.wait_ge(up_ready, i * CHUNKS + c + 1)
                        if not first:
                            dve.nop(nofuse=True)
                            dve.wait_ge(turned, (i - 1) * CHUNKS + c + 1)
                        nc.vector.tensor_copy(pre[:, c * FC:(c + 1) * FC], up_ps[c][:]).then_inc(pre_ready, 1)

                def take_y(i, s, turn):
                    if turn is not None:
                        dve.wait_ge(stored[s], turn * 16)
                        dve.nop(nofuse=True)
                    dve.wait_ge(y_ready, i + 1)
                    nc.vector.tensor_copy(y[:, s, :], y_ps[s][:]).then_inc(y_out, 1)

                take_x(0, 0)
                take_pre(0, first=True)
                take_x(1, 1)
                for n, s in ((1, 1), (2, 0)):
                    take_pre(n)
                    take_x(n + 1, 1 - s)
                    take_y(n - 1, 1 - s, None)
                with dve.Fori(1, TILES // 2 - 1) as i:
                    for n, s in ((i * 2 + 1, 1), (i * 2 + 2, 0)):
                        take_pre(n)
                        take_x(n + 1, 1 - s)
                        take_y(n - 1, 1 - s, i)
                take_pre(TILES - 1)
                take_y(TILES - 2, 0, TILES // 2 - 1)
                take_y(TILES - 1, 1, TILES // 2 - 1)

            @block.scalar
            def _(act):
                with act.Fori(0, TILES // 2) as i:
                    for s in range(2):
                        n = i * 2 + s
                        e = act.value_load(owner[0:1, ds(n, 1)], min_val=0, max_val=E - 1)
                        for c in range(CHUNKS):
                            act.wait_ge(turned, n * CHUNKS + c + 1)
                            act.nop(nofuse=True)
                            for j in range(PER):
                                m = c * PER + j
                                ins = nc.scalar.activation(hidT[:, s, m, :], turn_ps[c][:, j, :], ACT.Gelu,
                                                           bias=b1_sb[:, ds(e, 1), m:m + 1].rearrange("p a b -> p (a b)"))
                            ins.then_inc(hid_ready, 1)


def collect(core, name, n_picked, y_slots, slot, weight):
    nc, h = core.nc, core.h
    BUFS = 8
    with Layer(core, name) as L:
        got = L.sb("got", [TT, BUFS, C])
        arrived = [L.pool_dma_sem(f"arrived{s}") for s in range(BUFS)]
        added = L.sem("added")
        jobs = [(t, n) for t in range(NT) for n in range(n_picked)]
        with nc.Block() as block:

            @block.gpsimd
            def _(pool):
                for i, (t, n) in enumerate(jobs):
                    if i >= BUFS:
                        pool.wait_ge(added, i - BUFS + 1)
                    pool.indirect_dma_start(got[:, i % BUFS, :], None, y_slots,
                                            bass.IndirectOffsetOnAxis(ap=slot[:, n, t:t + 1], axis=0)).then_inc(arrived[i % BUFS], 16)

            @block.vector
            def _(dve):
                for i, (t, n) in enumerate(jobs):
                    dve.wait_ge(arrived[i % BUFS], 16 * (i // BUFS + 1))
                    if n:
                        dve.wait_ge(added, i)
                    nc.vector.scalar_tensor_tensor(out=h[:, t, :], in0=got[:, i % BUFS, :], scalar=weight[:, n, t:t + 1],
                                                   in1=h[:, t, :], op0=ALU.mult, op1=ALU.add).then_inc(added, 1)


def top1_experts(core):
    d = core.dram
    routed_layer(core, "f0", 1, PickTop1, d["f0_w1"], d["f0_b1"], d["f0_w2"], d["f0_b2"], d["f0_wg"], d["f0_bg"])


def top2_experts(core):
    d = core.dram
    routed_layer(core, "f3", 2, PickTop2, d["f3_w1"], d["f3_b1"], d["f3_w2"], d["f3_b2"], d["f3_wg"], None)


def head_rows(h):
    return slice(32 * (h % 4), 32 * (h % 4) + 16), h // 4


def softmax_attention(core):
    nc, h, ident, d = core.nc, core.h, core.ident, core.dram
    HEADS, HD, HALF = 16, 16, SEQ // 2
    G = HEADS // 4
    SCORE = float(C) ** -0.5
    with Layer(core, "a2") as L:
        xT = L.sb("xT", [P, KC, TOK])
        layer_norm(core, "a2ln", xT)
        wq = L.sb("wq", [P, KC, G * P])
        wk = L.sb("wk", [P, KC, G * P])
        bq = L.sb("bq", [P, G])
        bk = L.sb("bk", [P, G])
        wv = L.sb("wv", [P, KC, C])
        bv = L.sb("bv", [TT, C])
        wo = L.sb("wo", [P, KC, C])
        bo = L.sb("bo", [1, C])
        ones = L.sb("ones", [1, TT])
        x = L.sb("x", [P, KC, SEQ])
        q = L.sb("q", [P, 2, G, SEQ])
        k = L.sb("k", [P, 2, G, SEQ])
        v = L.sb("v", [HALF, 2, 2, C])
        top = L.sb("top", [HALF, HEADS, 2])
        total = L.sb("total", [HALF, 2, HEADS, 2])
        probs = L.sb("probs", [HALF, 3, 2, SEQ])
        probsT = L.sb("probsT", [HALF, 2, 2, SEQ])
        o = L.sb("o", [HALF, 2, C])
        oT = L.sb("oT", [P, KC, SEQ])
        score_ps = [L.ps(f"score_ps{s}", [HALF, 2, BANK // 2]) for s in range(3)]
        probsT_ps = [L.ps(f"probsT_ps{s}", [HALF, 2, BANK // 2]) for s in range(2)]
        o_ps = L.ps("o_ps", [HALF, 2, C])
        side_ps = [L.ps(f"side_ps{s}", [P, 2, BANK // 2]) for s in range(2)]
        loaded = L.sem("loaded")
        ones_set = L.sem("ones_set")
        x_ready = L.sem("x_ready")
        side_ready = L.sem("side_ready")
        act_out = L.sem("act_out")
        dve_out = L.sem("dve_out")
        score_ready = L.sem("score_ready")
        top_ready = L.sem("top_ready")
        probs_ready = L.sem("probs_ready")
        turned = L.sem("turned")
        probsT_ready = L.sem("probsT_ready")
        av_done = L.sem("av_done")
        o_ready = L.sem("o_ready")
        steps = L.sem("steps")
        loads = [(wq, "a2_wq"), (wk, "a2_wk"), (bq, "a2_bq"), (bk, "a2_bk"), (wv, "a2_wv"), (wo, "a2_wo"), (bo, "a2_bo")]
        all_loaded = 16 * (len(loads) + 1)

        side_at = {1: "oT", 3: "y", 5: "q01", 6: "q23", 8: "k01", 9: "k23", 11: "v"}
        order = list(side_at.values())

        def before(b, per, short):
            if isinstance(b, int) and b in (0, SEQS):
                return short if b == 0 else (SEQS - 1) * per + short
            return b * per + (2 * short - per)

        def sides(b, prologue=False):
            some = [(n, t) for n, t in side_at.items()
                    if (t in ("oT", "y")) <= (not (isinstance(b, int) and b == 0) and not prologue)
                    and (t in ("oT", "y") or not (isinstance(b, int) and b == SEQS - 1))]
            return {n: t for n, t in some}, [t for _, t in some]

        ACT_SIDE, DVE_SIDE = ("oT", "q01", "q23", "k01", "k23"), ("y", "v")

        def count(tasks, task, kinds):
            return len([t for t in tasks[:tasks.index(task)] if t in kinds])

        def over_turns(eng, turn, steps_of_turn=None, st=None):
            turn(0, 0)
            with eng.Fori(0, SEQS // 2 - 1) as i:
                if st is not None:
                    st.enter(i, 2 * steps_of_turn)
                turn(i * 2 + 1, 1)
                turn(i * 2 + 2, 0)
                if st is not None:
                    st.leave(SEQS // 2 - 1)
            turn(SEQS - 1, 1)

        with nc.Block() as block:

            @block.sync
            def _(sp):
                for dst, name in loads:
                    sp.dma_start(dst[:], d[name]).then_inc(loaded, 16)
                sp.dma_start(bv[:], d["a2_bv"].broadcast_to([TT, C])).then_inc(loaded, 16)

            @block.gpsimd
            def _(pool):
                nc.gpsimd.memset(ones[:], 1.0).then_inc(ones_set, 1)
                nc.gpsimd.tensor_copy(x[:], xT[:, :, 0:SEQ]).then_inc(x_ready, 1)
                pool.wait_ge(side_ready, 5)
                nc.gpsimd.tensor_copy(x[:], xT[:, :, SEQ:2 * SEQ]).then_inc(x_ready, 1)
                with pool.Fori(2, SEQS) as b:
                    pool.wait_ge(side_ready, b * 7 - 4)
                    nc.gpsimd.tensor_copy(x[:], xT[:, :, ds(b * SEQ, SEQ)]).then_inc(x_ready, 1)

            @block.tensor
            def _(pe):
                def side(b, s, task, tasks):
                    a0, d0 = (0, 0) if b is None else (before(b, 5, 4), before(b, 2, 1))
                    if task == "oT":
                        pe.wait_ge(o_ready, b)
                        pe.nop(nofuse=True)
                        pe.wait_ge(dve_out, d0)
                        for a in range(2):
                            for c in range(KC):
                                ins = nc.tensor.transpose(side_ps[0][:, c, a * HALF:(a + 1) * HALF], o[:, a, c * P:(c + 1) * P],
                                                          ident[0:HALF, 0:HALF])
                    elif task == "y":
                        pe.wait_ge(act_out, a0 + 1)
                        for a in range(2):
                            nc.tensor.matmul(side_ps[1][0:HALF, a, :], ones[:], bo[:], start=True, stop=False)
                            for c in range(KC):
                                ins = nc.tensor.matmul(side_ps[1][0:HALF, a, :], oT[:, c, a * HALF:(a + 1) * HALF], wo[:, c, :],
                                                       start=False, stop=(c == KC - 1))
                    elif task == "v":
                        pe.wait_ge(act_out, a0 + count(tasks, "k01", ACT_SIDE) + 1)
                        for a in range(2):
                            for c in range(KC):
                                ins = nc.tensor.matmul(side_ps[0][0:HALF, a, :], x[:, c, a * HALF:(a + 1) * HALF], wv[:, c, :],
                                                       start=(c == 0), stop=(c == KC - 1))
                    else:
                        w, g0 = (wq if task[0] == "q" else wk), (0 if task[1:] == "01" else 2)
                        bank = 0 if task[1:] == "01" else 1
                        if task == "q01":
                            pe.wait_ge(x_ready, 1 if b is None else b + 2)
                            if b is not None:
                                pe.nop(nofuse=True)
                                if "oT" in tasks:
                                    pe.wait_ge(act_out, a0 + 1)
                                else:
                                    pe.wait_ge(dve_out, d0)
                        if task == "q23" and b is not None:
                            if "y" in tasks:
                                pe.wait_ge(dve_out, d0 + 1)
                            else:
                                pe.wait_ge(act_out, a0)
                        if task[0] == "k":
                            pe.wait_ge(act_out, a0 + count(tasks, "q" + task[1:], ACT_SIDE) + 1)
                        for g in range(2):
                            for c in range(KC):
                                ins = nc.tensor.matmul(side_ps[bank][:, g, 0:SEQ], w[:, c, (g0 + g) * P:(g0 + g + 1) * P],
                                                       x[:, c, :], start=(c == 0), stop=(c == KC - 1))
                    ins.then_inc(side_ready, 1)

                def turn(b, s):
                    side_of, tasks = sides(b)
                    first = isinstance(b, int) and b == 0

                    def score(n):
                        rows, g = head_rows(n)
                        if n == 0:
                            pe.wait_ge(act_out, before(b, 5, 4))
                            pe.nop(nofuse=True)
                        if n >= 3:
                            pe.wait_ge(probs_ready, b * HEADS + n - 2)
                        for a in range(2):
                            ins = nc.tensor.matmul(score_ps[n % 3][:, a, 0:SEQ], q[rows, s, g, a * HALF:(a + 1) * HALF],
                                                   k[rows, s, g, :], start=True, stop=True)
                        ins.then_inc(score_ready, 1)

                    def turn_probs(n):
                        pe.wait_ge(probs_ready, b * HEADS + n + 1)
                        if n >= 2:
                            pe.nop(nofuse=True)
                            pe.wait_ge(probsT_ready, b * HEADS + n - 1)
                        for a in range(2):
                            for kh in range(2):
                                ins = nc.tensor.transpose(probsT_ps[n % 2][:, kh, a * HALF:(a + 1) * HALF],
                                                          probs[:, n % 3, a, kh * HALF:(kh + 1) * HALF], ident[0:HALF, 0:HALF])
                        ins.then_inc(turned, 1)

                    def mix(n):
                        pe.wait_ge(probsT_ready, b * HEADS + n + 1)
                        if n == 0:
                            pe.nop(nofuse=True)
                            pe.wait_ge(dve_out, before(b, 2, 1))
                            if not first:
                                pe.nop(nofuse=True)
                                pe.wait_ge(o_ready, b)
                        for a in range(2):
                            for kh in range(2):
                                ins = nc.tensor.matmul(o_ps[:, a, n * HD:(n + 1) * HD],
                                                       probsT[:, n % 2, kh, a * HALF:(a + 1) * HALF],
                                                       v[:, s, kh, n * HD:(n + 1) * HD], start=(kh == 0), stop=(kh == 1))
                        ins.then_inc(av_done, 1)

                    for n in range(HEADS + 3):
                        if n < HEADS:
                            score(n)
                        if n in side_of:
                            side(b, s, side_of[n], tasks)
                        if 2 <= n < HEADS + 2:
                            turn_probs(n - 2)
                        if n >= 3:
                            mix(n - 3)

                pe.wait_ge(loaded, all_loaded)
                pe.wait_ge(ones_set, 1)
                tasks = sides(0, prologue=True)[1]
                for task in tasks:
                    side(None, 1, task, tasks)
                over_turns(pe, turn)
                side(SEQS, 0, "oT", ["oT", "y"])
                side(SEQS, 0, "y", ["oT", "y"])

            @block.scalar
            def _(act):
                def side(b, s, task, tasks):
                    act.wait_ge(side_ready, (0 if b is None else before(b, 7, 5)) + tasks.index(task) + 1)
                    if task == "oT":
                        nc.scalar.copy(oT[:], side_ps[0][:, :, 0:SEQ]).then_inc(act_out, 1)
                        return
                    dst, bias = (q, bq) if task[0] == "q" else (k, bk)
                    g0, bank = (0, 0) if task[1:] == "01" else (2, 1)
                    for g in range(2):
                        ins = nc.scalar.activation(dst[:, s, g0 + g, :], side_ps[bank][:, g, 0:SEQ], ACT.Identity,
                                                   bias=bias[:, g0 + g:g0 + g + 1])
                    ins.then_inc(act_out, 1)

                def turn(b, s):
                    side_of, tasks = sides(b)
                    for n in range(HEADS):
                        act.wait_ge(top_ready, b * HEADS + n + 1)
                        if n >= 3:
                            act.wait_ge(turned, b * HEADS + n - 2)
                        for a in range(2):
                            ins = nc.scalar.activation(probs[:, n % 3, a, :], score_ps[n % 3][:, a, 0:SEQ], ACT.Exp,
                                                       bias=top[:, n, a:a + 1], scale=SCORE, accum_out=total[:, s, n, a:a + 1])
                        ins.then_inc(probs_ready, 1)
                        if side_of.get(n) in ACT_SIDE:
                            side(b, 1 - s, side_of[n], tasks)

                act.wait_ge(loaded, all_loaded)
                tasks = sides(0, prologue=True)[1]
                for task in tasks:
                    if task in ACT_SIDE:
                        side(None, 0, task, tasks)
                over_turns(act, turn)
                side(SEQS, 0, "oT", ["oT", "y"])

            @block.vector
            def _(dve):
                st = Steps(dve, steps)

                def take_v(b, s, tasks):
                    dve.wait_ge(side_ready, (0 if b is None else before(b, 7, 5)) + tasks.index("v") + 1)
                    nc.vector.tensor_tensor(v[:, s, :, :], side_ps[0][0:HALF, :, :], bv[:].unsqueeze(1).broadcast_to([TT, 2, C]),
                                            ALU.add).then_inc(dve_out, 1)

                def take_y(b):
                    dve.wait_ge(side_ready, before(b, 7, 5) + 2)
                    mine = h[:, ds(b * 2 - 2, 2), :]
                    nc.vector.tensor_tensor(mine, side_ps[1][0:HALF, :, :], mine, ALU.add).then_inc(dve_out, 1)

                def normalise(b, s):
                    dve.wait_ge(probs_ready, b * HEADS)
                    st.then(nc.vector.reciprocal(total[:, s, :, :], total[:, s, :, :]))
                    dve.wait_ge(av_done, b * HEADS)
                    for a in range(2):
                        ins = nc.vector.tensor_tensor(o[:, a, :].rearrange("p (n e) -> p n e", n=HEADS),
                                                      o_ps[:, a, :].rearrange("p (n e) -> p n e", n=HEADS),
                                                      total[:, s, :, a:a + 1].broadcast_to([HALF, HEADS, HD]), ALU.mult)
                    ins.then_inc(o_ready, 1)

                def turn(b, s):
                    side_of, tasks = sides(b)
                    for n in range(HEADS + 2):
                        if n < HEADS:
                            dve.wait_ge(score_ready, b * HEADS + n + 1)
                            st.then(nc.vector.reduce_max(top[:, n, :], score_ps[n % 3][:, :, 0:SEQ], AX.X))
                            nc.vector.tensor_scalar(top[:, n, :], top[:, n, :], -SCORE, None, ALU.mult).then_inc(top_ready, 1)
                        if n == 0 and "oT" in tasks:
                            normalise(b, 1 - s)
                        if side_of.get(n) == "v":
                            take_v(b, 1 - s, tasks)
                        if side_of.get(n) == "y":
                            take_y(b)
                        if n >= 2:
                            m = n - 2
                            dve.wait_ge(turned, b * HEADS + m + 1)
                            if m >= 2:
                                dve.wait_ge(av_done, b * HEADS + m - 1)
                            nc.vector.tensor_copy(probsT[:, m % 2, :, :], probsT_ps[m % 2][:, :, 0:SEQ]).then_inc(probsT_ready, 1)

                dve.wait_ge(loaded, all_loaded)
                take_v(None, 0, sides(0, prologue=True)[1])
                over_turns(dve, turn, HEADS + 1, st)
                normalise(SEQS, 1)
                take_y(SEQS)


def taylor_attention(core):
    nc, h, ident, d = core.nc, core.h, core.ident, core.dram
    HEADS, HD, HALF = 8, 16, SEQ // 2
    G, HC, VW = HEADS // 4, HEADS * HD, HEADS * (HD + 1)
    SCALE, DEN_EPS = float(HD) ** -0.5, 1e-5
    with Layer(core, "a0") as L:
        xT = L.sb("xT", [P, KC, TOK])
        gamma = L.sb("gamma", [P, KC])
        wq = L.sb("wq", [P, KC, G * P])
        wk = L.sb("wk", [P, KC, G * P])
        wv = L.sb("wv", [P, KC, HC])
        wo = L.sb("wo", [P, C])
        loaded = L.sem("loaded")
        with nc.Block() as block:

            @block.sync
            def _(sp):
                for dst, name in ((gamma, "a0_gamma"), (wq, "a0_wq"), (wk, "a0_wk"), (wv, "a0_wv"), (wo, "a0_wo")):
                    sp.dma_start(dst[:], d[name]).then_inc(loaded, 16)
                sp.wait_ge(loaded, 16 * 5)
        layer_norm(core, "a0ln", xT, rms_gain=gamma)
        ones = L.sb("ones", [HALF, HALF])
        one = L.sb("one", [P, 1])
        x = L.sb("x", [P, KC, SEQ])
        q = L.sb("q", [P, 2, G, SEQ])
        k = L.sb("k", [P, 2, G, SEQ])
        v = L.sb("v", [HALF, 2, 2, VW])
        square = L.sb("square", [HALF, 3, 2, SEQ])
        den = L.sb("den", [HALF, 2, HEADS])
        o = L.sb("o", [HALF, 2, HC])
        oT = L.sb("oT", [P, SEQ])
        s_ps = [L.ps(f"s_ps{s}", [HALF, 2, BANK // 2]) for s in range(3)]
        o_ps = [L.ps(f"o_ps{s}", [HALF, 2, BANK // 2]) for s in range(2)]
        side_ps = [L.ps(f"side_ps{s}", [P, 2, BANK // 2]) for s in range(2)]
        ones_set = L.sem("ones_set")
        x_ready = L.sem("x_ready")
        side_ready = L.sem("side_ready")
        act_out = L.sem("act_out")
        dve_out = L.sem("dve_out")
        s_ready = L.sem("s_ready")
        square_ready = L.sem("square_ready")
        av_done = L.sem("av_done")
        o_ready = L.sem("o_ready")
        steps = L.sem("steps")

        side_at = {1: "oT", 3: "y", 4: "q", 5: "k", 7: "v"}

        def before(b, per, short):
            if isinstance(b, int) and b in (0, SEQS):
                return short if b == 0 else (SEQS - 1) * per + short
            return b * per + (2 * short - per)

        def sides(b):
            start, end = (isinstance(b, int) and b == 0), (isinstance(b, int) and b == SEQS - 1)
            return {n: t for n, t in side_at.items() if not (start and t in ("oT", "y")) and not (end and t in ("q", "k", "v"))}

        def over_turns(eng, turn, steps_of_turn=None, st=None):
            turn(0, 0)
            with eng.Fori(0, SEQS // 2 - 1) as i:
                if st is not None:
                    st.enter(i, 2 * steps_of_turn)
                turn(i * 2 + 1, 1)
                turn(i * 2 + 2, 0)
                if st is not None:
                    st.leave(SEQS // 2 - 1)
            turn(SEQS - 1, 1)

        with nc.Block() as block:

            @block.gpsimd
            def _(pool):
                nc.gpsimd.memset(ones[:], 1.0)
                nc.gpsimd.memset(one[:], 1.0)
                nc.gpsimd.memset(v[:], 1.0).then_inc(ones_set, 1)
                nc.gpsimd.tensor_copy(x[:], xT[:, :, 0:SEQ]).then_inc(x_ready, 1)
                pool.wait_ge(side_ready, 3)
                nc.gpsimd.tensor_copy(x[:], xT[:, :, SEQ:2 * SEQ]).then_inc(x_ready, 1)
                with pool.Fori(2, SEQS) as b:
                    pool.wait_ge(side_ready, b * 5 - 4)
                    nc.gpsimd.tensor_copy(x[:], xT[:, :, ds(b * SEQ, SEQ)]).then_inc(x_ready, 1)

            @block.tensor
            def _(pe):
                def side(b, task, finishing):
                    a0, d0 = (0, 0) if b is None else (before(b, 3, 2), before(b, 2, 1))
                    if task == "oT":
                        pe.wait_ge(o_ready, b)
                        pe.nop(nofuse=True)
                        pe.wait_ge(dve_out, d0)
                        for a in range(2):
                            ins = nc.tensor.transpose(side_ps[0][:, 0, a * HALF:(a + 1) * HALF], o[:, a, :], ident[0:HALF, 0:HALF])
                    elif task == "y":
                        pe.wait_ge(act_out, a0 + 1)
                        for a in range(2):
                            ins = nc.tensor.matmul(side_ps[1][0:HALF, a, :], oT[:, a * HALF:(a + 1) * HALF], wo[:],
                                                   start=True, stop=True)
                    elif task == "v":
                        pe.wait_ge(act_out, a0 + finishing + 1)
                        for a in range(2):
                            for c in range(KC):
                                ins = nc.tensor.matmul(side_ps[0][0:HALF, a, 0:HC], x[:, c, a * HALF:(a + 1) * HALF], wv[:, c, :],
                                                       start=(c == 0), stop=(c == KC - 1))
                    else:
                        if task == "q":
                            pe.wait_ge(x_ready, 1 if b is None else b + 2)
                            if b is not None:
                                pe.nop(nofuse=True)
                                if finishing:
                                    pe.wait_ge(act_out, a0 + 1)
                                else:
                                    pe.wait_ge(dve_out, d0)
                        elif b is not None:
                            if finishing:
                                pe.wait_ge(dve_out, d0 + 1)
                            else:
                                pe.wait_ge(act_out, a0)
                        w, bank = (wq, 0) if task == "q" else (wk, 1)
                        for g in range(G):
                            for c in range(KC):
                                ins = nc.tensor.matmul(side_ps[bank][:, g, 0:SEQ], w[:, c, g * P:(g + 1) * P],
                                                       x[:, c, :], start=(c == 0), stop=(c == KC - 1))
                    ins.then_inc(side_ready, 1)

                def turn(b, s):
                    side_of = sides(b)

                    def score(n):
                        rows, g = head_rows(n)
                        if n == 0:
                            pe.wait_ge(act_out, before(b, 3, 2))
                            pe.nop(nofuse=True)
                        if n >= 3:
                            pe.wait_ge(square_ready, b * HEADS + n - 2)
                        for kh in range(2):
                            ins = nc.tensor.matmul(s_ps[n % 3][:, kh, 0:SEQ], k[rows, s, g, kh * HALF:(kh + 1) * HALF],
                                                   q[rows, s, g, :], start=True, stop=True)
                        ins.then_inc(s_ready, 1)

                    def mix(n):
                        pe.wait_ge(square_ready, b * HEADS + n + 1)
                        for a in range(2):
                            for kh in range(2):
                                ins = nc.tensor.matmul(o_ps[s][:, a, n * (HD + 1):(n + 1) * (HD + 1)],
                                                       square[:, n % 3, kh, a * HALF:(a + 1) * HALF],
                                                       v[:, s, kh, n * (HD + 1):(n + 1) * (HD + 1)], start=False, stop=(kh == 1),
                                                       skip_group_check=True)
                        ins.then_inc(av_done, 1)

                    for n in range(HEADS + 2):
                        if n < HEADS:
                            score(n)
                        if n == 1:
                            pe.wait_ge(dve_out, before(b, 2, 1))
                            for a in range(2):
                                for kh in range(2):
                                    nc.tensor.matmul(o_ps[s][:, a, 0:VW], ones[:], v[:, s, kh, :], start=(a == 0 and kh == 0),
                                                     stop=False, skip_group_check=True)
                        if n in side_of:
                            side(b, side_of[n], "oT" in side_of.values())
                        if n >= 2:
                            mix(n - 2)

                pe.wait_ge(ones_set, 1)
                for task in ("q", "k", "v"):
                    side(None, task, False)
                over_turns(pe, turn)
                side(SEQS, "oT", True)
                side(SEQS, "y", True)

            @block.scalar
            def _(act):
                def side(b, s, task, finishing):
                    number = {"oT": 1, "q": 1 + 2 * finishing, "k": 2 + 2 * finishing}[task]
                    act.wait_ge(side_ready, (0 if b is None else before(b, 5, 3)) + number)
                    if task == "oT":
                        ins = nc.scalar.copy(oT[:], side_ps[0][:, 0, 0:SEQ])
                    elif task == "q":
                        ins = nc.scalar.copy(q[:, s, :, :], side_ps[0][:, :, 0:SEQ])
                    else:
                        ins = nc.scalar.copy(k[:, s, :, :], side_ps[1][:, :, 0:SEQ])
                    ins.then_inc(act_out, 1)

                def turn(b, s):
                    side_of = sides(b)
                    for n in range(HEADS):
                        act.wait_ge(s_ready, b * HEADS + n + 1)
                        if n >= 3:
                            act.wait_ge(av_done, b * HEADS + n - 2)
                        nc.scalar.activation(square[:, n % 3, :, :], s_ps[n % 3][:, :, 0:SEQ], ACT.Square,
                                             bias=one[0:HALF, :], scale=SCALE).then_inc(square_ready, 1)
                        if side_of.get(n) in ("oT", "q", "k"):
                            side(b, 1 - s, side_of[n], "oT" in side_of.values())

                act.wait_ge(ones_set, 1)
                side(None, 0, "q", False)
                side(None, 0, "k", False)
                over_turns(act, turn)
                side(SEQS, 0, "oT", True)

            @block.vector
            def _(dve):
                st = Steps(dve, steps)

                def take_v(b, s, finishing):
                    dve.wait_ge(side_ready, (0 if b is None else before(b, 5, 3)) + 3 + 2 * finishing)
                    for a in range(2):
                        ins = nc.vector.tensor_copy(v[:, s, a, :].rearrange("p (n e) -> p n e", n=HEADS)[:, :, 0:HD],
                                                    side_ps[0][0:HALF, a, 0:HC].rearrange("p (n e) -> p n e", n=HEADS))
                    ins.then_inc(dve_out, 1)

                def take_y(b):
                    dve.wait_ge(side_ready, before(b, 5, 3) + 2)
                    mine = h[:, ds(b * 2 - 2, 2), :]
                    nc.vector.tensor_tensor(mine, side_ps[1][0:HALF, :, :], mine, ALU.add).then_inc(dve_out, 1)

                def normalise(b, s):
                    dve.wait_ge(av_done, b * HEADS)
                    both = o_ps[s][:, :, 0:VW].rearrange("p a (n e) -> p a n e", n=HEADS)
                    st.then(nc.vector.tensor_scalar(den[:].unsqueeze(3), both[:, :, :, HD:HD + 1], 0.5, DEN_EPS, ALU.mult, ALU.max))
                    st.then(nc.vector.reciprocal(den[:], den[:]))
                    for a in range(2):
                        ins = nc.vector.scalar_tensor_tensor(out=o[:, a, :].rearrange("p (n e) -> p n e", n=HEADS),
                                                             in0=both[:, a, :, 0:HD], scalar=0.5,
                                                             in1=den[:, a, :].unsqueeze(2).broadcast_to([HALF, HEADS, HD]),
                                                             op0=ALU.mult, op1=ALU.mult)
                    ins.then_inc(o_ready, 1)

                def turn(b, s):
                    tasks = list(sides(b).values())
                    if "oT" in tasks:
                        normalise(b, 1 - s)
                        take_y(b)
                    if "v" in tasks:
                        take_v(b, 1 - s, "oT" in tasks)

                dve.wait_ge(ones_set, 1)
                take_v(None, 0, False)
                over_turns(dve, turn, 2, st)
                normalise(SEQS, 1)
                take_y(SEQS)


def token_norm(core, name, u, gain, shift):
    nc, h = core.nc, core.h
    with Layer(core, name) as L:
        stats = L.sb("stats", [TT, UT, 6])
        moments = L.sb("moments", [TT, 2, UT, 2])
        eps_var = L.sb("eps_var", [TT, 2, UT])
        rstd = L.sb("rstd", [TT, 2, UT])
        power = L.sb("power", [TT, UT])
        steps = L.sem("steps")
        power_set = L.sem("power_set")
        var_ready = L.sem("var_ready")
        rstd_ready = L.sem("rstd_ready")
        y_ready = L.sem("y_ready")
        with nc.Block() as block:

            @block.vector
            def _(dve):
                st = Steps(dve, steps)
                nc.vector.memset(power[:], -0.5).then_inc(power_set, 1)
                with dve.Fori(0, NU) as i:
                    st.enter(i, 5)
                    for r, src in enumerate((h, u)):
                        for t in range(UT):
                            ins = nc.vector.bn_stats(stats[:, t, :], src[:, ds(i * UT + t, 1), :])
                        st.then(ins)
                        dve.nop(nofuse=True)
                        for t in range(UT):
                            ins = nc.vector.bn_aggr(moments[:, r, t, :], stats[:, t, :])
                        st.then(ins)
                        nc.vector.tensor_scalar(eps_var[:, r, :], moments[:, r, :, 1], LN_EPS, None,
                                                ALU.add).then_inc(var_ready, 1)
                        dve.wait_ge(rstd_ready, i * 2 + r + 1)
                        for t in range(UT):
                            tile = ds(i * UT + t, 1)
                            ins = nc.vector.tensor_scalar(u[:, tile, :], src[:, tile, :], moments[:, r, t, 0:1],
                                                          rstd[:, r, t:t + 1], ALU.subtract, ALU.mult)
                        if r == 0:
                            st.then(ins)
                            dve.nop(nofuse=True)
                        else:
                            ins.then_inc(y_ready, 1)
                    st.leave(NU)

            @block.gpsimd
            def _(pool):
                pool.wait_ge(power_set, 1)
                with pool.Fori(0, NU) as i:
                    for r in range(2):
                        pool.wait_ge(var_ready, i * 2 + r + 1)
                        nc.gpsimd.tensor_tensor(rstd[:, r, :], eps_var[:, r, :], power[:], ALU.pow).then_inc(rstd_ready, 1)
        gained = L.sem("gained")
        wide = [TT, NT // 2, C]
        with nc.Block() as block:

            @block.vector
            def _(dve):
                mine = u[:, 0:NT // 2, :]
                nc.vector.tensor_tensor(mine, mine, gain.unsqueeze(1).broadcast_to(wide), ALU.mult).then_inc(gained, 1)
                dve.wait_ge(gained, 1)
                nc.vector.tensor_tensor(mine, mine, shift.unsqueeze(1).broadcast_to(wide), ALU.add)

            @block.gpsimd
            def _(pool):
                mine = u[:, NT // 2:NT, :]
                nc.gpsimd.tensor_tensor(mine, mine, gain.unsqueeze(1).broadcast_to(wide), ALU.mult).then_inc(y_ready, 1)
                pool.wait_ge(y_ready, NU + 1)
                nc.gpsimd.tensor_tensor(mine, mine, shift.unsqueeze(1).broadcast_to(wide), ALU.add)


def kernel_spectrum(core, F, KR, KR2, KI):
    nc, d = core.nc, core.dram
    PI = 3.1415925
    ROUND = 12582912.0
    TURN = (6.28125, 0.0019350051879882812, 3.0199159819120313e-07)
    with Layer(core, "ks") as L:
        lre = L.sb("lre", [P, 1])
        lim = L.sb("lim", [P, 1])
        cre = L.sb("cre", [P, C])
        cim = L.sb("cim", [P, C])
        step_i = L.sb("step_i", [P, SEQ], I32)
        step = L.sb("step", [P, SEQ])
        decay = L.sb("decay", [P, SEQ])
        angle = L.sb("angle", [P, SEQ])
        turns = L.sb("turns", [P, SEQ])
        sine = L.sb("sine", [P, SEQ])
        half = L.sb("half", [P, SEQ])
        small = L.sb("small", [P, 10])
        term = L.sb("term", [P, 2, C])
        K = L.sb("K", [TT, 2, C])
        K_ps = L.ps("K_ps", [TT, 2, C])
        spec_ps = L.ps("spec_ps", [TT, 4, C])
        loaded, stepped, rates, args, waves = (L.sem(n) for n in ("loaded", "stepped", "rates", "args", "waves"))
        modes, k_ready, k_out, spectrum = (L.sem(n) for n in ("modes", "k_ready", "k_out", "spectrum"))
        steps = L.sem("steps")
        a, b, m, nr, t1, t2, wr, wi = (small[:, i:i + 1] for i in range(8))
        with nc.Block() as block:

            @block.sync
            def _(sp):
                for dst, name in ((lre, "a3_lre"), (lim, "a3_lim"), (cre, "a3_cre"), (cim, "a3_cim")):
                    sp.dma_start(dst[:], d[name]).then_inc(loaded, 16)

            @block.gpsimd
            def _(pool):
                nc.gpsimd.iota(step_i[:], [[1, SEQ]], base=0, channel_multiplier=0).then_inc(stepped, 1)

            @block.scalar
            def _(act):
                act.wait_ge(loaded, 64)
                nc.scalar.activation(a, lre[:], ACT.Exp)
                nc.scalar.activation(b, lim[:], ACT.Exp).then_inc(rates, 1)
                act.wait_ge(args, 1)
                nc.scalar.activation(decay[:], decay[:], ACT.Exp)
                nc.scalar.activation(sine[:], angle[:], ACT.Sin)
                nc.scalar.activation(half[:], angle[:], ACT.Sin, scale=0.5).then_inc(waves, 1)

            @block.vector
            def _(dve):
                st = Steps(dve, steps)
                V = nc.vector
                dve.wait_ge(stepped, 1)
                st.then(V.tensor_copy(step[:], step_i[:]))
                dve.wait_ge(rates, 1)
                V.tensor_scalar(decay[:], step[:], a, -1.0, ALU.mult, ALU.mult)
                st.then(V.tensor_scalar(angle[:], step[:], b, None, ALU.mult))
                st.then(V.tensor_scalar(turns[:], angle[:], 0.15915494309189535, ROUND, ALU.mult, ALU.add))
                st.then(V.tensor_scalar(turns[:], turns[:], ROUND, None, ALU.subtract))
                for part in TURN:
                    st.then(V.scalar_tensor_tensor(out=angle[:], in0=turns[:], scalar=-part, in1=angle[:],
                                                   op0=ALU.mult, op1=ALU.add))
                V.tensor_scalar(angle[:], angle[:], PI, -PI, ALU.min, ALU.max).then_inc(args, 1)
                dve.wait_ge(waves, 1)
                st.then(V.tensor_tensor(half[:], half[:], half[:], ALU.mult))
                st.then(V.tensor_scalar(half[:], half[:], -2.0, 1.0, ALU.mult, ALU.add))
                V.tensor_tensor(half[:], half[:], decay[:], ALU.mult)
                st.then(V.tensor_tensor(sine[:], sine[:], decay[:], ALU.mult))
                st.then(V.tensor_tensor(m, a, a, ALU.mult))
                V.tensor_scalar(nr, half[:, 1:2], 1.0, None, ALU.subtract)
                st.then(V.scalar_tensor_tensor(out=m, in0=b, scalar=b, in1=m, op0=ALU.mult, op1=ALU.add))
                V.tensor_tensor(t1, nr, a, ALU.mult)
                V.tensor_tensor(t2, sine[:, 1:2], a, ALU.mult)
                st.then(V.reciprocal(m, m))
                V.scalar_tensor_tensor(out=wr, in0=sine[:, 1:2], scalar=b, in1=t1, op0=ALU.mult, op1=ALU.subtract)
                st.then(V.scalar_tensor_tensor(out=wi, in0=nr, scalar=b, in1=t2, op0=ALU.mult, op1=ALU.add))
                V.tensor_scalar(wr, wr, m, None, ALU.mult)
                st.then(V.tensor_scalar(wi, wi, m, -1.0, ALU.mult, ALU.mult))
                V.tensor_scalar(term[:, 0, :], cim[:], wi, None, ALU.mult)
                st.then(V.tensor_scalar(term[:, 1, :], cre[:], wi, None, ALU.mult))
                st.then(V.scalar_tensor_tensor(out=term[:, 0, :], in0=cre[:], scalar=wr, in1=term[:, 0, :],
                                               op0=ALU.mult, op1=ALU.subtract))
                st.then(V.scalar_tensor_tensor(out=term[:, 1, :], in0=cim[:], scalar=wr, in1=term[:, 1, :],
                                               op0=ALU.mult, op1=ALU.add))
                V.tensor_scalar(term[:, 1, :], term[:, 1, :], -1.0, None, ALU.mult).then_inc(modes, 1)
                dve.wait_ge(k_ready, 1)
                V.tensor_copy(K[:], K_ps[:]).then_inc(k_out, 1)
                dve.wait_ge(spectrum, 1)
                V.tensor_copy(KR[:], spec_ps[:, 0:2, :])
                V.tensor_copy(KR2[:], spec_ps[:, 0:2, :])
                st.then(V.tensor_copy(KI[:], spec_ps[:, 2:4, :]))
                V.tensor_copy(KR2[0:1, 0, :], spec_ps[0:1, 2, :])
                V.memset(KI[0:1, 0, :], 0.0)

            @block.tensor
            def _(pe):
                pe.wait_ge(modes, 1)
                for s in range(2):
                    nc.tensor.matmul(K_ps[:, s, :], half[:, s * TT:(s + 1) * TT], term[:, 0, :], start=True, stop=False)
                    ins = nc.tensor.matmul(K_ps[:, s, :], sine[:, s * TT:(s + 1) * TT], term[:, 1, :], start=False, stop=True)
                ins.then_inc(k_ready, 1)
                pe.wait_ge(k_out, 1)
                for j in range(4):
                    for s in range(2):
                        ins = nc.tensor.matmul(spec_ps[:, j, :], F[:, s, j * TT:(j + 1) * TT], K[:, s, :],
                                               start=(s == 0), stop=(s == 1))
                ins.then_inc(spectrum, 1)


def long_convolution(core):
    nc, h, d = core.nc, core.h, core.dram
    with Layer(core, "a3") as L:
        u = L.sb("u", [TT, NT, C])
        gain = L.sb("gain", [TT, C])
        shift = L.sb("shift", [TT, C])
        skip = L.sb("skip", [TT, C])
        F = L.sb("F", [TT, 2, 2 * SEQ])
        G = L.sb("G", [TT, 4, SEQ])
        KR = L.sb("KR", [TT, 2, C])
        KR2 = L.sb("KR2", [TT, 2, C])
        KI = L.sb("KI", [TT, 2, C])
        loaded = L.sem("loaded")
        with nc.Block() as block:

            @block.sync
            def _(sp):
                for dst, name in ((gain, "a3_gain"), (shift, "a3_shift"), (skip, "a3_skip")):
                    sp.dma_start(dst[:], d[name].broadcast_to([TT, C])).then_inc(loaded, 16)
                for dst, name in ((F, "a3_F"), (G, "a3_G")):
                    sp.dma_start(dst[:], d[name]).then_inc(loaded, 16)
                sp.wait_ge(loaded, 16 * 5)
        kernel_spectrum(core, F, KR, KR2, KI)
        token_norm(core, "a3ln", u, gain[:], shift[:])
        prod = L.sb("prod", [TT, 4, 2, C])
        Y = L.sb("Y", [TT, 4, 2, C])
        ud = L.sb("ud", [TT, 4, C])
        f_ps = [L.ps(f"f_ps{j}", [TT, 2, 2, C]) for j in range(2)]
        y_ps = L.ps("y_ps", [TT, 2, 2, C])
        f_ready = L.sem("f_ready")
        prod_ready = L.sem("prod_ready")
        Y_ready = L.sem("Y_ready")
        y_ready = L.sem("y_ready")
        ud_ready = L.sem("ud_ready")
        done = L.sem("done")
        steps = L.sem("steps")
        with nc.Block() as block:

            @block.tensor
            def _(pe):
                with pe.Fori(0, SEQS // 2) as i:
                    pe.wait_ge(done, i + 1)
                    for j in range(2):
                        for part in range(2):
                            for s in range(2):
                                x = u[:, ds(i * 4, 4), :].rearrange("p (b s) c -> p b s c", s=2)[:, :, s, :]
                                ins = nc.tensor.matmul(f_ps[j][:, part, :, :], F[:, s, (2 * part + j) * TT:(2 * part + j + 1) * TT],
                                                       x, start=(s == 0), stop=(s == 1))
                        ins.then_inc(f_ready, 1)
                    pe.wait_ge(Y_ready, i * 2 + 2)
                    for s in range(2):
                        for slot in range(4):
                            ins = nc.tensor.matmul(y_ps[:, s, :, :], G[:, slot, s * TT:(s + 1) * TT], Y[:, slot, :, :],
                                                   start=(slot == 0), stop=(slot == 3))
                    ins.then_inc(y_ready, 1)

            @block.vector
            def _(dve):
                st = Steps(dve, steps)
                dve.sem_inc(done, 1)
                wide = [TT, 2, C]
                with dve.Fori(0, SEQS // 2) as i:
                    st.enter(i, 1)
                    for j in range(2):
                        dve.wait_ge(f_ready, i * 2 + j + 1)
                        if j == 1:
                            dve.nop(nofuse=True)
                            dve.wait_ge(Y_ready, i * 2 + 1)
                        cu, su = f_ps[j][:, 0, :, :], f_ps[j][:, 1, :, :]
                        kr, kr2, ki = (k[:, j:j + 1, :].broadcast_to(wide) for k in (KR, KR2, KI))
                        nc.vector.tensor_tensor(prod[:, 0, :, :], cu, kr, ALU.mult)
                        nc.vector.tensor_tensor(prod[:, 1, :, :], su, ki, ALU.mult)
                        nc.vector.tensor_tensor(prod[:, 2, :, :], su, kr2, ALU.mult)
                        nc.vector.tensor_tensor(prod[:, 3, :, :], cu, ki, ALU.mult).then_inc(prod_ready, 1)
                    dve.wait_ge(y_ready, i + 1)
                    mine = h[:, ds(i * 4, 4), :].rearrange("p (b s) c -> p s b c", s=2)
                    st.then(nc.vector.tensor_tensor(mine, y_ps[:], mine, ALU.add))
                    dve.wait_ge(ud_ready, i + 1)
                    nc.vector.tensor_tensor(h[:, ds(i * 4, 4), :], ud[:], h[:, ds(i * 4, 4), :], ALU.add).then_inc(done, 1)
                    st.leave(SEQS // 2)

            @block.gpsimd
            def _(pool):
                with pool.Fori(0, SEQS // 2) as i:
                    pool.wait_ge(done, i + 1)
                    nc.gpsimd.tensor_tensor(ud[:], u[:, ds(i * 4, 4), :], skip[:].unsqueeze(1).broadcast_to([TT, 4, C]),
                                            ALU.mult).then_inc(ud_ready, 1)
                    for j in range(2):
                        pool.wait_ge(prod_ready, i * 2 + j + 1)
                        nc.gpsimd.tensor_tensor(Y[:, j, :, :], prod[:, 0, :, :], prod[:, 1, :, :], ALU.subtract)
                        nc.gpsimd.tensor_tensor(Y[:, 2 + j, :, :], prod[:, 2, :, :], prod[:, 3, :, :],
                                                ALU.add).then_inc(Y_ready, 1)


ROUND = 12582912.0
QMAX = 32767.0
U16 = 65536.0


class Scale:

    def __init__(self, L, name):
        self.most = L.sb(f"{name}_most", [P, 1])
        self.all = L.sb(f"{name}_all", [P, 1])
        self.step = L.sb(f"{name}_step", [P, 1])
        self.inverse = L.sb(f"{name}_inverse", [P, 1])


def make_scales(core, name, pairs):
    nc = core.nc
    with Layer(core, name) as L:
        steps, most_ready, all_ready = L.sem("steps"), L.sem("most_ready"), L.sem("all_ready")
        with nc.Block() as block:

            @block.vector
            def _(dve):
                st = Steps(dve, steps)
                for s, maxima in pairs:
                    nc.vector.reduce_max(s.most[:], maxima, AX.X).then_inc(most_ready, 1)
                for n, (s, _) in enumerate(pairs):
                    dve.wait_ge(all_ready, n + 1)
                    st.then(nc.vector.tensor_scalar(s.step[:], s.all[:], 1.0 / QMAX, 1e-12, ALU.mult, ALU.max))
                    nc.vector.reciprocal(s.inverse[:], s.step[:])

            @block.gpsimd
            def _(pool):
                for n, (s, _) in enumerate(pairs):
                    pool.wait_ge(most_ready, n + 1)
                    nc.gpsimd.partition_all_reduce(s.all[:], s.most[:], P, bass.bass_isa.ReduceOp.max).then_inc(all_ready, 1)


def block_weights(core, name, jobs):
    nc, ident = core.nc, core.ident
    BLOCK, W_QMAX = 32, 7.0
    SQUARES = 4
    with Layer(core, name) as L:
        w = [L.sb(f"w{n}", list(src.shape)) for n, (src, _) in enumerate(jobs)]
        NB = w[0].shape[1] * w[0].shape[2] // BLOCK
        inverse = L.sb("inverse", [P, NB])
        step = L.sb("step", [P, NB])
        turned = [L.ps(f"turned{s}", [P, BANK]) for s in range(2)]
        loaded = [L.sem(f"loaded{n}") for n in range(len(jobs))]
        steps, w_ready, t_ready, t_out = (L.sem(n) for n in ("steps", "w_ready", "t_ready", "t_out"))
        wide = [P, NB, BLOCK]
        banks = w[0].shape[1] * w[0].shape[2] // P // SQUARES

        with nc.Block() as block:

            @block.sync
            def _(sp):
                for n, (src, _) in enumerate(jobs):
                    sp.dma_start(w[n][:], src).then_inc(loaded[n], 16)

            @block.vector
            def _(dve):
                st = Steps(dve, steps)
                for n in range(len(jobs)):
                    all_w = w[n][:]
                    blocks = all_w.rearrange("p t (n b) -> p (t n) b", b=BLOCK)
                    dve.wait_ge(loaded[n], 16)
                    st.then(nc.vector.reduce_max(step[:], blocks, AX.X, apply_absolute_value=True))
                    st.then(nc.vector.tensor_scalar(step[:], step[:], 1.0 / W_QMAX, 1e-12, ALU.mult, ALU.max))
                    st.then(nc.vector.reciprocal(inverse[:], step[:]))
                    st.then(nc.vector.tensor_tensor(blocks, blocks, inverse[:].unsqueeze(2).broadcast_to(wide), ALU.mult))
                    st.then(nc.vector.tensor_scalar(all_w, all_w, ROUND, ROUND, ALU.add, ALU.subtract))
                    st.then(nc.vector.tensor_scalar(all_w, all_w, W_QMAX, -W_QMAX - 1.0, ALU.min, ALU.max))
                    nc.vector.tensor_tensor(blocks, blocks, step[:].unsqueeze(2).broadcast_to(wide), ALU.mult).then_inc(w_ready, 1)
                    dve.wait_ge(w_ready, n + 1)

            @block.tensor
            def _(pe):
                for n in range(len(jobs)):
                    tiles = w[n].shape[1]
                    pe.wait_ge(w_ready, n + 1)
                    for g in range(banks):
                        number = n * banks + g
                        if number >= 2:
                            pe.wait_ge(t_out, number - 1)
                        for q in range(SQUARES * g, SQUARES * (g + 1)):
                            c, t = q // tiles, q % tiles
                            ins = nc.tensor.transpose(turned[number % 2][:, (q % SQUARES) * P:(q % SQUARES + 1) * P],
                                                      w[n][:, t, c * P:(c + 1) * P], ident[:])
                        ins.then_inc(t_ready, 1)

            @block.scalar
            def _(act):
                for n, (_, wT) in enumerate(jobs):
                    out = wT.rearrange("p c o -> p (c o)")
                    for g in range(banks):
                        number = n * banks + g
                        act.wait_ge(t_ready, number + 1)
                        nc.scalar.copy(out[:, g * BANK:(g + 1) * BANK], turned[number % 2][:]).then_inc(t_out, 1)


def quantised_mlp(core):
    nc, h, d = core.nc, core.h, core.dram
    I = d["f1_gate"].shape[1] * P
    M = I // P
    MH = M // 2
    with Layer(core, "f1") as L:
        gateT = L.sb("gateT", [P, KC, I])
        upT = L.sb("upT", [P, KC, I])
        downT = L.sb("downT", [P, M, C])
        block_weights(core, "f1w", [(d["f1_gate"], gateT[:]), (d["f1_up"], upT[:]), (d["f1_down"], downT[:])])
        rounder = L.sb("rounder", [P, 1])
        x_max = L.sb("x_max", [P, KC * NU])
        gate_max = L.sb("gate_max", [P, 2 * NU])
        up_max = L.sb("up_max", [P, 2 * NU])
        act_max = L.sb("act_max", [P, 2 * NU])
        out_max = L.sb("out_max", [P, 2 * NU])
        sx, sg, su, sa, so = (Scale(L, n) for n in ("sx", "sg", "su", "sa", "so"))
        act_step = L.sb("act_step", [P, 1])
        both_step = L.sb("both_step", [P, 1])
        gate = L.sb("gate", [P, M, TOK])

        def unit_of(tensor, u):
            return tensor[:, :, ds(u * UNIT, UNIT)]

        def half(u, s):
            return gate[:, s * MH:(s + 1) * MH, ds(u * UNIT, UNIT)]

        def product(banks, weights, xT, u, s):
            for n in range(MH):
                m = s * MH + n
                for k in range(KC):
                    ins = nc.tensor.matmul(banks[:, n, 0:UNIT], weights[:, k, m * P:(m + 1) * P],
                                           xT[:, k, ds(u * UNIT, UNIT)], start=(k == 0), stop=(k == KC - 1))
            return ins

        def rounded_to_int(out, src, scale):
            return nc.scalar.activation(out, src, ACT.Identity, bias=rounder[:], scale=scale.inverse[:])

        def clipped(part):
            return nc.vector.tensor_scalar(part, part, ROUND + QMAX, ROUND - QMAX - 1.0, ALU.min, ALU.max)

        def stepped(part, step):
            return nc.vector.tensor_scalar(part, part, ROUND, step[:], ALU.subtract, ALU.mult)

        with Layer(core, "f1x") as LX:
            xT = LX.sb("xT", [P, KC, TOK])
            layer_norm(core, "f1ln", xT)
            with nc.Block() as block:

                @block.vector
                def _(dve):
                    nc.vector.memset(rounder[:], ROUND)
                    nc.vector.reduce_max(x_max[:].rearrange("p (k u) -> p k u", k=KC),
                                         xT[:].rearrange("p k (u n) -> p k u n", u=NU), AX.X, apply_absolute_value=True)
            make_scales(core, "f1sx", [(sx, x_max[:])])

            with Layer(core, "f1p") as LP:
                g_ps = [LP.ps(f"g_ps{s}", [P, MH, BANK]) for s in range(2)]
                rounded, x_clipped, x_ready, g_ready, g_out = (
                    LP.sem(n) for n in ("rounded", "x_clipped", "x_ready", "g_ready", "g_out"))
                with nc.Block() as block:

                    @block.scalar
                    def _(act):
                        with act.Fori(0, NU) as u:
                            rounded_to_int(unit_of(xT, u), unit_of(xT, u), sx).then_inc(rounded, 1)
                        with act.Fori(0, NU) as u:
                            for s in range(2):
                                act.wait_ge(g_ready, u * 2 + s + 1)
                                nc.scalar.copy(half(u, s), g_ps[s][:, :, 0:UNIT]).then_inc(g_out, 1)

                    @block.vector
                    def _(dve):
                        with dve.Fori(0, NU) as u:
                            dve.wait_ge(rounded, u + 1)
                            clipped(unit_of(xT, u)).then_inc(x_clipped, 1)
                            dve.wait_ge(x_clipped, u + 1)
                            stepped(unit_of(xT, u), sx.step).then_inc(x_ready, 1)
                        with dve.Fori(0, NU) as u:
                            for s in range(2):
                                dve.wait_ge(g_out, u * 2 + s + 1)
                                nc.vector.tensor_reduce(gate_max[:, ds(u * 2 + s, 1)], half(u, s), AX.XY, ALU.max,
                                                        apply_absolute_value=True)

                    @block.tensor
                    def _(pe):
                        pe.wait_ge(x_ready, 1)
                        for s in range(2):
                            product(g_ps[s], gateT, xT, 0, s).then_inc(g_ready, 1)
                        with pe.Fori(1, NU) as u:
                            pe.wait_ge(x_ready, u + 1)
                            for s in range(2):
                                pe.wait_ge(g_out, u * 2 + s - 1)
                                product(g_ps[s], gateT, xT, u, s).then_inc(g_ready, 1)
            make_scales(core, "f1sg", [(sg, gate_max[:])])

            with Layer(core, "f1s") as LS:
                sig = LS.sb("sig", [P, 2, MH, UNIT])
                u_ps = [LS.ps(f"u_ps{s}", [P, MH, BANK]) for s in range(2)]
                rounded, q_ready, raw_ready, sig_ready, sig_used, u_ready, u_seen, step_set, steps = (LS.sem(n) for n in (
                    "rounded", "q_ready", "raw_ready", "sig_ready", "sig_used", "u_ready", "u_seen", "step_set", "steps"))

                def is_first(u):
                    return isinstance(u, int) and u == 0

                def over_units(eng, turn, st=None, steps_of_turn=0):
                    for s in range(2):
                        turn(0, s, ahead=2)
                    with eng.Fori(1, NU - 1) as u:
                        if st is not None:
                            st.enter(u - 1, 2 * steps_of_turn)
                        for s in range(2):
                            turn(u, s, ahead=2)
                        if st is not None:
                            st.leave(NU - 2)
                    turn(NU - 1, 0, ahead=1)
                    turn(NU - 1, 1, ahead=0)

                with nc.Block() as block:

                    @block.tensor
                    def _(pe):
                        def turn(u, s, ahead):
                            if not is_first(u):
                                pe.wait_ge(u_seen, u * 2 + s - 1)
                            product(u_ps[s], upT, xT, u, s).then_inc(u_ready, 1)

                        over_units(pe, turn)

                    @block.scalar
                    def _(act):
                        def round_gate(u, s):
                            rounded_to_int(half(u, s), half(u, s), sg).then_inc(rounded, 1)

                        def sigmoid(u, s):
                            j = u * 2 + s
                            act.wait_ge(q_ready, j + 1)
                            if not is_first(u):
                                act.nop(nofuse=True)
                                act.wait_ge(sig_used, j - 1)
                            act.nop(nofuse=True)
                            nc.scalar.activation(sig[:, s, :, :], half(u, s), ACT.Sigmoid, scale=U16).then_inc(raw_ready, 1)
                            act.wait_ge(raw_ready, j + 1)
                            act.nop(nofuse=True)
                            nc.scalar.activation(sig[:, s, :, :], sig[:, s, :, :], ACT.Identity, bias=rounder[:],
                                                 scale=U16).then_inc(sig_ready, 1)

                        def turn(u, s, ahead):
                            if ahead == 2:
                                round_gate(u + 1, s)
                            if ahead >= 1:
                                sigmoid(u + s, 1 - s)

                        round_gate(0, 0)
                        round_gate(0, 1)
                        sigmoid(0, 0)
                        over_units(act, turn)

                    @block.vector
                    def _(dve):
                        st = Steps(dve, steps)

                        def quantise(u, s):
                            dve.wait_ge(rounded, u * 2 + s + 1)
                            st.then(clipped(half(u, s)))
                            stepped(half(u, s), act_step).then_inc(q_ready, 1)

                        def turn(u, s, ahead):
                            j = u * 2 + s
                            if ahead == 2:
                                quantise(u + 1, s)
                            dve.wait_ge(u_ready, j + 1)
                            nc.vector.tensor_reduce(up_max[:, ds(j, 1)], u_ps[s][:, :, 0:UNIT], AX.XY, ALU.max,
                                                    apply_absolute_value=True).then_inc(u_seen, 1)
                            dve.wait_ge(sig_ready, j + 1)
                            st.then(nc.vector.tensor_scalar(sig[:, s, :, :], sig[:, s, :, :], ROUND, ROUND + U16 - 1.0, ALU.max, ALU.min))
                            st.then(nc.vector.scalar_tensor_tensor(out=half(u, s), in0=sig[:, s, :, :], scalar=-ROUND,
                                                                   in1=half(u, s), op0=ALU.add, op1=ALU.mult))
                            nc.vector.tensor_reduce(act_max[:, ds(j, 1)], half(u, s), AX.XY, ALU.max,
                                                    apply_absolute_value=True).then_inc(sig_used, 1)

                        nc.vector.tensor_scalar(act_step[:], sg.step[:], 1.0 / U16, None, ALU.mult).then_inc(step_set, 1)
                        dve.wait_ge(step_set, 1)
                        quantise(0, 0)
                        quantise(0, 1)
                        over_units(dve, turn, st, 3)
            make_scales(core, "f1sa", [(sa, act_max[:]), (su, up_max[:])])

            with Layer(core, "f1u") as LU:
                up = LU.sb("up", [P, 2, MH, UNIT])
                u_ps = [LU.ps(f"u_ps{s}", [P, MH, BANK]) for s in range(2)]
                u_ready, u_out, g_out, up_free, step_set, steps = (
                    LU.sem(n) for n in ("u_ready", "u_out", "g_out", "up_free", "step_set", "steps"))
                with nc.Block() as block:

                    @block.tensor
                    def _(pe):
                        for s in range(2):
                            product(u_ps[s], upT, xT, 0, s).then_inc(u_ready, 1)
                        with pe.Fori(1, NU) as u:
                            for s in range(2):
                                pe.wait_ge(u_out, u * 2 + s - 1)
                                product(u_ps[s], upT, xT, u, s).then_inc(u_ready, 1)

                    @block.scalar
                    def _(act):
                        def turn(u, s, first=False):
                            j = u * 2 + s
                            rounded_to_int(half(u, s), half(u, s), sa).then_inc(g_out, 1)
                            act.wait_ge(u_ready, j + 1)
                            if not first:
                                act.nop(nofuse=True)
                                act.wait_ge(up_free, j - 1)
                                act.nop(nofuse=True)
                            rounded_to_int(up[:, s, :, :], u_ps[s][:, :, 0:UNIT], su).then_inc(u_out, 1)

                        for s in range(2):
                            turn(0, s, first=True)
                        with act.Fori(1, NU) as u:
                            for s in range(2):
                                turn(u, s)

                    @block.vector
                    def _(dve):
                        st = Steps(dve, steps)
                        nc.vector.tensor_scalar(both_step[:], sa.step[:], su.step[:], None, ALU.mult).then_inc(step_set, 1)
                        dve.wait_ge(step_set, 1)
                        with dve.Fori(0, NU) as u:
                            st.enter(u, 2 * 3)
                            for s in range(2):
                                j = u * 2 + s
                                mine = up[:, s, :, :]
                                dve.wait_ge(g_out, j + 1)
                                clipped(half(u, s))
                                dve.wait_ge(u_out, j + 1)
                                st.then(clipped(mine))
                                st.then(stepped(mine, both_step))
                                st.then(nc.vector.scalar_tensor_tensor(out=half(u, s), in0=half(u, s), scalar=-ROUND, in1=mine,
                                                                       op0=ALU.add, op1=ALU.mult))
                                nc.vector.tensor_reduce(out_max[:, ds(j, 1)], half(u, s), AX.XY, ALU.max,
                                                        apply_absolute_value=True).then_inc(up_free, 1)
                            st.leave(NU)
        make_scales(core, "f1so", [(so, out_max[:])])

        with Layer(core, "f1d") as LD:
            q = LD.sb("q", [P, 2, M, UNIT])
            y_ps = [LD.ps(f"y_ps{s}", [TT, 2, BANK]) for s in range(2)]
            rounded, q_ready, y_ready, y_free, steps = (LD.sem(n) for n in ("rounded", "q_ready", "y_ready", "y_free", "steps"))
            with nc.Block() as block:

                @block.scalar
                def _(act):
                    with act.Fori(0, NU // 2) as i:
                        for s in range(2):
                            u = i * 2 + s
                            act.wait_ge(y_free, u + 1)
                            act.nop(nofuse=True)
                            nc.scalar.activation(q[:, s, :, :], gate[:, :, ds(u * UNIT, UNIT)], ACT.Identity, bias=rounder[:],
                                                 scale=so.inverse[:]).then_inc(rounded, 1)

                @block.tensor
                def _(pe):
                    with pe.Fori(0, NU // 2) as i:
                        for s in range(2):
                            u = i * 2 + s
                            pe.wait_ge(q_ready, u + 1)
                            for t in range(UT):
                                for m in range(M):
                                    ins = nc.tensor.matmul(y_ps[s][:, t // 2, (t % 2) * C:(t % 2 + 1) * C],
                                                           q[:, s, m, t * TT:(t + 1) * TT], downT[:, m, :],
                                                           start=(m == 0), stop=(m == M - 1))
                            ins.then_inc(y_ready, 1)

                @block.vector
                def _(dve):
                    st = Steps(dve, steps)
                    dve.sem_inc(y_free, 2)

                    def quantise(u, s):
                        dve.wait_ge(rounded, u + 1)
                        st.then(nc.vector.tensor_scalar(q[:, s, :, :], q[:, s, :, :], ROUND + QMAX, ROUND - QMAX - 1.0, ALU.min, ALU.max))
                        nc.vector.tensor_scalar(q[:, s, :, :], q[:, s, :, :], ROUND, so.step[:], ALU.subtract, ALU.mult).then_inc(q_ready, 1)

                    def add(u, s):
                        dve.wait_ge(y_ready, u + 1)
                        nc.vector.tensor_tensor(h[:, ds(u * UT, UT), :], y_ps[s][:, :, :].rearrange("p a (b c) -> p (a b) c", c=C),
                                                h[:, ds(u * UT, UT), :], ALU.add).then_inc(y_free, 1)

                    quantise(0, 0)
                    with dve.Fori(0, NU // 2 - 1) as i:
                        st.enter(i, 2)
                        for s in range(2):
                            quantise(i * 2 + s + 1, (s + 1) % 2)
                            add(i * 2 + s, s)
                        st.leave(NU // 2 - 1)
                    quantise(NU - 1, 1)
                    add(NU - 2, 0)
                    add(NU - 1, 1)


def recurrent_mix(core):
    nc, h, d = core.nc, core.h, core.dram
    HN, MIX, TM, TD = 16, 5, 32, 64
    G = C // P * HN // 2
    GN_EPS = 1e-5 * 64
    with Layer(core, "m1") as L:
        xT = L.sb("xT", [P, KC, TOK])
        layer_norm(core, "m1ln", xT)
        w1 = L.sb("w1", [P, KC, MIX * TM])
        w2a = L.sb("w2a", [P, C])
        w2b = L.sb("w2b", [TM, C])
        mx = L.sb("mx", [P, KC])
        mf = L.sb("mf", [P, MIX, KC])
        tdecay = L.sb("tdecay", [P, KC])
        td1 = L.sb("td1", [P, KC, TD])
        td2 = L.sb("td2", [TD, C])
        bonus = L.sb("bonus", [P, KC])
        wr, wk, wv, wg, wo = (L.sb(n, [P, KC, C]) for n in ("wr", "wk", "wv", "wg", "wo"))
        ln_w = L.sb("ln_w", [P, KC])
        ln_b = L.sb("ln_b", [P, KC])
        spread = L.sb("spread", [P, HN, P])
        gather = L.sb("gather", [P, HN, P])
        same = L.sb("same", [P, P])
        mean16 = L.sb("mean16", [P, P])
        xs = L.sb("xs", [P, KC, SEQ + 1])
        xx = L.sb("xx", [P, KC, SEQ])
        xxx = L.sb("xxx", [P, KC, SEQ])
        t5 = L.sb("t5", [P, 2, SEQ])
        mixed = L.sb("mixed", [P, 2, KC, SEQ])
        xf = L.sb("xf", [P, MIX, KC, SEQ])
        tw = L.sb("tw", [TD, SEQ])
        decay, r, k, v, g = (L.sb(n, [P, 2, KC, SEQ]) for n in ("decay", "r", "k", "v", "g"))
        ruk = L.sb("ruk", [P, KC, SEQ])
        yu = L.sb("yu", [P, KC, SEQ])
        kv = L.sb("kv", [P, 2, 2, SEQ])
        S = L.sb("S", [P, 2, 2, SEQ + 1])
        rS = L.sb("rS", [P, 2, 2, SEQ])
        y = L.sb("y", [P, KC, SEQ])
        square = L.sb("square", [P, KC, SEQ])
        gn_eps = L.sb("gn_eps", [P, 1])
        pr = [L.ps(f"pr{s}", [P, KC, BANK // 2]) for s in range(3)]
        vrep = [L.ps(f"vrep{s}", [P, 2, BANK // 2]) for s in range(2)]
        y_ps = L.ps("y_ps", [P, KC, BANK // 2])
        aux = L.ps("aux", [P, KC, BANK // 2])
        out_ps = L.ps("out_ps", [TT, 2, C])
        names = ("loaded const xs_ready xxx_ready pr_ready act_ev dve_ev xf_ready d_ready ruk_ready yu_ready vrep_ready "
                 "S_ready rS_ready y_part y_ready mean_ready yc_ready sq_ready var_ready std_ready z_ready "
                 "out_ready turn_done steps").split()
        (loaded, const, xs_ready, xxx_ready, pr_ready, act_ev, dve_ev, xf_ready, d_ready, ruk_ready, yu_ready, vrep_ready,
         S_ready, rS_ready, y_part, y_ready, mean_ready, yc_ready, sq_ready, var_ready, std_ready, z_ready,
         out_ready, turn_done, steps) = (L.sem(n) for n in names)
        loads = [(w1, "m1_w1"), (w2a, "m1_w2a"), (w2b, "m1_w2b"), (mx, "m1_mx"), (mf, "m1_mf"), (tdecay, "m1_tdecay"),
                 (td1, "m1_td1"), (td2, "m1_td2"), (bonus, "m1_bonus"), (wr, "m1_wr"), (wk, "m1_wk"), (wv, "m1_wv"),
                 (wg, "m1_wg"), (wo, "m1_wo"), (ln_w, "m1_lnw"), (ln_b, "m1_lnb"), (spread, "m1_spread"),
                 (gather, "m1_gather"), (same, "m1_same")]
        all_loaded = 16 * len(loads)

        PE_AT = {1: "t5", 2: "mix0", 3: "mix1", 4: "mix2", 5: "mix3", 6: "mix4", 9: "td1", 12: "k", 14: "td2"}
        DVE_AT = {0: "shift", 2: "mix0", 3: "mix1", 4: "mix2", 5: "mix3", 6: "mix4"}
        POOL_AT = {0: "shift", 3: "mix0", 4: "mix1", 5: "mix2", 6: "mix3", 7: "mix4"}

        def over_turns(eng, front, turn, st=None, steps_of_turn=None):
            front(0, 0)
            with eng.Fori(0, SEQS // 2 - 1) as i:
                if st is not None:
                    st.enter(i, 2 * steps_of_turn)
                turn(i * 2, 0)
                turn(i * 2 + 1, 1)
                if st is not None:
                    st.leave(SEQS // 2 - 1)
            turn(SEQS - 2, 0)
            turn(SEQS - 1, 1, last=True)

        with nc.Block() as block:

            @block.sync
            def _(sp):
                for dst, name in loads:
                    sp.dma_start(dst[:], d[name]).then_inc(loaded, 16)

            @block.gpsimd
            def _(pool):
                pool.wait_ge(loaded, all_loaded)
                nc.gpsimd.memset(xs[:], 0.0)
                nc.gpsimd.memset(S[:], 0.0)
                nc.gpsimd.memset(gn_eps[:], GN_EPS)
                nc.gpsimd.tensor_scalar(mean16[:], same[:], 1.0 / HN, None, ALU.mult).then_inc(const, 1)
                pool.wait_ge(const, 1)

                def front(b, s, task=None):
                    if task in (None, "shift"):
                        if not (isinstance(b, int) and b == 0):
                            pool.wait_ge(pr_ready, b * 12)
                            pool.nop(nofuse=True)
                            pool.wait_ge(xf_ready, b * MIX)
                        nc.gpsimd.tensor_copy(xs[:, :, 1:SEQ + 1], xT[:, :, ds(b * SEQ, SEQ)]).then_inc(xs_ready, 1)
                    for f in range(MIX):
                        if task in (None, f"mix{f}"):
                            pool.wait_ge(dve_ev, b * MIX + f + 1)
                            if f == 0:
                                pool.nop(nofuse=True)
                                pool.wait_ge(xs_ready, b + 1)
                            nc.gpsimd.tensor_tensor(xf[:, f, :, :], mixed[:, f % 2, :, :], xs[:, :, 1:SEQ + 1],
                                                    ALU.add).then_inc(xf_ready, 1)

                def turn(b, s, last=False):
                    for n in range(G):
                        c = n // (HN // 2)
                        if n == 0 and not last:
                            front(b + 1, 1 - s, "shift")
                        pool.wait_ge(S_ready, b * G + n + 1)
                        if n == 0:
                            pool.nop(nofuse=True)
                            pool.wait_ge(act_ev, b * 7 + 6)
                        if n >= 2:
                            pool.nop(nofuse=True)
                            pool.wait_ge(y_part, b * G + n - 1)
                        nc.gpsimd.tensor_tensor(rS[:, n % 2, :, :], S[:, n % 2, :, 0:SEQ],
                                                r[:, s, c:c + 1, :].broadcast_to([P, 2, SEQ]), ALU.mult).then_inc(rS_ready, 1)
                        if n > 0 and n in POOL_AT and not last:
                            front(b + 1, 1 - s, POOL_AT[n])

                over_turns(pool, front, turn)

            @block.tensor
            def _(pe):
                def project(n, lhs, rhs, rows=P):
                    for c in range(len(lhs)):
                        for i in range(len(rhs)):
                            ins = nc.tensor.matmul(pr[n % 3][0:rows, c, 0:SEQ], lhs[c][i], rhs[i],
                                                   start=(i == 0), stop=(i == len(rhs) - 1))
                    ins.then_inc(pr_ready, 1)

                def weights(w):
                    return [[w[:, i, c * P:(c + 1) * P] for i in range(KC)] for c in range(KC)]

                def stream(f):
                    return [xf[:, f, i, :] for i in range(KC)]

                def front(b, s, task=None):
                    if task in (None, "t5"):
                        pe.wait_ge(xxx_ready, b + 1)
                        for i in range(KC):
                            nc.tensor.matmul(pr[0][:, 0, 0:SEQ], w1[:, i, 0:4 * TM], xxx[:, i, :], start=(i == 0), stop=(i == KC - 1))
                        for i in range(KC):
                            ins = nc.tensor.matmul(pr[0][0:TM, 1, 0:SEQ], w1[:, i, 4 * TM:], xxx[:, i, :],
                                                   start=(i == 0), stop=(i == KC - 1))
                        ins.then_inc(pr_ready, 1)
                    for f in range(MIX):
                        if task in (None, f"mix{f}"):
                            if f == 0:
                                pe.wait_ge(act_ev, b * 7 + 1)
                            if f >= 3:
                                pe.wait_ge(dve_ev, b * MIX + f - 2)
                            rows = slice(TM * f, TM * f + TM)
                            lhs = [[(w2a[rows, c * P:(c + 1) * P] if f < 4 else w2b[:, c * P:(c + 1) * P])] for c in range(KC)]
                            project(f + 1, lhs, [t5[rows, 0, :] if f < 4 else t5[0:TM, 1, :]])
                    if task in (None, "td1"):
                        pe.wait_ge(xf_ready, b * MIX + 1)
                        pe.nop(nofuse=True)
                        pe.wait_ge(dve_ev, b * MIX + 3)
                        project(6, [[td1[:, i, :] for i in range(KC)]], stream(0), rows=TD)
                    if task in (None, "k"):
                        pe.wait_ge(dve_ev, b * MIX + 4)
                        pe.nop(nofuse=True)
                        pe.wait_ge(xf_ready, b * MIX + 2)
                        project(7, weights(wk), stream(1))
                    if task in (None, "td2"):
                        pe.wait_ge(dve_ev, b * MIX + 5)
                        pe.nop(nofuse=True)
                        pe.wait_ge(act_ev, b * 7 + 2)
                        project(8, [[td2[:, c * P:(c + 1) * P]] for c in range(KC)], [tw[:]])
                    if task in (None, "v"):
                        pe.wait_ge(xf_ready, b * MIX + 3)
                        project(9, weights(wv), stream(2))
                    if task in (None, "r"):
                        pe.wait_ge(xf_ready, b * MIX + 4)
                        pe.nop(nofuse=True)
                        pe.wait_ge(act_ev, b * 7 + 3)
                        project(10, weights(wr), stream(3))
                    if task in (None, "g"):
                        pe.wait_ge(xf_ready, b * MIX + 5)
                        pe.nop(nofuse=True)
                        pe.wait_ge(act_ev, b * 7 + 4)
                        project(11, weights(wg), stream(4))

                def turn(b, s, last=False):
                    def spread_v(n):
                        c, j = n // (HN // 2), 2 * (n % (HN // 2))
                        if n == 0:
                            pe.wait_ge(act_ev, b * 7 + 5)
                        if n >= 2:
                            pe.wait_ge(S_ready, b * G + n - 1)
                        for p in range(2):
                            ins = nc.tensor.matmul(vrep[n % 2][:, p, 0:SEQ], spread[:, j + p, :], v[:, s, c, :], start=True, stop=True)
                        ins.then_inc(vrep_ready, 1)

                    def sum_i(n):
                        c, j = n // (HN // 2), 2 * (n % (HN // 2))
                        pe.wait_ge(rS_ready, b * G + n + 1)
                        for p in range(2):
                            ins = nc.tensor.matmul(y_ps[:, c, 0:SEQ], gather[:, j + p, :], rS[:, n % 2, p, :],
                                                   start=(j + p == 0), stop=(j + p == HN - 1))
                        ins.then_inc(y_part, 1)

                    for n in range(G + 2):
                        if n < G:
                            spread_v(n)
                        if n == 2:
                            pe.wait_ge(ruk_ready, b + 1)
                            for c in range(KC):
                                ins = nc.tensor.matmul(aux[:, c, 0:SEQ], same[:], ruk[:, c, :], start=True, stop=True)
                            ins.then_inc(yu_ready, 1)
                        if n in PE_AT and not last:
                            front(b + 1, 1 - s, PE_AT[n])
                        if n >= 2:
                            sum_i(n - 2)
                    pe.wait_ge(y_ready, b + 1)
                    for c in range(KC):
                        ins = nc.tensor.matmul(aux[:, c, 0:SEQ], mean16[:], y[:, c, :], start=True, stop=True)
                    ins.then_inc(mean_ready, 1)
                    if not last:
                        front(b + 1, 1 - s, "v")
                    pe.wait_ge(sq_ready, b + 1)
                    for c in range(KC):
                        ins = nc.tensor.matmul(aux[:, c, 0:SEQ], mean16[:], square[:, c, :], start=True, stop=True)
                    ins.then_inc(var_ready, 1)
                    if not last:
                        front(b + 1, 1 - s, "r")
                        front(b + 1, 1 - s, "g")
                    pe.wait_ge(z_ready, b + 1)
                    for a in range(2):
                        for i in range(KC):
                            ins = nc.tensor.matmul(out_ps[:, a, :], y[:, i, a * TT:(a + 1) * TT], wo[:, i, :],
                                                   start=(i == 0), stop=(i == KC - 1))
                    ins.then_inc(out_ready, 1)

                pe.wait_ge(const, 1)
                over_turns(pe, front, turn)

            @block.scalar
            def _(act):
                def front(b, s, task=None):
                    if task in (None, "first"):
                        act.wait_ge(pr_ready, b * 12 + 1)
                        nc.scalar.activation(t5[:, 0, :], pr[0][:, 0, 0:SEQ], ACT.Tanh)
                        nc.scalar.activation(t5[0:TM, 1, :], pr[0][0:TM, 1, 0:SEQ], ACT.Tanh).then_inc(act_ev, 1)
                        act.wait_ge(pr_ready, b * 12 + 7)
                        nc.scalar.activation(tw[:], pr[0][0:TD, 0, 0:SEQ], ACT.Tanh).then_inc(act_ev, 1)
                        act.wait_ge(pr_ready, b * 12 + 8)
                        if not (isinstance(b, int) and b == 0):
                            act.nop(nofuse=True)
                            act.wait_ge(turn_done, b)
                        nc.scalar.copy(k[:, s, :, :], pr[1][:, :, 0:SEQ]).then_inc(act_ev, 1)
                        act.wait_ge(pr_ready, b * 12 + 9)
                        for c in range(KC):
                            ins = nc.scalar.activation(decay[:, s, c, :], pr[2][:, c, 0:SEQ], ACT.Exp, bias=tdecay[:, c:c + 1])
                        ins.then_inc(act_ev, 1)
                        act.wait_ge(act_ev, b * 7 + 4)
                        nc.scalar.activation(decay[:, s, :, :], decay[:, s, :, :], ACT.Exp, scale=-1.0).then_inc(d_ready, 1)
                    if task in (None, "v"):
                        act.wait_ge(pr_ready, b * 12 + 10)
                        nc.scalar.copy(v[:, s, :, :], pr[0][:, :, 0:SEQ]).then_inc(act_ev, 1)
                    if task in (None, "r g"):
                        act.wait_ge(pr_ready, b * 12 + 11)
                        nc.scalar.copy(r[:, s, :, :], pr[1][:, :, 0:SEQ]).then_inc(act_ev, 1)
                        act.wait_ge(pr_ready, b * 12 + 12)
                        nc.scalar.activation(g[:, s, :, :], pr[2][:, :, 0:SEQ], ACT.Silu).then_inc(act_ev, 1)

                def turn(b, s, last=False):
                    if not last:
                        front(b + 1, 1 - s, "first")
                    act.wait_ge(yc_ready, b + 1)
                    nc.scalar.activation(square[:], y[:], ACT.Square).then_inc(sq_ready, 1)
                    if not last:
                        front(b + 1, 1 - s, "v")
                    act.wait_ge(var_ready, b + 1)
                    nc.scalar.activation(square[:], aux[:, :, 0:SEQ], ACT.Sqrt, bias=gn_eps[:]).then_inc(std_ready, 1)
                    if not last:
                        front(b + 1, 1 - s, "r g")

                act.wait_ge(const, 1)
                over_turns(act, front, turn)

            @block.vector
            def _(dve):
                st = Steps(dve, steps)
                V = nc.vector

                def front(b, s, task=None):
                    if task in (None, "shift"):
                        dve.wait_ge(xs_ready, b + 1)
                        st.then(V.tensor_tensor(xx[:], xs[:, :, 0:SEQ], xs[:, :, 1:SEQ + 1], ALU.subtract))
                        for c in range(KC):
                            ins = V.scalar_tensor_tensor(out=xxx[:, c, :], in0=xx[:, c, :], scalar=mx[:, c:c + 1],
                                                         in1=xs[:, c, 1:SEQ + 1], op0=ALU.mult, op1=ALU.add)
                        ins.then_inc(xxx_ready, 1)
                    for f in range(MIX):
                        if task in (None, f"mix{f}"):
                            dve.wait_ge(pr_ready, b * 12 + f + 2)
                            if f >= 2:
                                dve.nop(nofuse=True)
                                dve.wait_ge(xf_ready, b * MIX + f - 1)
                            for c in range(KC):
                                ins = V.scalar_tensor_tensor(out=mixed[:, f % 2, c, :], in0=pr[(f + 1) % 3][:, c, 0:SEQ],
                                                             scalar=mf[:, f, c:c + 1], in1=xx[:, c, :], op0=ALU.add, op1=ALU.mult)
                            ins.then_inc(dve_ev, 1)

                def turn(b, s, last=False):
                    dve.wait_ge(act_ev, b * 7 + 6)
                    for c in range(KC):
                        ins = V.scalar_tensor_tensor(out=ruk[:, c, :], in0=r[:, s, c, :], scalar=bonus[:, c:c + 1],
                                                     in1=k[:, s, c, :], op0=ALU.mult, op1=ALU.mult)
                    ins.then_inc(ruk_ready, 1)
                    dve.wait_ge(d_ready, b + 1)
                    for n in range(G):
                        c = n // (HN // 2)
                        dve.wait_ge(vrep_ready, b * G + n + 1)
                        st.then(V.tensor_tensor(kv[:, n % 2, :, :], vrep[n % 2][:, :, 0:SEQ],
                                                k[:, s, c:c + 1, :].broadcast_to([P, 2, SEQ]), ALU.mult))
                        if n >= 2:
                            dve.nop(nofuse=True)
                            dve.wait_ge(rS_ready, b * G + n - 1)
                            dve.nop(nofuse=True)
                        for p in range(2):
                            ins = V.tensor_tensor_scan(S[:, n % 2, p, 1:SEQ], decay[:, s, c, 0:SEQ - 1], kv[:, n % 2, p, 0:SEQ - 1],
                                                       0.0, ALU.mult, ALU.add)
                        ins.then_inc(S_ready, 1)
                        if n == 5:
                            dve.wait_ge(yu_ready, b + 1)
                            V.tensor_tensor(yu[:], aux[:, :, 0:SEQ], v[:, s, :, :], ALU.mult)
                        if n in DVE_AT and not last:
                            front(b + 1, 1 - s, DVE_AT[n])
                    dve.wait_ge(y_part, (b + 1) * G)
                    V.tensor_tensor(y[:], y_ps[:, :, 0:SEQ], yu[:], ALU.add).then_inc(y_ready, 1)
                    dve.wait_ge(mean_ready, b + 1)
                    V.tensor_tensor(y[:], y[:], aux[:, :, 0:SEQ], ALU.subtract).then_inc(yc_ready, 1)
                    dve.wait_ge(std_ready, b + 1)
                    st.then(V.reciprocal(square[:], square[:]))
                    st.then(V.tensor_tensor(y[:], y[:], square[:], ALU.mult))
                    for c in range(KC):
                        ins = V.tensor_scalar(y[:, c, :], y[:, c, :], ln_w[:, c:c + 1], ln_b[:, c:c + 1], ALU.mult, ALU.add)
                    st.then(ins)
                    dve.nop(nofuse=True)
                    dve.wait_ge(act_ev, (b + 1) * 7)
                    V.tensor_tensor(y[:], y[:], g[:, s, :, :], ALU.mult).then_inc(z_ready, 1)
                    dve.wait_ge(out_ready, b + 1)
                    V.tensor_tensor(h[:, ds(b * 2, 2), :], out_ps[:], h[:, ds(b * 2, 2), :], ALU.add).then_inc(turn_done, 1)

                dve.wait_ge(const, 1)
                dve.sem_inc(turn_done, 1)
                over_turns(dve, front, turn, st, 1 + G + 3)


LAYERS = [token_patches, taylor_attention, top1_experts, recurrent_mix, quantised_mlp, softmax_attention, grouped_experts, long_convolution, top2_experts]


def tower(nc, dram, out):
    with ExitStack() as ctx:
        core = Core(nc, ctx, dram)
        constants(core)
        for layer in LAYERS:
            layer(core)
        store_stream(core, out)


def layouts(a):
    import numpy as np

    def cm(w):
        return w.reshape(-1, P, w.shape[-1]).transpose(1, 0, 2)

    def flat(w):
        return w.reshape(w.shape[0], -1)

    def columns(b):
        return b.reshape(-1, P).T

    def up(w):
        return w.reshape(w.shape[0], KC, P, -1).transpose(0, 2, 1, 3).reshape(w.shape[0], P, -1)

    def down(w):
        return w.reshape(w.shape[0], -1, P, w.shape[2]).transpose(0, 2, 1, 3).reshape(w.shape[0], P, -1)

    def bias(b):
        return b.reshape(b.shape[0], -1, P).transpose(0, 2, 1)

    d = {}
    patch = 16
    d["tok_x"] = a["x"].reshape(-1, patch).T
    d["tok_wh"] = a["L0_tok_W_h"].T
    d["tok_bh"] = columns(a["L0_tok_b_h"])
    d["tok_wo"] = cm(a["L0_tok_W_o"].T)
    d["tok_wr"] = np.concatenate([a["L0_tok_W_r"].T, a["L0_tok_b_r"][None], a["L0_tok_b_o"][None]])
    d["f0_wg"] = cm(a["L0_ffn_Wg"])
    d["f0_bg"] = a["L0_ffn_bg"][:, None]
    d["f0_w1"] = up(a["L0_ffn_W1"])
    d["f0_b1"] = bias(a["L0_ffn_b1"])
    d["f0_w2"] = down(a["L0_ffn_W2"])
    d["f0_b2"] = a["L0_ffn_b2"]
    d["f2_wg"] = cm(a["L2_ffn_gate_w"].T)
    d["f2_bias"] = a["L2_ffn_bias_e"][None]
    d["f2_w1"] = up(a["L2_ffn_up_w"].transpose(0, 2, 1))
    d["f2_w2"] = down(a["L2_ffn_down_w"].transpose(0, 2, 1))
    d["f2_s1"] = up(a["L2_ffn_shared_up"].T[None])
    d["f2_s2"] = down(a["L2_ffn_shared_down"].T[None])
    d["f3_wg"] = cm(a["L3_ffn_router_w"].T)
    d["f3_w1"] = up(a["L3_ffn_w1"].transpose(0, 2, 1))
    d["f3_b1"] = bias(a["L3_ffn_b1"])
    d["f3_w2"] = down(a["L3_ffn_w2"].transpose(0, 2, 1))
    d["f3_b2"] = a["L3_ffn_b2"]
    def spread(w):
        heads = w.reshape(w.shape[:-1] + (-1, 16))
        return np.concatenate([heads, np.zeros_like(heads)], -1).reshape(w.shape[:-1] + (-1,))

    for n in ("q", "k"):
        d["a2_w" + n] = cm(spread(a["L2_attn_W" + n].T))
        d["a2_b" + n] = columns(spread(a["L2_attn_b" + n]))
    for n in ("v", "o"):
        d["a2_w" + n] = cm(a["L2_attn_W" + n].T)
        d["a2_b" + n] = a["L2_attn_b" + n][None]
    def spread(w):
        heads = w.reshape(w.shape[:-1] + (-1, 16))
        return np.concatenate([heads, np.zeros_like(heads)], -1).reshape(w.shape[:-1] + (-1,))

    d["a0_gamma"] = columns(a["L0_attn_gamma"])
    d["a0_wq"] = cm(spread(a["L0_attn_w_q"]))
    kv = a["L0_attn_w_kv"]
    d["a0_wk"], d["a0_wv"] = cm(spread(kv[:, :kv.shape[1] // 2])), cm(kv[:, kv.shape[1] // 2:])
    d["a0_wo"] = a["L0_attn_w_out"]
    d["a3_lre"], d["a3_lim"] = a["L3_attn_Lambda_real"][:, None], a["L3_attn_Lambda_imag"][:, None]
    d["a3_cre"], d["a3_cim"] = a["L3_attn_C_real"].T, a["L3_attn_C_imag"].T
    d["a3_gain"], d["a3_shift"], d["a3_skip"] = (a["L3_attn_" + n][None] for n in ("ln_gamma", "ln_beta", "param_D"))
    f, t = np.arange(SEQ)[:, None], np.arange(SEQ)[None, :]
    turn = np.pi * ((f * t) % (2 * SEQ)) / SEQ
    sines = np.sin(turn)
    sines[0] = np.cos(np.pi * t[0])
    waves = np.concatenate([np.cos(turn), sines])
    weight = np.full((2, SEQ, 1), 2.0)
    weight[:, 0] = 1.0
    d["a3_F"] = waves.T.reshape(2, TT, 2 * SEQ).transpose(1, 0, 2).astype(np.float32)
    d["a3_G"] = (waves * weight.reshape(-1, 1) / (2 * SEQ)).reshape(4, TT, SEQ).transpose(1, 0, 2).astype(np.float32)
    d["f1_gate"], d["f1_up"], d["f1_down"] = (cm(a["L1_ffn_w_" + n]) for n in ("gate", "up", "down"))
    m = {n[len("L1_attn_"):]: v for n, v in a.items() if n.startswith("L1_attn_")}
    d["m1_w1"] = cm(m["time_maa_w1"])
    w2 = m["time_maa_w2"]
    d["m1_w2a"], d["m1_w2b"] = w2[:4].reshape(P, C), w2[4]
    d["m1_mx"] = columns(m["time_maa_x"].reshape(-1))
    d["m1_mf"] = np.stack([columns(m["time_maa_" + f].reshape(-1)) for f in "wkvrg"], 1)
    d["m1_tdecay"], d["m1_bonus"] = columns(m["time_decay"].reshape(-1)), columns(m["time_faaaa"].reshape(-1))
    d["m1_td1"], d["m1_td2"] = cm(m["time_decay_w1"]), m["time_decay_w2"]
    for n in "rkvgo":
        d["m1_w" + n] = cm(m["W_" + n])
    d["m1_lnw"], d["m1_lnb"] = columns(m["ln_w"]), columns(m["ln_b"])
    ch = np.arange(P)
    same = (ch[:, None] // 16 == ch[None, :] // 16)
    spread01 = (same[:, None, :] & (ch[:, None, None] % 16 == np.arange(16)[None, :, None])).astype(np.float32)
    d["m1_spread"], d["m1_gather"] = spread01, spread01.transpose(2, 1, 0)
    d["m1_same"] = same.astype(np.float32)
    return {n: np.ascontiguousarray(v) for n, v in d.items()}


def kernel(**inputs):
    import numpy as _np
    import concourse.bacc as _bacc
    from concourse import mybir as _mybir
    from concourse.bass_utils import run_bass_kernel_spmd as _run

    nc = _bacc.Bacc("TRN2", target_bir_lowering=False, num_devices=1)
    arrays, dram = {}, {}
    for name, a in layouts(inputs).items():
        arrays[f"in_{name}_dram"] = a
        dram[name] = nc.dram_tensor(f"in_{name}_dram", a.shape, _mybir.dt.from_np(a.dtype), kind="ExternalInput").ap()
    out = nc.dram_tensor("out_0_dram", (SEQS, SEQ, C), _mybir.dt.float32, kind="ExternalOutput").ap()
    tower(nc, dram, out)
    r = _run(nc, [arrays], core_ids=[0])
    return r.results[0]["out_0_dram"]
```

```python
from contextlib import ExitStack

import concourse.bass as bass
from concourse import mybir

F32 = mybir.dt.float32
I32 = mybir.dt.int32
BF16 = mybir.dt.bfloat16
ACT = mybir.ActivationFunctionType
ALU = mybir.AluOpType
AX = mybir.AxisListType
ds = bass.ds

SEQS = 16
SEQ = 250
C = 256
P = 128
KC = C // P
TT = 125
NT = SEQS * SEQ // TT
UT = 4
UNIT = UT * TT
NU = NT // UT
TOK = SEQS * SEQ
BANK = 512
LN_EPS = 1e-5


class Steps:

    def __init__(self, eng, sem):
        self.eng, self.sem, self.base, self.k, self.turn, self.per = eng, sem, 0, 0, None, 0

    def then(self, ins):
        ins.then_inc(self.sem, 1)
        self.k += 1
        value = self.base + self.k
        self.eng.wait_ge(self.sem, value if self.turn is None else self.turn * self.per + value)

    def enter(self, turn, per):
        self.base += self.k
        self.k, self.turn, self.per = 0, turn, per

    def leave(self, turns):
        assert self.k == self.per, (self.k, self.per)
        self.base += self.per * turns
        self.k, self.turn = 0, None


class Core:

    def __init__(self, nc, ctx, dram):
        self.nc, self.ctx, self.dram = nc, ctx, dram
        self.h = ctx.enter_context(nc.sbuf_tensor("h", [TT, NT, C], F32))
        self.ident = ctx.enter_context(nc.sbuf_tensor("ident", [P, P], F32))


class Layer:

    def __init__(self, core, name):
        self.core, self.nc, self.name, self.stack = core, core.nc, name, ExitStack()
        self.sems = []

    def __enter__(self):
        self.stack.__enter__()
        return self

    def __exit__(self, *a):
        if self.sems and a[0] is None:
            with self.nc.Block() as block:

                @block.gpsimd
                def _(pool):
                    for sem in self.sems:
                        pool.sem_clear(sem)
        return self.stack.__exit__(*a)

    def sb(self, name, shape, dt=F32):
        return self.stack.enter_context(self.nc.sbuf_tensor(f"{self.name}_{name}", shape, dt))

    def ps(self, name, shape, dt=F32):
        return self.stack.enter_context(self.nc.psum_tensor(f"{self.name}_{name}", shape, dt))

    def sem(self, name):
        self.sems.append(self.stack.enter_context(self.nc.semaphore(f"{self.name}_{name}")))
        return self.sems[-1]

    def pool_dma_sem(self, name):
        return self.core.ctx.enter_context(self.nc.semaphore(f"{self.name}_{name}"))


def constants(core):
    nc, ident = core.nc, core.ident
    with Layer(core, "const") as L:
        filled = L.sem("filled")
        with nc.Block() as block:

            @block.gpsimd
            def _(pool):
                nc.gpsimd.memset(ident[:], 0.0).then_inc(filled, 1)
                pool.wait_ge(filled, 1)
                nc.gpsimd.affine_select(out=ident[:], in_=ident[:], compare_op=ALU.not_equal, fill=1.0,
                                        base=0, pattern=[[-1, P]], channel_multiplier=1)


def store_stream(core, dst):
    nc = core.nc
    with Layer(core, "out") as L:
        stored = L.sem("stored")
        with nc.Block() as block:

            @block.sync
            def _(sp):
                sp.dma_start(dst.rearrange("b (s p) c -> p (b s) c", p=TT), core.h[:]).then_inc(stored, 16)
                sp.wait_ge(stored, 16)


def layer_norm(core, name, xT, rms_gain=None, keep=None, beside=None):
    nc, h, ident = core.nc, core.h, core.ident
    with Layer(core, name) as L:
        stats = L.sb("stats", [TT, 2, UT, 6])
        moments = L.sb("moments", [TT, 2, UT, 2])
        eps_var = L.sb("eps_var", [TT, 2, UT])
        power = L.sb("power", [TT, UT])
        rstd = L.sb("rstd", [TT, 2, UT])
        xn = L.sb("xn", [TT, 2, UT, C])
        square = L.sb("square", [TT, UT, C])
        norm2 = L.sb("norm2", [TT, 2, UT])
        rnorm = L.sb("rnorm", [TT, 2, UT])
        turned = [L.ps(f"turned{s}", [P, KC, BANK]) for s in range(2)]
        steps = L.sem("steps")
        power_set = L.sem("power_set")
        var_ready = L.sem("var_ready")
        rstd_ready = L.sem("rstd_ready")
        norm_ready = L.sem("norm_ready")
        rnorm_ready = L.sem("rnorm_ready")
        xn_ready = L.sem("xn_ready")
        xn_free = L.sem("xn_free")
        out_ready = L.sem("out_ready")
        kept = L.sem("kept")
        rms = rms_gain is not None

        with nc.Block() as block:

            @block.sync
            def _(sp):
                if beside is not None:
                    beside(sp)

            @block.vector
            def _(dve):
                st = Steps(dve, steps)
                nc.vector.memset(power[:], -0.5).then_inc(power_set, 1)

                def measure(u, s):
                    for t in range(UT):
                        ins = nc.vector.bn_stats(stats[:, s, t, :], h[:, ds(u * UT + t, 1), :])
                    st.then(ins)
                    dve.nop(nofuse=True)
                    for t in range(UT):
                        ins = nc.vector.bn_aggr(moments[:, s, t, :], stats[:, s, t, :])
                    st.then(ins)
                    nc.vector.tensor_scalar(eps_var[:, s, :], moments[:, s, :, 1], LN_EPS, None,
                                            ALU.add).then_inc(var_ready, 1)

                def normalise(u, s):
                    dve.wait_ge(rstd_ready, u + 1)
                    dve.nop(nofuse=True)
                    dve.wait_ge(xn_free, u + 1)
                    if keep is not None:
                        dve.nop(nofuse=True)
                        dve.wait_ge(kept, u + 1)
                    for t in range(UT):
                        ins = nc.vector.tensor_scalar(xn[:, s, t, :], h[:, ds(u * UT + t, 1), :].rearrange("p a c -> p (a c)"),
                                                      moments[:, s, t, 0:1], rstd[:, s, t:t + 1],
                                                      ALU.subtract, ALU.mult)
                    if rms:
                        st.then(ins)
                        st.then(nc.vector.tensor_tensor(square[:], xn[:, s, :, :], xn[:, s, :, :], ALU.mult))
                        st.then(nc.vector.reduce_sum(norm2[:, s, :], square[:], AX.X))
                        nc.vector.tensor_scalar(norm2[:, s, :], norm2[:, s, :], 1e-24, None,
                                                ALU.max).then_inc(norm_ready, 1)
                        dve.wait_ge(rnorm_ready, u + 1)
                        for t in range(UT):
                            ins = nc.vector.tensor_scalar(xn[:, s, t, :], xn[:, s, t, :], rnorm[:, s, t:t + 1],
                                                          float(C) ** 0.5, ALU.mult, ALU.mult)
                    ins.then_inc(xn_ready, 1)

                measure(0, 0)
                with dve.Fori(0, NU // 2 - 1) as i:
                    st.enter(i, 2 * (2 + (3 if rms else 0)))
                    for s in range(2):
                        measure(i * 2 + s + 1, 1 - s)
                        normalise(i * 2 + s, s)
                    st.leave(NU // 2 - 1)
                measure(NU - 1, 1)
                normalise(NU - 2, 0)
                normalise(NU - 1, 1)

            @block.gpsimd
            def _(pool):
                pool.wait_ge(power_set, 1)
                if keep is not None:
                    pool.sem_inc(kept, 2)
                with pool.Fori(0, NU // 2) as i:
                    for s in range(2):
                        u = i * 2 + s
                        pool.wait_ge(var_ready, u + 1)
                        nc.gpsimd.tensor_tensor(rstd[:, s, :], eps_var[:, s, :], power[:], ALU.pow).then_inc(rstd_ready, 1)
                        if rms:
                            pool.wait_ge(norm_ready, u + 1)
                            nc.gpsimd.tensor_tensor(rnorm[:, s, :], norm2[:, s, :], power[:], ALU.pow).then_inc(rnorm_ready, 1)
                        if keep is not None:
                            pool.wait_ge(xn_ready, u + 1)
                            nc.gpsimd.tensor_copy(keep[:, ds(u * UT, UT), :], xn[:, s, :, :]).then_inc(kept, 1)

            @block.tensor
            def _(pe):
                pe.sem_inc(xn_free, 2)
                with pe.Fori(0, NU // 2) as i:
                    for s in range(2):
                        u = i * 2 + s
                        pe.wait_ge(xn_ready, u + 1)
                        pe.wait_ge(out_ready, u + 1)
                        for t in range(UT):
                            for k in range(KC):
                                ins = nc.tensor.transpose(turned[s][:, k, t * TT:(t + 1) * TT],
                                                          xn[:, s, t, k * P:(k + 1) * P], ident[0:TT, 0:TT])
                        ins.then_inc(xn_free, 1)

            @block.scalar
            def _(act):
                act.sem_inc(out_ready, 2)
                with act.Fori(0, NU // 2) as i:
                    for s in range(2):
                        u = i * 2 + s
                        act.wait_ge(xn_free, u + 3)
                        for k in range(KC):
                            if rms:
                                ins = nc.scalar.activation(xT[:, k, ds(u * UNIT, UNIT)], turned[s][:, k, 0:UNIT],
                                                           ACT.Copy, scale=rms_gain[:, k:k + 1])
                            else:
                                ins = nc.scalar.activation(xT[:, k, ds(u * UNIT, UNIT)], turned[s][:, k, 0:UNIT], ACT.Copy)
                        ins.then_inc(out_ready, 1)


def token_patches(core):
    nc, h, dram = core.nc, core.h, core.dram
    hid_w, hid_tiles = dram["tok_wh"].shape[1], dram["tok_wh"].shape[1] // P
    pa, rows, mrows = dram["tok_x"].shape[0], dram["tok_wr"].shape[0], dram["tok_wh"].shape[0]
    with Layer(core, "tok") as L:
        patch = L.sb("patch", [rows, TOK])
        unit = L.sb("unit", [rows, 2, UNIT])
        wh = L.sb("wh", [mrows, hid_w])
        bh = L.sb("bh", [P, hid_tiles])
        wo = L.sb("wo", [P, hid_tiles, C])
        wr = L.sb("wr", [rows, C])
        hid = L.sb("hid", [P, 2, hid_tiles, UNIT])
        hid_ps = [L.ps(f"hid_ps{s}", [P, BANK]) for s in range(4)]
        y_ps = [L.ps(f"y_ps{s}", [TT, UT // 2, BANK]) for s in range(2)]
        ones_set = L.sem("ones_set")
        loaded = L.sem("loaded")
        unit_ready = L.sem("unit_ready")
        hid_ready = L.sem("hid_ready")
        hid_done = L.sem("hid_done")
        y_ready = L.sem("y_ready")
        y_free = L.sem("y_free")
        with nc.Block() as block:

            @block.sync
            def _(sp):
                sp.wait_ge(ones_set, 1)
                for dst, src in ((patch[0:pa, :], dram["tok_x"]), (wh[:], dram["tok_wh"]), (bh[:], dram["tok_bh"]),
                                 (wo[:], dram["tok_wo"]), (wr[:], dram["tok_wr"])):
                    sp.dma_start(dst, src).then_inc(loaded, 16)

            @block.gpsimd
            def _(pool):
                nc.gpsimd.memset(patch[:], 1.0).then_inc(ones_set, 1)
                pool.wait_ge(loaded, 16 * 5)
                with pool.Fori(0, NU // 2) as i:
                    for s in range(2):
                        u = i * 2 + s
                        pool.wait_ge(y_free, u + 1)
                        nc.gpsimd.tensor_copy(unit[:, s, :], patch[:, ds(u * UNIT, UNIT)]).then_inc(unit_ready, 1)

            @block.tensor
            def _(pe):
                with pe.Fori(0, NU // 2) as i:
                    for s in range(2):
                        u = i * 2 + s
                        pe.wait_ge(unit_ready, u + 1)
                        for m in range(hid_tiles):
                            pe.wait_ge(hid_done, u * hid_tiles + m + 1)
                            nc.tensor.matmul(hid_ps[m % 4][:, 0:UNIT], wh[:, m * P:(m + 1) * P], unit[0:mrows, s, :],
                                             start=True, stop=True).then_inc(hid_ready, 1)
                        pe.wait_ge(hid_done, u * hid_tiles + hid_tiles + 4)
                        pe.wait_ge(y_free, u + 1)
                        for t in range(UT):
                            y = y_ps[s][:, t // 2, (t % 2) * C:(t % 2 + 1) * C]
                            nc.tensor.matmul(y, unit[:, s, t * TT:(t + 1) * TT], wr[:], start=(t % 2 == 0), stop=False,
                                             skip_group_check=True)
                            for m in range(hid_tiles):
                                ins = nc.tensor.matmul(y, hid[:, s, m, t * TT:(t + 1) * TT], wo[:, m, :], start=False,
                                                       stop=(m == hid_tiles - 1), skip_group_check=True)
                        ins.then_inc(y_ready, 1)

            @block.scalar
            def _(act):
                act.sem_inc(hid_done, 4)
                act.wait_ge(loaded, 16 * 5)
                with act.Fori(0, NU // 2) as i:
                    for s in range(2):
                        u = i * 2 + s
                        act.wait_ge(y_free, u + 1)
                        for m in range(hid_tiles):
                            act.wait_ge(hid_ready, u * hid_tiles + m + 1)
                            nc.scalar.activation(hid[:, s, m, :], hid_ps[m % 4][:, 0:UNIT], ACT.Silu,
                                                 bias=bh[:, m:m + 1]).then_inc(hid_done, 1)

            @block.vector
            def _(dve):
                dve.sem_inc(y_free, 2)
                with dve.Fori(0, NU // 2) as i:
                    for s in range(2):
                        u = i * 2 + s
                        dve.wait_ge(y_ready, u + 1)
                        nc.vector.tensor_copy(h[:, ds(u * UT, UT), :],
                                              y_ps[s][:, :, :].rearrange("p a (b c) -> p (a b) c", c=C)).then_inc(y_free, 1)


def route(core, name, xT, v, wg, bg, pick, beside=None):
    nc, ident = core.nc, core.ident
    E = v.shape[2]
    with Layer(core, name) as L:
        wg_sb = L.sb("wg", [P, KC, E])
        bg_sb = L.sb("bg", [E, 1])
        logitT = L.sb("logitT", [E, 2, UNIT])
        before = L.sb("before", [TT, E, E])
        work = pick.buffers(L, E)
        logit_ps = [L.ps(f"logit_ps{s}", [E, BANK]) for s in range(2)]
        v_ps = L.ps("v_ps", [TT, NT, E])
        loaded = L.sem("loaded")
        table = L.sem("table")
        logit_ready = L.sem("logit_ready")
        logitT_ready = L.sem("logitT_ready")
        turned = L.sem("turned")
        steps = L.sem("steps")
        act_ready = L.sem("act_ready")
        act_asked = L.sem("act_asked")
        n_loads = 1 + (bg is not None) + pick.loads

        with nc.Block() as block:

            @block.sync
            def _(sp):
                sp.dma_start(wg_sb[:], wg).then_inc(loaded, 16)
                if bg is not None:
                    sp.dma_start(bg_sb[:], bg).then_inc(loaded, 16)
                pick.load(sp, work, loaded)
                if beside is not None:
                    beside.on_sp(sp)

            @block.gpsimd
            def _(pool):
                nc.gpsimd.memset(before[:], 1.0).then_inc(table, 1)
                pool.wait_ge(table, 1)
                nc.gpsimd.affine_select(out=before[:], in_=before[:], compare_op=ALU.is_gt, fill=0.0, base=0,
                                        pattern=[[1, E], [-1, E]], channel_multiplier=0).then_inc(table, 1)
                if beside is not None:
                    beside.on_pool(pool)

            @block.tensor
            def _(pe):
                pe.wait_ge(loaded, 16 * n_loads)
                for u in range(NU + 1):
                    if u < NU:
                        if u >= 2:
                            pe.wait_ge(logitT_ready, u - 1)
                        for k in range(KC):
                            ins = nc.tensor.matmul(logit_ps[u % 2][:, 0:UNIT], wg_sb[:, k, :], xT[:, k, u * UNIT:(u + 1) * UNIT],
                                                   start=(k == 0), stop=(k == KC - 1))
                        ins.then_inc(logit_ready, 1)
                    if u >= 1:
                        pe.wait_ge(logitT_ready, u)
                        for t in range(UT):
                            ins = nc.tensor.transpose(v_ps[:, (u - 1) * UT + t, :], logitT[:, (u - 1) % 2, t * TT:(t + 1) * TT],
                                                      ident[0:E, 0:E])
                        ins.then_inc(turned, 1)
                if beside is not None:
                    beside.on_pe(pe)

            @block.scalar
            def _(act):
                act.wait_ge(loaded, 16 * n_loads)
                for u in range(NU):
                    act.wait_ge(logit_ready, u + 1)
                    if u >= 2:
                        act.wait_ge(turned, u - 1)
                    if bg is not None:
                        ins = nc.scalar.activation(logitT[:, u % 2, :], logit_ps[u % 2][:, 0:UNIT], ACT.Identity, bias=bg_sb[:, 0:1])
                    else:
                        ins = nc.scalar.activation(logitT[:, u % 2, :], logit_ps[u % 2][:, 0:UNIT], pick.on_logits)
                    ins.then_inc(logitT_ready, 1)
                if pick.asks_act:
                    act.wait_ge(act_asked, 1)
                    pick.on_act(nc, work).then_inc(act_ready, 1)
                if beside is not None:
                    beside.on_act(act)

            @block.vector
            def _(dve):
                st = Steps(dve, steps)
                dve.wait_ge(table, 2)
                dve.wait_ge(loaded, 16 * n_loads)
                dve.wait_ge(turned, NU)
                st.then(nc.vector.tensor_copy(v[:], v_ps[:]))
                pick.run(nc, dve, st, v, before, work, act_asked, act_ready)


def rank_of(nc, st, v, before, gt, ge, rank):
    E = v.shape[2]
    other = v.unsqueeze(2).broadcast_to([TT, NT, E, E])
    g4 = gt.rearrange("p (t e) j -> p t e j", t=NT)
    q4 = ge.rearrange("p (t e) j -> p t e j", t=NT)
    mine4 = v.unsqueeze(3).broadcast_to([TT, NT, E, E])
    nc.vector.tensor_tensor(g4, other, mine4, ALU.is_gt)
    st.then(nc.vector.tensor_tensor(q4, other, mine4, ALU.is_equal))
    st.then(nc.vector.tensor_tensor(q4, q4, before.unsqueeze(1).broadcast_to([TT, NT, E, E]), ALU.mult))
    st.then(nc.vector.tensor_tensor(gt, gt, ge, ALU.add))
    st.then(nc.vector.reduce_sum(rank.rearrange("p t e -> p (t e)"), gt, AX.X))


class PickTop1:
    loads, asks_act, on_logits = 0, False, None

    def __init__(self, ranks=None):
        self.ranks = ranks

    def buffers(self, L, E):
        return dict(gt=L.sb("gt", [TT, NT * E, E]), ge=L.sb("ge", [TT, NT * E, E]), rank=self.ranks or L.sb("rank", [TT, NT, E]))

    def load(self, sp, w, loaded):
        pass

    def run(self, nc, dve, st, v, before, w, asked, answered):
        rank_of(nc, st, v[:], before[:], w["gt"][:], w["ge"][:], w["rank"][:])
        st.then(nc.vector.tensor_scalar(v[:], w["rank"][:], 0.5, None, ALU.is_lt))


def experts(core, name, xT, sel, n_experts, tiles, w1, w2):
    nc, h = core.nc, core.h
    slots = 2
    with Layer(core, name) as L:
        w1_sb = [L.sb(f"w1_{s}", [P, KC, tiles * P]) for s in range(slots)]
        w2_sb = [L.sb(f"w2_{s}", [P, tiles, C]) for s in range(slots)]
        hid = L.sb("hid", [P, 2, UNIT])
        relu = L.sb("relu", [P, 2, UNIT])
        hid_ps = [L.ps(f"hid_ps{s}", [P, BANK]) for s in range(2)]
        y_ps = [L.ps(f"y_ps{s}", [TT, UT // 2, BANK]) for s in range(2)]
        w_ready = [L.sem(f"w_ready{s}") for s in range(slots)]
        hid_ready = L.sem("hid_ready")
        hid_done = L.sem("hid_done")
        hid_used = L.sem("hid_used")
        y_ready = L.sem("y_ready")
        y_free = L.sem("y_free")
        relued = L.sem("relued")
        loads = 2
        body = 2 * tiles

        def over_experts(eng, run):
            with eng.Fori(0, n_experts // slots) as pair:
                for s in range(slots):
                    run(pair * slots + s, s, pair)

        with nc.Block() as block:

            @block.sync
            def _(sp):
                def load(e, s, turn):
                    for dst, src in ((w1_sb[s], w1), (w2_sb[s], w2)):
                        sp.dma_start(dst[:].rearrange("p a b -> p (a b)"), src[ds(e, 1)].rearrange("a p n -> p (a n)")).then_inc(w_ready[s], 16)
                for s in range(slots):
                    load(s, s, 0)
                with sp.Fori(1, n_experts // slots) as pair:
                    for s in range(slots):
                        sp.wait_ge(hid_used, (pair * slots + s - 1) * (NU * tiles) + 2)
                        load(pair * slots + s, s, pair)

            @block.tensor
            def _(pe):
                pe.sem_inc(hid_used, 2)

                def expert(e, s, turn):
                    pe.wait_ge(w_ready[s], (turn + 1) * (16 * loads))
                    pe.nop(nofuse=True)
                    with pe.Fori(0, NU // 2) as i:
                        first = e * (NU * tiles) + i * body
                        units = e * NU + i * 2

                        def up(q):
                            u, m = q // tiles, q % tiles
                            pe.wait_ge(hid_done, first + q + 1)
                            for k in range(KC):
                                ins = nc.tensor.matmul(hid_ps[q % 2][:, 0:UNIT], w1_sb[s][:, k, m * P:(m + 1) * P],
                                                       xT[:, k, ds((i * 2 + u) * UNIT, UNIT)],
                                                       start=(k == 0), stop=(k == KC - 1))
                            ins.then_inc(hid_ready, 1)

                        def down(q):
                            u, m = q // tiles, q % tiles
                            pe.wait_ge(hid_done, first + q + 3)
                            if m == 0:
                                pe.wait_ge(y_free, units + u + 1)
                            for t in range(UT):
                                y = y_ps[u][:, t // 2, (t % 2) * C:(t % 2 + 1) * C]
                                ins = nc.tensor.matmul(y, hid[:, q % 2, t * TT:(t + 1) * TT], w2_sb[s][:, m, :],
                                                       start=(m == 0 and t % 2 == 0), stop=(m == tiles - 1),
                                                       skip_group_check=True)
                            ins.then_inc(hid_used, 1)

                        for q in range(body):
                            up(q)
                            if q:
                                down(q - 1)
                        down(body - 1)
                over_experts(pe, expert)

            @block.scalar
            def _(act):
                act.sem_inc(hid_done, 2)

                def expert(e, s, turn):
                    act.wait_ge(w_ready[s], (turn + 1) * (16 * loads))
                    with act.Fori(0, NU // 2) as i:
                        first = e * (NU * tiles) + i * body
                        for q in range(body):
                            act.wait_ge(hid_ready, first + q + 1)
                            act.wait_ge(hid_used, first + q + 1)
                            nc.scalar.activation(relu[:, q % 2, :], hid_ps[q % 2][:, 0:UNIT], ACT.Relu).then_inc(relued, 1)
                            act.wait_ge(relued, first + q + 1)
                            nc.scalar.activation(hid[:, q % 2, :], relu[:, q % 2, :], ACT.Square).then_inc(hid_done, 1)
                over_experts(act, expert)

            @block.vector
            def _(dve):
                dve.sem_inc(y_free, 2)

                def expert(e, s, turn):
                    with dve.Fori(0, NU // 2) as i:
                        for u in range(2):
                            dve.wait_ge(hid_used, e * (NU * tiles) + i * body + (u + 1) * tiles + 2)
                            for t in range(UT):
                                tile = ds((i * 2 + u) * UT + t, 1)
                                y = y_ps[u][:, t // 2, (t % 2) * C:(t % 2 + 1) * C]
                                mine = h[:, tile, :].rearrange("p a c -> p (a c)")
                                weight = sel[:, tile, ds(e, 1)].rearrange("p a e -> p (a e)")
                                ins = nc.vector.scalar_tensor_tensor(out=mine, in0=y, scalar=weight, in1=mine,
                                                                     op0=ALU.mult, op1=ALU.add)
                            ins.then_inc(y_free, 1)
                over_experts(dve, expert)


class PickTop2:
    loads, asks_act, on_logits = 0, True, ACT.Copy

    def __init__(self, ranks=None):
        self.ranks = ranks

    def buffers(self, L, E):
        return dict(gt=L.sb("gt", [TT, NT * E, E]), ge=L.sb("ge", [TT, NT * E, E]), rank=self.ranks or L.sb("rank", [TT, NT, E]),
                    top=L.sb("top", [TT, NT]), fall=L.sb("fall", [TT, NT, E]), grown=L.sb("grown", [TT, NT, E]),
                    keep=L.sb("keep", [TT, NT, E]), total=L.sb("total", [TT, NT]))

    def load(self, sp, w, loaded):
        pass

    def on_act(self, nc, w):
        return nc.scalar.activation(w["grown"][:], w["fall"][:], ACT.Exp)

    def run(self, nc, dve, st, v, before, w, asked, answered):
        E = v.shape[2]
        st.then(nc.vector.reduce_max(w["top"][:], v[:], AX.X))
        nc.vector.tensor_tensor(w["fall"][:], v[:], w["top"][:].unsqueeze(2).broadcast_to([TT, NT, E]),
                                ALU.subtract).then_inc(asked, 1)
        rank_of(nc, st, v[:], before[:], w["gt"][:], w["ge"][:], w["rank"][:])
        st.then(nc.vector.tensor_scalar(w["keep"][:], w["rank"][:], 1.5, None, ALU.is_lt))
        dve.wait_ge(answered, 1)
        st.then(nc.vector.tensor_tensor(v[:], w["grown"][:], w["keep"][:], ALU.mult))
        st.then(nc.vector.reduce_sum(w["total"][:], v[:], AX.X))
        st.then(nc.vector.reciprocal(w["total"][:], w["total"][:]))
        st.then(nc.vector.tensor_tensor(v[:], v[:], w["total"][:].unsqueeze(2).broadcast_to([TT, NT, E]), ALU.mult))


class PickGrouped:
    asks_act, on_logits, loads = False, ACT.Sigmoid, 1
    GROUPS, SCALE = 4, 2.5

    def __init__(self, bias):
        self.bias = bias

    def buffers(self, L, E):
        G = self.GROUPS
        return dict(gt=L.sb("gt", [TT, NT * E, E]), ge=L.sb("ge", [TT, NT * E, E]), rank=L.sb("rank", [TT, NT, E]),
                    ggt=L.sb("ggt", [TT, NT * G, G]), gge=L.sb("gge", [TT, NT * G, G]), grank=L.sb("grank", [TT, NT, G]),
                    biased=L.sb("biased", [TT, NT, E]), bias=L.sb("bias", [TT, E]), hi=L.sb("hi", [TT, NT * G, 2]),
                    lo=L.sb("lo", [TT, NT * G, 2]), first=L.sb("first", [TT, NT, G]), second=L.sb("second", [TT, NT, G]),
                    runner=L.sb("runner", [TT, NT, G]), total=L.sb("total", [TT, NT]), gbefore=L.sb("gbefore", [TT, G, G]))

    def load(self, sp, w, loaded):
        sp.dma_start(w["bias"][:], self.bias.broadcast_to([TT, self.bias.shape[1]])).then_inc(loaded, 16)

    def run(self, nc, dve, st, v, before, w, asked, answered):
        E, G = v.shape[2], self.GROUPS
        n = E // G
        biased, hi, lo = w["biased"][:], w["hi"][:], w["lo"][:]
        wide = [TT, NT, E]
        nc.vector.tensor_copy(w["gbefore"][:], before[:, 0:G, 0:G])
        st.then(nc.vector.tensor_tensor(biased, v[:], w["bias"][:].unsqueeze(1).broadcast_to(wide), ALU.add))
        b4 = biased.rearrange("p t (g a b) -> p (t g) a b", g=G, a=2)
        nc.vector.tensor_tensor(hi, b4[:, :, 0, :], b4[:, :, 1, :], ALU.max)
        st.then(nc.vector.tensor_tensor(lo, b4[:, :, 0, :], b4[:, :, 1, :], ALU.min))
        flat = [w[x][:].rearrange("p t g -> p (t g)") for x in ("first", "second", "runner")]
        nc.vector.tensor_tensor(flat[0], hi[:, :, 0], hi[:, :, 1], ALU.max)
        nc.vector.tensor_tensor(flat[1], hi[:, :, 0], hi[:, :, 1], ALU.min)
        st.then(nc.vector.tensor_tensor(flat[2], lo[:, :, 0], lo[:, :, 1], ALU.max))
        st.then(nc.vector.tensor_tensor(flat[1], flat[1], flat[2], ALU.max))
        st.then(nc.vector.tensor_tensor(flat[0], flat[0], flat[1], ALU.add))
        rank_of(nc, st, w["first"][:], w["gbefore"][:], w["ggt"][:], w["gge"][:], w["grank"][:])
        st.then(nc.vector.tensor_scalar(w["grank"][:], w["grank"][:], 1.5, None, ALU.is_lt))
        in_group = w["grank"][:].rearrange("p t g -> p (t g)").unsqueeze(2).broadcast_to([TT, NT * G, n])
        b3 = biased.rearrange("p t (g n) -> p (t g) n", g=G)
        st.then(nc.vector.tensor_tensor(b3, b3, in_group, ALU.mult))
        rank_of(nc, st, biased, before[:], w["gt"][:], w["ge"][:], w["rank"][:])
        st.then(nc.vector.scalar_tensor_tensor(out=v[:], in0=w["rank"][:], scalar=3.5, in1=v[:], op0=ALU.is_lt, op1=ALU.mult))
        st.then(nc.vector.reduce_sum(w["total"][:], v[:], AX.X))
        st.then(nc.vector.tensor_scalar(w["total"][:], w["total"][:], 1e-20, None, ALU.add))
        st.then(nc.vector.reciprocal(w["total"][:], w["total"][:]))
        st.then(nc.vector.tensor_scalar(w["total"][:], w["total"][:], self.SCALE, None, ALU.mult))
        st.then(nc.vector.tensor_tensor(v[:], v[:], w["total"][:].unsqueeze(2).broadcast_to(wide), ALU.mult))


class SharedExpert:

    def __init__(self, core, L, xT, w1, w2):
        self.nc, self.h, self.xT, self.w1, self.w2 = core.nc, core.h, xT, w1, w2
        self.tiles = w2.shape[1] // C
        self.w1_sb = L.sb("w1", [P, KC, self.tiles * P])
        self.w2_sb = L.sb("w2", [P, self.tiles, C])
        self.relu = L.sb("relu", [P, 2, UNIT])
        self.hid = L.sb("hid", [P, 2, UNIT])
        self.y = L.sb("y", [TT, 2, UT // 2, BANK])
        self.hid_ps = [L.ps(f"hid_ps{s}", [P, BANK]) for s in range(2)]
        self.y_ps = L.ps("y_ps", [TT, UT // 2, BANK])
        self.w_loaded = L.sem("w_loaded")
        self.hid_ready = L.sem("hid_ready")
        self.relued = L.sem("relued")
        self.hid_done = L.sem("hid_done")
        self.hid_used = L.sem("hid_used")
        self.y_out = L.sem("y_out")
        self.added = L.sem("added")

    def on_sp(self, sp):
        sp.dma_start(self.w1_sb[:].rearrange("p k f -> p (k f)"), self.w1).then_inc(self.w_loaded, 16)
        sp.dma_start(self.w2_sb[:].rearrange("p m c -> p (m c)"), self.w2).then_inc(self.w_loaded, 16)

    def on_pe(self, pe):
        nc, tiles = self.nc, self.tiles
        pe.sem_inc(self.hid_used, 2)
        pe.wait_ge(self.w_loaded, 32)
        with pe.Fori(0, NU // 2) as i:

            def up(q):
                u, m = q // tiles, q % tiles
                pe.wait_ge(self.hid_done, i * (2 * tiles) + q + 1)
                for k in range(KC):
                    ins = nc.tensor.matmul(self.hid_ps[q % 2][:, 0:UNIT], self.w1_sb[:, k, m * P:(m + 1) * P],
                                           self.xT[:, k, ds((i * 2 + u) * UNIT, UNIT)], start=(k == 0), stop=(k == KC - 1))
                ins.then_inc(self.hid_ready, 1)

            def down(q):
                u, m = q // tiles, q % tiles
                pe.wait_ge(self.hid_done, i * (2 * tiles) + q + 3)
                if m == 0:
                    pe.wait_ge(self.y_out, i * 2 + u + 1)
                for t in range(UT):
                    ins = nc.tensor.matmul(self.y_ps[:, t // 2, (t % 2) * C:(t % 2 + 1) * C], self.hid[:, q % 2, t * TT:(t + 1) * TT],
                                           self.w2_sb[:, m, :], start=(m == 0 and t % 2 == 0), stop=(m == tiles - 1),
                                           skip_group_check=True)
                ins.then_inc(self.hid_used, 1)

            for q in range(2 * tiles):
                up(q)
                if q:
                    down(q - 1)
            down(2 * tiles - 1)

    def on_act(self, act):
        nc, tiles = self.nc, self.tiles
        act.sem_inc(self.hid_done, 2)
        act.sem_inc(self.y_out, 1)
        with act.Fori(0, NU // 2) as i:
            for q in range(2 * tiles):
                number = i * (2 * tiles) + q
                act.wait_ge(self.hid_ready, number + 1)
                act.wait_ge(self.hid_used, number + 1)
                nc.scalar.activation(self.relu[:, q % 2, :], self.hid_ps[q % 2][:, 0:UNIT], ACT.Relu).then_inc(self.relued, 1)
                act.wait_ge(self.relued, number + 1)
                nc.scalar.activation(self.hid[:, q % 2, :], self.relu[:, q % 2, :], ACT.Square).then_inc(self.hid_done, 1)
                if q % tiles == tiles - 1:
                    u = q // tiles
                    act.wait_ge(self.hid_used, number + 3)
                    act.wait_ge(self.added, i * 2 + u + 1)
                    nc.scalar.copy(self.y[:, u, :, :], self.y_ps[:]).then_inc(self.y_out, 1)

    def on_pool(self, pool):
        nc, h = self.nc, self.h
        pool.sem_inc(self.added, 2)
        with pool.Fori(0, NU // 2) as i:
            for u in range(2):
                pool.wait_ge(self.y_out, i * 2 + u + 2)
                pool.nop(nofuse=True)
                mine = h[:, ds((i * 2 + u) * UT, UT), :]
                nc.gpsimd.tensor_tensor(mine, self.y[:, u, :, :].rearrange("p a (b c) -> p (a b) c", c=C), mine,
                                        ALU.add).then_inc(self.added, 1)


def grouped_experts(core):
    d = core.dram
    E, tiles = d["f2_w1"].shape[0], d["f2_w2"].shape[2] // C
    with Layer(core, "f2") as L:
        xT = L.sb("xT", [P, KC, TOK])
        sel = L.sb("sel", [TT, NT, E])
        layer_norm(core, "f2ln", xT)
        with Layer(core, "f2sh") as LS:
            shared = SharedExpert(core, LS, xT, d["f2_s1"][0], d["f2_s2"][0])
            route(core, "f2rt", xT, sel, d["f2_wg"], None, PickGrouped(d["f2_bias"]), beside=shared)
        experts(core, "f2ex", xT, sel, E, tiles, d["f2_w1"], d["f2_w2"])


def routed_layer(core, name, n_picked, pick, w1, b1, w2, b2, wg, bg):
    nc, h, ident = core.nc, core.h, core.ident
    E, F = w1.shape[0], w1.shape[2] // KC
    FT = F // P
    FC = min(F, BANK)
    CLEARED = 8
    TILES = -(-(TOK * n_picked + E * (P - 1)) // (P * CLEARED)) * CLEARED
    ROUNDER = 12582912.0
    x_slots = nc.dram_tensor(f"{name}_x_slots", (TILES * P, C), F32, kind="Internal").ap()
    y_slots = nc.dram_tensor(f"{name}_y_slots", (TILES * P, C), F32, kind="Internal").ap()
    with Layer(core, name) as L:
        w1_sb = L.sb("w1", [P, E, KC * F])
        b1_sb = L.sb("b1", [P, E, FT])
        b2_sb = L.sb("b2", [1, E, C])
        ones = L.sb("ones", [1, P])
        weight = L.sb("weight", [TT, n_picked, NT])
        slot = L.sb("slot", [TT, n_picked, NT], mybir.dt.uint32)
        owner = L.sb("owner", [1, TILES], I32)
        w1_loaded = L.sem("w1_loaded")
        cleared = L.sem("cleared")
        with Layer(core, name + "p") as LP:
            xT = LP.sb("xT", [P, KC, TOK])
            keep = LP.sb("keep", [TT, NT, C])
            sel = LP.sb("sel", [TT, NT, E])
            ranks = LP.sb("ranks", [TT, NT, E])
            zeros = LP.sb("zeros", [P, C])
            zeroed = LP.sem("zeroed")
            with nc.Block() as block:

                @block.gpsimd
                def _(pool):
                    nc.gpsimd.memset(ones[:], 1.0)
                    nc.gpsimd.memset(zeros[:], 0.0).then_inc(zeroed, 1)

            def start_loads(sp):
                sp.wait_ge(zeroed, 1)
                with sp.Fori(0, TILES // CLEARED) as i:
                    sp.dma_start(x_slots[ds(i * CLEARED * P, CLEARED * P), :].rearrange("(p a) c -> p a c", a=CLEARED),
                                 zeros[:].unsqueeze(1).broadcast_to([P, CLEARED, C])).then_inc(cleared, 16)
                sp.dma_start(w1_sb[:], w1.rearrange("e p n -> p e n")).then_inc(w1_loaded, 16)
                sp.dma_start(b1_sb[:], b1.rearrange("e p n -> p e n")).then_inc(w1_loaded, 16)
                sp.dma_start(b2_sb[0:1, :, :].rearrange("a e c -> a (e c)"), b2.rearrange("(a e) c -> a (e c)", a=1)).then_inc(w1_loaded, 16)

            layer_norm(core, name + "ln", xT, keep=keep, beside=start_loads)
            route(core, name + "rt", xT, sel, wg, bg, pick(ranks))
            assign_slots(core, name + "as", n_picked, TILES, sel, ranks, weight, slot, owner, ROUNDER)
            sent = LP.pool_dma_sem("sent")
            with nc.Block() as block:

                @block.gpsimd
                def _(pool):
                    pool.wait_ge(cleared, 16 * (TILES // CLEARED))
                    for t in range(NT):
                        for n in range(n_picked):
                            pool.indirect_dma_start(x_slots, bass.IndirectOffsetOnAxis(ap=slot[:, n, t:t + 1], axis=0),
                                                    keep[:, t, :], None).then_inc(sent, 16)
                    pool.wait_ge(sent, 16 * NT * n_picked)
        slot_experts(core, name + "ex", TILES, E, FT, FC, w1_sb, b1_sb, w2, b2_sb, ones, owner, x_slots, y_slots, w1_loaded)
        collect(core, name + "co", n_picked, y_slots, slot, weight)


def assign_slots(core, name, n_picked, TILES, sel, ranks, weight, slot, owner, ROUNDER):
    nc = core.nc
    E = sel.shape[2]
    with Layer(core, name) as L:
        before = L.sb("before", [TT, TT])
        ones = L.sb("ones", [TT, TT])
        ones_row = L.sb("ones_row", [TT, NT])
        chosen = L.sb("chosen", [TT, NT, E])
        total = L.sb("total", [TT, NT, E])
        running = L.sb("running", [TT, NT, E])
        position = L.sb("position", [TT, NT, E])
        hot = L.sb("hot", [TT, NT, E])
        value = L.sb("value", [TT, NT])
        tiles = L.sb("tiles", [TT, E])
        ends = L.sb("ends", [TT, E])
        first = L.sb("first", [TT, E])
        number_i = L.sb("number_i", [1, TILES], I32)
        number = L.sb("number", [1, TILES])
        past = L.sb("past", [1, TILES, E])
        who = L.sb("who", [1, TILES])
        pos_ps = L.ps("pos_ps", [TT, NT * E])
        total_ps = L.ps("total_ps", [TT, NT * E])
        const, chosen_ready, counted, steps = (L.sem(n) for n in ("const", "chosen_ready", "counted", "steps"))
        with nc.Block() as block:

            @block.gpsimd
            def _(pool):
                nc.gpsimd.memset(ones[:], 1.0).then_inc(const, 1)
                nc.gpsimd.memset(ones_row[:], 1.0)
                nc.gpsimd.iota(number_i[:], [[1, TILES]], base=0, channel_multiplier=0)
                pool.wait_ge(const, 1)
                nc.gpsimd.affine_select(out=before[:], in_=ones[:], compare_op=ALU.is_gt, fill=0.0, base=0,
                                        pattern=[[1, TT]], channel_multiplier=-1).then_inc(const, 1)

            @block.tensor
            def _(pe):
                pe.wait_ge(const, 2)
                pe.wait_ge(chosen_ready, 1)
                flat = chosen[:].rearrange("p t e -> p (t e)")
                nc.tensor.matmul(pos_ps[:], before[:], flat, start=True, stop=True)
                nc.tensor.matmul(total_ps[:], ones[:], flat, start=True, stop=True).then_inc(counted, 1)

            @block.vector
            def _(dve):
                st = Steps(dve, steps)
                V = nc.vector
                V.tensor_scalar(chosen[:], ranks[:], n_picked - 0.5, None, ALU.is_lt).then_inc(chosen_ready, 1)
                dve.wait_ge(const, 2)
                dve.wait_ge(counted, 1)
                st.then(V.tensor_copy(total[:].rearrange("p t e -> p (t e)"), total_ps[:]))
                for e in range(E):
                    ins = V.tensor_tensor_scan(running[:, :, e], ones_row[:], total[:, :, e], 0.0, ALU.mult, ALU.add)
                st.then(ins)
                st.then(V.tensor_scalar(tiles[:], running[:, NT - 1, :], 1.0 / P, 0.5 - 0.5 / P, ALU.mult, ALU.add))
                st.then(V.tensor_scalar(tiles[:], tiles[:], ROUNDER, ROUNDER, ALU.add, ALU.subtract))
                st.then(V.tensor_tensor_scan(ends[:], ones_row[:, 0:E], tiles[:], 0.0, ALU.mult, ALU.add))
                st.then(V.tensor_tensor(first[:], ends[:], tiles[:], ALU.subtract))
                st.then(V.tensor_scalar(first[:], first[:], float(P), None, ALU.mult))
                V.tensor_copy(number[:], number_i[:])
                st.then(V.tensor_tensor(position[:], running[:], total[:], ALU.subtract))
                st.then(V.tensor_tensor(position[:].rearrange("p t e -> p (t e)"), position[:].rearrange("p t e -> p (t e)"),
                                        pos_ps[:], ALU.add))
                st.then(V.tensor_tensor(position[:], position[:], first[:].unsqueeze(1).broadcast_to([TT, NT, E]), ALU.add))
                for n in range(n_picked):
                    st.then(V.tensor_scalar(hot[:], ranks[:], float(n), None, ALU.is_equal))
                    st.then(V.tensor_tensor(chosen[:], hot[:], position[:], ALU.mult))
                    st.then(V.reduce_sum(value[:], chosen[:], AX.X))
                    st.then(V.tensor_copy(slot[:, n, :], value[:]))
                    st.then(V.tensor_tensor(chosen[:], hot[:], sel[:], ALU.mult))
                    st.then(V.reduce_sum(weight[:, n, :], chosen[:], AX.X))
                st.then(V.tensor_tensor(past[:], ends[0:1, :].unsqueeze(1).broadcast_to([1, TILES, E]),
                                        number[:].unsqueeze(2).broadcast_to([1, TILES, E]), ALU.is_le))
                st.then(V.reduce_sum(who[:], past[:], AX.X))
                st.then(V.tensor_scalar(who[:], who[:], float(E - 1), None, ALU.min))
                V.tensor_copy(owner[:], who[:])


def slot_experts(core, name, TILES, E, FT, FC, w1_sb, b1_sb, w2, b2_sb, ones, owner, x_slots, y_slots, w1_loaded):
    nc, ident = core.nc, core.ident
    F = FT * P
    CHUNKS = F // FC
    PER = FC // P
    with Layer(core, name) as L:
        w2_sb = L.sb("w2", [P, E, FT * C])
        x = L.sb("x", [P, 2, C])
        xT = L.sb("xT", [P, 2, KC, P])
        pre = L.sb("pre", [P, F])
        hidT = L.sb("hidT", [P, 2, FT, P])
        y = L.sb("y", [P, 2, C])
        xT_ps = L.ps("xT_ps", [P, KC, P])
        up_ps = [L.ps(f"up_ps{c}", [P, FC]) for c in range(CHUNKS)]
        turn_ps = [L.ps(f"turn_ps{c}", [P, PER, P]) for c in range(CHUNKS)]
        y_ps = [L.ps(f"y_ps{s}", [P, C]) for s in range(2)]
        w2_loaded, stored = L.sem("w2_loaded"), [L.pool_dma_sem(f"stored{s}") for s in range(2)]
        x_loaded = [L.sem(f"x_loaded{s}") for s in range(2)]
        x_turned, xT_ready, up_ready, pre_ready, turned, hid_ready, y_ready, y_out = (
            L.sem(n) for n in ("x_turned", "xT_ready", "up_ready", "pre_ready", "turned", "hid_ready", "y_ready", "y_out"))
        with nc.Block() as block:

            @block.sync
            def _(sp):
                def fetch(i, s):
                    sp.dma_start(x[:, s, :], x_slots[ds(i * P, P), :]).then_inc(x_loaded[s], 16)

                fetch(0, 0)
                fetch(1, 1)
                sp.dma_start(w2_sb[:], w2.rearrange("e p n -> p e n")).then_inc(w2_loaded, 16)
                with sp.Fori(0, TILES // 2 - 1) as i:
                    for s in range(2):
                        sp.wait_ge(x_turned, i * 2 + s + 1)
                        fetch(i * 2 + s + 2, s)

            @block.gpsimd
            def _(pool):
                with pool.Fori(0, TILES // 2) as i:
                    for s in range(2):
                        pool.wait_ge(y_out, i * 2 + s + 1)
                        pool.dma_start(y_slots[ds((i * 2 + s) * P, P), :], y[:, s, :]).then_inc(stored[s], 16)
                for s in range(2):
                    pool.wait_ge(stored[s], 16 * (TILES // 2))

            @block.tensor
            def _(pe):
                def turn_x(i, s, turn):
                    pe.wait_ge(x_loaded[s], (turn + 1) * 16)
                    for k in range(KC):
                        ins = nc.tensor.transpose(xT_ps[:, k, :], x[:, s, k * P:(k + 1) * P], ident[:])
                    ins.then_inc(x_turned, 1)

                pe.wait_ge(w1_loaded, 16 * 3)
                turn_x(0, 0, 0)

                def expert_of(i):
                    return pe.value_load(owner[0:1, ds(i, 1)], min_val=0, max_val=E - 1)

                def up(i, s):
                    e = expert_of(i)
                    pe.wait_ge(xT_ready, i + 1)
                    for c in range(CHUNKS):
                        for k in range(KC):
                            ins = nc.tensor.matmul(up_ps[c][:], xT[:, s, k, :],
                                                   w1_sb[:, ds(e, 1), k * F + c * FC:k * F + (c + 1) * FC].rearrange("p a f -> p (a f)"),
                                                   start=(k == 0), stop=(k == KC - 1))
                        ins.then_inc(up_ready, 1)

                def turn_pre(i):
                    for c in range(CHUNKS):
                        pe.wait_ge(pre_ready, i * CHUNKS + c + 1)
                        for j in range(PER):
                            m = c * PER + j
                            ins = nc.tensor.transpose(turn_ps[c][:, j, :], pre[:, m * P:(m + 1) * P], ident[:])
                        ins.then_inc(turned, 1)

                def down(i, s):
                    e = expert_of(i)
                    pe.wait_ge(hid_ready, (i + 1) * CHUNKS)
                    nc.tensor.matmul(y_ps[s][:], ones[:], b2_sb[:, ds(e, 1), :].rearrange("p a f -> p (a f)"), start=True, stop=False)
                    for m in range(FT):
                        ins = nc.tensor.matmul(y_ps[s][:], hidT[:, s, m, :],
                                               w2_sb[:, ds(e, 1), m * C:(m + 1) * C].rearrange("p a f -> p (a f)"),
                                               start=False, stop=(m == FT - 1))
                    ins.then_inc(y_ready, 1)

                up(0, 0)
                turn_x(1, 1, 0)
                turn_pre(0)
                pe.wait_ge(w2_loaded, 16)
                with pe.Fori(0, TILES // 2 - 1) as i:
                    for n, s, turn in ((i * 2 + 1, 1, i + 1), (i * 2 + 2, 0, i + 1)):
                        up(n, s)
                        turn_x(n + 1, 1 - s, turn)
                        down(n - 1, 1 - s)
                        turn_pre(n)
                up(TILES - 1, 1)
                down(TILES - 2, 0)
                turn_pre(TILES - 1)
                down(TILES - 1, 1)

            @block.vector
            def _(dve):
                def take_x(i, s):
                    dve.wait_ge(x_turned, i + 1)
                    nc.vector.tensor_copy(xT[:, s, :, :], xT_ps[:]).then_inc(xT_ready, 1)

                def take_pre(i, first=False):
                    for c in range(CHUNKS):
                        dve.wait_ge(up_ready, i * CHUNKS + c + 1)
                        if not first:
                            dve.nop(nofuse=True)
                            dve.wait_ge(turned, (i - 1) * CHUNKS + c + 1)
                        nc.vector.tensor_copy(pre[:, c * FC:(c + 1) * FC], up_ps[c][:]).then_inc(pre_ready, 1)

                def take_y(i, s, turn):
                    if turn is not None:
                        dve.wait_ge(stored[s], turn * 16)
                        dve.nop(nofuse=True)
                    dve.wait_ge(y_ready, i + 1)
                    nc.vector.tensor_copy(y[:, s, :], y_ps[s][:]).then_inc(y_out, 1)

                take_x(0, 0)
                take_pre(0, first=True)
                take_x(1, 1)
                for n, s in ((1, 1), (2, 0)):
                    take_pre(n)
                    take_x(n + 1, 1 - s)
                    take_y(n - 1, 1 - s, None)
                with dve.Fori(1, TILES // 2 - 1) as i:
                    for n, s in ((i * 2 + 1, 1), (i * 2 + 2, 0)):
                        take_pre(n)
                        take_x(n + 1, 1 - s)
                        take_y(n - 1, 1 - s, i)
                take_pre(TILES - 1)
                take_y(TILES - 2, 0, TILES // 2 - 1)
                take_y(TILES - 1, 1, TILES // 2 - 1)

            @block.scalar
            def _(act):
                with act.Fori(0, TILES // 2) as i:
                    for s in range(2):
                        n = i * 2 + s
                        e = act.value_load(owner[0:1, ds(n, 1)], min_val=0, max_val=E - 1)
                        for c in range(CHUNKS):
                            act.wait_ge(turned, n * CHUNKS + c + 1)
                            act.nop(nofuse=True)
                            for j in range(PER):
                                m = c * PER + j
                                ins = nc.scalar.activation(hidT[:, s, m, :], turn_ps[c][:, j, :], ACT.Gelu,
                                                           bias=b1_sb[:, ds(e, 1), m:m + 1].rearrange("p a b -> p (a b)"))
                            ins.then_inc(hid_ready, 1)


def collect(core, name, n_picked, y_slots, slot, weight):
    nc, h = core.nc, core.h
    BUFS = 8
    with Layer(core, name) as L:
        got = L.sb("got", [TT, BUFS, C])
        arrived = [L.pool_dma_sem(f"arrived{s}") for s in range(BUFS)]
        added = L.sem("added")
        jobs = [(t, n) for t in range(NT) for n in range(n_picked)]
        with nc.Block() as block:

            @block.gpsimd
            def _(pool):
                for i, (t, n) in enumerate(jobs):
                    if i >= BUFS:
                        pool.wait_ge(added, i - BUFS + 1)
                    pool.indirect_dma_start(got[:, i % BUFS, :], None, y_slots,
                                            bass.IndirectOffsetOnAxis(ap=slot[:, n, t:t + 1], axis=0)).then_inc(arrived[i % BUFS], 16)

            @block.vector
            def _(dve):
                for i, (t, n) in enumerate(jobs):
                    dve.wait_ge(arrived[i % BUFS], 16 * (i // BUFS + 1))
                    if n:
                        dve.wait_ge(added, i)
                    nc.vector.scalar_tensor_tensor(out=h[:, t, :], in0=got[:, i % BUFS, :], scalar=weight[:, n, t:t + 1],
                                                   in1=h[:, t, :], op0=ALU.mult, op1=ALU.add).then_inc(added, 1)


def top1_experts(core):
    d = core.dram
    routed_layer(core, "f0", 1, PickTop1, d["f0_w1"], d["f0_b1"], d["f0_w2"], d["f0_b2"], d["f0_wg"], d["f0_bg"])


def top2_experts(core):
    d = core.dram
    routed_layer(core, "f3", 2, PickTop2, d["f3_w1"], d["f3_b1"], d["f3_w2"], d["f3_b2"], d["f3_wg"], None)


def head_rows(h):
    return slice(32 * (h % 4), 32 * (h % 4) + 16), h // 4


def softmax_attention(core):
    nc, h, ident, d = core.nc, core.h, core.ident, core.dram
    HEADS, HD, HALF = 16, 16, SEQ // 2
    G = HEADS // 4
    SCORE = float(C) ** -0.5
    with Layer(core, "a2") as L:
        xT = L.sb("xT", [P, KC, TOK])
        wq = L.sb("wq", [P, KC, G * P])
        wk = L.sb("wk", [P, KC, G * P])
        bq = L.sb("bq", [P, G])
        bk = L.sb("bk", [P, G])
        wv = L.sb("wv", [P, KC, C])
        bv = L.sb("bv", [TT, C])
        wo = L.sb("wo", [P, KC, C])
        bo = L.sb("bo", [1, C])
        ones = L.sb("ones", [1, TT])
        loads = [(wq, "a2_wq"), (wk, "a2_wk"), (bq, "a2_bq"), (bk, "a2_bk"), (wv, "a2_wv"), (wo, "a2_wo"), (bo, "a2_bo")]
        all_loaded = 16 * (len(loads) + 1)
        loaded = L.sem("loaded")

        def load(sp):
            for dst, name in loads:
                sp.dma_start(dst[:], d[name]).then_inc(loaded, 16)
            sp.dma_start(bv[:], d["a2_bv"].broadcast_to([TT, C])).then_inc(loaded, 16)

        layer_norm(core, "a2ln", xT, beside=load)
        x = L.sb("x", [P, KC, SEQ])
        q = L.sb("q", [P, 2, G, SEQ])
        k = L.sb("k", [P, 2, G, SEQ])
        v = L.sb("v", [HALF, 2, 2, HEADS, 2 * HD])
        top = L.sb("top", [HALF, HEADS, 2])
        total = L.sb("total", [HALF, 2, HEADS, 2])
        probs = L.sb("probs", [HALF, 3, 2, SEQ])
        probsT = L.sb("probsT", [HALF, 2, 2, SEQ])
        share = L.sb("share", [HALF, 2, C])
        shareT = L.sb("shareT", [P, KC, SEQ])
        oT = L.sb("oT", [P, KC, SEQ])
        score_ps = [L.ps(f"score_ps{s}", [HALF, 2, BANK // 2]) for s in range(3)]
        probsT_ps = [L.ps(f"probsT_ps{s}", [HALF, 2, BANK // 2]) for s in range(2)]
        oT_ps = L.ps("oT_ps", [P, KC, BANK // 2])
        side_ps = [L.ps(f"side_ps{s}", [P, 2, BANK // 2]) for s in range(2)]
        ones_set = L.sem("ones_set")
        bias_scaled = L.sem("bias_scaled")
        x_ready = L.sem("x_ready")
        side_ready = L.sem("side_ready")
        act_out = L.sem("act_out")
        dve_out = L.sem("dve_out")
        score_ready = L.sem("score_ready")
        top_ready = L.sem("top_ready")
        probs_ready = L.sem("probs_ready")
        turned = L.sem("turned")
        probsT_ready = L.sem("probsT_ready")
        av_done = L.sem("av_done")
        share_ready = L.sem("share_ready")
        o_ready = L.sem("o_ready")
        steps = L.sem("steps")

        side_at = {1: "share", 4: "y", 5: "q01", 6: "q23", 8: "k01", 9: "k23", 11: "v"}
        order = list(side_at.values())

        def before(b, per, short):
            if isinstance(b, int) and b in (0, SEQS):
                return short if b == 0 else (SEQS - 1) * per + short
            return b * per + (2 * short - per)

        def sides(b, prologue=False):
            some = [(n, t) for n, t in side_at.items()
                    if (t in ("share", "y")) <= (not (isinstance(b, int) and b == 0) and not prologue)
                    and (t in ("share", "y") or not (isinstance(b, int) and b == SEQS - 1))]
            return {n: t for n, t in some}, [t for _, t in some]

        ACT_SIDE, DVE_SIDE = ("share", "q01", "q23", "k01", "k23"), ("y", "v")

        def count(tasks, task, kinds):
            return len([t for t in tasks[:tasks.index(task)] if t in kinds])

        def over_turns(eng, turn, steps_of_turn=None, st=None):
            turn(0, 0)
            with eng.Fori(0, SEQS // 2 - 1) as i:
                if st is not None:
                    st.enter(i, 2 * steps_of_turn)
                turn(i * 2 + 1, 1)
                turn(i * 2 + 2, 0)
                if st is not None:
                    st.leave(SEQS // 2 - 1)
            turn(SEQS - 1, 1)

        with nc.Block() as block:

            @block.gpsimd
            def _(pool):
                nc.gpsimd.memset(v[:], 0.0)
                nc.gpsimd.memset(ones[:], 1.0).then_inc(ones_set, 1)
                nc.gpsimd.tensor_copy(x[:], xT[:, :, 0:SEQ]).then_inc(x_ready, 1)
                pool.wait_ge(side_ready, 5)
                nc.gpsimd.tensor_copy(x[:], xT[:, :, SEQ:2 * SEQ]).then_inc(x_ready, 1)
                with pool.Fori(2, SEQS) as b:
                    pool.wait_ge(side_ready, b * 7 - 4)
                    nc.gpsimd.tensor_copy(x[:], xT[:, :, ds(b * SEQ, SEQ)]).then_inc(x_ready, 1)

            @block.tensor
            def _(pe):
                def side(b, s, task, tasks):
                    a0, d0 = (0, 0) if b is None else (before(b, 5, 4), before(b, 2, 1))
                    if task == "share":
                        pe.wait_ge(share_ready, b)
                        pe.nop(nofuse=True)
                        pe.wait_ge(dve_out, d0)
                        for a in range(2):
                            for c in range(KC):
                                ins = nc.tensor.transpose(side_ps[0][:, c, a * HALF:(a + 1) * HALF], share[:, a, c * P:(c + 1) * P],
                                                          ident[0:HALF, 0:HALF])
                    elif task == "y":
                        pe.wait_ge(o_ready, b)
                        for a in range(2):
                            nc.tensor.matmul(side_ps[1][0:HALF, a, :], ones[:], bo[:], start=True, stop=False)
                            for c in range(KC):
                                ins = nc.tensor.matmul(side_ps[1][0:HALF, a, :], oT[:, c, a * HALF:(a + 1) * HALF], wo[:, c, :],
                                                       start=False, stop=(c == KC - 1))
                    elif task == "v":
                        pe.wait_ge(act_out, a0 + count(tasks, "k01", ACT_SIDE) + 1)
                        for a in range(2):
                            for c in range(KC):
                                ins = nc.tensor.matmul(side_ps[0][0:HALF, a, :], x[:, c, a * HALF:(a + 1) * HALF], wv[:, c, :],
                                                       start=(c == 0), stop=(c == KC - 1))
                    else:
                        w, g0 = (wq if task[0] == "q" else wk), (0 if task[1:] == "01" else 2)
                        bank = 0 if task[1:] == "01" else 1
                        if task == "q01":
                            pe.wait_ge(x_ready, 1 if b is None else b + 2)
                            if b is not None:
                                pe.nop(nofuse=True)
                                if "share" in tasks:
                                    pe.wait_ge(act_out, a0 + 1)
                                else:
                                    pe.wait_ge(dve_out, d0)
                        if task == "q23" and b is not None:
                            if "y" in tasks:
                                pe.wait_ge(dve_out, d0 + 1)
                            else:
                                pe.wait_ge(act_out, a0)
                        if task[0] == "k":
                            pe.wait_ge(act_out, a0 + count(tasks, "q" + task[1:], ACT_SIDE) + 1)
                        for g in range(2):
                            for c in range(KC):
                                ins = nc.tensor.matmul(side_ps[bank][:, g, 0:SEQ], w[:, c, (g0 + g) * P:(g0 + g + 1) * P],
                                                       x[:, c, :], start=(c == 0), stop=(c == KC - 1))
                    ins.then_inc(side_ready, 1)

                def turn(b, s):
                    side_of, tasks = sides(b)
                    first = isinstance(b, int) and b == 0

                    def score(n):
                        rows, g = head_rows(n)
                        if n == 0:
                            pe.wait_ge(act_out, before(b, 5, 4))
                            pe.nop(nofuse=True)
                        for a in range(2):
                            ins = nc.tensor.matmul(score_ps[n % 3][:, a, 0:SEQ], q[rows, s, g, a * HALF:(a + 1) * HALF],
                                                   k[rows, s, g, :], start=True, stop=True)
                        ins.then_inc(score_ready, 1)

                    def turn_probs(n):
                        pe.wait_ge(probs_ready, b * HEADS + n + 1)
                        for a in range(2):
                            for kh in range(2):
                                ins = nc.tensor.transpose(probsT_ps[n % 2][:, kh, a * HALF:(a + 1) * HALF],
                                                          probs[:, n % 3, a, kh * HALF:(kh + 1) * HALF], ident[0:HALF, 0:HALF])
                        ins.then_inc(turned, 1)

                    def mix(n):
                        pe.wait_ge(probsT_ready, b * HEADS + n + 1)
                        if n == 0:
                            pe.nop(nofuse=True)
                            pe.wait_ge(dve_out, before(b, 2, 1))
                            if not first:
                                pe.nop(nofuse=True)
                                pe.wait_ge(o_ready, b)
                        block32 = 2 * HD * (n // 2 % (P // (2 * HD)))
                        for kh in range(2):
                            ins = nc.tensor.matmul(oT_ps[block32:block32 + 2 * HD, n // (P // HD), 0:SEQ], v[:, s, kh, n, :],
                                                   probsT[:, n % 2, kh, :], start=(n % 2 == 0 and kh == 0),
                                                   stop=(n % 2 == 1 and kh == 1))
                        ins.then_inc(av_done, 1)

                    for n in range(HEADS + 3):
                        if n < HEADS:
                            score(n)
                        if 2 <= n < HEADS + 2:
                            turn_probs(n - 2)
                        if n >= 3:
                            mix(n - 3)
                        if n in side_of:
                            side(b, s, side_of[n], tasks)

                pe.wait_ge(loaded, all_loaded)
                pe.wait_ge(ones_set, 1)
                tasks = sides(0, prologue=True)[1]
                for task in tasks:
                    side(None, 1, task, tasks)
                over_turns(pe, turn)
                side(SEQS, 0, "share", ["share", "y"])
                side(SEQS, 0, "y", ["share", "y"])

            @block.scalar
            def _(act):
                def side(b, s, task, tasks):
                    act.wait_ge(side_ready, (0 if b is None else before(b, 7, 5)) + tasks.index(task) + 1)
                    if task == "share":
                        nc.scalar.copy(shareT[:], side_ps[0][:, :, 0:SEQ]).then_inc(act_out, 1)
                        return
                    dst, bias = (q, bq) if task[0] == "q" else (k, bk)
                    g0, bank = (0, 0) if task[1:] == "01" else (2, 1)
                    for g in range(2):
                        ins = nc.scalar.activation(dst[:, s, g0 + g, :], side_ps[bank][:, g, 0:SEQ], ACT.Identity,
                                                   bias=bias[:, g0 + g:g0 + g + 1], scale=SCORE if task[0] == "q" else 1.0)
                    ins.then_inc(act_out, 1)

                def turn(b, s):
                    side_of, tasks = sides(b)
                    for n in range(HEADS):
                        act.wait_ge(top_ready, b * HEADS + n + 1)
                        for a in range(2):
                            ins = nc.scalar.activation(probs[:, n % 3, a, :], score_ps[n % 3][:, a, 0:SEQ], ACT.Exp,
                                                       bias=top[:, n, a:a + 1], accum_out=total[:, s, n, a:a + 1])
                        ins.then_inc(probs_ready, 1)
                        if side_of.get(n) in ACT_SIDE:
                            side(b, 1 - s, side_of[n], tasks)

                act.wait_ge(loaded, all_loaded)
                act.wait_ge(bias_scaled, 1)
                tasks = sides(0, prologue=True)[1]
                for task in tasks:
                    if task in ACT_SIDE:
                        side(None, 0, task, tasks)
                over_turns(act, turn)
                side(SEQS, 0, "share", ["share", "y"])

            @block.vector
            def _(dve):
                st = Steps(dve, steps)

                def take_v(b, s, tasks):
                    dve.wait_ge(side_ready, (0 if b is None else before(b, 7, 5)) + tasks.index("v") + 1)
                    for kh in range(2):
                        for e in range(2):
                            pairs = [t.rearrange("p (m e i) -> p m e i", e=2, i=HD)[:, :, e, :] for t in (side_ps[0][0:HALF, kh, :], bv[:])]
                            mine = v[:, s, kh, :, :].rearrange("p (m e) i -> p m e i", e=2)[:, :, e, e * HD:(e + 1) * HD]
                            ins = nc.vector.tensor_tensor(mine, pairs[0], pairs[1], ALU.add)
                    ins.then_inc(dve_out, 1)

                def take_y(b):
                    dve.wait_ge(side_ready, before(b, 7, 5) + 2)
                    mine = h[:, ds(b * 2 - 2, 2), :]
                    nc.vector.tensor_tensor(mine, side_ps[1][0:HALF, :, :], mine, ALU.add).then_inc(dve_out, 1)

                def make_share(b, s):
                    dve.wait_ge(probs_ready, b * HEADS)
                    st.then(nc.vector.reciprocal(total[:, s, :, :], total[:, s, :, :]))
                    for a in range(2):
                        ins = nc.vector.tensor_copy(share[:, a, :].rearrange("p (n e) -> p n e", n=HEADS),
                                                    total[:, s, :, a:a + 1].broadcast_to([HALF, HEADS, HD]))
                    ins.then_inc(share_ready, 1)

                def normalise(b):
                    dve.wait_ge(av_done, b * HEADS)
                    dve.wait_ge(act_out, before(b, 5, 4) + 1)
                    nc.vector.tensor_tensor(oT[:], oT_ps[:, :, 0:SEQ], shareT[:], ALU.mult).then_inc(o_ready, 1)

                def turn(b, s):
                    side_of, tasks = sides(b)
                    for n in range(HEADS + 2):
                        if n < HEADS:
                            dve.wait_ge(score_ready, b * HEADS + n + 1)
                            nc.vector.tensor_reduce(top[:, n, :], score_ps[n % 3][:, :, 0:SEQ], AX.X, ALU.max,
                                                    negate=True).then_inc(top_ready, 1)
                        if n == 0 and "share" in tasks:
                            make_share(b, 1 - s)
                        if n == 2 and "share" in tasks:
                            normalise(b)
                        if side_of.get(n) == "v":
                            take_v(b, 1 - s, tasks)
                        if side_of.get(n) == "y":
                            take_y(b)
                        if n >= 2:
                            m = n - 2
                            dve.wait_ge(turned, b * HEADS + m + 1)
                            nc.vector.tensor_copy(probsT[:, m % 2, :, :], probsT_ps[m % 2][:, :, 0:SEQ]).then_inc(probsT_ready, 1)

                dve.wait_ge(loaded, all_loaded)
                nc.vector.tensor_scalar(bq[:], bq[:], SCORE, None, ALU.mult).then_inc(bias_scaled, 1)
                take_v(None, 0, sides(0, prologue=True)[1])
                over_turns(dve, turn, 1, st)
                make_share(SEQS, 1)
                normalise(SEQS)
                take_y(SEQS)


def taylor_attention(core):
    nc, h, ident, d = core.nc, core.h, core.ident, core.dram
    HEADS, HD, HALF = 8, 16, SEQ // 2
    G, HC = HEADS // 4, HEADS * HD
    SCALE, DEN_EPS = float(HD) ** -0.5, 1e-5
    with Layer(core, "a0") as L:
        xT = L.sb("xT", [P, KC, TOK])
        gamma = L.sb("gamma", [P, KC])
        wq = L.sb("wq", [P, KC, G * P])
        wk = L.sb("wk", [P, KC, G * P])
        wv = L.sb("wv", [P, KC, HC])
        wo = L.sb("wo", [P, G, C])
        gamma_loaded, loaded, cleared = L.sem("gamma_loaded"), L.sem("loaded"), L.sem("cleared")
        with nc.Block() as block:

            @block.sync
            def _(sp):
                sp.dma_start(gamma[:], d["a0_gamma"]).then_inc(gamma_loaded, 16)
                sp.wait_ge(gamma_loaded, 16)

            @block.gpsimd
            def _(pool):
                nc.gpsimd.memset(wo[:], 0.0).then_inc(cleared, 1)

        def load(sp):
            for dst, name in ((wq, "a0_wq"), (wk, "a0_wk"), (wv, "a0_wv")):
                sp.dma_start(dst[:], d[name]).then_inc(loaded, 16)
            sp.wait_ge(cleared, 1)
            for n in range(HEADS):
                rows, g = head_rows(n)
                sp.dma_start(wo[rows, g, :], d["a0_wo"][n * HD:(n + 1) * HD, :]).then_inc(loaded, 16)
            sp.wait_ge(loaded, 16 * (3 + HEADS))

        layer_norm(core, "a0ln", xT, rms_gain=gamma, beside=load)
        ones = L.sb("ones", [HALF, SEQ])
        one = L.sb("one", [P, 1])
        x = L.sb("x", [P, KC, SEQ])
        q = L.sb("q", [P, 2, G, SEQ])
        k = L.sb("k", [P, 2, G, SEQ])
        v = L.sb("v", [HALF, 2, 2, HEADS, 2 * HD])
        lower = L.sb("lower", [P, P])
        square = L.sb("square", [HALF, 3, 2, SEQ])
        o = L.sb("o", [P, G, SEQ])
        den = L.sb("den", [P, G, SEQ])
        oT = L.sb("oT", [P, G, SEQ])
        s_ps = [L.ps(f"s_ps{s}", [HALF, 2, BANK // 2]) for s in range(3)]
        o_ps = [L.ps(f"o_ps{s}", [P, G, BANK // 2]) for s in range(2)]
        side_ps = [L.ps(f"side_ps{s}", [P, 2, BANK // 2]) for s in range(2)]
        ones_set = L.sem("ones_set")
        x_ready = L.sem("x_ready")
        side_ready = L.sem("side_ready")
        act_out = L.sem("act_out")
        dve_out = L.sem("dve_out")
        s_ready = L.sem("s_ready")
        square_ready = L.sem("square_ready")
        av_done = L.sem("av_done")
        o_ready = L.sem("o_ready")
        oT_ready = L.sem("oT_ready")
        steps = L.sem("steps")

        side_at = {1: "den", 4: "y", 5: "q", 6: "k", 7: "v"}

        def before(b, per, short):
            if isinstance(b, int) and b in (0, SEQS):
                return short if b == 0 else (SEQS - 1) * per + short
            return b * per + (2 * short - per)

        def sides(b):
            start, end = (isinstance(b, int) and b == 0), (isinstance(b, int) and b == SEQS - 1)
            return {n: t for n, t in side_at.items() if not (start and t in ("den", "y")) and not (end and t in ("q", "k", "v"))}

        def over_turns(eng, turn, steps_of_turn=None, st=None):
            turn(0, 0)
            with eng.Fori(0, SEQS // 2 - 1) as i:
                if st is not None:
                    st.enter(i, 2 * steps_of_turn)
                turn(i * 2 + 1, 1)
                turn(i * 2 + 2, 0)
                if st is not None:
                    st.leave(SEQS // 2 - 1)
            turn(SEQS - 1, 1)

        with nc.Block() as block:

            @block.gpsimd
            def _(pool):
                nc.gpsimd.memset(ones[:], 1.0)
                nc.gpsimd.memset(one[:], 1.0)
                for e in range(2):
                    nc.gpsimd.tensor_copy(lower[:].rearrange("p (n e i) -> p n e i", e=2, i=HD)[:, :, e, :],
                                          ident[:].rearrange("p (n e i) -> p n e i", e=2, i=HD)[:, :, 1, :])
                nc.gpsimd.memset(v[:], 1.0).then_inc(ones_set, 1)
                nc.gpsimd.tensor_copy(x[:], xT[:, :, 0:SEQ]).then_inc(x_ready, 1)
                pool.wait_ge(side_ready, 3)
                nc.gpsimd.tensor_copy(x[:], xT[:, :, SEQ:2 * SEQ]).then_inc(x_ready, 1)
                with pool.Fori(2, SEQS) as b:
                    pool.wait_ge(side_ready, b * 5 - 4)
                    nc.gpsimd.tensor_copy(x[:], xT[:, :, ds(b * SEQ, SEQ)]).then_inc(x_ready, 1)

            @block.tensor
            def _(pe):
                def side(b, task, finishing):
                    a0, d0 = (0, 0) if b is None else (before(b, 2, 2), before(b, 3, 1))
                    if task == "den":
                        pe.wait_ge(o_ready, b)
                        pe.nop(nofuse=True)
                        pe.wait_ge(dve_out, d0)
                        for g in range(G):
                            ins = nc.tensor.matmul(side_ps[0][:, g, 0:SEQ], lower[:], o[:, g, :], start=True, stop=True)
                    elif task == "y":
                        pe.wait_ge(oT_ready, b)
                        for a in range(2):
                            for g in range(G):
                                ins = nc.tensor.matmul(side_ps[1][0:HALF, a, :], oT[:, g, a * HALF:(a + 1) * HALF], wo[:, g, :],
                                                       start=(g == 0), stop=(g == G - 1))
                    elif task == "v":
                        pe.wait_ge(act_out, a0 + 1)
                        for a in range(2):
                            for c in range(KC):
                                ins = nc.tensor.matmul(side_ps[0][0:HALF, a, 0:HC], x[:, c, a * HALF:(a + 1) * HALF], wv[:, c, :],
                                                       start=(c == 0), stop=(c == KC - 1))
                    else:
                        if task == "q":
                            pe.wait_ge(x_ready, 1 if b is None else b + 2)
                            if b is not None:
                                pe.nop(nofuse=True)
                                if finishing:
                                    pe.wait_ge(dve_out, d0 + 1)
                                else:
                                    pe.wait_ge(dve_out, d0)
                        elif b is not None:
                            if finishing:
                                pe.wait_ge(dve_out, d0 + 2)
                            else:
                                pe.wait_ge(act_out, a0)
                        w, bank = (wq, 0) if task == "q" else (wk, 1)
                        for g in range(G):
                            for c in range(KC):
                                ins = nc.tensor.matmul(side_ps[bank][:, g, 0:SEQ], w[:, c, g * P:(g + 1) * P],
                                                       x[:, c, :], start=(c == 0), stop=(c == KC - 1))
                    ins.then_inc(side_ready, 1)

                def turn(b, s):
                    side_of = sides(b)

                    def score(n):
                        rows, g = head_rows(n)
                        if n == 0:
                            pe.wait_ge(act_out, before(b, 2, 2))
                            pe.nop(nofuse=True)
                        for kh in range(2):
                            ins = nc.tensor.matmul(s_ps[n % 3][:, kh, 0:SEQ], k[rows, s, g, kh * HALF:(kh + 1) * HALF],
                                                   q[rows, s, g, :], start=True, stop=True)
                        ins.then_inc(s_ready, 1)

                    def mix(n):
                        pe.wait_ge(square_ready, b * HEADS + n + 1)
                        rows = slice(32 * (n % 4), 32 * (n % 4) + 2 * HD)
                        for kh in range(2):
                            ins = nc.tensor.matmul(o_ps[s][rows, n // 4, 0:SEQ], v[:, s, kh, n, :], square[:, n % 3, kh, :],
                                                   start=False, stop=(kh == 1), skip_group_check=True)
                        ins.then_inc(av_done, 1)

                    for n in range(HEADS + 2):
                        if n < HEADS:
                            score(n)
                        if n == 1:
                            pe.wait_ge(dve_out, before(b, 3, 1))
                            for g in range(G):
                                for kh in range(2):
                                    nc.tensor.matmul(o_ps[s][:, g, 0:SEQ], v[:, s, kh, 4 * g:4 * g + 4, :].rearrange("p n e -> p (n e)"),
                                                     ones[:], start=(g == 0 and kh == 0), stop=False, skip_group_check=True)
                        if n >= 2:
                            mix(n - 2)
                        if n in side_of:
                            side(b, side_of[n], "den" in side_of.values())

                pe.wait_ge(ones_set, 1)
                for task in ("q", "k", "v"):
                    side(None, task, False)
                over_turns(pe, turn)
                side(SEQS, "den", True)
                side(SEQS, "y", True)

            @block.scalar
            def _(act):
                def side(b, s, task, finishing):
                    number = {"q": 1, "k": 2}[task] + 2 * finishing
                    act.wait_ge(side_ready, (0 if b is None else before(b, 5, 3)) + number)
                    if task == "q":
                        ins = nc.scalar.copy(q[:, s, :, :], side_ps[0][:, :, 0:SEQ])
                    else:
                        ins = nc.scalar.copy(k[:, s, :, :], side_ps[1][:, :, 0:SEQ])
                    ins.then_inc(act_out, 1)

                def turn(b, s):
                    side_of = sides(b)
                    for n in range(HEADS):
                        act.wait_ge(s_ready, b * HEADS + n + 1)
                        nc.scalar.activation(square[:, n % 3, :, :], s_ps[n % 3][:, :, 0:SEQ], ACT.Square,
                                             bias=one[0:HALF, :], scale=SCALE).then_inc(square_ready, 1)
                        if side_of.get(n) in ("q", "k"):
                            side(b, 1 - s, side_of[n], "den" in side_of.values())

                act.wait_ge(ones_set, 1)
                side(None, 0, "q", False)
                side(None, 0, "k", False)
                over_turns(act, turn)

            @block.vector
            def _(dve):
                st = Steps(dve, steps)

                def take_v(b, s, finishing):
                    dve.wait_ge(side_ready, (0 if b is None else before(b, 5, 3)) + 3 + 2 * finishing)
                    for a in range(2):
                        ins = nc.vector.tensor_copy(v[:, s, a, :, 0:HD],
                                                    side_ps[0][0:HALF, a, 0:HC].rearrange("p (n e) -> p n e", n=HEADS))
                    ins.then_inc(dve_out, 1)

                def take_y(b):
                    dve.wait_ge(side_ready, before(b, 5, 3) + 2)
                    mine = h[:, ds(b * 2 - 2, 2), :]
                    nc.vector.tensor_tensor(mine, side_ps[1][0:HALF, :, :], mine, ALU.add).then_inc(dve_out, 1)

                def normalise(b, s):
                    dve.wait_ge(av_done, b * HEADS)
                    nc.vector.tensor_copy(o[:], o_ps[s][:, :, 0:SEQ]).then_inc(o_ready, 1)
                    dve.wait_ge(side_ready, before(b, 5, 3) + 1)
                    nc.vector.tensor_scalar(den[:], side_ps[0][:, :, 0:SEQ], 0.5, DEN_EPS, ALU.mult, ALU.max).then_inc(dve_out, 1)
                    dve.wait_ge(dve_out, before(b, 3, 1) + 1)
                    st.then(nc.vector.reciprocal(den[:], den[:]))
                    nc.vector.scalar_tensor_tensor(out=oT[:], in0=o[:], scalar=0.5, in1=den[:], op0=ALU.mult,
                                                   op1=ALU.mult).then_inc(oT_ready, 1)

                def turn(b, s):
                    tasks = list(sides(b).values())
                    if "den" in tasks:
                        normalise(b, 1 - s)
                        take_y(b)
                    if "v" in tasks:
                        take_v(b, 1 - s, "den" in tasks)

                dve.wait_ge(ones_set, 1)
                take_v(None, 0, False)
                over_turns(dve, turn, 1, st)
                normalise(SEQS, 1)
                take_y(SEQS)


def token_norm(core, name, u, gain, shift):
    nc, h = core.nc, core.h
    with Layer(core, name) as L:
        stats = L.sb("stats", [TT, UT, 6])
        moments = L.sb("moments", [TT, 2, UT, 2])
        eps_var = L.sb("eps_var", [TT, 2, UT])
        rstd = L.sb("rstd", [TT, 2, UT])
        power = L.sb("power", [TT, UT])
        steps = L.sem("steps")
        power_set = L.sem("power_set")
        var_ready = L.sem("var_ready")
        rstd_ready = L.sem("rstd_ready")
        y_ready = L.sem("y_ready")
        gained = L.sem("gained")
        wide = [TT, UT, C]

        def unit_of(i):
            return u[:, ds(i * UT, UT), :]

        with nc.Block() as block:

            @block.vector
            def _(dve):
                st = Steps(dve, steps)
                nc.vector.memset(power[:], -0.5).then_inc(power_set, 1)
                with dve.Fori(0, NU) as i:
                    st.enter(i, 5)
                    for r, src in enumerate((h, u)):
                        for t in range(UT):
                            ins = nc.vector.bn_stats(stats[:, t, :], src[:, ds(i * UT + t, 1), :])
                        st.then(ins)
                        dve.nop(nofuse=True)
                        for t in range(UT):
                            ins = nc.vector.bn_aggr(moments[:, r, t, :], stats[:, t, :])
                        st.then(ins)
                        nc.vector.tensor_scalar(eps_var[:, r, :], moments[:, r, :, 1], LN_EPS, None,
                                                ALU.add).then_inc(var_ready, 1)
                        dve.wait_ge(rstd_ready, i * 2 + r + 1)
                        for t in range(UT):
                            tile = ds(i * UT + t, 1)
                            ins = nc.vector.tensor_scalar(u[:, tile, :], src[:, tile, :], moments[:, r, t, 0:1],
                                                          rstd[:, r, t:t + 1], ALU.subtract, ALU.mult)
                        if r == 0:
                            st.then(ins)
                            dve.nop(nofuse=True)
                        else:
                            ins.then_inc(y_ready, 1)
                    st.leave(NU)

            @block.gpsimd
            def _(pool):
                pool.wait_ge(power_set, 1)
                def power_of(i, r):
                    pool.wait_ge(var_ready, i * 2 + r + 1)
                    nc.gpsimd.tensor_tensor(rstd[:, r, :], eps_var[:, r, :], power[:], ALU.pow).then_inc(rstd_ready, 1)

                def scaled(i):
                    pool.wait_ge(y_ready, i + 1)
                    pool.nop(nofuse=True)
                    nc.gpsimd.tensor_tensor(unit_of(i), unit_of(i), gain.unsqueeze(1).broadcast_to(wide), ALU.mult).then_inc(gained, 1)

                def shifted(i):
                    pool.wait_ge(gained, i + 1)
                    pool.nop(nofuse=True)
                    nc.gpsimd.tensor_tensor(unit_of(i), unit_of(i), shift.unsqueeze(1).broadcast_to(wide), ALU.add)

                power_of(0, 0)
                power_of(0, 1)
                with pool.Fori(1, NU) as i:
                    power_of(i, 0)
                    scaled(i - 1)
                    power_of(i, 1)
                    shifted(i - 1)
                scaled(NU - 1)
                shifted(NU - 1)


def kernel_spectrum(core, F, KR, KR2, KI):
    nc, d = core.nc, core.dram
    PI = 3.1415925
    ROUND = 12582912.0
    TURN = (6.28125, 0.0019350051879882812, 3.0199159819120313e-07)
    with Layer(core, "ks") as L:
        lre = L.sb("lre", [P, 1])
        lim = L.sb("lim", [P, 1])
        cre = L.sb("cre", [P, C])
        cim = L.sb("cim", [P, C])
        step_i = L.sb("step_i", [P, SEQ], I32)
        step = L.sb("step", [P, SEQ])
        decay = L.sb("decay", [P, SEQ])
        angle = L.sb("angle", [P, SEQ])
        turns = L.sb("turns", [P, SEQ])
        sine = L.sb("sine", [P, SEQ])
        half = L.sb("half", [P, SEQ])
        small = L.sb("small", [P, 10])
        term = L.sb("term", [P, 2, C])
        K = L.sb("K", [TT, 2, C])
        K_ps = L.ps("K_ps", [TT, 2, C])
        spec_ps = L.ps("spec_ps", [TT, 4, C])
        loaded, stepped, rates, args, waves = (L.sem(n) for n in ("loaded", "stepped", "rates", "args", "waves"))
        modes, k_ready, k_out, spectrum = (L.sem(n) for n in ("modes", "k_ready", "k_out", "spectrum"))
        steps = L.sem("steps")
        a, b, m, nr, t1, t2, wr, wi = (small[:, i:i + 1] for i in range(8))
        with nc.Block() as block:

            @block.sync
            def _(sp):
                for dst, name in ((lre, "a3_lre"), (lim, "a3_lim"), (cre, "a3_cre"), (cim, "a3_cim")):
                    sp.dma_start(dst[:], d[name]).then_inc(loaded, 16)

            @block.gpsimd
            def _(pool):
                nc.gpsimd.iota(step_i[:], [[1, SEQ]], base=0, channel_multiplier=0).then_inc(stepped, 1)

            @block.scalar
            def _(act):
                act.wait_ge(loaded, 64)
                nc.scalar.activation(a, lre[:], ACT.Exp)
                nc.scalar.activation(b, lim[:], ACT.Exp).then_inc(rates, 1)
                act.wait_ge(args, 1)
                nc.scalar.activation(decay[:], decay[:], ACT.Exp)
                nc.scalar.activation(sine[:], angle[:], ACT.Sin)
                nc.scalar.activation(half[:], angle[:], ACT.Sin, scale=0.5).then_inc(waves, 1)

            @block.vector
            def _(dve):
                st = Steps(dve, steps)
                V = nc.vector
                dve.wait_ge(stepped, 1)
                st.then(V.tensor_copy(step[:], step_i[:]))
                dve.wait_ge(rates, 1)
                V.tensor_scalar(decay[:], step[:], a, -1.0, ALU.mult, ALU.mult)
                st.then(V.tensor_scalar(angle[:], step[:], b, None, ALU.mult))
                st.then(V.tensor_scalar(turns[:], angle[:], 0.15915494309189535, ROUND, ALU.mult, ALU.add))
                st.then(V.tensor_scalar(turns[:], turns[:], ROUND, None, ALU.subtract))
                for part in TURN:
                    st.then(V.scalar_tensor_tensor(out=angle[:], in0=turns[:], scalar=-part, in1=angle[:],
                                                   op0=ALU.mult, op1=ALU.add))
                V.tensor_scalar(angle[:], angle[:], PI, -PI, ALU.min, ALU.max).then_inc(args, 1)
                dve.wait_ge(waves, 1)
                st.then(V.tensor_tensor(half[:], half[:], half[:], ALU.mult))
                st.then(V.tensor_scalar(half[:], half[:], -2.0, 1.0, ALU.mult, ALU.add))
                V.tensor_tensor(half[:], half[:], decay[:], ALU.mult)
                st.then(V.tensor_tensor(sine[:], sine[:], decay[:], ALU.mult))
                st.then(V.tensor_tensor(m, a, a, ALU.mult))
                V.tensor_scalar(nr, half[:, 1:2], 1.0, None, ALU.subtract)
                st.then(V.scalar_tensor_tensor(out=m, in0=b, scalar=b, in1=m, op0=ALU.mult, op1=ALU.add))
                V.tensor_tensor(t1, nr, a, ALU.mult)
                V.tensor_tensor(t2, sine[:, 1:2], a, ALU.mult)
                st.then(V.reciprocal(m, m))
                V.scalar_tensor_tensor(out=wr, in0=sine[:, 1:2], scalar=b, in1=t1, op0=ALU.mult, op1=ALU.subtract)
                st.then(V.scalar_tensor_tensor(out=wi, in0=nr, scalar=b, in1=t2, op0=ALU.mult, op1=ALU.add))
                V.tensor_scalar(wr, wr, m, None, ALU.mult)
                st.then(V.tensor_scalar(wi, wi, m, -1.0, ALU.mult, ALU.mult))
                V.tensor_scalar(term[:, 0, :], cim[:], wi, None, ALU.mult)
                st.then(V.tensor_scalar(term[:, 1, :], cre[:], wi, None, ALU.mult))
                st.then(V.scalar_tensor_tensor(out=term[:, 0, :], in0=cre[:], scalar=wr, in1=term[:, 0, :],
                                               op0=ALU.mult, op1=ALU.subtract))
                st.then(V.scalar_tensor_tensor(out=term[:, 1, :], in0=cim[:], scalar=wr, in1=term[:, 1, :],
                                               op0=ALU.mult, op1=ALU.add))
                V.tensor_scalar(term[:, 1, :], term[:, 1, :], -1.0, None, ALU.mult).then_inc(modes, 1)
                dve.wait_ge(k_ready, 1)
                V.tensor_copy(K[:], K_ps[:]).then_inc(k_out, 1)
                dve.wait_ge(spectrum, 1)
                V.tensor_copy(KR[:], spec_ps[:, 0:2, :])
                V.tensor_copy(KR2[:], spec_ps[:, 0:2, :])
                st.then(V.tensor_copy(KI[:], spec_ps[:, 2:4, :]))
                V.tensor_copy(KR2[0:1, 0, :], spec_ps[0:1, 2, :])
                V.memset(KI[0:1, 0, :], 0.0)

            @block.tensor
            def _(pe):
                pe.wait_ge(modes, 1)
                for s in range(2):
                    nc.tensor.matmul(K_ps[:, s, :], half[:, s * TT:(s + 1) * TT], term[:, 0, :], start=True, stop=False)
                    ins = nc.tensor.matmul(K_ps[:, s, :], sine[:, s * TT:(s + 1) * TT], term[:, 1, :], start=False, stop=True)
                ins.then_inc(k_ready, 1)
                pe.wait_ge(k_out, 1)
                for j in range(4):
                    for s in range(2):
                        ins = nc.tensor.matmul(spec_ps[:, j, :], F[:, s, j * TT:(j + 1) * TT], K[:, s, :],
                                               start=(s == 0), stop=(s == 1))
                ins.then_inc(spectrum, 1)


def long_convolution(core):
    nc, h, d = core.nc, core.h, core.dram
    PAIRS = SEQS // 2
    with Layer(core, "a3") as L:
        u = L.sb("u", [TT, NT, C])
        gain = L.sb("gain", [TT, C])
        shift = L.sb("shift", [TT, C])
        skip = L.sb("skip", [TT, C])
        F = L.sb("F", [TT, 2, 2 * SEQ])
        G = L.sb("G", [TT, 4, SEQ])
        KR = L.sb("KR", [TT, 2, C])
        KR2 = L.sb("KR2", [TT, 2, C])
        KI = L.sb("KI", [TT, 2, C])
        loaded = L.sem("loaded")
        with nc.Block() as block:

            @block.sync
            def _(sp):
                for dst, name in ((gain, "a3_gain"), (shift, "a3_shift"), (skip, "a3_skip")):
                    sp.dma_start(dst[:], d[name].broadcast_to([TT, C])).then_inc(loaded, 16)
                for dst, name in ((F, "a3_F"), (G, "a3_G")):
                    sp.dma_start(dst[:], d[name]).then_inc(loaded, 16)
                sp.wait_ge(loaded, 16 * 5)
        kernel_spectrum(core, F, KR, KR2, KI)
        token_norm(core, "a3ln", u, gain[:], shift[:])
        prod = L.sb("prod", [TT, 2, 4, 2, C])
        Y = L.sb("Y", [TT, 4, 2, C])
        ud = L.sb("ud", [TT, 4, C])
        f_ps = [L.ps(f"f_ps{j}", [TT, 2, 2, C]) for j in range(2)]
        y_ps = L.ps("y_ps", [TT, 2, 2, C])
        f_ready = L.sem("f_ready")
        prod_ready = L.sem("prod_ready")
        Y_ready = L.sem("Y_ready")
        y_ready = L.sem("y_ready")
        ud_ready = L.sem("ud_ready")
        done = L.sem("done")
        ud_used = L.sem("ud_used")
        with nc.Block() as block:

            @block.tensor
            def _(pe):
                def forward(i):
                    for j in range(2):
                        if not (isinstance(i, int) and i == 0):
                            pe.wait_ge(prod_ready, i * 2 + j - 1)
                        for part in range(2):
                            for s in range(2):
                                x = u[:, ds(i * 4, 4), :].rearrange("p (b s) c -> p b s c", s=2)[:, :, s, :]
                                ins = nc.tensor.matmul(f_ps[j][:, part, :, :], F[:, s, (2 * part + j) * TT:(2 * part + j + 1) * TT],
                                                       x, start=(s == 0), stop=(s == 1))
                        ins.then_inc(f_ready, 1)

                def inverse(i):
                    if not (isinstance(i, int) and i == 0):
                        pe.wait_ge(done, i)
                        pe.nop(nofuse=True)
                    pe.wait_ge(Y_ready, i * 2 + 2)
                    for s in range(2):
                        for slot in range(4):
                            ins = nc.tensor.matmul(y_ps[:, s, :, :], G[:, slot, s * TT:(s + 1) * TT], Y[:, slot, :, :],
                                                   start=(slot == 0), stop=(slot == 3))
                    ins.then_inc(y_ready, 1)

                forward(0)
                forward(1)
                inverse(0)
                with pe.Fori(1, PAIRS - 1) as i:
                    forward(i + 1)
                    inverse(i)
                inverse(PAIRS - 1)

            @block.vector
            def _(dve):
                wide = [TT, 2, C]

                def products(i):
                    for j in range(2):
                        dve.wait_ge(f_ready, i * 2 + j + 1)
                        if not (isinstance(i, int) and i == 0):
                            dve.nop(nofuse=True)
                            dve.wait_ge(Y_ready, i * 2 + j - 1)
                        cu, su = f_ps[j][:, 0, :, :], f_ps[j][:, 1, :, :]
                        kr, kr2, ki = (k[:, j:j + 1, :].broadcast_to(wide) for k in (KR, KR2, KI))
                        nc.vector.tensor_tensor(prod[:, j, 0, :, :], cu, kr, ALU.mult)
                        nc.vector.tensor_tensor(prod[:, j, 1, :, :], su, ki, ALU.mult)
                        nc.vector.tensor_tensor(prod[:, j, 2, :, :], su, kr2, ALU.mult)
                        nc.vector.tensor_tensor(prod[:, j, 3, :, :], cu, ki, ALU.mult).then_inc(prod_ready, 1)

                def add(i):
                    dve.wait_ge(y_ready, i + 1)
                    mine = h[:, ds(i * 4, 4), :].rearrange("p (b s) c -> p s b c", s=2)
                    nc.vector.tensor_tensor(mine, y_ps[:], mine, ALU.add).then_inc(done, 1)
                    dve.wait_ge(ud_ready, i + 1)
                    dve.nop(nofuse=True)
                    dve.wait_ge(done, i + 1)
                    nc.vector.tensor_tensor(h[:, ds(i * 4, 4), :], ud[:], h[:, ds(i * 4, 4), :], ALU.add).then_inc(ud_used, 1)

                products(0)
                with dve.Fori(1, PAIRS) as i:
                    products(i)
                    add(i - 1)
                add(PAIRS - 1)

            @block.gpsimd
            def _(pool):
                def skipped(i, first=False):
                    if not first:
                        pool.wait_ge(ud_used, i)
                        pool.nop(nofuse=True)
                    nc.gpsimd.tensor_tensor(ud[:], u[:, ds(i * 4, 4), :], skip[:].unsqueeze(1).broadcast_to([TT, 4, C]),
                                            ALU.mult).then_inc(ud_ready, 1)

                def sums(i, first=False):
                    for j in range(2):
                        pool.wait_ge(prod_ready, i * 2 + j + 1)
                        if j == 0 and not first:
                            pool.nop(nofuse=True)
                            pool.wait_ge(y_ready, i)
                        nc.gpsimd.tensor_tensor(Y[:, j, :, :], prod[:, j, 0, :, :], prod[:, j, 1, :, :], ALU.subtract)
                        nc.gpsimd.tensor_tensor(Y[:, 2 + j, :, :], prod[:, j, 2, :, :], prod[:, j, 3, :, :],
                                                ALU.add).then_inc(Y_ready, 1)

                sums(0, first=True)
                skipped(0, first=True)
                with pool.Fori(1, PAIRS) as i:
                    sums(i)
                    skipped(i)


ROUND = 12582912.0
QMAX = 32767.0
U16 = 65536.0


class Scale:

    def __init__(self, L, name):
        self.most = L.sb(f"{name}_most", [P, 1])
        self.all = L.sb(f"{name}_all", [P, 1])
        self.step = L.sb(f"{name}_step", [P, 1])
        self.inverse = L.sb(f"{name}_inverse", [P, 1])


def make_scales(core, name, pairs):
    nc = core.nc
    with Layer(core, name) as L:
        steps, most_ready, all_ready = L.sem("steps"), L.sem("most_ready"), L.sem("all_ready")
        with nc.Block() as block:

            @block.vector
            def _(dve):
                st = Steps(dve, steps)
                for s, maxima in pairs:
                    nc.vector.reduce_max(s.most[:], maxima, AX.X).then_inc(most_ready, 1)
                for n, (s, _) in enumerate(pairs):
                    dve.wait_ge(all_ready, n + 1)
                    st.then(nc.vector.tensor_scalar(s.step[:], s.all[:], 1.0 / QMAX, 1e-12, ALU.mult, ALU.max))
                    nc.vector.reciprocal(s.inverse[:], s.step[:])

            @block.gpsimd
            def _(pool):
                for n, (s, _) in enumerate(pairs):
                    pool.wait_ge(most_ready, n + 1)
                    nc.gpsimd.partition_all_reduce(s.all[:], s.most[:], P, bass.bass_isa.ReduceOp.max).then_inc(all_ready, 1)


def block_weights(core, name, jobs):
    nc, ident = core.nc, core.ident
    BLOCK, W_QMAX = 32, 7.0
    SQUARES = 4
    with Layer(core, name) as L:
        w = [L.sb(f"w{n}", list(src.shape)) for n, (src, _) in enumerate(jobs)]
        NB = w[0].shape[1] * w[0].shape[2] // BLOCK
        inverse = L.sb("inverse", [P, NB])
        step = L.sb("step", [P, NB])
        turned = [L.ps(f"turned{s}", [P, BANK]) for s in range(2)]
        loaded = [L.sem(f"loaded{n}") for n in range(len(jobs))]
        steps, w_ready, t_ready, t_out = (L.sem(n) for n in ("steps", "w_ready", "t_ready", "t_out"))
        wide = [P, NB, BLOCK]
        banks = w[0].shape[1] * w[0].shape[2] // P // SQUARES

        with nc.Block() as block:

            @block.sync
            def _(sp):
                for n, (src, _) in enumerate(jobs):
                    sp.dma_start(w[n][:], src).then_inc(loaded[n], 16)

            @block.vector
            def _(dve):
                st = Steps(dve, steps)
                for n in range(len(jobs)):
                    all_w = w[n][:]
                    blocks = all_w.rearrange("p t (n b) -> p (t n) b", b=BLOCK)
                    dve.wait_ge(loaded[n], 16)
                    st.then(nc.vector.reduce_max(step[:], blocks, AX.X, apply_absolute_value=True))
                    st.then(nc.vector.tensor_scalar(step[:], step[:], 1.0 / W_QMAX, 1e-12, ALU.mult, ALU.max))
                    st.then(nc.vector.reciprocal(inverse[:], step[:]))
                    st.then(nc.vector.tensor_tensor(blocks, blocks, inverse[:].unsqueeze(2).broadcast_to(wide), ALU.mult))
                    st.then(nc.vector.tensor_scalar(all_w, all_w, ROUND, ROUND, ALU.add, ALU.subtract))
                    st.then(nc.vector.tensor_scalar(all_w, all_w, W_QMAX, -W_QMAX - 1.0, ALU.min, ALU.max))
                    nc.vector.tensor_tensor(blocks, blocks, step[:].unsqueeze(2).broadcast_to(wide), ALU.mult).then_inc(w_ready, 1)
                    dve.wait_ge(w_ready, n + 1)

            @block.tensor
            def _(pe):
                for n in range(len(jobs)):
                    tiles = w[n].shape[1]
                    pe.wait_ge(w_ready, n + 1)
                    for g in range(banks):
                        number = n * banks + g
                        if number >= 2:
                            pe.wait_ge(t_out, number - 1)
                        for q in range(SQUARES * g, SQUARES * (g + 1)):
                            c, t = q // tiles, q % tiles
                            ins = nc.tensor.transpose(turned[number % 2][:, (q % SQUARES) * P:(q % SQUARES + 1) * P],
                                                      w[n][:, t, c * P:(c + 1) * P], ident[:])
                        ins.then_inc(t_ready, 1)

            @block.scalar
            def _(act):
                for n, (_, wT) in enumerate(jobs):
                    out = wT.rearrange("p c o -> p (c o)")
                    for g in range(banks):
                        number = n * banks + g
                        act.wait_ge(t_ready, number + 1)
                        nc.scalar.copy(out[:, g * BANK:(g + 1) * BANK], turned[number % 2][:]).then_inc(t_out, 1)


def quantised_mlp(core):
    nc, h, d = core.nc, core.h, core.dram
    I = d["f1_gate"].shape[1] * P
    M = I // P
    MH = M // 2
    with Layer(core, "f1") as L:
        gateT = L.sb("gateT", [P, KC, I])
        upT = L.sb("upT", [P, KC, I])
        downT = L.sb("downT", [P, M, C])
        block_weights(core, "f1w", [(d["f1_gate"], gateT[:]), (d["f1_up"], upT[:]), (d["f1_down"], downT[:])])
        rounder = L.sb("rounder", [P, 1])
        x_max = L.sb("x_max", [P, KC * NU])
        gate_max = L.sb("gate_max", [P, 2 * NU])
        up_max = L.sb("up_max", [P, 2 * NU])
        act_max = L.sb("act_max", [P, 2 * NU])
        out_max = L.sb("out_max", [P, 2 * NU])
        sx, sg, su, sa, so = (Scale(L, n) for n in ("sx", "sg", "su", "sa", "so"))
        act_step = L.sb("act_step", [P, 1])
        both_step = L.sb("both_step", [P, 1])
        gate = L.sb("gate", [P, M, TOK])

        def unit_of(tensor, u):
            return tensor[:, :, ds(u * UNIT, UNIT)]

        def half(u, s):
            return gate[:, s * MH:(s + 1) * MH, ds(u * UNIT, UNIT)]

        def product(banks, weights, xT, u, s):
            for n in range(MH):
                m = s * MH + n
                for k in range(KC):
                    ins = nc.tensor.matmul(banks[:, n, 0:UNIT], weights[:, k, m * P:(m + 1) * P],
                                           xT[:, k, ds(u * UNIT, UNIT)], start=(k == 0), stop=(k == KC - 1))
            return ins

        def rounded_to_int(out, src, scale):
            return nc.scalar.activation(out, src, ACT.Identity, bias=rounder[:], scale=scale.inverse[:])

        def clipped(part):
            return nc.vector.tensor_scalar(part, part, ROUND + QMAX, ROUND - QMAX - 1.0, ALU.min, ALU.max)

        def stepped(part, step):
            return nc.vector.tensor_scalar(part, part, ROUND, step[:], ALU.subtract, ALU.mult)

        with Layer(core, "f1x") as LX:
            xT = LX.sb("xT", [P, KC, TOK])
            layer_norm(core, "f1ln", xT)
            with nc.Block() as block:

                @block.vector
                def _(dve):
                    nc.vector.memset(rounder[:], ROUND)
                    nc.vector.reduce_max(x_max[:].rearrange("p (k u) -> p k u", k=KC),
                                         xT[:].rearrange("p k (u n) -> p k u n", u=NU), AX.X, apply_absolute_value=True)
            make_scales(core, "f1sx", [(sx, x_max[:])])

            with Layer(core, "f1p") as LP:
                g_ps = [LP.ps(f"g_ps{s}", [P, MH, BANK]) for s in range(2)]
                rounded, x_clipped, x_ready, g_ready, g_out = (
                    LP.sem(n) for n in ("rounded", "x_clipped", "x_ready", "g_ready", "g_out"))
                with nc.Block() as block:

                    @block.scalar
                    def _(act):
                        with act.Fori(0, NU) as u:
                            rounded_to_int(unit_of(xT, u), unit_of(xT, u), sx).then_inc(rounded, 1)
                        with act.Fori(0, NU) as u:
                            for s in range(2):
                                act.wait_ge(g_ready, u * 2 + s + 1)
                                nc.scalar.copy(half(u, s), g_ps[s][:, :, 0:UNIT]).then_inc(g_out, 1)

                    @block.vector
                    def _(dve):
                        with dve.Fori(0, NU) as u:
                            dve.wait_ge(rounded, u + 1)
                            clipped(unit_of(xT, u)).then_inc(x_clipped, 1)
                            dve.wait_ge(x_clipped, u + 1)
                            stepped(unit_of(xT, u), sx.step).then_inc(x_ready, 1)
                        with dve.Fori(0, NU) as u:
                            for s in range(2):
                                dve.wait_ge(g_out, u * 2 + s + 1)
                                nc.vector.tensor_reduce(gate_max[:, ds(u * 2 + s, 1)], half(u, s), AX.XY, ALU.max,
                                                        apply_absolute_value=True)

                    @block.tensor
                    def _(pe):
                        pe.wait_ge(x_ready, 1)
                        for s in range(2):
                            product(g_ps[s], gateT, xT, 0, s).then_inc(g_ready, 1)
                        with pe.Fori(1, NU) as u:
                            pe.wait_ge(x_ready, u + 1)
                            for s in range(2):
                                pe.wait_ge(g_out, u * 2 + s - 1)
                                product(g_ps[s], gateT, xT, u, s).then_inc(g_ready, 1)
            make_scales(core, "f1sg", [(sg, gate_max[:])])

            with Layer(core, "f1s") as LS:
                sig = LS.sb("sig", [P, 2, MH, UNIT])
                u_ps = [LS.ps(f"u_ps{s}", [P, MH, BANK]) for s in range(2)]
                rounded, q_ready, raw_ready, sig_ready, sig_used, u_ready, u_seen, step_set, steps = (LS.sem(n) for n in (
                    "rounded", "q_ready", "raw_ready", "sig_ready", "sig_used", "u_ready", "u_seen", "step_set", "steps"))

                def is_first(u):
                    return isinstance(u, int) and u == 0

                def over_units(eng, turn, st=None, steps_of_turn=0):
                    for s in range(2):
                        turn(0, s, ahead=2)
                    with eng.Fori(1, NU - 1) as u:
                        if st is not None:
                            st.enter(u - 1, 2 * steps_of_turn)
                        for s in range(2):
                            turn(u, s, ahead=2)
                        if st is not None:
                            st.leave(NU - 2)
                    turn(NU - 1, 0, ahead=1)
                    turn(NU - 1, 1, ahead=0)

                with nc.Block() as block:

                    @block.tensor
                    def _(pe):
                        def turn(u, s, ahead):
                            if not is_first(u):
                                pe.wait_ge(u_seen, u * 2 + s - 1)
                            product(u_ps[s], upT, xT, u, s).then_inc(u_ready, 1)

                        over_units(pe, turn)

                    @block.scalar
                    def _(act):
                        def round_gate(u, s):
                            rounded_to_int(half(u, s), half(u, s), sg).then_inc(rounded, 1)

                        def sigmoid(u, s):
                            j = u * 2 + s
                            act.wait_ge(q_ready, j + 1)
                            if not is_first(u):
                                act.nop(nofuse=True)
                                act.wait_ge(sig_used, j - 1)
                            act.nop(nofuse=True)
                            nc.scalar.activation(sig[:, s, :, :], half(u, s), ACT.Sigmoid, scale=U16).then_inc(raw_ready, 1)
                            act.wait_ge(raw_ready, j + 1)
                            act.nop(nofuse=True)
                            nc.scalar.activation(sig[:, s, :, :], sig[:, s, :, :], ACT.Identity, bias=rounder[:],
                                                 scale=U16).then_inc(sig_ready, 1)

                        def turn(u, s, ahead):
                            if ahead == 2:
                                round_gate(u + 1, s)
                            if ahead >= 1:
                                sigmoid(u + s, 1 - s)

                        round_gate(0, 0)
                        round_gate(0, 1)
                        sigmoid(0, 0)
                        over_units(act, turn)

                    @block.vector
                    def _(dve):
                        st = Steps(dve, steps)

                        def quantise(u, s):
                            dve.wait_ge(rounded, u * 2 + s + 1)
                            st.then(clipped(half(u, s)))
                            stepped(half(u, s), act_step).then_inc(q_ready, 1)

                        def turn(u, s, ahead):
                            j = u * 2 + s
                            if ahead == 2:
                                quantise(u + 1, s)
                            dve.wait_ge(u_ready, j + 1)
                            nc.vector.tensor_reduce(up_max[:, ds(j, 1)], u_ps[s][:, :, 0:UNIT], AX.XY, ALU.max,
                                                    apply_absolute_value=True).then_inc(u_seen, 1)
                            dve.wait_ge(sig_ready, j + 1)
                            st.then(nc.vector.tensor_scalar(sig[:, s, :, :], sig[:, s, :, :], ROUND, ROUND + U16 - 1.0, ALU.max, ALU.min))
                            st.then(nc.vector.scalar_tensor_tensor(out=half(u, s), in0=sig[:, s, :, :], scalar=-ROUND,
                                                                   in1=half(u, s), op0=ALU.add, op1=ALU.mult))
                            nc.vector.tensor_reduce(act_max[:, ds(j, 1)], half(u, s), AX.XY, ALU.max,
                                                    apply_absolute_value=True).then_inc(sig_used, 1)

                        nc.vector.tensor_scalar(act_step[:], sg.step[:], 1.0 / U16, None, ALU.mult).then_inc(step_set, 1)
                        dve.wait_ge(step_set, 1)
                        quantise(0, 0)
                        quantise(0, 1)
                        over_units(dve, turn, st, 3)
            make_scales(core, "f1sa", [(sa, act_max[:]), (su, up_max[:])])

            with Layer(core, "f1u") as LU:
                up = LU.sb("up", [P, 2, MH, UNIT])
                u_ps = [LU.ps(f"u_ps{s}", [P, MH, BANK]) for s in range(2)]
                u_ready, u_out, g_out, up_free, step_set, steps = (
                    LU.sem(n) for n in ("u_ready", "u_out", "g_out", "up_free", "step_set", "steps"))
                with nc.Block() as block:

                    @block.tensor
                    def _(pe):
                        for s in range(2):
                            product(u_ps[s], upT, xT, 0, s).then_inc(u_ready, 1)
                        with pe.Fori(1, NU) as u:
                            for s in range(2):
                                pe.wait_ge(u_out, u * 2 + s - 1)
                                product(u_ps[s], upT, xT, u, s).then_inc(u_ready, 1)

                    @block.scalar
                    def _(act):
                        def turn(u, s, first=False):
                            j = u * 2 + s
                            rounded_to_int(half(u, s), half(u, s), sa).then_inc(g_out, 1)
                            act.wait_ge(u_ready, j + 1)
                            if not first:
                                act.nop(nofuse=True)
                                act.wait_ge(up_free, j - 1)
                                act.nop(nofuse=True)
                            rounded_to_int(up[:, s, :, :], u_ps[s][:, :, 0:UNIT], su).then_inc(u_out, 1)

                        for s in range(2):
                            turn(0, s, first=True)
                        with act.Fori(1, NU) as u:
                            for s in range(2):
                                turn(u, s)

                    @block.vector
                    def _(dve):
                        st = Steps(dve, steps)
                        nc.vector.tensor_scalar(both_step[:], sa.step[:], su.step[:], None, ALU.mult).then_inc(step_set, 1)
                        dve.wait_ge(step_set, 1)
                        with dve.Fori(0, NU) as u:
                            st.enter(u, 2 * 3)
                            for s in range(2):
                                j = u * 2 + s
                                mine = up[:, s, :, :]
                                dve.wait_ge(g_out, j + 1)
                                clipped(half(u, s))
                                dve.wait_ge(u_out, j + 1)
                                st.then(clipped(mine))
                                st.then(stepped(mine, both_step))
                                st.then(nc.vector.scalar_tensor_tensor(out=half(u, s), in0=half(u, s), scalar=-ROUND, in1=mine,
                                                                       op0=ALU.add, op1=ALU.mult))
                                nc.vector.tensor_reduce(out_max[:, ds(j, 1)], half(u, s), AX.XY, ALU.max,
                                                        apply_absolute_value=True).then_inc(up_free, 1)
                            st.leave(NU)
        make_scales(core, "f1so", [(so, out_max[:])])

        with Layer(core, "f1d") as LD:
            q = LD.sb("q", [P, 2, M, UNIT])
            y_ps = [LD.ps(f"y_ps{s}", [TT, 2, BANK]) for s in range(2)]
            rounded, q_ready, y_ready, y_free, steps = (LD.sem(n) for n in ("rounded", "q_ready", "y_ready", "y_free", "steps"))
            with nc.Block() as block:

                @block.scalar
                def _(act):
                    with act.Fori(0, NU // 2) as i:
                        for s in range(2):
                            u = i * 2 + s
                            act.wait_ge(y_free, u + 1)
                            act.nop(nofuse=True)
                            nc.scalar.activation(q[:, s, :, :], gate[:, :, ds(u * UNIT, UNIT)], ACT.Identity, bias=rounder[:],
                                                 scale=so.inverse[:]).then_inc(rounded, 1)

                @block.tensor
                def _(pe):
                    with pe.Fori(0, NU // 2) as i:
                        for s in range(2):
                            u = i * 2 + s
                            pe.wait_ge(q_ready, u + 1)
                            for t in range(UT):
                                for m in range(M):
                                    ins = nc.tensor.matmul(y_ps[s][:, t // 2, (t % 2) * C:(t % 2 + 1) * C],
                                                           q[:, s, m, t * TT:(t + 1) * TT], downT[:, m, :],
                                                           start=(m == 0), stop=(m == M - 1))
                            ins.then_inc(y_ready, 1)

                @block.vector
                def _(dve):
                    st = Steps(dve, steps)
                    dve.sem_inc(y_free, 2)

                    def quantise(u, s):
                        dve.wait_ge(rounded, u + 1)
                        st.then(nc.vector.tensor_scalar(q[:, s, :, :], q[:, s, :, :], ROUND + QMAX, ROUND - QMAX - 1.0, ALU.min, ALU.max))
                        nc.vector.tensor_scalar(q[:, s, :, :], q[:, s, :, :], ROUND, so.step[:], ALU.subtract, ALU.mult).then_inc(q_ready, 1)

                    def add(u, s):
                        dve.wait_ge(y_ready, u + 1)
                        nc.vector.tensor_tensor(h[:, ds(u * UT, UT), :], y_ps[s][:, :, :].rearrange("p a (b c) -> p (a b) c", c=C),
                                                h[:, ds(u * UT, UT), :], ALU.add).then_inc(y_free, 1)

                    quantise(0, 0)
                    with dve.Fori(0, NU // 2 - 1) as i:
                        st.enter(i, 2)
                        for s in range(2):
                            quantise(i * 2 + s + 1, (s + 1) % 2)
                            add(i * 2 + s, s)
                        st.leave(NU // 2 - 1)
                    quantise(NU - 1, 1)
                    add(NU - 2, 0)
                    add(NU - 1, 1)


def recurrent_mix(core):
    nc, h, d = core.nc, core.h, core.dram
    HN, MIX, TM, TD = 16, 5, 32, 64
    G = C // P * HN // 2
    GN_EPS = 1e-5 * 64
    with Layer(core, "m1") as L:
        xT = L.sb("xT", [P, KC, TOK])
        w1 = L.sb("w1", [P, KC, MIX * TM])
        w2a = L.sb("w2a", [P, C])
        w2b = L.sb("w2b", [TM, C])
        mx = L.sb("mx", [P, KC])
        mf = L.sb("mf", [P, MIX, KC])
        tdecay = L.sb("tdecay", [P, KC])
        td1 = L.sb("td1", [P, KC, TD])
        td2 = L.sb("td2", [TD, C])
        bonus = L.sb("bonus", [P, KC])
        wr, wk, wv, wg, wo = (L.sb(n, [P, KC, C]) for n in ("wr", "wk", "wv", "wg", "wo"))
        ln_w = L.sb("ln_w", [P, KC])
        ln_b = L.sb("ln_b", [P, KC])
        spread = L.sb("spread", [P, HN, P])
        gather = L.sb("gather", [P, HN, P])
        same = L.sb("same", [P, P])
        mean16 = L.sb("mean16", [P, P])
        loads = [(w1, "m1_w1"), (w2a, "m1_w2a"), (w2b, "m1_w2b"), (mx, "m1_mx"), (mf, "m1_mf"), (tdecay, "m1_tdecay"),
                 (td1, "m1_td1"), (td2, "m1_td2"), (bonus, "m1_bonus"), (wr, "m1_wr"), (wk, "m1_wk"), (wv, "m1_wv"),
                 (wg, "m1_wg"), (wo, "m1_wo"), (ln_w, "m1_lnw"), (ln_b, "m1_lnb"), (spread, "m1_spread"),
                 (gather, "m1_gather"), (same, "m1_same")]
        all_loaded = 16 * len(loads)
        loaded = L.sem("loaded")

        def load(sp):
            for dst, name in loads:
                sp.dma_start(dst[:], d[name]).then_inc(loaded, 16)

        layer_norm(core, "m1ln", xT, beside=load)
        xs = L.sb("xs", [P, KC, SEQ + 1])
        xx = L.sb("xx", [P, KC, SEQ])
        xxx = L.sb("xxx", [P, KC, SEQ])
        t5 = L.sb("t5", [P, 2, SEQ])
        mixed = L.sb("mixed", [P, 2, KC, SEQ])
        xf = L.sb("xf", [P, MIX, KC, SEQ])
        tw = L.sb("tw", [TD, SEQ])
        decay, r, k, v, g = (L.sb(n, [P, 2, KC, SEQ]) for n in ("decay", "r", "k", "v", "g"))
        ruk = L.sb("ruk", [P, KC, SEQ])
        yu = L.sb("yu", [P, KC, SEQ])
        kv = L.sb("kv", [P, 3, 2, SEQ])
        S = L.sb("S", [P, 3, 2, SEQ + 1])
        rS = L.sb("rS", [P, 3, 2, SEQ])
        y = L.sb("y", [P, KC, SEQ])
        square = L.sb("square", [P, KC, SEQ])
        gn_eps = L.sb("gn_eps", [P, 1])
        pr = [L.ps(f"pr{s}", [P, KC, BANK // 2]) for s in range(3)]
        vrep = [L.ps(f"vrep{s}", [P, 2, BANK // 2]) for s in range(2)]
        y_ps = L.ps("y_ps", [P, KC, BANK // 2])
        aux = L.ps("aux", [P, KC, BANK // 2])
        out_ps = L.ps("out_ps", [TT, 2, C])
        names = ("const xs_ready xxx_ready pr_ready act_ev dve_ev xf_ready d_ready ruk_ready yu_ready vrep_ready kv_ready "
                 "S_ready rS_ready y_part y_ready mean_ready yc_ready sq_ready var_ready std_ready z_ready "
                 "out_ready turn_done steps").split()
        (const, xs_ready, xxx_ready, pr_ready, act_ev, dve_ev, xf_ready, d_ready, ruk_ready, yu_ready, vrep_ready, kv_ready,
         S_ready, rS_ready, y_part, y_ready, mean_ready, yc_ready, sq_ready, var_ready, std_ready, z_ready,
         out_ready, turn_done, steps) = (L.sem(n) for n in names)

        PE_AT = {1: ["t5", "mean"], 2: ["mix0"], 3: ["mix1"], 4: ["mix2", "var"], 5: ["mix3"], 6: ["mix4"], 8: ["td1"],
                 9: ["out"], 10: ["yu"], 11: ["k"], 13: ["td2"], 15: ["v"], 16: ["r"], 17: ["g"]}
        DVE_AT = {0: ["sum", "shift"], 2: ["centre", "mix0"], 3: ["ruk", "mix1"], 4: ["mix2"], 5: ["mix3"], 6: ["inverse", "mix4"],
                  7: ["scale"], 10: ["add"], 11: ["yu"]}
        POOL_AT = {0: "shift", 3: "mix0", 4: "mix1", 5: "mix2", 6: "mix3", 7: "mix4"}
        BACK = ("sum", "centre", "inverse", "scale", "add", "mean", "var", "out")

        def tasks_of(table, n, first, last):
            return [t for t in table.get(n, []) if (t in BACK and not first) or t in ("ruk", "yu")
                    or (t not in BACK and t not in ("ruk", "yu") and not last)]

        def over_turns(eng, front, turn, st=None, steps_of_turn=None):
            front(0, 0)
            turn(0, 0, first=True)
            with eng.Fori(0, SEQS // 2 - 1) as i:
                if st is not None:
                    st.enter(i, 2 * steps_of_turn)
                turn(i * 2 + 1, 1)
                turn(i * 2 + 2, 0)
                if st is not None:
                    st.leave(SEQS // 2 - 1)
            turn(SEQS - 1, 1, last=True)

        with nc.Block() as block:

            @block.gpsimd
            def _(pool):
                pool.wait_ge(loaded, all_loaded)
                nc.gpsimd.memset(xs[:], 0.0)
                nc.gpsimd.memset(S[:], 0.0)
                nc.gpsimd.memset(gn_eps[:], GN_EPS)
                nc.gpsimd.tensor_scalar(mean16[:], same[:], 1.0 / HN, None, ALU.mult).then_inc(const, 1)
                pool.wait_ge(const, 1)

                def front(b, s, task=None):
                    if task in (None, "shift"):
                        if not (isinstance(b, int) and b == 0):
                            pool.wait_ge(pr_ready, b * 12)
                            pool.nop(nofuse=True)
                            pool.wait_ge(xf_ready, b * MIX)
                        nc.gpsimd.tensor_copy(xs[:, :, 1:SEQ + 1], xT[:, :, ds(b * SEQ, SEQ)]).then_inc(xs_ready, 1)
                    for f in range(MIX):
                        if task in (None, f"mix{f}"):
                            pool.wait_ge(dve_ev, b * MIX + f + 1)
                            if f == 0:
                                pool.nop(nofuse=True)
                                pool.wait_ge(xs_ready, b + 1)
                            nc.gpsimd.tensor_tensor(xf[:, f, :, :], mixed[:, f % 2, :, :], xs[:, :, 1:SEQ + 1],
                                                    ALU.add).then_inc(xf_ready, 1)

                def turn(b, s, first=False, last=False):
                    for n in range(G):
                        c = n // (HN // 2)
                        if n == 0 and not last:
                            front(b + 1, 1 - s, "shift")
                        pool.wait_ge(S_ready, b * G + n + 1)
                        if n == 0:
                            pool.nop(nofuse=True)
                            pool.wait_ge(act_ev, b * 7 + 6)
                        if n >= 3:
                            pool.nop(nofuse=True)
                            pool.wait_ge(y_part, b * G + n - 2)
                        nc.gpsimd.tensor_tensor(rS[:, n % 3, :, :], S[:, n % 3, :, 0:SEQ],
                                                r[:, s, c:c + 1, :].broadcast_to([P, 2, SEQ]), ALU.mult).then_inc(rS_ready, 1)
                        if n > 0 and n in POOL_AT and not last:
                            front(b + 1, 1 - s, POOL_AT[n])

                over_turns(pool, front, turn)

            @block.tensor
            def _(pe):
                def project(n, lhs, rhs, rows=P):
                    for c in range(len(lhs)):
                        for i in range(len(rhs)):
                            ins = nc.tensor.matmul(pr[n % 3][0:rows, c, 0:SEQ], lhs[c][i], rhs[i],
                                                   start=(i == 0), stop=(i == len(rhs) - 1))
                    ins.then_inc(pr_ready, 1)

                def weights(w):
                    return [[w[:, i, c * P:(c + 1) * P] for i in range(KC)] for c in range(KC)]

                def stream(f):
                    return [xf[:, f, i, :] for i in range(KC)]

                def front(b, s, task=None):
                    if task in (None, "t5"):
                        pe.wait_ge(xxx_ready, b + 1)
                        for i in range(KC):
                            nc.tensor.matmul(pr[0][:, 0, 0:SEQ], w1[:, i, 0:4 * TM], xxx[:, i, :], start=(i == 0), stop=(i == KC - 1))
                        for i in range(KC):
                            ins = nc.tensor.matmul(pr[0][0:TM, 1, 0:SEQ], w1[:, i, 4 * TM:], xxx[:, i, :],
                                                   start=(i == 0), stop=(i == KC - 1))
                        ins.then_inc(pr_ready, 1)
                    for f in range(MIX):
                        if task in (None, f"mix{f}"):
                            if f == 0:
                                pe.wait_ge(act_ev, b * 7 + 1)
                            if f >= 3:
                                pe.wait_ge(dve_ev, b * MIX + f - 2)
                            rows = slice(TM * f, TM * f + TM)
                            lhs = [[(w2a[rows, c * P:(c + 1) * P] if f < 4 else w2b[:, c * P:(c + 1) * P])] for c in range(KC)]
                            project(f + 1, lhs, [t5[rows, 0, :] if f < 4 else t5[0:TM, 1, :]])
                    if task in (None, "td1"):
                        pe.wait_ge(xf_ready, b * MIX + 1)
                        pe.nop(nofuse=True)
                        pe.wait_ge(dve_ev, b * MIX + 3)
                        project(6, [[td1[:, i, :] for i in range(KC)]], stream(0), rows=TD)
                    if task in (None, "k"):
                        pe.wait_ge(dve_ev, b * MIX + 4)
                        pe.nop(nofuse=True)
                        pe.wait_ge(xf_ready, b * MIX + 2)
                        project(7, weights(wk), stream(1))
                    if task in (None, "td2"):
                        pe.wait_ge(dve_ev, b * MIX + 5)
                        pe.nop(nofuse=True)
                        pe.wait_ge(act_ev, b * 7 + 2)
                        project(8, [[td2[:, c * P:(c + 1) * P]] for c in range(KC)], [tw[:]])
                    if task in (None, "v"):
                        pe.wait_ge(xf_ready, b * MIX + 3)
                        project(9, weights(wv), stream(2))
                    if task in (None, "r"):
                        pe.wait_ge(xf_ready, b * MIX + 4)
                        pe.nop(nofuse=True)
                        pe.wait_ge(act_ev, b * 7 + 3)
                        project(10, weights(wr), stream(3))
                    if task in (None, "g"):
                        pe.wait_ge(xf_ready, b * MIX + 5)
                        pe.nop(nofuse=True)
                        pe.wait_ge(act_ev, b * 7 + 4)
                        project(11, weights(wg), stream(4))

                def back(b, task):
                    if task == "mean":
                        pe.wait_ge(y_ready, b)
                        for c in range(KC):
                            ins = nc.tensor.matmul(aux[:, c, 0:SEQ], mean16[:], y[:, c, :], start=True, stop=True)
                        ins.then_inc(mean_ready, 1)
                    elif task == "var":
                        pe.wait_ge(sq_ready, b)
                        for c in range(KC):
                            ins = nc.tensor.matmul(aux[:, c, 0:SEQ], mean16[:], square[:, c, :], start=True, stop=True)
                        ins.then_inc(var_ready, 1)
                    else:
                        pe.wait_ge(z_ready, b)
                        for a in range(2):
                            for i in range(KC):
                                ins = nc.tensor.matmul(out_ps[:, a, :], y[:, i, a * TT:(a + 1) * TT], wo[:, i, :],
                                                       start=(i == 0), stop=(i == KC - 1))
                        ins.then_inc(out_ready, 1)

                def turn(b, s, first=False, last=False):
                    def spread_v(n):
                        c, j = n // (HN // 2), 2 * (n % (HN // 2))
                        if n == 0:
                            pe.wait_ge(act_ev, b * 7 + 5)
                        if n >= 2:
                            pe.wait_ge(kv_ready, b * G + n - 1)
                        for p in range(2):
                            ins = nc.tensor.matmul(vrep[n % 2][:, p, 0:SEQ], spread[:, j + p, :], v[:, s, c, :], start=True, stop=True)
                        ins.then_inc(vrep_ready, 1)

                    def sum_i(n):
                        c, j = n // (HN // 2), 2 * (n % (HN // 2))
                        pe.wait_ge(rS_ready, b * G + n + 1)
                        for p in range(2):
                            ins = nc.tensor.matmul(y_ps[:, c, 0:SEQ], gather[:, j + p, :], rS[:, n % 3, p, :],
                                                   start=(j + p == 0), stop=(j + p == HN - 1))
                        ins.then_inc(y_part, 1)

                    for n in range(G + 3):
                        if n < G:
                            spread_v(n)
                        if n >= 3:
                            if n == 3 and not first:
                                pe.wait_ge(y_ready, b)
                            sum_i(n - 3)
                        for task in tasks_of(PE_AT, n, first, last):
                            if task in BACK:
                                back(b, task)
                            elif task == "yu":
                                pe.wait_ge(ruk_ready, b + 1)
                                for c in range(KC):
                                    ins = nc.tensor.matmul(aux[:, c, 0:SEQ], same[:], ruk[:, c, :], start=True, stop=True)
                                ins.then_inc(yu_ready, 1)
                            else:
                                front(b + 1, 1 - s, task)

                pe.wait_ge(const, 1)
                over_turns(pe, front, turn)
                for task in ("mean", "var", "out"):
                    back(SEQS, task)

            @block.scalar
            def _(act):
                def front(b, s, task=None):
                    if task in (None, "t5"):
                        act.wait_ge(pr_ready, b * 12 + 1)
                        nc.scalar.activation(t5[:, 0, :], pr[0][:, 0, 0:SEQ], ACT.Tanh)
                        nc.scalar.activation(t5[0:TM, 1, :], pr[0][0:TM, 1, 0:SEQ], ACT.Tanh).then_inc(act_ev, 1)
                    if task in (None, "rest"):
                        act.wait_ge(pr_ready, b * 12 + 7)
                        nc.scalar.activation(tw[:], pr[0][0:TD, 0, 0:SEQ], ACT.Tanh).then_inc(act_ev, 1)
                        act.wait_ge(pr_ready, b * 12 + 8)
                        if not (isinstance(b, int) and b < 2):
                            act.nop(nofuse=True)
                            act.wait_ge(y_ready, b - 1)
                        nc.scalar.copy(k[:, s, :, :], pr[1][:, :, 0:SEQ]).then_inc(act_ev, 1)
                        act.wait_ge(pr_ready, b * 12 + 9)
                        for c in range(KC):
                            ins = nc.scalar.activation(decay[:, s, c, :], pr[2][:, c, 0:SEQ], ACT.Exp, bias=tdecay[:, c:c + 1])
                        ins.then_inc(act_ev, 1)
                        act.wait_ge(act_ev, b * 7 + 4)
                        nc.scalar.activation(decay[:, s, :, :], decay[:, s, :, :], ACT.Exp, scale=-1.0).then_inc(d_ready, 1)
                        act.wait_ge(pr_ready, b * 12 + 10)
                        nc.scalar.copy(v[:, s, :, :], pr[0][:, :, 0:SEQ]).then_inc(act_ev, 1)
                        act.wait_ge(pr_ready, b * 12 + 11)
                        nc.scalar.copy(r[:, s, :, :], pr[1][:, :, 0:SEQ]).then_inc(act_ev, 1)
                        act.wait_ge(pr_ready, b * 12 + 12)
                        if not (isinstance(b, int) and b < 2):
                            act.nop(nofuse=True)
                            act.wait_ge(turn_done, b - 1)
                        nc.scalar.activation(g[:, s, :, :], pr[2][:, :, 0:SEQ], ACT.Silu).then_inc(act_ev, 1)

                def back(b):
                    act.wait_ge(yc_ready, b)
                    nc.scalar.activation(square[:], y[:], ACT.Square).then_inc(sq_ready, 1)
                    act.wait_ge(var_ready, b)
                    nc.scalar.activation(square[:], aux[:, :, 0:SEQ], ACT.Sqrt, bias=gn_eps[:]).then_inc(std_ready, 1)

                def turn(b, s, first=False, last=False):
                    if not last:
                        front(b + 1, 1 - s, "t5")
                    if not first:
                        back(b)
                    if not last:
                        front(b + 1, 1 - s, "rest")

                act.wait_ge(const, 1)
                over_turns(act, front, turn)
                back(SEQS)

            @block.vector
            def _(dve):
                st = Steps(dve, steps)
                V = nc.vector

                def front(b, s, task=None):
                    if task in (None, "shift"):
                        dve.wait_ge(xs_ready, b + 1)
                        st.then(V.tensor_tensor(xx[:], xs[:, :, 0:SEQ], xs[:, :, 1:SEQ + 1], ALU.subtract))
                        for c in range(KC):
                            ins = V.scalar_tensor_tensor(out=xxx[:, c, :], in0=xx[:, c, :], scalar=mx[:, c:c + 1],
                                                         in1=xs[:, c, 1:SEQ + 1], op0=ALU.mult, op1=ALU.add)
                        ins.then_inc(xxx_ready, 1)
                    for f in range(MIX):
                        if task in (None, f"mix{f}"):
                            dve.wait_ge(pr_ready, b * 12 + f + 2)
                            if f >= 2:
                                dve.nop(nofuse=True)
                                dve.wait_ge(xf_ready, b * MIX + f - 1)
                            for c in range(KC):
                                ins = V.scalar_tensor_tensor(out=mixed[:, f % 2, c, :], in0=pr[(f + 1) % 3][:, c, 0:SEQ],
                                                             scalar=mf[:, f, c:c + 1], in1=xx[:, c, :], op0=ALU.add, op1=ALU.mult)
                            ins.then_inc(dve_ev, 1)

                def make_kv(b, s, n):
                    c = n // (HN // 2)
                    dve.wait_ge(vrep_ready, b * G + n + 1)
                    if n >= 3:
                        dve.nop(nofuse=True)
                        dve.wait_ge(S_ready, b * G + n - 2)
                    V.tensor_tensor(kv[:, n % 3, :, :], vrep[n % 2][:, :, 0:SEQ],
                                    k[:, s, c:c + 1, :].broadcast_to([P, 2, SEQ]), ALU.mult).then_inc(kv_ready, 1)

                def back(b, s, task):
                    if task == "sum":
                        dve.wait_ge(y_part, b * G)
                        V.tensor_tensor(y[:], y_ps[:, :, 0:SEQ], yu[:], ALU.add).then_inc(y_ready, 1)
                    elif task == "centre":
                        dve.wait_ge(mean_ready, b)
                        V.tensor_tensor(y[:], y[:], aux[:, :, 0:SEQ], ALU.subtract).then_inc(yc_ready, 1)
                    elif task == "inverse":
                        dve.wait_ge(std_ready, b)
                        st.then(V.reciprocal(square[:], square[:]))
                    elif task == "scale":
                        st.then(V.tensor_tensor(y[:], y[:], square[:], ALU.mult))
                        for c in range(KC):
                            ins = V.tensor_scalar(y[:, c, :], y[:, c, :], ln_w[:, c:c + 1], ln_b[:, c:c + 1], ALU.mult, ALU.add)
                        st.then(ins)
                        dve.nop(nofuse=True)
                        dve.wait_ge(act_ev, b * 7)
                        V.tensor_tensor(y[:], y[:], g[:, s, :, :], ALU.mult).then_inc(z_ready, 1)
                    else:
                        dve.wait_ge(out_ready, b)
                        V.tensor_tensor(h[:, ds(b * 2 - 2, 2), :], out_ps[:], h[:, ds(b * 2 - 2, 2), :], ALU.add).then_inc(turn_done, 1)

                def turn(b, s, first=False, last=False):
                    dve.wait_ge(act_ev, b * 7 + 5)
                    dve.nop(nofuse=True)
                    dve.wait_ge(d_ready, b + 1)
                    for n in range(G):
                        c = n // (HN // 2)
                        make_kv(b, s, n)
                        dve.wait_ge(kv_ready, b * G + n + 1)
                        if n >= 3:
                            dve.nop(nofuse=True)
                            dve.wait_ge(rS_ready, b * G + n - 2)
                            dve.nop(nofuse=True)
                        for p in range(2):
                            ins = V.tensor_tensor_scan(S[:, n % 3, p, 1:SEQ], decay[:, s, c, 0:SEQ - 1], kv[:, n % 3, p, 0:SEQ - 1],
                                                       0.0, ALU.mult, ALU.add)
                        ins.then_inc(S_ready, 1)
                        for task in tasks_of(DVE_AT, n, first, last):
                            if task in BACK:
                                back(b, 1 - s, task)
                            elif task == "ruk":
                                dve.wait_ge(act_ev, b * 7 + 6)
                                for c2 in range(KC):
                                    ins = V.scalar_tensor_tensor(out=ruk[:, c2, :], in0=r[:, s, c2, :], scalar=bonus[:, c2:c2 + 1],
                                                                 in1=k[:, s, c2, :], op0=ALU.mult, op1=ALU.mult)
                                ins.then_inc(ruk_ready, 1)
                            elif task == "yu":
                                dve.wait_ge(yu_ready, b + 1)
                                V.tensor_tensor(yu[:], aux[:, :, 0:SEQ], v[:, s, :, :], ALU.mult)
                            else:
                                front(b + 1, 1 - s, task)

                dve.wait_ge(const, 1)
                over_turns(dve, front, turn, st, steps_of_turn=1 + 3)
                for task in ("sum", "centre", "inverse", "scale", "add"):
                    back(SEQS, 1, task)


LAYERS = [token_patches, taylor_attention, top1_experts, recurrent_mix, quantised_mlp, softmax_attention, grouped_experts, long_convolution, top2_experts]


def tower(nc, dram, out):
    with ExitStack() as ctx:
        core = Core(nc, ctx, dram)
        constants(core)
        for layer in LAYERS:
            layer(core)
        store_stream(core, out)


def layouts(a):
    import numpy as np

    def cm(w):
        return w.reshape(-1, P, w.shape[-1]).transpose(1, 0, 2)

    def columns(b):
        return b.reshape(-1, P).T

    def up(w):
        return w.reshape(w.shape[0], KC, P, -1).transpose(0, 2, 1, 3).reshape(w.shape[0], P, -1)

    def down(w):
        return w.reshape(w.shape[0], -1, P, w.shape[2]).transpose(0, 2, 1, 3).reshape(w.shape[0], P, -1)

    def bias(b):
        return b.reshape(b.shape[0], -1, P).transpose(0, 2, 1)

    d = {}
    patch = 16
    d["tok_x"] = a["x"].reshape(-1, patch).T
    d["tok_wh"] = a["L0_tok_W_h"].T
    d["tok_bh"] = columns(a["L0_tok_b_h"])
    d["tok_wo"] = cm(a["L0_tok_W_o"].T)
    d["tok_wr"] = np.concatenate([a["L0_tok_W_r"].T, a["L0_tok_b_r"][None], a["L0_tok_b_o"][None]])
    d["f0_wg"] = cm(a["L0_ffn_Wg"])
    d["f0_bg"] = a["L0_ffn_bg"][:, None]
    d["f0_w1"] = up(a["L0_ffn_W1"])
    d["f0_b1"] = bias(a["L0_ffn_b1"])
    d["f0_w2"] = down(a["L0_ffn_W2"])
    d["f0_b2"] = a["L0_ffn_b2"]
    d["f2_wg"] = cm(a["L2_ffn_gate_w"].T)
    d["f2_bias"] = a["L2_ffn_bias_e"][None]
    d["f2_w1"] = up(a["L2_ffn_up_w"].transpose(0, 2, 1))
    d["f2_w2"] = down(a["L2_ffn_down_w"].transpose(0, 2, 1))
    d["f2_s1"] = up(a["L2_ffn_shared_up"].T[None])
    d["f2_s2"] = down(a["L2_ffn_shared_down"].T[None])
    d["f3_wg"] = cm(a["L3_ffn_router_w"].T)
    d["f3_w1"] = up(a["L3_ffn_w1"].transpose(0, 2, 1))
    d["f3_b1"] = bias(a["L3_ffn_b1"])
    d["f3_w2"] = down(a["L3_ffn_w2"].transpose(0, 2, 1))
    d["f3_b2"] = a["L3_ffn_b2"]
    def spread(w):
        heads = w.reshape(w.shape[:-1] + (-1, 16))
        return np.concatenate([heads, np.zeros_like(heads)], -1).reshape(w.shape[:-1] + (-1,))

    for n in ("q", "k"):
        d["a2_w" + n] = cm(spread(a["L2_attn_W" + n].T))
        d["a2_b" + n] = columns(spread(a["L2_attn_b" + n]))
    for n in ("v", "o"):
        d["a2_w" + n] = cm(a["L2_attn_W" + n].T)
        d["a2_b" + n] = a["L2_attn_b" + n][None]
    def spread(w):
        heads = w.reshape(w.shape[:-1] + (-1, 16))
        return np.concatenate([heads, np.zeros_like(heads)], -1).reshape(w.shape[:-1] + (-1,))

    d["a0_gamma"] = columns(a["L0_attn_gamma"])
    d["a0_wq"] = cm(spread(a["L0_attn_w_q"]))
    kv = a["L0_attn_w_kv"]
    d["a0_wk"], d["a0_wv"] = cm(spread(kv[:, :kv.shape[1] // 2])), cm(kv[:, kv.shape[1] // 2:])
    d["a0_wo"] = a["L0_attn_w_out"]
    d["a3_lre"], d["a3_lim"] = a["L3_attn_Lambda_real"][:, None], a["L3_attn_Lambda_imag"][:, None]
    d["a3_cre"], d["a3_cim"] = a["L3_attn_C_real"].T, a["L3_attn_C_imag"].T
    d["a3_gain"], d["a3_shift"], d["a3_skip"] = (a["L3_attn_" + n][None] for n in ("ln_gamma", "ln_beta", "param_D"))
    f, t = np.arange(SEQ)[:, None], np.arange(SEQ)[None, :]
    turn = np.pi * ((f * t) % (2 * SEQ)) / SEQ
    sines = np.sin(turn)
    sines[0] = np.cos(np.pi * t[0])
    waves = np.concatenate([np.cos(turn), sines])
    weight = np.full((2, SEQ, 1), 2.0)
    weight[:, 0] = 1.0
    d["a3_F"] = waves.T.reshape(2, TT, 2 * SEQ).transpose(1, 0, 2).astype(np.float32)
    d["a3_G"] = (waves * weight.reshape(-1, 1) / (2 * SEQ)).reshape(4, TT, SEQ).transpose(1, 0, 2).astype(np.float32)
    d["f1_gate"], d["f1_up"], d["f1_down"] = (cm(a["L1_ffn_w_" + n]) for n in ("gate", "up", "down"))
    m = {n[len("L1_attn_"):]: v for n, v in a.items() if n.startswith("L1_attn_")}
    d["m1_w1"] = cm(m["time_maa_w1"])
    w2 = m["time_maa_w2"]
    d["m1_w2a"], d["m1_w2b"] = w2[:4].reshape(P, C), w2[4]
    d["m1_mx"] = columns(m["time_maa_x"].reshape(-1))
    d["m1_mf"] = np.stack([columns(m["time_maa_" + f].reshape(-1)) for f in "wkvrg"], 1)
    d["m1_tdecay"], d["m1_bonus"] = columns(m["time_decay"].reshape(-1)), columns(m["time_faaaa"].reshape(-1))
    d["m1_td1"], d["m1_td2"] = cm(m["time_decay_w1"]), m["time_decay_w2"]
    for n in "rkvgo":
        d["m1_w" + n] = cm(m["W_" + n])
    d["m1_lnw"], d["m1_lnb"] = columns(m["ln_w"]), columns(m["ln_b"])
    ch = np.arange(P)
    same = (ch[:, None] // 16 == ch[None, :] // 16)
    spread01 = (same[:, None, :] & (ch[:, None, None] % 16 == np.arange(16)[None, :, None])).astype(np.float32)
    d["m1_spread"], d["m1_gather"] = spread01, spread01.transpose(2, 1, 0)
    d["m1_same"] = same.astype(np.float32)
    return {n: np.ascontiguousarray(v) for n, v in d.items()}


def kernel(**inputs):
    import numpy as _np
    import concourse.bacc as _bacc
    from concourse import mybir as _mybir
    from concourse.bass_utils import run_bass_kernel_spmd as _run

    nc = _bacc.Bacc("TRN2", target_bir_lowering=False, num_devices=1)
    arrays, dram = {}, {}
    for name, a in layouts(inputs).items():
        arrays[f"in_{name}_dram"] = a
        dram[name] = nc.dram_tensor(f"in_{name}_dram", a.shape, _mybir.dt.from_np(a.dtype), kind="ExternalInput").ap()
    out = nc.dram_tensor("out_0_dram", (SEQS, SEQ, C), _mybir.dt.float32, kind="ExternalOutput").ap()
    tower(nc, dram, out)
    r = _run(nc, [arrays], core_ids=[0])
    return r.results[0]["out_0_dram"]
```
